# Optimizing a Trainium2 kernel written in Bass

```python
import numpy as np
import jax
import jax.numpy as jnp

def _softmax(x, axis=-1):
    return jax.nn.softmax(x, axis=axis)

def _gelu(x):
    return jax.nn.gelu(x, approximate=True)

def _silu(x):
    return jax.nn.silu(x)

def _sigmoid(x):
    return jax.nn.sigmoid(x)

def _layernorm(x, axis=-1, eps=1e-05):
    m = jnp.mean(x, axis=axis, keepdims=True)
    v = jnp.var(x, axis=axis, keepdims=True)
    return (x - m) / jnp.sqrt(v + eps)

def _scatter_add(tgt, idx, src, axis=0):
    return tgt.at[idx].add(src)

def _segment_sum(src, seg, n):
    return jax.ops.segment_sum(src, seg, n)
kernel_name = 'mk_hybrid_d4_jaxref_r8_cddede'

def setup_inputs(seed: int=0):
    np.random.seed(seed)
    _w = jnp.asarray

    def _L0_attn_a_setup():
        import jax, jax.numpy as jnp
        import numpy as np
        B, S, D = (2, 256, 128)
        H, P = (16, 64)
        NUM_OUT = 128
        key = jax.random.key(seed)
        ks = jax.random.split(key, 9)
        sc = 0.05
        return {'x': jax.random.normal(ks[0], (B, S, D), jnp.float32), 'q_w': jax.random.normal(ks[1], (H, P, D), jnp.float32) * sc, 'q_b': jax.random.normal(ks[2], (H, 1, P), jnp.float32) * sc, 'k_w': jax.random.normal(ks[3], (H, P, D), jnp.float32) * sc, 'k_b': jax.random.normal(ks[4], (H, 1, P), jnp.float32) * sc, 'v_w': jax.random.normal(ks[5], (H, P, D), jnp.float32) * sc, 'v_b': jax.random.normal(ks[6], (H, 1, P), jnp.float32) * sc, 'l_w': jax.random.normal(ks[7], (NUM_OUT, P * H), jnp.float32) * sc, 'l_b': jax.random.normal(ks[8], (1, NUM_OUT), jnp.float32) * sc}
    _L0_attn_a_in = _L0_attn_a_setup()

    def _L0_attn_b_setup():
        import jax, jax.numpy as jnp
        import numpy as np
        N_HEAD = 16
        K_KEEP = 391
        RECENCY = 64
        key = jax.random.key(seed)
        k1, k2, k3 = jax.random.split(key, 3)
        B, T, C = (2, 256, 128)
        x = jax.random.normal(k1, (B, T, C), dtype=jnp.float32)
        w_attn = jax.random.normal(k2, (3 * C, C), dtype=jnp.float32) * 0.02
        w_proj = jax.random.normal(k3, (C, C), dtype=jnp.float32) * 0.02
        return {'x': x, 'w_attn': w_attn, 'w_proj': w_proj}
    _L0_attn_b_in = _L0_attn_b_setup()

    def _L0_ffn_setup():
        import jax, jax.numpy as jnp
        import numpy as np
        B, S, D = (2, 256, 128)
        E, K, F = (16, 2, 64)
        FS = 128
        key = jax.random.key(seed)
        ks = jax.random.split(key, 8)

        def w(k, shape, fan_in):
            return jax.random.normal(k, shape, jnp.float32) / np.sqrt(fan_in).astype(np.float32)
        return {'x': jax.random.normal(ks[0], (B, S, D), jnp.float32), 'Wr': w(ks[1], (D, E), D), 'Wg': w(ks[2], (E, D, F), D), 'Wu': w(ks[3], (E, D, F), D), 'Wd': w(ks[4], (E, F, D), F), 'Sg': w(ks[5], (D, FS), D), 'Su': w(ks[6], (D, FS), D), 'Sd': w(ks[7], (FS, D), FS)}
    _L0_ffn_in = _L0_ffn_setup()

    def _L1_attn_a_setup():
        import jax, jax.numpy as jnp
        import numpy as np
        N_EMBD = 128
        N_HEAD = 8
        HEAD_DIM = N_EMBD // N_HEAD
        EPS = 1e-06

        def _lrpe(xh, theta, n):
            idx = jnp.arange(n, dtype=xh.dtype).reshape(1, n, 1)
            th = theta * idx
            th = th[None]
            return jnp.concatenate([xh * jnp.cos(th), xh * jnp.sin(th)], axis=-1)

        def _srmsnorm(y):
            ms = jnp.mean(jnp.square(y), axis=-1, keepdims=True)
            return y * jax.lax.rsqrt(ms + EPS)
        key = jax.random.key(seed)
        ks = jax.random.split(key, 8)
        b, n = (2, 256)
        x = jax.random.normal(ks[0], (b, n, N_EMBD), dtype=jnp.float32)
        slope_rate = -jax.random.uniform(ks[1], (N_HEAD, 1, 1), dtype=jnp.float32)
        s = 0.02
        qkvu_w = jax.random.normal(ks[2], (4 * N_EMBD, N_EMBD), dtype=jnp.float32) * s
        qkvu_b = jnp.zeros((4 * N_EMBD,), dtype=jnp.float32)
        out_w = jax.random.normal(ks[3], (N_EMBD, N_EMBD), dtype=jnp.float32) * s
        out_b = jnp.zeros((N_EMBD,), dtype=jnp.float32)
        d = N_EMBD
        theta = (10000.0 ** (-2.0 / d * jnp.arange(d, dtype=jnp.float32))).reshape(N_HEAD, 1, HEAD_DIM)
        return {'x': x, 'slope_rate': slope_rate, 'qkvu_w': qkvu_w, 'qkvu_b': qkvu_b, 'out_w': out_w, 'out_b': out_b, 'theta': theta}
    _L1_attn_a_in = _L1_attn_a_setup()

    def _L1_attn_b_setup():
        import jax, jax.numpy as jnp
        import numpy as np
        import math
        B, S, D = (4, 256, 128)
        H, DEG, DH, BUS, SLOTS = (8, 4, 32, 128, 64)
        EPS = 1.1920929e-07

        def _rms(x, w):
            return x * jax.lax.rsqrt(jnp.mean(x * x, axis=-1, keepdims=True) + EPS) * w
        key = jax.random.key(seed)
        ks = jax.random.split(key, 20)
        g = lambda k, shape, s=0.02: jax.random.normal(k, shape, jnp.float32) * s
        return {'x': jax.random.normal(ks[0], (B, S, D), jnp.float32), 'w_norm_in': jnp.ones((D,), jnp.float32), 'w_norm_out': jnp.ones((D,), jnp.float32), 'router_w1': g(ks[1], (D, D // 2)), 'router_w2': g(ks[2], (D // 2, 3)), 'router_b2': jnp.full((3,), 0.5, jnp.float32), 'ttt_w1': g(ks[3], (D, D // 4)), 'ttt_b1': jnp.zeros((D // 4,), jnp.float32), 'ttt_w2': g(ks[4], (D // 4, H * DEG)), 'ttt_b2': jnp.zeros((H * DEG,), jnp.float32), 'lambdas': jnp.array([0.9995, 0.9995, 0.997, 0.997, 0.995, 0.995, 0.97, 0.95], jnp.float32), 'slr_wq1': g(ks[5], (D, DH)), 'slr_wq2': g(ks[6], (D, DH)), 'slr_wk1': g(ks[7], (D, DH)), 'slr_wk2': g(ks[8], (D, DH)), 'slr_wv': g(ks[9], (D, DH)), 'slr_wo': g(ks[10], (DH, D)), 'slr_lam': jnp.array(0.5, jnp.float32), 'landmarks': g(ks[11], (SLOTS, D), 0.5), 'mix_w': g(ks[12], (2 * D, D)), 'bus_compress': g(ks[13], (D, BUS)), 'bus_expand': g(ks[14], (BUS, D)), 'bus_publish': g(ks[15], (BUS, BUS))}
    _L1_attn_b_in = _L1_attn_b_setup()

    def _L1_ffn_setup():
        import jax, jax.numpy as jnp
        import numpy as np
        EPS = 1e-05

        def _quantize(W):
            gamma = jnp.mean(jnp.abs(W))
            return jnp.clip(jnp.round(W / (gamma + EPS)), -1.0, 1.0)
        key = jax.random.key(seed)
        k_x, k_w1, k_b1, k_w2, k_b2 = jax.random.split(key, 5)
        n_embd = 128
        d_ff = 4 * n_embd
        B, S = (4, 512)
        bound1 = 1.0 / np.sqrt(n_embd)
        bound2 = 1.0 / np.sqrt(d_ff)
        x = jax.random.normal(k_x, (B, S, n_embd), dtype=jnp.float32)
        W1 = jax.random.uniform(k_w1, (d_ff, n_embd), jnp.float32, -bound1, bound1)
        b1 = jax.random.uniform(k_b1, (d_ff,), jnp.float32, -bound1, bound1)
        W2 = jax.random.uniform(k_w2, (n_embd, d_ff), jnp.float32, -bound2, bound2)
        b2 = jax.random.uniform(k_b2, (n_embd,), jnp.float32, -bound2, bound2)
        return {'x': x, 'W1': W1, 'b1': b1, 'W2': W2, 'b2': b2}
    _L1_ffn_in = _L1_ffn_setup()

    def _L2_attn_a_setup():
        import jax, jax.numpy as jnp
        import numpy as np
        D_MODEL = 128
        N_HEADS = 64
        D_HEAD = D_MODEL // N_HEADS
        B = 2
        S = 256

        def _xavier(key, fan):
            lim = np.sqrt(6.0 / (2 * fan)).astype(np.float32)
            return jax.random.uniform(key, (fan, fan), dtype=jnp.float32, minval=-lim, maxval=lim)
        key = jax.random.key(seed)
        ks = jax.random.split(key, 9)
        blim = 1.0 / np.sqrt(D_MODEL)

        def bias(k):
            return jax.random.uniform(k, (D_MODEL,), dtype=jnp.float32, minval=-blim, maxval=blim)
        return {'x': jax.random.normal(ks[0], (B, S, D_MODEL), dtype=jnp.float32), 'Wq': _xavier(ks[1], D_MODEL), 'bq': bias(ks[2]), 'Wk': _xavier(ks[3], D_MODEL), 'bk': bias(ks[4]), 'Wv': _xavier(ks[5], D_MODEL), 'bv': bias(ks[6]), 'Wo': _xavier(ks[7], D_MODEL), 'bo': jnp.zeros((D_MODEL,), dtype=jnp.float32), 'beta': jnp.zeros((1,), dtype=jnp.float32)}
    _L2_attn_a_in = _L2_attn_a_setup()

    def _L2_attn_b_setup():
        import jax, jax.numpy as jnp
        import numpy as np
        from jax import lax
        D_MODEL, D_INNER, D_STATE, D_CONV, DT_RANK = (128, 256, 16, 4, 64)
        BATCH, SEQLEN = (1, 256)

        def silu(v):
            return v * jax.nn.sigmoid(v)
        key = jax.random.key(seed)
        ks = jax.random.split(key, 9)
        s = 0.02
        x = jax.random.normal(ks[0], (BATCH, SEQLEN, D_MODEL), jnp.float32)
        in_proj_w = jax.random.normal(ks[1], (2 * D_INNER, D_MODEL), jnp.float32) * s
        conv_w = jax.random.normal(ks[2], (D_INNER, D_CONV), jnp.float32) * 0.2
        conv_b = jax.random.normal(ks[3], (D_INNER,), jnp.float32) * 0.01
        x_proj_w = jax.random.normal(ks[4], (DT_RANK + 2 * D_STATE, D_INNER), jnp.float32) * s
        dt_proj_w = jax.random.uniform(ks[5], (D_INNER, DT_RANK), jnp.float32, -DT_RANK ** (-0.5), DT_RANK ** (-0.5))
        dt = jnp.exp(jax.random.uniform(ks[6], (D_INNER,), jnp.float32) * (np.log(0.1) - np.log(0.001)) + np.log(0.001))
        dt = jnp.clip(dt, 0.0001, None)
        dt_proj_b = dt + jnp.log(-jnp.expm1(-dt))
        A_log = jnp.log(jnp.tile(jnp.arange(1, D_STATE + 1, dtype=jnp.float32), (D_INNER, 1)))
        D = jnp.ones((D_INNER,), jnp.float32)
        out_proj_w = jax.random.normal(ks[7], (D_MODEL, D_INNER), jnp.float32) * s
        return dict(x=x, in_proj_w=in_proj_w, conv_w=conv_w, conv_b=conv_b, x_proj_w=x_proj_w, dt_proj_w=dt_proj_w, dt_proj_b=dt_proj_b, A_log=A_log, D=D, out_proj_w=out_proj_w)
    _L2_attn_b_in = _L2_attn_b_setup()

    def _L2_ffn_setup():
        import jax, jax.numpy as jnp
        import numpy as np
        from jax import lax
        D = 128
        H = 176
        E = 8
        K = 2
        ROUTER_SCALE = 1.0

        def _expert(x, w1, b1, w3, b3, w2, b2):
            h = jax.nn.silu((x @ w1 + b1) * (x @ w3 + b3))
            return h @ w2 + b2
        key = jax.random.key(seed)
        ks = jax.random.split(key, 16)
        s = 0.02
        inp = {'x': jax.random.normal(ks[0], (2, 256, D), dtype=jnp.float32), 'gate_w': jax.random.normal(ks[1], (E, D), dtype=jnp.float32) * s, 'gate_b': jax.random.normal(ks[2], (E,), dtype=jnp.float32) * s, 'w1': jax.random.normal(ks[3], (E, D, H), dtype=jnp.float32) * s, 'b1': jax.random.normal(ks[4], (E, H), dtype=jnp.float32) * s, 'w3': jax.random.normal(ks[5], (E, D, H), dtype=jnp.float32) * s, 'b3': jax.random.normal(ks[6], (E, H), dtype=jnp.float32) * s, 'w2': jax.random.normal(ks[7], (E, H, D), dtype=jnp.float32) * s, 'b2': jax.random.normal(ks[8], (E, D), dtype=jnp.float32) * s, 'sw1': jax.random.normal(ks[9], (D, H), dtype=jnp.float32) * s, 'sb1': jax.random.normal(ks[10], (H,), dtype=jnp.float32) * s, 'sw3': jax.random.normal(ks[11], (D, H), dtype=jnp.float32) * s, 'sb3': jax.random.normal(ks[12], (H,), dtype=jnp.float32) * s, 'sw2': jax.random.normal(ks[13], (H, D), dtype=jnp.float32) * s, 'sb2': jax.random.normal(ks[14], (D,), dtype=jnp.float32) * s}
        return inp
    _L2_ffn_in = _L2_ffn_setup()

    def _L3_attn_a_setup():
        import jax, jax.numpy as jnp
        import numpy as np
        B, L, E, H = (1, 512, 128, 16)
        D = E // H
        EPS = 1e-06
        key = jax.random.key(seed)
        k1, k2, k3 = jax.random.split(key, 3)
        x = jax.random.normal(k1, (B, L, E), dtype=jnp.float32)
        qkv_w = jax.random.normal(k2, (E, 3 * E), dtype=jnp.float32) / np.sqrt(E)
        qkv_b = jnp.zeros((3 * E,), dtype=jnp.float32)
        out_w = jax.random.normal(k3, (E, E), dtype=jnp.float32) / np.sqrt(E)
        out_b = jnp.zeros((E,), dtype=jnp.float32)
        return {'x': x, 'qkv_w': qkv_w, 'qkv_b': qkv_b, 'out_w': out_w, 'out_b': out_b}
    _L3_attn_a_in = _L3_attn_a_setup()

    def _L3_attn_b_setup():
        import jax, jax.numpy as jnp
        import numpy as np
        DIM, D_INNER, D_STATE, DT_RANK, D_CONV = (128, 256, 16, 64, 4)
        BATCH, SEQ = (2, 128)

        def _silu(v):
            return v * jax.nn.sigmoid(v)

        def _ssm_forward(x, in_proj_w, conv_w, conv_b, x_proj_w, dt_proj_w, dt_proj_b, A_log, D_param, out_proj_w):
            b, l, _ = x.shape
            d_inner, d_conv = (conv_w.shape[0], conv_w.shape[2])
            dt_rank, n = (dt_proj_w.shape[0], A_log.shape[1])
            x_and_res = x @ in_proj_w
            xp, res = (x_and_res[..., :d_inner], x_and_res[..., d_inner:])
            h = jax.lax.conv_general_dilated(xp.transpose(0, 2, 1), conv_w, window_strides=(1,), padding=[(d_conv - 1, 0)], dimension_numbers=('NCH', 'OIH', 'NCH'), feature_group_count=d_inner) + conv_b[None, :, None]
            h = _silu(h.transpose(0, 2, 1))
            A = -jnp.exp(A_log)
            x_dbl = h @ x_proj_w
            dlt, Bm, Cm = (x_dbl[..., :dt_rank], x_dbl[..., dt_rank:dt_rank + n], x_dbl[..., dt_rank + n:])
            delta = jax.nn.softplus(dlt @ dt_proj_w + dt_proj_b)
            deltaA = jnp.exp(jnp.einsum('bld,dn->bldn', delta, A))
            deltaB_u = (delta * h)[..., None] * Bm[:, :, None, :]

            def step(state, t):
                dA_t, dBu_t, c_t = t
                state = dA_t * state + dBu_t
                y_t = jnp.einsum('bdn,bn->bd', state, c_t)
                return (state, y_t)
            init = jnp.zeros((b, d_inner, n), h.dtype)
            _, ys = jax.lax.scan(step, init, (deltaA.transpose(1, 0, 2, 3), deltaB_u.transpose(1, 0, 2, 3), Cm.transpose(1, 0, 2)))
            y = ys.transpose(1, 0, 2) + h * D_param
            y = y * _silu(res)
            return y @ out_proj_w
        key = jax.random.key(seed)
        ks = jax.random.split(key, 9)
        s = 0.02
        A = jnp.tile(jnp.arange(1, D_STATE + 1, dtype=jnp.float32), (D_INNER, 1))
        return {'x': jax.random.normal(ks[0], (BATCH, SEQ, DIM), jnp.float32), 'in_proj_w': jax.random.normal(ks[1], (DIM, 2 * D_INNER), jnp.float32) * s, 'conv_w': jax.random.normal(ks[2], (D_INNER, 1, D_CONV), jnp.float32) * 0.2, 'conv_b': jax.random.normal(ks[3], (D_INNER,), jnp.float32) * 0.1, 'x_proj_w': jax.random.normal(ks[4], (D_INNER, DT_RANK + 2 * D_STATE), jnp.float32) * s, 'dt_proj_w': jax.random.normal(ks[5], (DT_RANK, D_INNER), jnp.float32) * s, 'dt_proj_b': jax.random.normal(ks[6], (D_INNER,), jnp.float32) * 0.1, 'A_log': jnp.log(A), 'D_param': jnp.ones((D_INNER,), jnp.float32), 'out_proj_w': jax.random.normal(ks[7], (D_INNER, DIM), jnp.float32) * s}
    _L3_attn_b_in = _L3_attn_b_setup()

    def _L3_ffn_setup():
        import jax, jax.numpy as jnp
        import numpy as np
        from jax import lax
        T, B, I, M, O = (32, 64, 128, 128, 128)

        def _xavier(key, shape):
            fan_out, fan_in = shape
            limit = float(np.sqrt(6.0 / (fan_in + fan_out)))
            return jax.random.uniform(key, shape, jnp.float32, -limit, limit)
        key = jax.random.key(seed)
        ks = jax.random.split(key, 9)
        x = jax.random.normal(ks[0], (T, B, I), jnp.float32)
        return {'x': x, 'wf': _xavier(ks[1], (M, I)), 'uf': _xavier(ks[2], (M, M)), 'bf': jnp.zeros((M,), jnp.float32), 'wi': _xavier(ks[3], (M, I)), 'ui': _xavier(ks[4], (M, M)), 'bi': jnp.zeros((M,), jnp.float32), 'wc': _xavier(ks[5], (M, I)), 'uc': _xavier(ks[6], (M, M)), 'bc': jnp.zeros((M,), jnp.float32), 'wo': _xavier(ks[7], (O, I)), 'uo': _xavier(ks[8], (O, M)), 'bo': jnp.zeros((O,), jnp.float32), 'in_c': jnp.zeros((M,), jnp.float32)}
    _L3_ffn_in = _L3_ffn_setup()
    _d = {'L0_attn_a_x': _L0_attn_a_in['x'], 'L0_attn_a_q_w': _L0_attn_a_in['q_w'], 'L0_attn_a_q_b': _L0_attn_a_in['q_b'], 'L0_attn_a_k_w': _L0_attn_a_in['k_w'], 'L0_attn_a_k_b': _L0_attn_a_in['k_b'], 'L0_attn_a_v_w': _L0_attn_a_in['v_w'], 'L0_attn_a_v_b': _L0_attn_a_in['v_b'], 'L0_attn_a_l_w': _L0_attn_a_in['l_w'], 'L0_attn_a_l_b': _L0_attn_a_in['l_b'], 'L0_attn_b_w_attn': _L0_attn_b_in['w_attn'], 'L0_attn_b_w_proj': _L0_attn_b_in['w_proj'], 'L0_ffn_Wr': _L0_ffn_in['Wr'], 'L0_ffn_Wg': _L0_ffn_in['Wg'], 'L0_ffn_Wu': _L0_ffn_in['Wu'], 'L0_ffn_Wd': _L0_ffn_in['Wd'], 'L0_ffn_Sg': _L0_ffn_in['Sg'], 'L0_ffn_Su': _L0_ffn_in['Su'], 'L0_ffn_Sd': _L0_ffn_in['Sd'], 'L1_attn_a_slope_rate': _L1_attn_a_in['slope_rate'], 'L1_attn_a_qkvu_w': _L1_attn_a_in['qkvu_w'], 'L1_attn_a_qkvu_b': _L1_attn_a_in['qkvu_b'], 'L1_attn_a_out_w': _L1_attn_a_in['out_w'], 'L1_attn_a_out_b': _L1_attn_a_in['out_b'], 'L1_attn_a_theta': _L1_attn_a_in['theta'], 'L1_attn_b_w_norm_in': _L1_attn_b_in['w_norm_in'], 'L1_attn_b_w_norm_out': _L1_attn_b_in['w_norm_out'], 'L1_attn_b_router_w1': _L1_attn_b_in['router_w1'], 'L1_attn_b_router_w2': _L1_attn_b_in['router_w2'], 'L1_attn_b_router_b2': _L1_attn_b_in['router_b2'], 'L1_attn_b_ttt_w1': _L1_attn_b_in['ttt_w1'], 'L1_attn_b_ttt_b1': _L1_attn_b_in['ttt_b1'], 'L1_attn_b_ttt_w2': _L1_attn_b_in['ttt_w2'], 'L1_attn_b_ttt_b2': _L1_attn_b_in['ttt_b2'], 'L1_attn_b_lambdas': _L1_attn_b_in['lambdas'], 'L1_attn_b_slr_wq1': _L1_attn_b_in['slr_wq1'], 'L1_attn_b_slr_wq2': _L1_attn_b_in['slr_wq2'], 'L1_attn_b_slr_wk1': _L1_attn_b_in['slr_wk1'], 'L1_attn_b_slr_wk2': _L1_attn_b_in['slr_wk2'], 'L1_attn_b_slr_wv': _L1_attn_b_in['slr_wv'], 'L1_attn_b_slr_wo': _L1_attn_b_in['slr_wo'], 'L1_attn_b_slr_lam': _L1_attn_b_in['slr_lam'], 'L1_attn_b_landmarks': _L1_attn_b_in['landmarks'], 'L1_attn_b_mix_w': _L1_attn_b_in['mix_w'], 'L1_attn_b_bus_compress': _L1_attn_b_in['bus_compress'], 'L1_attn_b_bus_expand': _L1_attn_b_in['bus_expand'], 'L1_attn_b_bus_publish': _L1_attn_b_in['bus_publish'], 'L1_ffn_W1': _L1_ffn_in['W1'], 'L1_ffn_b1': _L1_ffn_in['b1'], 'L1_ffn_W2': _L1_ffn_in['W2'], 'L1_ffn_b2': _L1_ffn_in['b2'], 'L2_attn_a_Wq': _L2_attn_a_in['Wq'], 'L2_attn_a_bq': _L2_attn_a_in['bq'], 'L2_attn_a_Wk': _L2_attn_a_in['Wk'], 'L2_attn_a_bk': _L2_attn_a_in['bk'], 'L2_attn_a_Wv': _L2_attn_a_in['Wv'], 'L2_attn_a_bv': _L2_attn_a_in['bv'], 'L2_attn_a_Wo': _L2_attn_a_in['Wo'], 'L2_attn_a_bo': _L2_attn_a_in['bo'], 'L2_attn_a_beta': _L2_attn_a_in['beta'], 'L2_attn_b_in_proj_w': _L2_attn_b_in['in_proj_w'], 'L2_attn_b_conv_w': _L2_attn_b_in['conv_w'], 'L2_attn_b_conv_b': _L2_attn_b_in['conv_b'], 'L2_attn_b_x_proj_w': _L2_attn_b_in['x_proj_w'], 'L2_attn_b_dt_proj_w': _L2_attn_b_in['dt_proj_w'], 'L2_attn_b_dt_proj_b': _L2_attn_b_in['dt_proj_b'], 'L2_attn_b_A_log': _L2_attn_b_in['A_log'], 'L2_attn_b_D': _L2_attn_b_in['D'], 'L2_attn_b_out_proj_w': _L2_attn_b_in['out_proj_w'], 'L2_ffn_gate_w': _L2_ffn_in['gate_w'], 'L2_ffn_gate_b': _L2_ffn_in['gate_b'], 'L2_ffn_w1': _L2_ffn_in['w1'], 'L2_ffn_b1': _L2_ffn_in['b1'], 'L2_ffn_w3': _L2_ffn_in['w3'], 'L2_ffn_b3': _L2_ffn_in['b3'], 'L2_ffn_w2': _L2_ffn_in['w2'], 'L2_ffn_b2': _L2_ffn_in['b2'], 'L2_ffn_sw1': _L2_ffn_in['sw1'], 'L2_ffn_sb1': _L2_ffn_in['sb1'], 'L2_ffn_sw3': _L2_ffn_in['sw3'], 'L2_ffn_sb3': _L2_ffn_in['sb3'], 'L2_ffn_sw2': _L2_ffn_in['sw2'], 'L2_ffn_sb2': _L2_ffn_in['sb2'], 'L3_attn_a_qkv_w': _L3_attn_a_in['qkv_w'], 'L3_attn_a_qkv_b': _L3_attn_a_in['qkv_b'], 'L3_attn_a_out_w': _L3_attn_a_in['out_w'], 'L3_attn_a_out_b': _L3_attn_a_in['out_b'], 'L3_attn_b_in_proj_w': _L3_attn_b_in['in_proj_w'], 'L3_attn_b_conv_w': _L3_attn_b_in['conv_w'], 'L3_attn_b_conv_b': _L3_attn_b_in['conv_b'], 'L3_attn_b_x_proj_w': _L3_attn_b_in['x_proj_w'], 'L3_attn_b_dt_proj_w': _L3_attn_b_in['dt_proj_w'], 'L3_attn_b_dt_proj_b': _L3_attn_b_in['dt_proj_b'], 'L3_attn_b_A_log': _L3_attn_b_in['A_log'], 'L3_attn_b_D_param': _L3_attn_b_in['D_param'], 'L3_attn_b_out_proj_w': _L3_attn_b_in['out_proj_w'], 'L3_ffn_wf': _L3_ffn_in['wf'], 'L3_ffn_uf': _L3_ffn_in['uf'], 'L3_ffn_bf': _L3_ffn_in['bf'], 'L3_ffn_wi': _L3_ffn_in['wi'], 'L3_ffn_ui': _L3_ffn_in['ui'], 'L3_ffn_bi': _L3_ffn_in['bi'], 'L3_ffn_wc': _L3_ffn_in['wc'], 'L3_ffn_uc': _L3_ffn_in['uc'], 'L3_ffn_bc': _L3_ffn_in['bc'], 'L3_ffn_wo': _L3_ffn_in['wo'], 'L3_ffn_uo': _L3_ffn_in['uo'], 'L3_ffn_bo': _L3_ffn_in['bo'], 'L3_ffn_in_c': _L3_ffn_in['in_c']}
    _x0 = _d['L0_attn_a_x']
    _d['L0_attn_a_x'] = jax.random.normal(jax.random.fold_in(jax.random.key(seed), 1), (4, 512, 128), dtype=_x0.dtype)
    del _x0
    return _d

def reference(L0_attn_a_x, L0_attn_a_q_w, L0_attn_a_q_b, L0_attn_a_k_w, L0_attn_a_k_b, L0_attn_a_v_w, L0_attn_a_v_b, L0_attn_a_l_w, L0_attn_a_l_b, L0_attn_b_w_attn, L0_attn_b_w_proj, L0_ffn_Wr, L0_ffn_Wg, L0_ffn_Wu, L0_ffn_Wd, L0_ffn_Sg, L0_ffn_Su, L0_ffn_Sd, L1_attn_a_slope_rate, L1_attn_a_qkvu_w, L1_attn_a_qkvu_b, L1_attn_a_out_w, L1_attn_a_out_b, L1_attn_a_theta, L1_attn_b_w_norm_in, L1_attn_b_w_norm_out, L1_attn_b_router_w1, L1_attn_b_router_w2, L1_attn_b_router_b2, L1_attn_b_ttt_w1, L1_attn_b_ttt_b1, L1_attn_b_ttt_w2, L1_attn_b_ttt_b2, L1_attn_b_lambdas, L1_attn_b_slr_wq1, L1_attn_b_slr_wq2, L1_attn_b_slr_wk1, L1_attn_b_slr_wk2, L1_attn_b_slr_wv, L1_attn_b_slr_wo, L1_attn_b_slr_lam, L1_attn_b_landmarks, L1_attn_b_mix_w, L1_attn_b_bus_compress, L1_attn_b_bus_expand, L1_attn_b_bus_publish, L1_ffn_W1, L1_ffn_b1, L1_ffn_W2, L1_ffn_b2, L2_attn_a_Wq, L2_attn_a_bq, L2_attn_a_Wk, L2_attn_a_bk, L2_attn_a_Wv, L2_attn_a_bv, L2_attn_a_Wo, L2_attn_a_bo, L2_attn_a_beta, L2_attn_b_in_proj_w, L2_attn_b_conv_w, L2_attn_b_conv_b, L2_attn_b_x_proj_w, L2_attn_b_dt_proj_w, L2_attn_b_dt_proj_b, L2_attn_b_A_log, L2_attn_b_D, L2_attn_b_out_proj_w, L2_ffn_gate_w, L2_ffn_gate_b, L2_ffn_w1, L2_ffn_b1, L2_ffn_w3, L2_ffn_b3, L2_ffn_w2, L2_ffn_b2, L2_ffn_sw1, L2_ffn_sb1, L2_ffn_sw3, L2_ffn_sb3, L2_ffn_sw2, L2_ffn_sb2, L3_attn_a_qkv_w, L3_attn_a_qkv_b, L3_attn_a_out_w, L3_attn_a_out_b, L3_attn_b_in_proj_w, L3_attn_b_conv_w, L3_attn_b_conv_b, L3_attn_b_x_proj_w, L3_attn_b_dt_proj_w, L3_attn_b_dt_proj_b, L3_attn_b_A_log, L3_attn_b_D_param, L3_attn_b_out_proj_w, L3_ffn_wf, L3_ffn_uf, L3_ffn_bf, L3_ffn_wi, L3_ffn_ui, L3_ffn_bi, L3_ffn_wc, L3_ffn_uc, L3_ffn_bc, L3_ffn_wo, L3_ffn_uo, L3_ffn_bo, L3_ffn_in_c):

    def _L0_attn_a_ref(x, q_w, q_b, k_w, k_b, v_w, v_b, l_w, l_b):
        import jax, jax.numpy as jnp
        import numpy as np
        B, S, D = (2, 256, 128)
        H, P = (16, 64)
        NUM_OUT = 128
        q = jnp.einsum('bsd,hpd->bhsp', x, q_w) + q_b
        k = jnp.einsum('bsd,hpd->bhsp', x, k_w) + k_b
        v = jnp.einsum('bsd,hpd->bhsp', x, v_w) + v_b
        scores = jnp.einsum('bhqp,bhkp->bhqk', q, k) / jnp.sqrt(jnp.float32(P))
        attn = jax.nn.softmax(scores, axis=2)
        ctx = jnp.einsum('bhqk,bhkp->bqhp', attn, v)
        concat = ctx.reshape(ctx.shape[0], ctx.shape[1], H * P)
        out = concat @ l_w.T + l_b
        return out

    def _L0_attn_b_ref(x, w_attn, w_proj):
        import jax, jax.numpy as jnp
        import numpy as np
        N_HEAD = 16
        K_KEEP = 391
        RECENCY = 64
        B, T, C = x.shape
        H = N_HEAD
        D = C // H
        inv_sqrt_d = float(D) ** (-0.5)
        qkv = x @ w_attn.T
        q, k, v = jnp.split(qkv, 3, axis=2)
        q = q.reshape(B, T, H, D).transpose(0, 2, 1, 3)
        k = k.reshape(B, T, H, D).transpose(0, 2, 1, 3)
        v = v.reshape(B, T, H, D).transpose(0, 2, 1, 3)
        scores = jnp.einsum('bhqd,bhkd->bhqk', q, k) * inv_sqrt_d
        causal = jnp.tril(jnp.ones((T, T), dtype=bool))
        scores = jnp.where(causal[None, None], scores, -jnp.inf)
        attn_weights = jax.nn.softmax(scores, axis=-1)
        mean_importance = attn_weights.mean(axis=2)
        mean_importance = mean_importance.at[:, :, -RECENCY:].set(1.0)
        k_keep = min(K_KEEP, T)
        _, idx = jax.lax.top_k(mean_importance, k_keep)
        idx_e = idx[..., None]
        K_keep = jnp.take_along_axis(k, idx_e, axis=2)
        V_keep = jnp.take_along_axis(v, idx_e, axis=2)
        s2 = jnp.einsum('bhqd,bhkd->bhqk', q, K_keep) * inv_sqrt_d
        a2 = jax.nn.softmax(s2, axis=-1)
        out = jnp.einsum('bhqk,bhkd->bhqd', a2, V_keep)
        out = out.transpose(0, 2, 1, 3).reshape(B, T, C)
        return out @ w_proj.T

    def _L0_ffn_ref(x, Wr, Wg, Wu, Wd, Sg, Su, Sd):
        import jax, jax.numpy as jnp
        import numpy as np
        B, S, D = (2, 256, 128)
        E, K, F = (16, 2, 64)
        FS = 128
        b, s, d = x.shape
        T = b * s
        xf = x.reshape(T, d)
        shared = jax.nn.silu(xf @ Sg) * (xf @ Su) @ Sd
        probs = jax.nn.softmax(xf @ Wr, axis=-1)
        topk_p, topk_i = jax.lax.top_k(probs, K)
        n_exp = Wr.shape[1]
        cw = jnp.zeros((T, n_exp), x.dtype).at[jnp.arange(T)[:, None], topk_i].add(topk_p)

        def step(acc, ew):
            wg, wu, wd, c = ew
            y = jax.nn.silu(xf @ wg) * (xf @ wu) @ wd
            return (acc + y * c[:, None], None)
        routed, _ = jax.lax.scan(step, jnp.zeros_like(xf), (Wg, Wu, Wd, cw.T))
        return (routed + shared).reshape(b, s, d)

    def _L1_attn_a_ref(x, slope_rate, qkvu_w, qkvu_b, out_w, out_b, theta):
        import jax, jax.numpy as jnp
        import numpy as np
        N_EMBD = 128
        N_HEAD = 8
        HEAD_DIM = N_EMBD // N_HEAD
        EPS = 1e-06

        def _lrpe(xh, theta, n):
            idx = jnp.arange(n, dtype=xh.dtype).reshape(1, n, 1)
            th = theta * idx
            th = th[None]
            return jnp.concatenate([xh * jnp.cos(th), xh * jnp.sin(th)], axis=-1)

        def _srmsnorm(y):
            ms = jnp.mean(jnp.square(y), axis=-1, keepdims=True)
            return y * jax.lax.rsqrt(ms + EPS)
        b, n, hd = x.shape
        h = N_HEAD
        qkvu = x @ qkvu_w.T + qkvu_b
        q, k, v, u = jnp.split(qkvu, 4, axis=-1)

        def to_heads(t):
            return t.reshape(b, n, h, hd // h).transpose(0, 2, 1, 3)
        q, k, v = (to_heads(q), to_heads(k), to_heads(v))
        q = jax.nn.silu(q)
        k = jax.nn.silu(k)
        q = _lrpe(q, theta, n)
        k = _lrpe(k, theta, n)
        tril = jnp.tril(jnp.ones((n, n), dtype=x.dtype))
        mask = jnp.exp(slope_rate * tril)
        energy = jnp.einsum('bhne,bhme->bhnm', q, k) * mask[None]
        out = jnp.einsum('bhnm,bhmd->bhnd', energy, v)
        out = out.transpose(0, 2, 1, 3).reshape(b, n, hd)
        out = _srmsnorm(out)
        out = u * out
        out = out @ out_w.T + out_b
        return out

    def _L1_attn_b_ref(x, w_norm_in, w_norm_out, router_w1, router_w2, router_b2, ttt_w1, ttt_b1, ttt_w2, ttt_b2, lambdas, slr_wq1, slr_wq2, slr_wk1, slr_wk2, slr_wv, slr_wo, slr_lam, landmarks, mix_w, bus_compress, bus_expand, bus_publish):
        import jax, jax.numpy as jnp
        import numpy as np
        import math
        B, S, D = (4, 256, 128)
        H, DEG, DH, BUS, SLOTS = (8, 4, 32, 128, 64)
        EPS = 1.1920929e-07

        def _rms(x, w):
            return x * jax.lax.rsqrt(jnp.mean(x * x, axis=-1, keepdims=True) + EPS) * w
        b, s, d = x.shape
        hd = d // H
        residual = x
        xn = _rms(x, w_norm_in)
        route_in = xn.mean(axis=1)
        logits = jax.nn.silu(route_in @ router_w1) @ router_w2 + router_b2
        probs = jax.nn.softmax(logits, axis=-1)
        p_medium, p_full = (probs[:, 1], probs[:, 2])
        ttt = (jax.nn.silu(route_in @ ttt_w1 + ttt_b1) @ ttt_w2 + ttt_b2).reshape(b, H, DEG)
        ttt_scale = 0.1 * jnp.tanh(ttt)
        xh = xn.reshape(b, s, H, hd).transpose(1, 0, 2, 3)
        lam = lambdas[None, :, None]

        def ema_step(state, xt):
            state = lam * state + (1.0 - lam) * xt
            return (state, state)
        _, ys = jax.lax.scan(ema_step, jnp.zeros((b, H, hd), x.dtype), xh)
        ssm_out = ys.transpose(1, 0, 2, 3).reshape(b, s, d)
        q1, q2 = (xn @ slr_wq1, xn @ slr_wq2)
        k1, k2 = (xn @ slr_wk1, xn @ slr_wk2)
        v = xn @ slr_wv
        sc = 1.0 / math.sqrt(DH)
        a1 = jax.nn.softmax(jnp.einsum('bqd,bkd->bqk', q1, k1) * sc, axis=-1)
        a2 = jax.nn.softmax(jnp.einsum('bqd,bkd->bqk', q2, k2) * sc, axis=-1)
        ctx = jnp.einsum('bqk,bkd->bqd', a1 - slr_lam * a2, v)
        slr_out = ctx @ slr_wo
        mixed = ssm_out + (p_medium + p_full)[:, None, None] * slr_out
        qy = xn[:, -1:, :]
        kk = jnp.broadcast_to(landmarks[None], (b, SLOTS, d))
        attn = jax.nn.softmax(jnp.einsum('bqd,bkd->bqk', qy, kk) / math.sqrt(d), axis=-1)
        arc_ctx = jnp.einsum('bqk,bkd->bqd', attn, kk)
        mixed = mixed.at[:, -1:, :].add(p_full[:, None, None] * arc_ctx)
        out = jnp.concatenate([mixed, xn], axis=-1) @ mix_w
        out = residual + _rms(out, w_norm_out)
        summary = out.mean(axis=1, keepdims=True) @ bus_compress
        published = summary @ bus_publish
        aw = jax.nn.softmax(jnp.einsum('bqd,bkd->bqk', summary, published) / math.sqrt(BUS), axis=-1)
        context = jnp.einsum('bqk,bkd->bqd', aw, published)
        out = out + 0.1 * (context @ bus_expand)
        return out

    def _L1_ffn_ref(x, W1, b1, W2, b2):
        import jax, jax.numpy as jnp
        import numpy as np
        EPS = 1e-05

        def _quantize(W):
            gamma = jnp.mean(jnp.abs(W))
            return jnp.clip(jnp.round(W / (gamma + EPS)), -1.0, 1.0)
        Wq1 = _quantize(W1)
        Wq2 = _quantize(W2)
        h = jax.nn.relu(jnp.einsum('bsd,fd->bsf', x, Wq1) + b1)
        out = jnp.einsum('bsf,df->bsd', h, Wq2) + b2
        return out

    def _L2_attn_a_ref(x, Wq, bq, Wk, bk, Wv, bv, Wo, bo, beta):
        import jax, jax.numpy as jnp
        import numpy as np
        D_MODEL = 128
        N_HEADS = 64
        D_HEAD = D_MODEL // N_HEADS
        B = 2
        S = 256

        def _xavier(key, fan):
            lim = np.sqrt(6.0 / (2 * fan)).astype(np.float32)
            return jax.random.uniform(key, (fan, fan), dtype=jnp.float32, minval=-lim, maxval=lim)
        b, s, dm = x.shape
        h, d = (N_HEADS, D_HEAD)

        def heads(y):
            return y.reshape(b, s, h, d).transpose(0, 2, 1, 3).reshape(b * h, s, d)
        q = heads(x @ Wq.T + bq)
        k = heads(x @ Wk.T + bk)
        v = heads(x @ Wv.T + bv)
        be = jnp.exp(beta)
        q = jax.nn.softmax(be * q, axis=-1)
        k = jax.nn.softmax(be * k, axis=-1)
        kv = jnp.cumsum(jnp.einsum('zsD,zsd->zsDd', k, v), axis=1)
        kn = jnp.cumsum(k, axis=1)
        num = jnp.einsum('zsD,zsDd->zsd', q, kv)
        den = jnp.sum(q * kn, axis=-1, keepdims=True)
        out = num / den
        out = out.reshape(b, h, s, d).transpose(0, 2, 1, 3).reshape(b, s, dm)
        return out @ Wo.T + bo

    def _L2_attn_b_ref(x, in_proj_w, conv_w, conv_b, x_proj_w, dt_proj_w, dt_proj_b, A_log, D, out_proj_w):
        import jax, jax.numpy as jnp
        import numpy as np
        from jax import lax
        D_MODEL, D_INNER, D_STATE, D_CONV, DT_RANK = (128, 256, 16, 4, 64)
        BATCH, SEQLEN = (1, 256)

        def silu(v):
            return v * jax.nn.sigmoid(v)
        b, L, _ = x.shape
        di, n = A_log.shape
        xz = x @ in_proj_w.T
        xi, z = (xz[..., :di], xz[..., di:])
        xt = xi.transpose(0, 2, 1)
        w = conv_w[:, None, :]
        xc = lax.conv_general_dilated(xt, w, (1,), [(D_CONV - 1, 0)], dimension_numbers=('NCH', 'OIH', 'NCH'), feature_group_count=di)
        u = silu(xc + conv_b[None, :, None]).transpose(0, 2, 1)
        x_dbl = u @ x_proj_w.T
        dtr = x_dbl[..., :DT_RANK]
        Bc = x_dbl[..., DT_RANK:DT_RANK + n]
        Cc = x_dbl[..., DT_RANK + n:]
        delta = jax.nn.softplus(dtr @ dt_proj_w.T + dt_proj_b)
        A = -jnp.exp(A_log)

        def step(h, inp):
            d_t, b_t, c_t, u_t = inp
            dA = jnp.exp(d_t[:, :, None] * A)
            h = dA * h + (d_t * u_t)[:, :, None] * b_t[:, None, :]
            y = jnp.einsum('bdn,bn->bd', h, c_t)
            return (h, y)
        h0 = jnp.zeros((b, di, n), x.dtype)
        _, ys = lax.scan(step, h0, (delta.transpose(1, 0, 2), Bc.transpose(1, 0, 2), Cc.transpose(1, 0, 2), u.transpose(1, 0, 2)))
        y = ys.transpose(1, 0, 2)
        y = (y + u * D) * silu(z)
        return y @ out_proj_w.T

    def _L2_ffn_ref(x, gate_w, gate_b, w1, b1, w3, b3, w2, b2, sw1, sb1, sw3, sb3, sw2, sb2):
        import jax, jax.numpy as jnp
        import numpy as np
        from jax import lax
        D = 128
        H = 176
        E = 8
        K = 2
        ROUTER_SCALE = 1.0

        def _expert(x, w1, b1, w3, b3, w2, b2):
            h = jax.nn.silu((x @ w1 + b1) * (x @ w3 + b3))
            return h @ w2 + b2
        shape = x.shape
        xf = x.reshape(-1, D)
        T = xf.shape[0]
        scores = jax.nn.softmax(xf @ gate_w.T, axis=-1)
        biased = scores + gate_b
        _, idx = lax.top_k(biased, K)
        w = jnp.take_along_axis(scores, idx, axis=-1) * ROUTER_SCALE
        rw = jnp.zeros((T, E), dtype=xf.dtype).at[jnp.arange(T)[:, None], idx].add(w)
        h = jax.nn.silu((jnp.einsum('td,edh->teh', xf, w1) + b1) * (jnp.einsum('td,edh->teh', xf, w3) + b3))
        oe = jnp.einsum('teh,ehd->ted', h, w2) + b2
        y = jnp.einsum('te,ted->td', rw, oe)
        z = _expert(xf, sw1, sb1, sw3, sb3, sw2, sb2)
        return (y + z).reshape(shape)

    def _L3_attn_a_ref(x, qkv_w, qkv_b, out_w, out_b):
        import jax, jax.numpy as jnp
        import numpy as np
        B, L, E, H = (1, 512, 128, 16)
        D = E // H
        EPS = 1e-06
        b, l, e = x.shape
        qkv = x @ qkv_w + qkv_b
        q, k, v = jnp.split(qkv, 3, axis=-1)
        q = q.reshape(b, l, H, D).transpose(0, 2, 1, 3)
        k = k.reshape(b, l, H, D).transpose(0, 2, 1, 3)
        v = v.reshape(b, l, H, D).transpose(0, 2, 1, 3)
        q_prime = jax.nn.elu(q) + 1.0
        k_prime = jax.nn.elu(k) + 1.0
        kv_prod = jnp.einsum('bhld,bhle->bhlde', k_prime, v)
        kv_cumsum = jnp.cumsum(kv_prod, axis=2)
        context = jnp.einsum('bhld,bhlde->bhle', q_prime, kv_cumsum)
        k_cumsum = jnp.cumsum(k_prime, axis=2)
        norm = jnp.einsum('bhld,bhld->bhl', q_prime, k_cumsum)
        output = context / (norm[..., None] + EPS)
        output = output.transpose(0, 2, 1, 3).reshape(b, l, e)
        return output @ out_w + out_b

    def _L3_attn_b_ref(x, in_proj_w, conv_w, conv_b, x_proj_w, dt_proj_w, dt_proj_b, A_log, D_param, out_proj_w):
        import jax, jax.numpy as jnp
        import numpy as np
        DIM, D_INNER, D_STATE, DT_RANK, D_CONV = (128, 256, 16, 64, 4)
        BATCH, SEQ = (2, 128)

        def _silu(v):
            return v * jax.nn.sigmoid(v)

        def _ssm_forward(x, in_proj_w, conv_w, conv_b, x_proj_w, dt_proj_w, dt_proj_b, A_log, D_param, out_proj_w):
            b, l, _ = x.shape
            d_inner, d_conv = (conv_w.shape[0], conv_w.shape[2])
            dt_rank, n = (dt_proj_w.shape[0], A_log.shape[1])
            x_and_res = x @ in_proj_w
            xp, res = (x_and_res[..., :d_inner], x_and_res[..., d_inner:])
            h = jax.lax.conv_general_dilated(xp.transpose(0, 2, 1), conv_w, window_strides=(1,), padding=[(d_conv - 1, 0)], dimension_numbers=('NCH', 'OIH', 'NCH'), feature_group_count=d_inner) + conv_b[None, :, None]
            h = _silu(h.transpose(0, 2, 1))
            A = -jnp.exp(A_log)
            x_dbl = h @ x_proj_w
            dlt, Bm, Cm = (x_dbl[..., :dt_rank], x_dbl[..., dt_rank:dt_rank + n], x_dbl[..., dt_rank + n:])
            delta = jax.nn.softplus(dlt @ dt_proj_w + dt_proj_b)
            deltaA = jnp.exp(jnp.einsum('bld,dn->bldn', delta, A))
            deltaB_u = (delta * h)[..., None] * Bm[:, :, None, :]

            def step(state, t):
                dA_t, dBu_t, c_t = t
                state = dA_t * state + dBu_t
                y_t = jnp.einsum('bdn,bn->bd', state, c_t)
                return (state, y_t)
            init = jnp.zeros((b, d_inner, n), h.dtype)
            _, ys = jax.lax.scan(step, init, (deltaA.transpose(1, 0, 2, 3), deltaB_u.transpose(1, 0, 2, 3), Cm.transpose(1, 0, 2)))
            y = ys.transpose(1, 0, 2) + h * D_param
            y = y * _silu(res)
            return y @ out_proj_w
        return _ssm_forward(x, in_proj_w, conv_w, conv_b, x_proj_w, dt_proj_w, dt_proj_b, A_log, D_param, out_proj_w)

    def _L3_ffn_ref(x, wf, uf, bf, wi, ui, bi, wc, uc, bc, wo, uo, bo, in_c):
        import jax, jax.numpy as jnp
        import numpy as np
        from jax import lax
        T, B, I, M, O = (32, 64, 128, 128, 128)

        def _xavier(key, shape):
            fan_out, fan_in = shape
            limit = float(np.sqrt(6.0 / (fan_in + fan_out)))
            return jax.random.uniform(key, shape, jnp.float32, -limit, limit)
        batch = x.shape[1]
        c0 = jnp.broadcast_to(in_c, (batch, in_c.shape[0]))

        def step(c, xt):
            ft = jax.nn.sigmoid(xt @ wf.T + c @ uf.T + bf)
            it = jax.nn.sigmoid(xt @ wi.T + c @ ui.T + bi)
            gt = jnp.tanh(xt @ wc.T + c @ uc.T + bc)
            c = ft * c + it * gt
            return (c, None)
        c_final, _ = lax.scan(step, c0, x)
        h = jnp.tanh(jnp.einsum('tbi,oi->tbo', x, wo) + c_final @ uo.T + bo)
        return h
    x = L0_attn_a_x
    x = x + _L0_attn_a_ref(_layernorm(x, axis=-1), L0_attn_a_q_w, L0_attn_a_q_b, L0_attn_a_k_w, L0_attn_a_k_b, L0_attn_a_v_w, L0_attn_a_v_b, L0_attn_a_l_w, L0_attn_a_l_b)
    x = x + _L0_ffn_ref(_layernorm(x, axis=-1), L0_ffn_Wr, L0_ffn_Wg, L0_ffn_Wu, L0_ffn_Wd, L0_ffn_Sg, L0_ffn_Su, L0_ffn_Sd)
    x = x + _L0_attn_b_ref(_layernorm(x, axis=-1), L0_attn_b_w_attn, L0_attn_b_w_proj)
    x = x + _L0_ffn_ref(_layernorm(x, axis=-1), L0_ffn_Wr, L0_ffn_Wg, L0_ffn_Wu, L0_ffn_Wd, L0_ffn_Sg, L0_ffn_Su, L0_ffn_Sd)
    x = x + _L1_attn_a_ref(_layernorm(x, axis=-1), L1_attn_a_slope_rate, L1_attn_a_qkvu_w, L1_attn_a_qkvu_b, L1_attn_a_out_w, L1_attn_a_out_b, L1_attn_a_theta)
    x = x + _L1_ffn_ref(_layernorm(x, axis=-1), L1_ffn_W1, L1_ffn_b1, L1_ffn_W2, L1_ffn_b2)
    x = x + _L1_attn_b_ref(_layernorm(x, axis=-1), L1_attn_b_w_norm_in, L1_attn_b_w_norm_out, L1_attn_b_router_w1, L1_attn_b_router_w2, L1_attn_b_router_b2, L1_attn_b_ttt_w1, L1_attn_b_ttt_b1, L1_attn_b_ttt_w2, L1_attn_b_ttt_b2, L1_attn_b_lambdas, L1_attn_b_slr_wq1, L1_attn_b_slr_wq2, L1_attn_b_slr_wk1, L1_attn_b_slr_wk2, L1_attn_b_slr_wv, L1_attn_b_slr_wo, L1_attn_b_slr_lam, L1_attn_b_landmarks, L1_attn_b_mix_w, L1_attn_b_bus_compress, L1_attn_b_bus_expand, L1_attn_b_bus_publish)
    x = x + _L1_ffn_ref(_layernorm(x, axis=-1), L1_ffn_W1, L1_ffn_b1, L1_ffn_W2, L1_ffn_b2)
    x = x + _L2_attn_a_ref(_layernorm(x, axis=-1), L2_attn_a_Wq, L2_attn_a_bq, L2_attn_a_Wk, L2_attn_a_bk, L2_attn_a_Wv, L2_attn_a_bv, L2_attn_a_Wo, L2_attn_a_bo, L2_attn_a_beta)
    x = x + _L2_ffn_ref(_layernorm(x, axis=-1), L2_ffn_gate_w, L2_ffn_gate_b, L2_ffn_w1, L2_ffn_b1, L2_ffn_w3, L2_ffn_b3, L2_ffn_w2, L2_ffn_b2, L2_ffn_sw1, L2_ffn_sb1, L2_ffn_sw3, L2_ffn_sb3, L2_ffn_sw2, L2_ffn_sb2)
    x = x + _L2_attn_b_ref(_layernorm(x, axis=-1), L2_attn_b_in_proj_w, L2_attn_b_conv_w, L2_attn_b_conv_b, L2_attn_b_x_proj_w, L2_attn_b_dt_proj_w, L2_attn_b_dt_proj_b, L2_attn_b_A_log, L2_attn_b_D, L2_attn_b_out_proj_w)
    x = x + _L2_ffn_ref(_layernorm(x, axis=-1), L2_ffn_gate_w, L2_ffn_gate_b, L2_ffn_w1, L2_ffn_b1, L2_ffn_w3, L2_ffn_b3, L2_ffn_w2, L2_ffn_b2, L2_ffn_sw1, L2_ffn_sb1, L2_ffn_sw3, L2_ffn_sb3, L2_ffn_sw2, L2_ffn_sb2)
    x = x + _L3_attn_a_ref(_layernorm(x, axis=-1), L3_attn_a_qkv_w, L3_attn_a_qkv_b, L3_attn_a_out_w, L3_attn_a_out_b)
    x = x + _L3_ffn_ref(_layernorm(x, axis=-1), L3_ffn_wf, L3_ffn_uf, L3_ffn_bf, L3_ffn_wi, L3_ffn_ui, L3_ffn_bi, L3_ffn_wc, L3_ffn_uc, L3_ffn_bc, L3_ffn_wo, L3_ffn_uo, L3_ffn_bo, L3_ffn_in_c)
    x = x + _L3_attn_b_ref(_layernorm(x, axis=-1), L3_attn_b_in_proj_w, L3_attn_b_conv_w, L3_attn_b_conv_b, L3_attn_b_x_proj_w, L3_attn_b_dt_proj_w, L3_attn_b_dt_proj_b, L3_attn_b_A_log, L3_attn_b_D_param, L3_attn_b_out_proj_w)
    x = x + _L3_ffn_ref(_layernorm(x, axis=-1), L3_ffn_wf, L3_ffn_uf, L3_ffn_bf, L3_ffn_wi, L3_ffn_ui, L3_ffn_bi, L3_ffn_wc, L3_ffn_uc, L3_ffn_bc, L3_ffn_wo, L3_ffn_uo, L3_ffn_bo, L3_ffn_in_c)
    return x

_drawn_inputs = setup_inputs


def setup_inputs(seed=0):
    import zlib

    import numpy as np

    out = dict(_drawn_inputs(seed))
    spreads = {'L1_attn_a_qkvu_b': (0.0, 0.1),
     'L1_attn_a_out_b': (0.0, 0.1),
     'L1_attn_b_w_norm_in': (1.0, 0.2),
     'L1_attn_b_w_norm_out': (1.0, 0.2),
     'L1_attn_b_router_b2': (0.5, 0.2),
     'L1_attn_b_ttt_b1': (0.0, 0.1),
     'L1_attn_b_ttt_b2': (0.0, 0.1),
     'L2_attn_a_bo': (0.0, 0.1),
     'L2_attn_b_D': (1.0, 0.2),
     'L3_attn_a_qkv_b': (0.0, 0.1),
     'L3_attn_a_out_b': (0.0, 0.1),
     'L3_attn_b_D_param': (1.0, 0.2),
     'L3_ffn_bf': (0.0, 0.1),
     'L3_ffn_bi': (0.0, 0.1),
     'L3_ffn_bc': (0.0, 0.1),
     'L3_ffn_bo': (0.0, 0.1),
     'L3_ffn_in_c': (0.0, 0.1)}
    factors = {}
    for name, (base, spread) in spreads.items():
        noise = np.random.default_rng([zlib.crc32(name.encode()), seed]).standard_normal(out[name].shape)
        drawn = base * np.exp(spread * noise) if base else spread * noise
        out[name] = jnp.asarray(drawn.astype(out[name].dtype))
    for name, factor in factors.items():
        out[name] = (out[name] * factor).astype(out[name].dtype)
    return out
```

```python
from contextlib import ExitStack

import numpy as np

import concourse.bass as bass
from concourse import mybir

F32 = mybir.dt.float32
BF16 = mybir.dt.bfloat16
ALU = mybir.AluOpType
ACT = mybir.ActivationFunctionType
AX = mybir.AxisListType

B, S, D = 4, 512, 128
P = 128
TT = S // P
LN_EPS = 1e-5
NEG = -1e30

PLAN = list(range(16))


class Signal:

    def __init__(self, sem, per):
        self.sem, self.per = sem, per

    def at(self, b, k):
        return b * self.per + (k + 1)


class Layer:

    def __init__(self, nc, name, core, groups, **signals):
        self.nc, self.name, self.core = nc, name, core
        self.ctx = ExitStack()
        self.sems, self.signals = [], {}
        for key, per in signals.items():
            sem = nc.alloc_semaphore(f"{name}_{key}")
            self.sems.append(sem)
            nc.sync.sem_inc(sem, 1)
            self.signals[key] = Signal(sem, per)
        for eng in (nc.tensor, nc.scalar, nc.vector, nc.gpsimd):
            wait_weights(eng, core, "const", *groups)
        nc.all_engine_barrier()

    def __getitem__(self, key):
        return self.signals[key]

    def sb(self, key, shape, dt=F32):
        return self.ctx.enter_context(self.nc.sbuf_tensor(f"{self.name}_{key}", shape, dt))

    def ps(self, key, shape, dt=F32):
        return self.ctx.enter_context(self.nc.psum_tensor(f"{self.name}_{key}", shape, dt))

    def close(self):
        self.ctx.close()
        self.nc.clear_and_free_semaphores(self.sems)
        self.nc.all_engine_barrier()


def wait_weights(eng, core, *groups):
    for g in groups:
        eng.wait_ge(core.landed[g], 16)


class Core:

    def __init__(self, x, weights, landed, columns):
        self.x, self.weights, self.landed, self.columns = x, weights, landed, columns

    def w(self, group, name, lo=0, hi=None):
        at, rows, width = self.columns[group][name]
        hi = width if hi is None else hi
        return self.weights[group][0:rows, at + lo:at + hi]

    def batch(self, b):
        return self.x[:, bass.ds(b * S, S)]



LN_SIGNALS = dict(
    ln_xc=1,
    ln_sq=2,
    ln_var=1,
    ln_eps=1,
    ln_rstd=1,
    ln_diag=1,
    ln_spread=1,
    ln_xn=1,
)


def ln_buffers(L, bank, var):
    L.ln_ps_xc, L.ln_ps_var, L.ln_ps_spread = bank, var, bank
    L.ln_centred = L.sb("ln_centred", [P, S])
    L.ln_square = L.sb("ln_square", [P, S])
    L.ln_small = L.sb("ln_small", [P, 2, TT])
    L.ln_diagonals = L.sb("ln_diagonals", [P, TT, P])


def ln_tensor(pe, L, b):
    c = L.core
    pe.wait_ge(L["ln_xn"].sem, L["ln_xn"].at(b, 0))
    pe.matmul(L.ln_ps_xc, c.w("const", "centre"), c.batch(b), start=True, stop=True).then_inc(L["ln_xc"].sem, 1)
    pe.wait_ge(L["ln_sq"].sem, L["ln_sq"].at(b, 2))
    pe.wait_ge(L["ln_eps"].sem, L["ln_eps"].at(b, 0))
    for t in range(TT):
        mm = pe.matmul(L.ln_ps_var[:, t:t + 1], L.ln_square[:, t * P:(t + 1) * P], c.w("const", "mean", 0, 1),
                       start=True, stop=True)
    mm.then_inc(L["ln_var"].sem, 1)
    pe.wait_ge(L["ln_diag"].sem, L["ln_diag"].at(b, 1))
    pe.matmul(L.ln_ps_spread, c.w("const", "ones"), L.ln_diagonals[:, :, :], start=True, stop=True)\
        .then_inc(L["ln_spread"].sem, 1)


def ln_scalar(act, L, b):
    act.wait_ge(L["ln_xc"].sem, L["ln_xc"].at(b, 1))
    act.wait_ge(L["ln_xn"].sem, L["ln_xn"].at(b, 0))
    act.activation(L.ln_square[:, :], L.ln_ps_xc, ACT.Square).then_inc(L["ln_sq"].sem, 1)
    act.activation(L.ln_centred[:, :], L.ln_ps_xc, ACT.Copy).then_inc(L["ln_sq"].sem, 1)


def ln_vector(dve, L, b, xn):
    c = L.core
    dve.wait_ge(L["ln_var"].sem, L["ln_var"].at(b, 1))
    dve.tensor_scalar(L.ln_small[:, 0, :], L.ln_ps_var, LN_EPS, None, ALU.add).then_inc(L["ln_eps"].sem, 1)
    dve.wait_ge(L["ln_rstd"].sem, L["ln_rstd"].at(b, 1))
    dve.tensor_tensor(L.ln_diagonals[:, :, :], c.w("const", "eye").unsqueeze(1).to_broadcast([P, TT, P]),
                      L.ln_small[:, 1, :].unsqueeze(2).to_broadcast([P, TT, P]), ALU.mult)\
        .then_inc(L["ln_diag"].sem, 1)
    dve.wait_ge(L["ln_spread"].sem, L["ln_spread"].at(b, 1))
    dve.tensor_tensor(xn, L.ln_centred[:, :], L.ln_ps_spread, ALU.mult).then_inc(L["ln_xn"].sem, 1)


def ln_pool(pool, L, b):
    pool.wait_ge(L["ln_eps"].sem, L["ln_eps"].at(b, 1))
    pool.tensor_tensor(L.ln_small[:, 1, :], L.ln_small[:, 0, :], L.core.w("const", "minus_half"), ALU.pow)\
        .then_inc(L["ln_rstd"].sem, 1)

HEADS, HD = 16, 64


def query_softmax_attention(nc, core, name):
    PAIRS = HEADS // 2
    STEPS = PAIRS * TT
    L = Layer(nc, name, core, ["mha"], **LN_SIGNALS,
              v_ps=2 * TT,
              v_sb=2 * TT,
              qk_ps=2 * PAIRS,
              qk_sb=2 * PAIRS,
              scores=STEPS,
              top=STEPS,
              shift=STEPS,
              probs=2 * STEPS,
              inverse=STEPS,
              vs=STEPS,
              ctx_ps=STEPS,
              ctx_sb=PAIRS,
              joined=PAIRS,
              done=1)
    with L.ctx:
        g = "mha"
        scale = float(HD) ** -0.5
        xn = L.sb("xn", [P, S])
        v = L.sb("v", [P, TT, HEADS * HD])
        q, k = L.sb("q", [P, 2, S]), L.sb("k", [P, 2, S])
        probs = L.sb("probs", [P, 2, 2, S])
        vs = L.sb("vs", [P, 2, 2, HD])
        heads_out = L.sb("heads_out", [P, 2, S])
        stats = L.sb("stats", [P, 2, 4, 2])
        psp = L.ps("psp", [P, 2, 2, S])
        psq = L.ps("psq", [P, S])
        ps_ctx, out, bank = L.ps("ps_ctx", [P, S]), L.ps("out", [P, S]), L.ps("bank", [P, S])
        ln_buffers(L, bank[:, :], psq[:, 0:TT])

        def project(pe, b, hp):
            for i, (w, ps) in enumerate((("wq", bank), ("wk", psq))):
                if hp == 0:
                    pe.wait_ge(L["v_sb"].sem, L["v_sb"].at(b, 2 * TT))
                else:
                    pe.wait_ge(L["qk_sb"].sem, L["qk_sb"].at(b, 2 * (hp - 1) + i + 1))
                pe.matmul(ps[:, :], core.w(g, w, hp * P, (hp + 1) * P), xn[:, :], start=True, stop=True)\
                    .then_inc(L["qk_ps"].sem, 1)

        def score(pe, b, s):
            hp, kt = divmod(s, TT)
            if kt == 0:
                pe.wait_ge(L["qk_sb"].sem, L["qk_sb"].at(b, 2 * hp + 2))
            pe.wait_ge(L["probs"].sem, L["probs"].at(b, 2 * max(s - 1, 0)))
            for i in range(2):
                r = slice(i * HD, (i + 1) * HD)
                mm = pe.matmul(psp[:, s % 2, i, :], k[r, hp % 2, kt * P:(kt + 1) * P], q[r, hp % 2, :],
                               start=True, stop=True)
            mm.then_inc(L["scores"].sem, 1)

        def context(pe, b, s):
            hp, kt = divmod(s, TT)
            pe.wait_ge(L["vs"].sem, L["vs"].at(b, s + 1))
            if kt == 0:
                pe.wait_ge(L["ctx_sb"].sem, L["ctx_sb"].at(b, hp))
            for i in range(2):
                mm = pe.matmul(ps_ctx[i * HD:(i + 1) * HD, :], vs[:, s % 2, i, :], probs[:, s % 2, i, :],
                               start=kt == 0, stop=kt == TT - 1)
            mm.then_inc(L["ctx_ps"].sem, 1)

        def join(pe, b, hp):
            pe.wait_ge(L["ctx_sb"].sem, L["ctx_sb"].at(b, hp + 1))
            if hp == 0:
                pe.wait_ge(L["done"].sem, L["done"].at(b, 0))
            pe.matmul(out[:, :], core.w(g, "wl", hp * P, (hp + 1) * P), heads_out[:, hp % 2, :],
                      start=hp == 0, stop=hp == PAIRS - 1).then_inc(L["joined"].sem, 1)

        with nc.Block() as block:
            @block.tensor
            def _(pe):
                with pe.Fori(0, B) as b:
                    ln_tensor(pe, L, b)
                    pe.wait_ge(L["ln_xn"].sem, L["ln_xn"].at(b, 1))
                    for n in range(2 * TT):
                        t, half = divmod(n, 2)
                        ps = (bank, psq)[half]
                        if n >= 2:
                            pe.wait_ge(L["v_sb"].sem, L["v_sb"].at(b, n - 1))
                        pe.matmul(ps[:, :], xn[:, t * P:(t + 1) * P], core.w(g, "wv", half * S, (half + 1) * S),
                                  start=True, stop=True).then_inc(L["v_ps"].sem, 1)
                    project(pe, b, 0)
                    score(pe, b, 0)
                    for s in range(STEPS):
                        hp, kt = divmod(s, TT)
                        if kt == 1 and hp + 1 < PAIRS:
                            project(pe, b, hp + 1)
                        if s + 1 < STEPS:
                            score(pe, b, s + 1)
                        context(pe, b, s)
                        if kt == 2 and hp >= 1:
                            join(pe, b, hp - 1)
                    join(pe, b, PAIRS - 1)

            def bias_qk(act, b, hp):
                for i, (n, to, ps) in enumerate((("bq", q, bank), ("bk", k, psq))):
                    act.wait_ge(L["qk_ps"].sem, L["qk_ps"].at(b, 2 * hp + i + 1))
                    act.wait_ge(L["scores"].sem, L["scores"].at(b, TT * max(hp - 1, 0)))
                    act.activation(to[:, hp % 2, :], ps[:, :], ACT.Identity, bias=core.w(g, n, hp, hp + 1))\
                        .then_inc(L["qk_sb"].sem, 1)

            @block.scalar
            def _(act):
                with act.Fori(0, B) as b:
                    ln_scalar(act, L, b)
                    bias_qk(act, b, 0)
                    for s in range(STEPS):
                        hp, kt = divmod(s, TT)
                        act.wait_ge(L["shift"].sem, L["shift"].at(b, s + 1))
                        act.wait_ge(L["ctx_ps"].sem, L["ctx_ps"].at(b, max(s - 1, 0)))
                        for i in range(2):
                            act.activation(probs[:, s % 2, i, :], psp[:, s % 2, i, :], ACT.Exp,
                                           bias=stats[:, s % 2, 1, i:i + 1], scale=scale,
                                           accum_out=stats[:, s % 2, 2, i:i + 1]).then_inc(L["probs"].sem, 1)
                        if kt == 1 and hp + 1 < PAIRS:
                            bias_qk(act, b, hp + 1)

            def maxima(dve, b, s):
                dve.wait_ge(L["scores"].sem, L["scores"].at(b, s + 1))
                dve.wait_ge(L["inverse"].sem, L["inverse"].at(b, max(s - 1, 0)))
                dve.tensor_reduce(stats[:, s % 2, 0, :], psp[:, s % 2, :, :], AX.X, ALU.max).then_inc(L["top"].sem, 1)
                dve.wait_ge(L["top"].sem, L["top"].at(b, s + 1))
                dve.tensor_scalar(stats[:, s % 2, 1, :], stats[:, s % 2, 0, :], -scale, None, ALU.mult)\
                    .then_inc(L["shift"].sem, 1)

            def scale_v(dve, b, s):
                hp, kt = divmod(s, TT)
                dve.wait_ge(L["probs"].sem, L["probs"].at(b, 2 * s + 2))
                dve.wait_ge(L["vs"].sem, L["vs"].at(b, max(s - 1, 0)))
                dve.reciprocal(stats[:, s % 2, 3, :], stats[:, s % 2, 2, :]).then_inc(L["inverse"].sem, 1)
                dve.wait_ge(L["inverse"].sem, L["inverse"].at(b, s + 1))
                dve.wait_ge(L["ctx_ps"].sem, L["ctx_ps"].at(b, max(s - 1, 0)))
                dve.tensor_tensor(vs[:, s % 2, :, :],
                                  v[:, kt, hp * P:(hp + 1) * P].rearrange("p (i d) -> p i d", i=2),
                                  stats[:, s % 2, 3, :].unsqueeze(2).to_broadcast([P, 2, HD]), ALU.mult)\
                    .then_inc(L["vs"].sem, 1)

            def take_context(dve, b, hp):
                dve.wait_ge(L["ctx_ps"].sem, L["ctx_ps"].at(b, TT * (hp + 1)))
                dve.wait_ge(L["joined"].sem, L["joined"].at(b, max(hp - 1, 0)))
                dve.tensor_copy(heads_out[:, hp % 2, :], ps_ctx[:, :]).then_inc(L["ctx_sb"].sem, 1)

            @block.vector
            def _(dve):
                with dve.Fori(0, B) as b:
                    ln_vector(dve, L, b, xn[:, :])
                    dve.wait_ge(L["vs"].sem, L["vs"].at(b, 0))
                    for n in range(2 * TT):
                        t, half = divmod(n, 2)
                        dve.wait_ge(L["v_ps"].sem, L["v_ps"].at(b, n + 1))
                        dve.tensor_tensor(v[:, t, half * S:(half + 1) * S], (bank, psq)[half][:, :],
                                          core.w(g, "bv", half * S, (half + 1) * S), ALU.add).then_inc(L["v_sb"].sem, 1)
                    maxima(dve, b, 0)
                    for s in range(STEPS):
                        hp, kt = divmod(s, TT)
                        if s + 1 < STEPS:
                            maxima(dve, b, s + 1)
                        if s == 0:
                            dve.wait_ge(L["v_sb"].sem, L["v_sb"].at(b, 2 * TT))
                        scale_v(dve, b, s)
                        if kt == 0 and hp >= 1:
                            take_context(dve, b, hp - 1)
                    take_context(dve, b, PAIRS - 1)
                    dve.wait_ge(L["joined"].sem, L["joined"].at(b, PAIRS))
                    dve.scalar_tensor_tensor(out=core.batch(b), in0=out[:, :], scalar=core.w(g, "bl"),
                                             in1=core.batch(b), op0=ALU.add, op1=ALU.add).then_inc(L["done"].sem, 1)

            @block.gpsimd
            def _(pool):
                with pool.Fori(0, B) as b:
                    ln_pool(pool, L, b)
    L.close()


def routed_ffn(nc, core, name, group, E, routed, shared, gated):
    NT = routed + shared
    total = core.columns[group]["w1"][2]
    rows = [min(P, total - m * P) for m in range(NT)]
    PARTS = 3 * E
    L = Layer(nc, name, core, [group], **LN_SIGNALS,
              logits=1,
              route=23,
              expd=1,
              turned=1,
              rows_in=1 + gated,
              up=NT,
              first=NT,
              product=NT,
              silu=NT,
              spread=routed,
              hidden=routed,
              down=NT + gated,
              cast=3, done=1)
    with L.ctx:
        xn = L.sb("xn", [P, S])
        pick16 = L.sb("pick16", [PARTS, routed * P], BF16)
        eye16 = L.sb("eye16", [P, P], BF16)
        small = L.sb("small", [P, 4, TT])
        e = L.sb("e", [P, TT, E])
        prob = L.sb("prob", [P, TT, E])
        key = L.sb("key", [P, TT, E])
        tie = L.sb("tie", [P, TT, E])
        chosen = L.sb("chosen", [P, 2, TT, E])
        cw = L.sb("cw", [P, TT, E])
        rest = L.sb("rest", [P, 2, TT, E])
        parts_wide = L.sb("parts", [P, TT, P], BF16)
        parts = parts_wide[:, :, 0:PARTS].rearrange("p t (a e) -> p t a e", e=E)
        cw_rows = L.sb("cw_rows", [E, S])
        part_rows = L.sb("part_rows", [PARTS, S], BF16)
        first = L.sb("first", [P, 2, S])
        product = L.sb("product", [P, 2, S])
        act_out = L.sb("act_out", [P, 2, S])
        h = L.sb("h", [P, 2, S])
        psg, psu = L.ps("psg", [P, 2, S]), L.ps("psu", [P, 2, S])
        psc, out, bank, ps_small = (L.ps(k, [P, S]) for k in ("psc", "out", "bank", "ps_small"))
        ln_buffers(L, bank[:, :], ps_small[:, 0:TT])
        logits = ps_small[:, TT:TT + TT * E].rearrange("p (t e) -> p t e", e=E)
        ps_parts = ps_small[:, S // 2:S].bitcast(BF16)
        w1, w3, w2 = (core.w(group, k) for k in ("w1", "w3", "w2"))
        eye = core.w("const", "eye")
        falling = core.w("const", "falling" if E == 16 else "falling8").rearrange("p (t e) -> p t e", e=E)

        def over_e(col):
            return col.unsqueeze(2).to_broadcast([P, TT, E])

        def up(pe, b, m):
            M = rows[m]
            pe.wait_ge(L["first"].sem, L["first"].at(b, max(m - 1, 0)))
            pe.wait_ge(L["product"].sem, L["product"].at(b, max(m - 1, 0)))
            pe.matmul(psg[0:M, m % 2, :], w1[:, m * P:m * P + M], xn[:, :], start=True, stop=True)
            pe.matmul(psu[0:M, m % 2, :], w3[:, m * P:m * P + M], xn[:, :], start=True, stop=True)\
                .then_inc(L["up"].sem, 1)

        def spread(pe, b, m):
            pe.wait_ge(L["hidden"].sem, L["hidden"].at(b, m))
            pe.matmul(psc[:, :], pick16[:, m * P:(m + 1) * P], part_rows[:, :], start=True, stop=True)\
                .then_inc(L["spread"].sem, 1)

        def down(pe, b, m):
            M = rows[m]
            if m < routed:
                pe.wait_ge(L["hidden"].sem, L["hidden"].at(b, m + 1))
            elif gated:
                pe.wait_ge(L["silu"].sem, L["silu"].at(b, m + 1))
            else:
                pe.wait_ge(L["product"].sem, L["product"].at(b, m + 1))
            pe.matmul(out[:, :], w2[0:M, m * P:(m + 1) * P], h[0:M, m % 2, :], start=m == 0,
                      stop=m == NT - 1 and not gated).then_inc(L["down"].sem, 1)

        def factor(act, b, m):
            M = rows[m]
            act.wait_ge(L["up"].sem, L["up"].at(b, m + 1))
            act.wait_ge(L["product"].sem, L["product"].at(b, max(m - 1, 0)))
            if gated:
                act.activation(first[0:M, m % 2, :], psg[0:M, m % 2, :], ACT.Identity,
                               bias=core.w(group, "b1", m, m + 1)[0:M, :]).then_inc(L["first"].sem, 1)
            else:
                act.activation(first[0:M, m % 2, :], psg[0:M, m % 2, :], ACT.Silu).then_inc(L["first"].sem, 1)

        def silu(act, b, m):
            M = rows[m]
            act.wait_ge(L["product"].sem, L["product"].at(b, m + 1))
            if m < routed:
                act.wait_ge(L["hidden"].sem, L["hidden"].at(b, max(m - 1, 0)))
                to = act_out
            else:
                act.wait_ge(L["down"].sem, L["down"].at(b, m - 1))
                to = h
            act.activation(to[0:M, m % 2, :], product[0:M, m % 2, :], ACT.Silu).then_inc(L["silu"].sem, 1)

        def multiply(dve, b, m):
            M = rows[m]
            dve.wait_ge(L["first"].sem, L["first"].at(b, m + 1))
            if gated:
                dve.wait_ge(L["silu"].sem, L["silu"].at(b, max(m - 1, 0)))
                dve.scalar_tensor_tensor(out=product[0:M, m % 2, :], in0=psu[0:M, m % 2, :],
                                         scalar=core.w(group, "b3", m, m + 1)[0:M, :], in1=first[0:M, m % 2, :],
                                         op0=ALU.add, op1=ALU.mult).then_inc(L["product"].sem, 1)
                return
            dve.wait_ge(L["hidden"].sem, L["hidden"].at(b, max(m - 1, 0)))
            to = product
            if m >= routed:
                dve.wait_ge(L["down"].sem, L["down"].at(b, m - 1))
                to = h
            dve.tensor_tensor(to[0:M, m % 2, :], psu[0:M, m % 2, :], first[0:M, m % 2, :], ALU.mult)\
                .then_inc(L["product"].sem, 1)

        def finish(dve, b, m):
            if gated:
                dve.wait_ge(L["silu"].sem, L["silu"].at(b, m + 1))
            else:
                dve.wait_ge(L["product"].sem, L["product"].at(b, m + 1))
            dve.wait_ge(L["spread"].sem, L["spread"].at(b, m + 1))
            dve.wait_ge(L["down"].sem, L["down"].at(b, max(m - 1, 0)))
            dve.tensor_tensor(h[:, m % 2, :], (act_out if gated else product)[:, m % 2, :], psc[:, :], ALU.mult)\
                .then_inc(L["hidden"].sem, 1)

        def choose(dve, b):
            dve.wait_ge(L["logits"].sem, L["logits"].at(b, 1))
            dve.tensor_reduce(small[:, 0, :], logits, AX.X, ALU.max).then_inc(L["route"].sem, 1)
            dve.wait_ge(L["route"].sem, L["route"].at(b, 1))
            dve.tensor_tensor(e[:, :, :], logits, over_e(small[:, 0, :]), ALU.subtract).then_inc(L["route"].sem, 1)
            dve.wait_ge(L["expd"].sem, L["expd"].at(b, 1))
            dve.tensor_reduce(small[:, 1, :], e[:, :, :], AX.X, ALU.add).then_inc(L["route"].sem, 1)
            dve.wait_ge(L["route"].sem, L["route"].at(b, 3))
            dve.reciprocal(small[:, 2, :], small[:, 1, :]).then_inc(L["route"].sem, 1)
            dve.wait_ge(L["route"].sem, L["route"].at(b, 4))
            dve.tensor_tensor(prob[:, :, :], e[:, :, :], over_e(small[:, 2, :]), ALU.mult).then_inc(L["route"].sem, 1)
            dve.wait_ge(L["route"].sem, L["route"].at(b, 5))
            if gated:
                bias = core.w(group, "gate_b").rearrange("p (t e) -> p t e", e=E)
                dve.tensor_tensor(key[:, :, :], prob[:, :, :], bias, ALU.add).then_inc(L["route"].sem, 1)
            else:
                dve.tensor_copy(key[:, :, :], prob[:, :, :]).then_inc(L["route"].sem, 1)
            n = 6
            for i in range(2):
                dve.wait_ge(L["route"].sem, L["route"].at(b, n))
                dve.tensor_reduce(small[:, 3, :], key[:, :, :], AX.X, ALU.max).then_inc(L["route"].sem, 1)
                dve.wait_ge(L["route"].sem, L["route"].at(b, n + 1))
                dve.tensor_tensor(tie[:, :, :], key[:, :, :], over_e(small[:, 3, :]), ALU.is_equal)\
                    .then_inc(L["route"].sem, 1)
                dve.wait_ge(L["route"].sem, L["route"].at(b, n + 2))
                dve.tensor_tensor(tie[:, :, :], tie[:, :, :], falling, ALU.mult).then_inc(L["route"].sem, 1)
                dve.wait_ge(L["route"].sem, L["route"].at(b, n + 3))
                dve.tensor_reduce(small[:, 3, :], tie[:, :, :], AX.X, ALU.max).then_inc(L["route"].sem, 1)
                dve.wait_ge(L["route"].sem, L["route"].at(b, n + 4))
                dve.tensor_tensor(chosen[:, i, :, :], tie[:, :, :], over_e(small[:, 3, :]), ALU.is_equal)\
                    .then_inc(L["route"].sem, 1)
                dve.wait_ge(L["route"].sem, L["route"].at(b, n + 5))
                if i == 0:
                    dve.scalar_tensor_tensor(out=key[:, :, :], in0=chosen[:, 0, :, :], scalar=NEG, in1=key[:, :, :],
                                             op0=ALU.mult, op1=ALU.add).then_inc(L["route"].sem, 1)
                    n += 6
            dve.tensor_tensor(chosen[:, 0, :, :], chosen[:, 0, :, :], chosen[:, 1, :, :], ALU.add)\
                .then_inc(L["route"].sem, 1)
            dve.wait_ge(L["route"].sem, L["route"].at(b, 18))
            dve.tensor_tensor(cw[:, :, :], chosen[:, 0, :, :], prob[:, :, :], ALU.mult).then_inc(L["route"].sem, 1)
            dve.wait_ge(L["route"].sem, L["route"].at(b, 19))
            dve.tensor_copy(parts[:, :, 0, :], cw[:, :, :]).then_inc(L["route"].sem, 1)
            dve.wait_ge(L["route"].sem, L["route"].at(b, 20))
            dve.tensor_tensor(rest[:, 0, :, :], cw[:, :, :], parts[:, :, 0, :], ALU.subtract).then_inc(L["route"].sem, 1)
            dve.wait_ge(L["route"].sem, L["route"].at(b, 21))
            dve.tensor_copy(parts[:, :, 1, :], rest[:, 0, :, :]).then_inc(L["route"].sem, 1)
            dve.wait_ge(L["route"].sem, L["route"].at(b, 22))
            dve.tensor_tensor(parts[:, :, 2, :], rest[:, 0, :, :], parts[:, :, 1, :], ALU.subtract)\
                .then_inc(L["route"].sem, 1)

        STEPS = 23
        with nc.Block() as block:
            @block.tensor
            def _(pe):
                pe.wait_ge(L["cast"].sem, L["cast"].at(0, 3))
                with pe.Fori(0, B) as b:
                    ln_tensor(pe, L, b)
                    pe.wait_ge(L["ln_xn"].sem, L["ln_xn"].at(b, 1))
                    for t in range(TT):
                        mm = pe.matmul(logits[:, t, :], xn[:, t * P:(t + 1) * P], core.w(group, "wr"),
                                       start=True, stop=True)
                    mm.then_inc(L["logits"].sem, 1)
                    up(pe, b, 0)
                    up(pe, b, 1)
                    pe.wait_ge(L["route"].sem, L["route"].at(b, STEPS))
                    pe.wait_ge(L["hidden"].sem, L["hidden"].at(b, 0))
                    if gated:
                        for t in range(TT):
                            pe.transpose(psc[0:E, t * P:(t + 1) * P], cw[:, t, :], eye)
                    for t in range(TT):
                        mm = pe.transpose(ps_parts[:, t * P:(t + 1) * P], parts_wide[:, t, :], eye16[:, :])
                    mm.then_inc(L["turned"].sem, 1)
                    pe.wait_ge(L["rows_in"].sem, L["rows_in"].at(b, 2 if gated else 1))
                    pe.wait_ge(L["done"].sem, L["done"].at(b, 0))
                    spread(pe, b, 0)
                    for m in range(NT):
                        if m + 2 < NT:
                            up(pe, b, m + 2)
                        down(pe, b, m)
                        if m + 1 < routed:
                            spread(pe, b, m + 1)
                    if gated:
                        pe.matmul(out[:, :], core.w(group, "b2"), cw_rows[:, :], start=False, stop=True)\
                            .then_inc(L["down"].sem, 1)

            @block.scalar
            def _(act):
                with act.Fori(0, B) as b:
                    ln_scalar(act, L, b)
                    act.wait_ge(L["route"].sem, L["route"].at(b, 2))
                    act.activation(e[:, :, :], e[:, :, :], ACT.Exp).then_inc(L["expd"].sem, 1)
                    factor(act, b, 0)
                    factor(act, b, 1)
                    act.wait_ge(L["turned"].sem, L["turned"].at(b, 1))
                    act.activation(part_rows[:, :], ps_parts[0:PARTS, :], ACT.Copy).then_inc(L["rows_in"].sem, 1)
                    for m in range(NT):
                        if gated:
                            silu(act, b, m)
                        if m + 2 < NT:
                            factor(act, b, m + 2)

            @block.vector
            def _(dve):
                dve.wait_ge(L["cast"].sem, L["cast"].at(0, 1))
                with dve.Fori(0, B) as b:
                    ln_vector(dve, L, b, xn[:, :])
                    choose(dve, b)
                    if gated:
                        dve.wait_ge(L["turned"].sem, L["turned"].at(b, 1))
                        dve.tensor_copy(cw_rows[:, :], psc[0:E, :]).then_inc(L["rows_in"].sem, 1)
                    multiply(dve, b, 0)
                    for m in range(NT):
                        if m + 1 < NT:
                            multiply(dve, b, m + 1)
                        if m < routed:
                            finish(dve, b, m)
                    dve.wait_ge(L["down"].sem, L["down"].at(b, NT + gated))
                    dve.scalar_tensor_tensor(out=core.batch(b), in0=out[:, :],
                                             scalar=core.w(group, "sb2") if gated else 0.0, in1=core.batch(b),
                                             op0=ALU.add, op1=ALU.add).then_inc(L["done"].sem, 1)

            @block.gpsimd
            def _(pool):
                pool.memset(parts_wide[:, :, :], 0.0).then_inc(L["cast"].sem, 1)
                pool.tensor_copy(pick16[:, :], core.w(group, "pick")).then_inc(L["cast"].sem, 1)
                pool.tensor_copy(eye16[:, :], eye).then_inc(L["cast"].sem, 1)
                with pool.Fori(0, B) as b:
                    ln_pool(pool, L, b)
    L.close()

KH, KHD = 16, 8
KJ, KG = 4, 4
KEPT, RECENT = 391, 64
DROPPED = S - KEPT
OLD = S - RECENT
UNITS = KJ * TT * 2
SHIFT_ROW = KHD + 1


def unit(u):
    return u // (2 * TT), u // 2 % TT, u % 2


def keep_attention(nc, core, name):
    ROUNDS = DROPPED // 8
    L = Layer(nc, name, core, ["keep"], **LN_SIGNALS, cast=3, zero=2,
              p1=2 * KJ, e1=2 * KJ,
              s1=UNITS, top1=UNITS, shift1=UNITS, exp1=2 * UNITS, inv1=UNITS, pick1=UNITS, sums1=UNITS, added=1,
              choice=2 * ROUNDS + 13,
              masked=1,
              current=1,
              pv=TT, v=TT,
              p2=2 * KJ, e2=2 * KJ,
              s2=UNITS, top2=UNITS, low2=UNITS,
              rows=KJ, q2=KJ,
              st=UNITS, exp2=UNITS, av=UNITS,
              c_sb=KJ, c_turn=KJ, c_inv=KJ, c_out=KJ,
              o_turn=1, o_sb=1, projected=1, done=1)
    with L.ctx:
        w = lambda n, *a: core.w("keep", n, *a)
        scale = float(KHD) ** -0.5
        xn = L.sb("xn", [P, B * S])
        cur = L.sb("cur", [P, S])
        q, k, q2 = (L.sb(n, [P, 2, S]) for n in ("q", "k", "q2"))
        probs = L.sb("probs", [P, 2, 2, S])
        stats = L.sb("stats", [P, 2, 4, 2])
        pick = L.sb("pick", [P, 2, 2, 32])
        sums = L.sb("sums", [P, S])
        work = L.sb("work", [P, OLD])
        best = L.sb("best", [P, 8])
        lt, eq, cum = (L.sb(n, [P, OLD]) for n in ("lt", "eq", "cum"))
        counts = L.sb("counts", [P, 2])
        mask, bmask = L.sb("mask", [P, S]), L.sb("bmask", [P, S])
        low = L.sb("low", [P, 2, TT, P])
        v = L.sb("v", [P, TT, KH * 32])
        c_sb = L.sb("c_sb", [P, S])
        c_inv = L.sb("c_inv", [P, TT, KG])
        outs, outs_t = L.sb("outs", [P, TT, D]), L.sb("outs_t", [P, S])
        eye16, later16 = L.sb("eye16", [P, P], BF16), L.sb("later16", [P, P], BF16)
        ring = L.ps("ring", [P, 2, 2, S])
        acc, psq, pst, out = (L.ps(n, [P, S]) for n in ("acc", "psq", "pst", "out"))
        ln_buffers(L, psq[:, :], out[:, 0:TT])
        eye = core.w("const", "eye")

        def batch_of(t, b):
            return t[:, bass.ds(b * S, S)]

        def rows_of_group(u, i):
            g = 2 * (u % 2) + i
            return slice(32 * g, 32 * g + 32)


        def project1(pe, b, j):
            for i, (n, ps) in enumerate((("wq", psq), ("wk", pst))):
                if j:
                    pe.wait_ge(L["e1"].sem, L["e1"].at(b, 2 * (j - 1) + i + 1))
                pe.matmul(ps[:, :], w(n, j * P, (j + 1) * P), batch_of(xn, b), start=True, stop=True)\
                    .then_inc(L["p1"].sem, 1)

        def score1(pe, b, u):
            j, t, _ = unit(u)
            qt = TT - 1 - t
            N = (qt + 1) * P
            if u % (2 * TT) == 0:
                pe.wait_ge(L["e1"].sem, L["e1"].at(b, 2 * j + 2))
            pe.wait_ge(L["exp1"].sem, L["exp1"].at(b, 2 * max(u - 1, 0)))
            for i in range(2):
                r = rows_of_group(u, i)
                pe.matmul(ring[:, u % 2, i, 0:N], q[r, j % 2, qt * P:(qt + 1) * P], k[r, j % 2, 0:N],
                          start=True, stop=True, skip_group_check=True)
            for i in range(2):
                mm = pe.matmul(ring[:, u % 2, i, qt * P:N], eye16[:, :], later16[:, :], start=False, stop=True,
                               skip_group_check=True)
            mm.then_inc(L["s1"].sem, 1)

        def importance(pe, b, u):
            _, t, _ = unit(u)
            N = (TT - t) * P
            pe.wait_ge(L["pick1"].sem, L["pick1"].at(b, u + 1))
            if u == 0:
                pe.wait_ge(L["added"].sem, L["added"].at(b, 0))
            for i in range(2):
                mm = pe.matmul(acc[rows_of_group(u, i), 0:N], pick[:, u % 2, i, :], probs[:, u % 2, i, 0:N],
                               start=u < 2, stop=True, skip_group_check=True)
            mm.then_inc(L["sums1"].sem, 1)

        def maxima1(dve, b, u):
            N = (TT - unit(u)[1]) * P
            dve.wait_ge(L["s1"].sem, L["s1"].at(b, u + 1))
            dve.wait_ge(L["inv1"].sem, L["inv1"].at(b, max(u - 1, 0)))
            dve.tensor_reduce(stats[:, u % 2, 0, :], ring[:, u % 2, :, 0:N], AX.X, ALU.max).then_inc(L["top1"].sem, 1)
            dve.wait_ge(L["top1"].sem, L["top1"].at(b, u + 1))
            dve.tensor_scalar(stats[:, u % 2, 1, :], stats[:, u % 2, 0, :], -scale, None, ALU.mult)\
                .then_inc(L["shift1"].sem, 1)

        def inverse1(dve, b, u):
            j = unit(u)[0]
            dve.wait_ge(L["exp1"].sem, L["exp1"].at(b, 2 * u + 2))
            dve.wait_ge(L["pick1"].sem, L["pick1"].at(b, max(u - 1, 0)))
            dve.reciprocal(stats[:, u % 2, 3, :], stats[:, u % 2, 2, :]).then_inc(L["inv1"].sem, 1)
            dve.wait_ge(L["inv1"].sem, L["inv1"].at(b, u + 1))
            dve.wait_ge(L["sums1"].sem, L["sums1"].at(b, max(u - 1, 0)))
            at = core.columns["const"]["units32"][0]
            hot = core.weights["const"][:, bass.ds(b * (KJ * 32) + (at + j * 32), 32)]
            dve.tensor_tensor(pick[:, u % 2, :, :], hot.unsqueeze(1).to_broadcast([P, 2, 32]),
                              stats[:, u % 2, 3, :].unsqueeze(2).to_broadcast([P, 2, 32]), ALU.mult)\
                .then_inc(L["pick1"].sem, 1)


        def choose(dve):
            dve.wait_ge(L["added"].sem, L["added"].at(B - 1, 1))
            dve.tensor_scalar(work[:, :], sums[:, 0:OLD], -1.0, None, ALU.mult)\
                .then_inc(L["choice"].sem, 1)
            dve.wait_ge(L["choice"].sem, L["choice"].at(0, 1))
            for r in range(ROUNDS):
                dve.max(best[:, :], work[:, :])\
                    .then_inc(L["choice"].sem, 1)
                dve.wait_ge(L["choice"].sem, L["choice"].at(0, 2 * r + 2))
                dve.match_replace(out=work[:, :], in_to_replace=best[:, :], in_values=work[:, :], imm_value=NEG)\
                    .then_inc(L["choice"].sem, 1)
                dve.wait_ge(L["choice"].sem, L["choice"].at(0, 2 * r + 3))
            n = 2 * ROUNDS + 1
            dve.max(best[:, :], work[:, :])\
                .then_inc(L["choice"].sem, 1)
            dve.wait_ge(L["choice"].sem, L["choice"].at(0, n + 1))
            last = best[:, (DROPPED - 1) % 8:(DROPPED - 1) % 8 + 1]
            dve.tensor_scalar(work[:, :], sums[:, 0:OLD], -1.0, None, ALU.mult)\
                .then_inc(L["choice"].sem, 1)
            dve.wait_ge(L["choice"].sem, L["choice"].at(0, n + 2))
            dve.tensor_scalar(lt[:, :], work[:, :], last, None, ALU.is_gt)\
                .then_inc(L["choice"].sem, 1)
            dve.wait_ge(L["choice"].sem, L["choice"].at(0, n + 3))
            dve.tensor_scalar(eq[:, :], work[:, :], last, None, ALU.is_equal)\
                .then_inc(L["choice"].sem, 1)
            dve.wait_ge(L["choice"].sem, L["choice"].at(0, n + 4))
            dve.tensor_reduce(counts[:, 0:1], lt[:, :], AX.X, ALU.add)\
                .then_inc(L["choice"].sem, 1)
            dve.wait_ge(L["choice"].sem, L["choice"].at(0, n + 5))
            dve.tensor_tensor_scan(cum[:, :], core.w("const", "ones_s", 0, OLD), eq[:, :], 0.0, ALU.mult, ALU.add)\
                .then_inc(L["choice"].sem, 1)
            dve.wait_ge(L["choice"].sem, L["choice"].at(0, n + 6))
            dve.tensor_scalar(counts[:, 1:2], counts[:, 0:1], cum[:, OLD - 1:OLD], -float(DROPPED), ALU.add, ALU.add)\
                .then_inc(L["choice"].sem, 1)
            dve.wait_ge(L["choice"].sem, L["choice"].at(0, n + 7))
            dve.tensor_tensor(work[:, :], eq[:, :], cum[:, :], ALU.subtract)\
                .then_inc(L["choice"].sem, 1)
            dve.wait_ge(L["choice"].sem, L["choice"].at(0, n + 8))
            dve.tensor_scalar(work[:, :], work[:, :], counts[:, 1:2], 0.0, ALU.add, ALU.is_le)\
                .then_inc(L["choice"].sem, 1)
            dve.wait_ge(L["choice"].sem, L["choice"].at(0, n + 9))
            dve.tensor_tensor(work[:, :], work[:, :], eq[:, :], ALU.mult)\
                .then_inc(L["choice"].sem, 1)
            dve.wait_ge(L["choice"].sem, L["choice"].at(0, n + 10))
            dve.tensor_tensor(work[:, :], work[:, :], lt[:, :], ALU.add)\
                .then_inc(L["choice"].sem, 1)
            dve.wait_ge(L["choice"].sem, L["choice"].at(0, n + 11))
            dve.tensor_scalar(mask[:, 0:OLD], work[:, :], NEG, None, ALU.mult)\
                .then_inc(L["choice"].sem, 1)
            dve.wait_ge(L["choice"].sem, L["choice"].at(0, n + 12))


        def project2(pe, b, j):
            if j == 0:
                pe.wait_ge(L["v"].sem, L["v"].at(b, TT))
            else:
                pe.wait_ge(L["q2"].sem, L["q2"].at(b, j))
                pe.wait_ge(L["c_out"].sem, L["c_out"].at(b, max(j - 1, 0)))
                pe.wait_ge(L["e2"].sem, L["e2"].at(b, 2 * j))
            pe.matmul(psq[:, :], w("wq", j * P, (j + 1) * P), cur[:, :], start=True, stop=True)\
                .then_inc(L["p2"].sem, 1)
            if j == 0:
                pe.wait_ge(L["masked"].sem, L["masked"].at(b, 1))
            pe.matmul(pst[:, :], w("wk", j * P, (j + 1) * P), cur[:, :], start=True, stop=False)
            pe.matmul(pst[:, :], core.w("const", "mask_rows", j * P, (j + 1) * P), bmask[:, :],
                      start=False, stop=True).then_inc(L["p2"].sem, 1)

        def score2(pe, b, u):
            j, t, _ = unit(u)
            if u % (2 * TT) == 0:
                pe.wait_ge(L["e2"].sem, L["e2"].at(b, 2 * j + 2))
            pe.wait_ge(L["top2"].sem, L["top2"].at(b, u))
            for i in range(2):
                r = rows_of_group(u, i)
                mm = pe.matmul(ring[:, 0, i, :], q[r, j % 2, t * P:(t + 1) * P], k[r, j % 2, :], start=True, stop=True)
            mm.then_inc(L["s2"].sem, 1)

        def score_by_keys(pe, b, u):
            j, t, _ = unit(u)
            pe.wait_ge(L["q2"].sem, L["q2"].at(b, j + 1))
            pe.wait_ge(L["exp2"].sem, L["exp2"].at(b, u))
            for i in range(2):
                r = rows_of_group(u, i)
                mm = pe.matmul(ring[:, 1, i, :], k[r, j % 2, t * P:(t + 1) * P], q2[r, j % 2, :], start=True, stop=True)
            mm.then_inc(L["st"].sem, 1)

        def contexts(pe, b, u):
            j, t, p = unit(u)
            pe.wait_ge(L["exp2"].sem, L["exp2"].at(b, u + 1))
            if u % (2 * TT) == 0:
                pe.wait_ge(L["c_sb"].sem, L["c_sb"].at(b, j))
            for i in range(2):
                h = j * KG + 2 * p + i
                mm = pe.matmul(acc[rows_of_group(u, i), :], v[:, t, 32 * h:32 * h + 32], probs[:, u % 2, i, :],
                               start=t == 0, stop=t == TT - 1)
            mm.then_inc(L["av"].sem, 1)

        with nc.Block() as block:
            @block.tensor
            def _(pe):
                pe.wait_ge(L["cast"].sem, L["cast"].at(0, 2))
                with pe.Fori(0, B) as b:
                    pe.wait_ge(L["e1"].sem, L["e1"].at(b, 0))
                    ln_tensor(pe, L, b)
                    pe.wait_ge(L["ln_xn"].sem, L["ln_xn"].at(b, 1))
                    project1(pe, b, 0)
                    score1(pe, b, 0)
                    for u in range(UNITS):
                        if u % (2 * TT) == 2 and u // (2 * TT) + 1 < KJ:
                            project1(pe, b, u // (2 * TT) + 1)
                        if u + 1 < UNITS:
                            score1(pe, b, u + 1)
                        importance(pe, b, u)
                pe.wait_ge(L["choice"].sem, L["choice"].at(0, L["choice"].per))
                with pe.Fori(0, B) as b:
                    pe.wait_ge(L["o_sb"].sem, L["o_sb"].at(b, 0))
                    pe.wait_ge(L["c_out"].sem, L["c_out"].at(b, 0))
                    pe.wait_ge(L["current"].sem, L["current"].at(b, 1))
                    for t in range(TT):
                        if t >= 2:
                            pe.wait_ge(L["v"].sem, L["v"].at(b, t - 1))
                        pe.matmul((psq, pst)[t % 2][:, :], cur[:, t * P:(t + 1) * P], w("wv"), start=True, stop=True)\
                            .then_inc(L["pv"].sem, 1)
                    for jj in range(KJ + 1):
                        if jj < KJ:
                            project2(pe, b, jj)
                        for n in range(2 * TT):
                            if jj < KJ:
                                score2(pe, b, 2 * TT * jj + n)
                            if jj:
                                u = 2 * TT * (jj - 1) + n
                                score_by_keys(pe, b, u)
                                if n:
                                    contexts(pe, b, u - 1)
                        if jj:
                            contexts(pe, b, 2 * TT * jj - 1)
                        if jj < KJ:
                            pe.wait_ge(L["low2"].sem, L["low2"].at(b, 2 * TT * (jj + 1)))
                            pe.wait_ge(L["e2"].sem, L["e2"].at(b, 2 * jj + 2))
                            for t in range(TT):
                                mm = pe.transpose(psq[:, t * P:(t + 1) * P], low[:, jj % 2, t, :], eye)
                            mm.then_inc(L["rows"].sem, 1)
                        if jj:
                            pe.wait_ge(L["c_sb"].sem, L["c_sb"].at(b, jj))
                            pe.wait_ge(L["e2"].sem, L["e2"].at(b, 2 * min(jj + 1, KJ)))
                            pe.wait_ge(L["c_out"].sem, L["c_out"].at(b, jj - 1))
                            for t in range(TT):
                                mm = pe.transpose(pst[:, t * P:(t + 1) * P], c_sb[:, t * P:(t + 1) * P], eye)
                            mm.then_inc(L["c_turn"].sem, 1)
                    pe.wait_ge(L["c_out"].sem, L["c_out"].at(b, KJ))
                    pe.wait_ge(L["q2"].sem, L["q2"].at(b, KJ))
                    for t in range(TT):
                        mm = pe.transpose(psq[:, t * P:(t + 1) * P], outs[:, t, :], eye)
                    mm.then_inc(L["o_turn"].sem, 1)
                    pe.wait_ge(L["o_sb"].sem, L["o_sb"].at(b, 1))
                    pe.wait_ge(L["done"].sem, L["done"].at(b, 0))
                    pe.matmul(out[:, :], w("wo"), outs_t[:, :], start=True, stop=True).then_inc(L["projected"].sem, 1)

            @block.scalar
            def _(act):
                def take1(b, j):
                    for i, (to, ps) in enumerate(((q, psq), (k, pst))):
                        act.wait_ge(L["p1"].sem, L["p1"].at(b, 2 * j + i + 1))
                        act.wait_ge(L["s1"].sem, L["s1"].at(b, 2 * TT * max(j - 1, 0)))
                        act.activation(to[:, j % 2, :], ps[:, :], ACT.Copy).then_inc(L["e1"].sem, 1)

                def take2(b, j):
                    for i, (to, ps, bias) in enumerate(((q, psq, "q_ones"), (k, pst, "k_ones"))):
                        act.wait_ge(L["p2"].sem, L["p2"].at(b, 2 * j + i + 1))
                        act.wait_ge(L["s2"].sem, L["s2"].at(b, 2 * TT * max(j - 1, 0)))
                        act.wait_ge(L["st"].sem, L["st"].at(b, 2 * TT * max(j - 1, 0)))
                        act.wait_ge(L["q2"].sem, L["q2"].at(b, max(j - 1, 0)))
                        act.activation(to[:, j % 2, :], ps[:, :], ACT.Identity, bias=core.w("const", bias))\
                            .then_inc(L["e2"].sem, 1)

                with act.Fori(0, B) as b:
                    ln_scalar(act, L, b)
                    take1(b, 0)
                    for u in range(UNITS):
                        N = (TT - unit(u)[1]) * P
                        act.wait_ge(L["shift1"].sem, L["shift1"].at(b, u + 1))
                        act.wait_ge(L["sums1"].sem, L["sums1"].at(b, max(u - 1, 0)))
                        for i in range(2):
                            act.activation(probs[:, u % 2, i, 0:N], ring[:, u % 2, i, 0:N], ACT.Exp,
                                           bias=stats[:, u % 2, 1, i:i + 1], scale=scale,
                                           accum_out=stats[:, u % 2, 2, i:i + 1]).then_inc(L["exp1"].sem, 1)
                        if u % (2 * TT) == 2 and u // (2 * TT) + 1 < KJ:
                            take1(b, u // (2 * TT) + 1)
                act.wait_ge(L["ln_xn"].sem, L["ln_xn"].at(B - 1, 1))
                with act.Fori(0, B) as b:
                    act.wait_ge(L["p2"].sem, L["p2"].at(b, 0))
                    act.activation(cur[:, :], batch_of(xn, b), ACT.Copy).then_inc(L["current"].sem, 1)
                    for jj in range(KJ + 1):
                        if jj < KJ:
                            take2(b, jj)
                        if jj:
                            for n in range(2 * TT):
                                u = 2 * TT * (jj - 1) + n
                                act.wait_ge(L["st"].sem, L["st"].at(b, u + 1))
                                act.wait_ge(L["av"].sem, L["av"].at(b, max(u - 1, 0)))
                                act.activation(probs[:, u % 2, :, :], ring[:, 1, :, :], ACT.Exp, scale=scale)\
                                    .then_inc(L["exp2"].sem, 1)
                            act.wait_ge(L["av"].sem, L["av"].at(b, 2 * TT * jj))
                            act.wait_ge(L["c_turn"].sem, L["c_turn"].at(b, jj - 1))
                            act.activation(c_sb[:, :], acc[:, :], ACT.Copy).then_inc(L["c_sb"].sem, 1)
                    act.wait_ge(L["o_turn"].sem, L["o_turn"].at(b, 1))
                    act.activation(outs_t[:, :], psq[:, :], ACT.Copy).then_inc(L["o_sb"].sem, 1)

            @block.vector
            def _(dve):
                dve.memset(sums[:, :], 0.0).then_inc(L["zero"].sem, 1)
                dve.memset(mask[:, :], 0.0).then_inc(L["zero"].sem, 1)
                dve.wait_ge(L["zero"].sem, L["zero"].at(0, 2))
                with dve.Fori(0, B) as b:
                    ln_vector(dve, L, b, batch_of(xn, b))
                    maxima1(dve, b, 0)
                    for u in range(UNITS):
                        if u + 1 < UNITS:
                            maxima1(dve, b, u + 1)
                        inverse1(dve, b, u)
                    dve.wait_ge(L["sums1"].sem, L["sums1"].at(b, UNITS))
                    dve.tensor_tensor(sums[:, :], acc[:, :], sums[:, :], ALU.add).then_inc(L["added"].sem, 1)
                choose(dve)
                dve.wait_ge(L["cast"].sem, L["cast"].at(0, 3))
                with dve.Fori(0, B) as b:
                    dve.wait_ge(L["p2"].sem, L["p2"].at(b, 0))
                    at = core.columns["const"]["batch_rows"][0]
                    dve.tensor_scalar(bmask[:, :], mask[:, :], core.weights["const"][:, bass.ds(b + at, 1)], None,
                                      ALU.mult).then_inc(L["masked"].sem, 1)
                    for t in range(TT):
                        dve.wait_ge(L["pv"].sem, L["pv"].at(b, t + 1))
                        dve.tensor_tensor(v[:, t, :], (psq, pst)[t % 2][:, :], core.w("const", "v_ones"), ALU.add)\
                            .then_inc(L["v"].sem, 1)
                    for jj in range(KJ + 1):
                        if jj < KJ:
                            for n in range(2 * TT):
                                u = 2 * TT * jj + n
                                _, t, p = unit(u)
                                dve.wait_ge(L["s2"].sem, L["s2"].at(b, u + 1))
                                dve.tensor_reduce(stats[:, u % 2, 0, :], ring[:, 0, :, :], AX.X, ALU.max)\
                                    .then_inc(L["top2"].sem, 1)
                                dve.wait_ge(L["top2"].sem, L["top2"].at(b, u + 1))
                                dve.wait_ge(L["rows"].sem, L["rows"].at(b, max(jj - 1, 0)))
                                to = low[:, jj % 2, t, :].rearrange("p (g c) -> p g c", g=KG)
                                dve.tensor_scalar(to[:, 2 * p:2 * p + 2, SHIFT_ROW], stats[:, u % 2, 0, :], -1.0, None,
                                                  ALU.mult).then_inc(L["low2"].sem, 1)
                            dve.wait_ge(L["rows"].sem, L["rows"].at(b, jj + 1))
                            dve.wait_ge(L["st"].sem, L["st"].at(b, 2 * TT * max(jj - 1, 0)))
                            dve.tensor_tensor(q2[:, jj % 2, :], q[:, jj % 2, :], psq[:, :], ALU.add)\
                                .then_inc(L["q2"].sem, 1)
                        if jj:
                            j = jj - 1
                            dve.wait_ge(L["c_turn"].sem, L["c_turn"].at(b, jj))
                            turned = pst[:, :].rearrange("p (t g c) -> p t g c", t=TT, g=KG)
                            dve.reciprocal(c_inv[:, :, :], turned[:, :, :, KHD]).then_inc(L["c_inv"].sem, 1)
                            dve.wait_ge(L["c_inv"].sem, L["c_inv"].at(b, jj))
                            dve.wait_ge(L["o_turn"].sem, L["o_turn"].at(b, 0))
                            dve.tensor_tensor(
                                outs[:, :, 32 * j:32 * j + 32].rearrange("p t (g c) -> p t g c", g=KG),
                                turned[:, :, :, 0:KHD], c_inv[:, :, :].unsqueeze(3).to_broadcast([P, TT, KG, KHD]),
                                ALU.mult).then_inc(L["c_out"].sem, 1)
                    dve.wait_ge(L["projected"].sem, L["projected"].at(b, 1))
                    dve.tensor_tensor(core.batch(b), out[:, :], core.batch(b), ALU.add).then_inc(L["done"].sem, 1)

            @block.gpsimd
            def _(pool):
                pool.tensor_copy(eye16[:, :], eye).then_inc(L["cast"].sem, 1)
                pool.tensor_copy(later16[:, :], core.w("const", "later")).then_inc(L["cast"].sem, 1)
                pool.memset(low[:, :, :, :], 0.0).then_inc(L["cast"].sem, 1)
                with pool.Fori(0, B) as b:
                    ln_pool(pool, L, b)
    L.close()

LH, LHD = 8, 16
FG = 2
HG = LH // FG


def linear_attention(nc, core, name):
    NSTEP = FG * HG
    L = Layer(nc, name, core, ["light"], **LN_SIGNALS, masks=LH, vscale=1,
              angle=16, table=FG,
              proj=2 * FG,
              feats=2 * FG,
              rot=2 * FG,
              vu=2 * TT,
              vu_sb=2 * TT,
              v_late=1,
              kturn=FG, ktok=FG,
              states=FG,
              states_sb=FG,
              energy=NSTEP,
              masked=NSTEP,
              mixed=1,
              squares=TT, inv=2, outs=TT, turned=1, outs_sb=1, projected=1, done=1)
    with L.ctx:
        g = "light"
        w = lambda n, *a: core.w(g, n, *a)
        xn = L.sb("xn", [P, S])
        table = L.sb("table", [P, FG, S])
        turns = L.sb("turns", [P, 2, S])
        wholes = L.sb("wholes", [P, S], mybir.dt.int32)
        feats = L.sb("feats", [P, 2, FG, S])
        qk = L.sb("qk", [P, 2, FG, S])
        v, u = L.sb("v", [P, TT, D]), L.sb("u", [P, TT, D])
        v_late = L.sb("v_late", [P, TT, D])
        growth = L.sb("growth", [P, D])
        ktok = L.sb("ktok", [P, FG, TT, P])
        state = L.sb("state", [P, FG, TT, D // FG])
        masks = L.sb("masks", [P, LH, P])
        energy = L.sb("energy", [P, NSTEP, S])
        square = L.sb("square", [P, D])
        sums = L.sb("sums", [P, 3, TT])
        outs = L.sb("outs", [P, TT, D])
        outs_t = L.sb("outs_t", [P, S])
        bank = L.ps("bank", [P, S])
        small = L.ps("small", [P, S])
        pe4 = L.ps("pe4", [P, HG, S])
        pmix = L.ps("pmix", [P, TT, D])
        pout = L.ps("pout", [P, S])
        ln_buffers(L, bank[:, :], small[:, 0:TT])
        eye = core.w("const", "eye")
        TWO_PI = 2 * np.pi
        c1 = float(np.float32(6.28125))
        c2 = float(np.float32(np.round((TWO_PI - c1) * 2 ** 20) / 2 ** 20))
        c3 = float(np.float32(TWO_PI - c1 - c2))
        magic = 1.5 * 2.0 ** 23

        with nc.Block() as block:
            @block.tensor
            def _(pe):
                with pe.Fori(0, B) as b:
                    ln_tensor(pe, L, b)
                    pe.wait_ge(L["ln_xn"].sem, L["ln_xn"].at(b, 1))
                    pe.wait_ge(L["masked"].sem, L["masked"].at(b, 0))
                    for i in range(2):
                        for j in range(FG):
                            pe.matmul(pe4[:, i * FG + j, :], w(("wq", "wk")[i], j * P, (j + 1) * P), xn[:, :],
                                      start=True, stop=True).then_inc(L["proj"].sem, 1)
                    pe.wait_ge(L["states_sb"].sem, L["states_sb"].at(b, 0))
                    pe.wait_ge(L["done"].sem, L["done"].at(b, 0))
                    for i, (n, ps) in enumerate((("wv", small), ("wu", pout))):
                        for t in range(TT):
                            pe.matmul(ps[:, t * P:(t + 1) * P], xn[:, t * P:(t + 1) * P], w(n),
                                      start=True, stop=True).then_inc(L["vu"].sem, 1)
                    for j in range(FG):
                        pe.wait_ge(L["rot"].sem, L["rot"].at(b, FG + j + 1))
                        if j >= 1:
                            pe.wait_ge(L["ktok"].sem, L["ktok"].at(b, j))
                        for t in range(TT):
                            mm = pe.transpose(bank[:, t * P:(t + 1) * P], qk[:, 1, j, t * P:(t + 1) * P], eye)
                        mm.then_inc(L["kturn"].sem, 1)
                    pe.wait_ge(L["vu_sb"].sem, L["vu_sb"].at(b, 2 * TT))
                    pe.wait_ge(L["v_late"].sem, L["v_late"].at(b, 1))
                    for j in range(FG):
                        pe.wait_ge(L["ktok"].sem, L["ktok"].at(b, j + 1))
                        c = slice(j * (D // FG), (j + 1) * (D // FG))
                        for t in range(TT):
                            others = [o for o in range(TT) if o != t]
                            at = (j * TT + t) * (D // FG)
                            for o in others:
                                mm = pe.matmul(small[:, at:at + D // FG], ktok[:, j, o, :],
                                               (v_late if o < t else v)[:, o, c],
                                               start=o == others[0], stop=o == others[-1])
                        mm.then_inc(L["states"].sem, 1)
                    for j in range(FG):
                        pe.wait_ge(L["rot"].sem, L["rot"].at(b, FG + j + 1))
                        for h in range(HG):
                            r = slice(32 * h, 32 * h + 32)
                            if j == 0:
                                pe.wait_ge(L["feats"].sem, L["feats"].at(b, 2 * FG))
                            else:
                                pe.wait_ge(L["masked"].sem, L["masked"].at(b, h + 1))
                            for t in range(TT):
                                tk = slice(t * P, (t + 1) * P)
                                mm = pe.matmul(pe4[:, h, tk], qk[r, 1, j, tk], qk[r, 0, j, tk], start=True, stop=True)
                            mm.then_inc(L["energy"].sem, 1)
                    pe.wait_ge(L["outs"].sem, L["outs"].at(b, 0))
                    pe.wait_ge(L["states_sb"].sem, L["states_sb"].at(b, FG))
                    pe.wait_ge(L["masked"].sem, L["masked"].at(b, NSTEP))
                    for t in range(TT):
                        for j in range(FG):
                            at = j * (D // FG)
                            pe.matmul(pmix[:, t, at:at + D // FG], qk[:, 0, j, t * P:(t + 1) * P], state[:, j, t, :],
                                      start=True, stop=True, skip_group_check=True)
                            for h in range(HG):
                                hh = j * HG + h
                                mm = pe.matmul(pmix[:, t, hh * LHD:(hh + 1) * LHD], energy[:, hh, t * P:(t + 1) * P],
                                               v[:, t, hh * LHD:(hh + 1) * LHD], start=False, stop=True,
                                               skip_group_check=True)
                    mm.then_inc(L["mixed"].sem, 1)
                    pe.wait_ge(L["outs"].sem, L["outs"].at(b, TT))
                    for t in range(TT):
                        mm = pe.transpose(bank[:, t * P:(t + 1) * P], outs[:, t, :], eye)
                    mm.then_inc(L["turned"].sem, 1)
                    pe.wait_ge(L["outs_sb"].sem, L["outs_sb"].at(b, 1))
                    pe.matmul(pout[:, :], w("wo"), outs_t[:, :], start=True, stop=True).then_inc(L["projected"].sem, 1)

            @block.scalar
            def _(act):
                for h in range(LH):
                    act.activation(masks[:, h, :], core.w("const", "upper"), ACT.Exp, scale=w("slope", h, h + 1))\
                        .then_inc(L["masks"].sem, 1)
                act.activation(growth[:, :], w("slope_cols"), ACT.Exp).then_inc(L["vscale"].sem, 1)
                for j in range(FG):
                    act.wait_ge(L["angle"].sem, L["angle"].at(0, 8 * (j + 1)))
                    act.activation(table[:, j, :], turns[:, j, :], ACT.Sin).then_inc(L["table"].sem, 1)
                with act.Fori(0, B) as b:
                    ln_scalar(act, L, b)
                    for i in range(2):
                        for j in range(FG):
                            n = i * FG + j
                            act.wait_ge(L["proj"].sem, L["proj"].at(b, n + 1))
                            act.wait_ge(L["rot"].sem, L["rot"].at(b, 0))
                            act.activation(feats[:, i, j, :], pe4[:, n, :], ACT.Silu,
                                           bias=w(("bq", "bk")[i], j, j + 1)).then_inc(L["feats"].sem, 1)
                    for j in range(FG):
                        act.wait_ge(L["kturn"].sem, L["kturn"].at(b, j + 1))
                        act.activation(ktok[:, j, :, :], bank[:, :].rearrange("p (t c) -> p t c", t=TT), ACT.Copy)\
                            .then_inc(L["ktok"].sem, 1)
                    for t in range(TT):
                        act.wait_ge(L["mixed"].sem, L["mixed"].at(b, 1))
                        if t:
                            act.wait_ge(L["squares"].sem, L["squares"].at(b, t))
                        act.activation(square[:, :], pmix[:, t, :], ACT.Square, accum_out=sums[:, 0, t:t + 1])\
                            .then_inc(L["squares"].sem, 1)
                    act.wait_ge(L["turned"].sem, L["turned"].at(b, 1))
                    act.activation(outs_t[:, :], bank[:, :], ACT.Copy).then_inc(L["outs_sb"].sem, 1)

            @block.vector
            def _(dve):
                for j in range(FG):
                    t0, t1 = turns[:, j, :], feats[:, 0, 0, :]
                    dve.tensor_scalar(t0, core.w("const", "token"), w("theta", j, j + 1), None, ALU.mult)\
                        .then_inc(L["angle"].sem, 1)
                    dve.wait_ge(L["angle"].sem, L["angle"].at(0, 8 * j + 1))
                    dve.tensor_scalar(t1, t0, w("shift", j, j + 1), 1.0 / TWO_PI, ALU.add, ALU.mult)\
                        .then_inc(L["angle"].sem, 1)
                    dve.wait_ge(L["angle"].sem, L["angle"].at(0, 8 * j + 2))
                    dve.tensor_scalar(t1, t1, magic, magic, ALU.add, ALU.subtract).then_inc(L["angle"].sem, 1)
                    for n, cc in enumerate((c1, c2, c3)):
                        dve.wait_ge(L["angle"].sem, L["angle"].at(0, 8 * j + 3 + n))
                        dve.scalar_tensor_tensor(out=t0, in0=t1, scalar=-cc, in1=t0, op0=ALU.mult, op1=ALU.add)\
                            .then_inc(L["angle"].sem, 1)
                    dve.wait_ge(L["angle"].sem, L["angle"].at(0, 8 * j + 6))
                    dve.tensor_scalar(t0, t0, w("shift", j, j + 1), float(np.float32(3.1415925)), ALU.add, ALU.min)\
                        .then_inc(L["angle"].sem, 1)
                    dve.wait_ge(L["angle"].sem, L["angle"].at(0, 8 * j + 7))
                    dve.tensor_scalar(t0, t0, -float(np.float32(3.1415925)), None, ALU.max).then_inc(L["angle"].sem, 1)
                dve.wait_ge(L["masks"].sem, L["masks"].at(0, LH))
                dve.wait_ge(L["vscale"].sem, L["vscale"].at(0, 1))
                dve.wait_ge(L["table"].sem, L["table"].at(0, FG))
                with dve.Fori(0, B) as b:
                    ln_vector(dve, L, b, xn[:, :])
                    dve.wait_ge(L["outs"].sem, L["outs"].at(b, 0))
                    for i, (to, ps, bias) in enumerate(((v, small, "bv"), (u, pout, "bu"))):
                        for t in range(TT):
                            dve.wait_ge(L["vu"].sem, L["vu"].at(b, TT * (i + 1)))
                            dve.tensor_tensor(to[:, t, :], ps[:, t * P:(t + 1) * P], w(bias), ALU.add)\
                                .then_inc(L["vu_sb"].sem, 1)
                    dve.wait_ge(L["vu_sb"].sem, L["vu_sb"].at(b, TT))
                    dve.tensor_tensor(v_late[:, :, :], v[:, :, :],
                                      growth[:, :].unsqueeze(1).to_broadcast([P, TT, D]), ALU.mult)\
                        .then_inc(L["v_late"].sem, 1)
                    for i in range(2):
                        for j in range(FG):
                            dve.wait_ge(L["feats"].sem, L["feats"].at(b, i * FG + j + 1))
                            dve.tensor_tensor(qk[:, i, j, :], feats[:, i, j, :], table[:, j, :], ALU.mult)\
                                .then_inc(L["rot"].sem, 1)
                    for j in range(FG):
                        dve.wait_ge(L["states"].sem, L["states"].at(b, FG))
                        W = TT * (D // FG)
                        dve.tensor_tensor(state[:, j, :, :],
                                          small[:, j * W:(j + 1) * W].rearrange("p (t c) -> p t c", t=TT),
                                          core.w("const", "block4").unsqueeze(1).to_broadcast([P, TT, D // FG]),
                                          ALU.mult).then_inc(L["states_sb"].sem, 1)
                    for s in range(NSTEP):
                        dve.wait_ge(L["energy"].sem, L["energy"].at(b, s + 1))
                        dve.tensor_tensor(energy[:, s, :].rearrange("p (t c) -> p t c", t=TT),
                                          pe4[:, s % HG, :].rearrange("p (t c) -> p t c", t=TT),
                                          masks[:, s, :].unsqueeze(1).to_broadcast([P, TT, P]), ALU.mult)\
                            .then_inc(L["masked"].sem, 1)
                    dve.wait_ge(L["squares"].sem, L["squares"].at(b, TT))
                    dve.tensor_scalar(sums[:, 1, :], sums[:, 0, :], 1.0 / D, 1e-6, ALU.mult, ALU.add)\
                        .then_inc(L["inv"].sem, 1)
                    dve.wait_ge(L["inv"].sem, L["inv"].at(b, 2))
                    for t in range(TT):
                        dve.wait_ge(L["vu_sb"].sem, L["vu_sb"].at(b, 2 * TT))
                        dve.scalar_tensor_tensor(out=outs[:, t, :], in0=pmix[:, t, :], scalar=sums[:, 2, t:t + 1],
                                                 in1=u[:, t, :], op0=ALU.mult, op1=ALU.mult).then_inc(L["outs"].sem, 1)
                    dve.wait_ge(L["projected"].sem, L["projected"].at(b, 1))
                    dve.scalar_tensor_tensor(out=core.batch(b), in0=pout[:, :], scalar=w("bo"), in1=core.batch(b),
                                             op0=ALU.add, op1=ALU.add).then_inc(L["done"].sem, 1)

            @block.gpsimd
            def _(pool):
                with pool.Fori(0, B) as b:
                    ln_pool(pool, L, b)
                    pool.wait_ge(L["inv"].sem, L["inv"].at(b, 1))
                    pool.tensor_tensor(sums[:, 2, :], sums[:, 1, :], core.w("const", "minus_half"), ALU.pow)\
                        .then_inc(L["inv"].sem, 1)
    L.close()

DFF = 512
FT = DFF // P


def quantise(nc, core):
    L = Layer(nc, "quant", core, ["bitffn"], rowsum=2, total=1, gamma=2, scaled=2, rounded=2, clipped=2)
    with L.ctx:
        rowsum = L.sb("rowsums", [P, 2])
        gamma = L.sb("gammas", [P, 2])
        total = L.ps("totals", [P, 2])
        mats = [core.w("bitffn", "w1"), core.w("bitffn", "w2")]
        magic = 1.5 * 2.0 ** 23
        with nc.Block() as block:
            @block.vector
            def _(dve):
                for i, w in enumerate(mats):
                    dve.tensor_reduce(rowsum[:, i:i + 1], w, AX.X, ALU.add, apply_absolute_value=True)\
                        .then_inc(L["rowsum"].sem, 1)
                dve.wait_ge(L["total"].sem, L["total"].at(0, 1))
                dve.tensor_scalar(gamma[:, :], total[:, :], 1.0 / (DFF * D), 1e-5, ALU.mult, ALU.add)\
                    .then_inc(L["gamma"].sem, 1)
                dve.wait_ge(L["gamma"].sem, L["gamma"].at(0, 1))
                dve.reciprocal(gamma[:, :], gamma[:, :]).then_inc(L["gamma"].sem, 1)
                dve.wait_ge(L["gamma"].sem, L["gamma"].at(0, 2))
                for i, w in enumerate(mats):
                    dve.tensor_scalar(w, w, gamma[:, i:i + 1], None, ALU.mult).then_inc(L["scaled"].sem, 1)
                    dve.wait_ge(L["scaled"].sem, L["scaled"].at(0, i + 1))
                    dve.tensor_scalar(w, w, magic, magic, ALU.add, ALU.subtract).then_inc(L["rounded"].sem, 1)
                    dve.wait_ge(L["rounded"].sem, L["rounded"].at(0, i + 1))
                    dve.tensor_scalar(w, w, 1.0, -1.0, ALU.min, ALU.max).then_inc(L["clipped"].sem, 1)

            @block.tensor
            def _(pe):
                pe.wait_ge(L["rowsum"].sem, L["rowsum"].at(0, 2))
                pe.matmul(total[:, :], core.w("const", "ones"), rowsum[:, :], start=True, stop=True)\
                    .then_inc(L["total"].sem, 1)
    L.close()


def bit_ffn(nc, core, name):
    L = Layer(nc, name, core, ["bitffn"], **LN_SIGNALS, up=FT, hidden=FT, down=FT, done=1)
    with L.ctx:
        xn = L.sb("xn", [P, S])
        h = L.sb("h", [P, 2, S])
        out = L.ps("out", [P, S])
        ln_buffers(L, L.ps("ln", [P, S])[:, :], L.ps("var", [P, TT])[:, :])
        up = L.ps("up", [P, 2, S])
        w1, w2 = core.w("bitffn", "w1"), core.w("bitffn", "w2")
        b1, b2 = core.w("bitffn", "b1"), core.w("bitffn", "b2")
        def down(pe, b, m):
            pe.wait_ge(L["hidden"].sem, L["hidden"].at(b, m + 1))
            if m == 0:
                pe.wait_ge(L["done"].sem, L["done"].at(b, 0))
            pe.matmul(out[:, :], w2[:, m * P:(m + 1) * P], h[:, m % 2, :], start=m == 0, stop=m == FT - 1)\
                .then_inc(L["down"].sem, 1)

        with nc.Block() as block:
            @block.tensor
            def _(pe):
                with pe.Fori(0, B) as b:
                    ln_tensor(pe, L, b)
                    pe.wait_ge(L["ln_xn"].sem, L["ln_xn"].at(b, 1))
                    for m in range(FT):
                        pe.wait_ge(L["hidden"].sem, L["hidden"].at(b, max(m - 1, 0)))
                        pe.matmul(up[:, m % 2, :], w1[:, m * P:(m + 1) * P], xn[:, :], start=True, stop=True)\
                            .then_inc(L["up"].sem, 1)
                        if m >= 1:
                            down(pe, b, m - 1)
                    down(pe, b, FT - 1)

            @block.scalar
            def _(act):
                with act.Fori(0, B) as b:
                    ln_scalar(act, L, b)
                    for m in range(FT):
                        act.wait_ge(L["up"].sem, L["up"].at(b, m + 1))
                        act.wait_ge(L["down"].sem, L["down"].at(b, max(m - 1, 0)))
                        act.activation(h[:, m % 2, :], up[:, m % 2, :], ACT.Relu, bias=b1[:, m:m + 1])\
                            .then_inc(L["hidden"].sem, 1)

            @block.vector
            def _(dve):
                with dve.Fori(0, B) as b:
                    ln_vector(dve, L, b, xn[:, :])
                    dve.wait_ge(L["down"].sem, L["down"].at(b, FT))
                    dve.scalar_tensor_tensor(out=core.batch(b), in0=out[:, :], scalar=b2, in1=core.batch(b),
                                             op0=ALU.add, op1=ALU.add).then_inc(L["done"].sem, 1)

            @block.gpsimd
            def _(pool):
                with pool.Fori(0, B) as b:
                    ln_pool(pool, L, b)
    L.close()

SH = 32
SLOTS = 64
RMS_EPS = 1.1920929e-07


def landmark_layer(nc, core, name):
    NA = 2 * TT
    L = Layer(nc, name, core, ["slr"], **LN_SIGNALS, lam=2,
              sq=2, var=2, eps=2, rstd=2, diag=2, spread=2,
              xn=2,
              route=3,
              hid=1, hid_sb=1, wide=1, logit=1, lmax=3, lexp=1, lsum=3,
              decayed=1, ema=1,
              qk=2, qk_sb=2, v_ps=1, v_sb=1,
              scores=NA, top=NA, shift=NA, probs=NA, inv=2 * TT, second=TT, mixp=TT,
              turn=TT, turn_sb=TT, averaged=1, ctx_sb=1, slr=1, joined=1,
              qwide=1, lscore=1, attn=5, aexp=1, arc=2,
              mix=1, mix_sb=1, scaled=1, result=1,
              mean=1, bus=3, bus_sb=3, final=1, done=1)
    with L.ctx:
        g = "slr"
        w = lambda n, *a: core.w(g, n, *a)
        xl, xn, sq = (L.sb(n, [P, S]) for n in ("xl", "xn", "sq"))
        small = L.sb("small", [P, 2, 2, TT])
        diag = L.sb("diag", [P, TT, P])
        col = L.sb("col", [P, 32])
        wide = L.sb("wide", [P, P])
        probs3 = L.sb("probs3", [P, 8])
        lam_row = L.sb("lam_row", [P, S])
        drive, ema, joined = (L.sb(n, [P, S]) for n in ("drive", "ema", "joined"))
        qk = L.sb("qk", [2 * SH, 2, S])
        v = L.sb("v", [P, TT, SH])
        stats = L.sb("stats", [P, 4, NA])
        probs = L.sb("probs", [P, NA, S])
        turned = L.sb("turned", [P, TT, S])
        ctx_t = L.sb("ctx_t", [SH, S])
        qwide = L.sb("qwide", [P, P])
        attn = L.sb("attn", [P, 3, SLOTS])
        mix, result = L.sb("mix", [P, S]), L.sb("result", [P, S])
        bank, ps_small, pa, pb, pc, pt, pu, out = (L.ps(n, [P, S]) for n in
                                                  ("bank", "ps_small", "pa", "pb", "pc", "pt", "pu", "out"))
        ln_buffers(L, bank[:, :], ps_small[:, 0:TT])
        eye = core.w("const", "eye")
        ones = core.w("const", "ones")
        C_MEAN, C_HID, C_P, C_MX, C_SUM, C_INV, C_PMF, C_LAM1, C_AMX, C_ASUM, C_AINV, C_ARC, C_M2, C_B0, C_B1, C_B2, \
            C_NMX, C_SHIFT = range(18)

        def c(i):
            return col[:, i:i + 1]

        def rms_tensor(pe, b, i):
            pe.wait_ge(L["sq"].sem, L["sq"].at(b, i + 1))
            for t in range(TT):
                mm = pe.matmul(ps_small[:, 8 + TT * i + t:9 + TT * i + t], sq[:, t * P:(t + 1) * P],
                               core.w("const", "mean", 0, 1), start=True, stop=True)
            mm.then_inc(L["var"].sem, 1)
            pe.wait_ge(L["diag"].sem, L["diag"].at(b, i + 1))
            pe.matmul(pa[:, :], ones, diag[:, :, :], start=True, stop=True).then_inc(L["spread"].sem, 1)

        def rms_vector(dve, b, i):
            dve.wait_ge(L["var"].sem, L["var"].at(b, i + 1))
            at = 8 + TT * i
            dve.tensor_scalar(small[:, i, 0, :], ps_small[:, at:at + TT], RMS_EPS, None, ALU.add)\
                .then_inc(L["eps"].sem, 1)
            dve.wait_ge(L["rstd"].sem, L["rstd"].at(b, i + 1))
            dve.wait_ge(L["spread"].sem, L["spread"].at(b, i))
            dve.tensor_tensor(diag[:, :, :], eye.unsqueeze(1).to_broadcast([P, TT, P]),
                              small[:, i, 1, :].unsqueeze(2).to_broadcast([P, TT, P]), ALU.mult)\
                .then_inc(L["diag"].sem, 1)

        def rms_pool(pool, b, i):
            pool.wait_ge(L["eps"].sem, L["eps"].at(b, i + 1))
            pool.tensor_tensor(small[:, i, 1, :], small[:, i, 0, :], core.w("const", "minus_half"), ALU.pow)\
                .then_inc(L["rstd"].sem, 1)

        sc = 1.0 / float(SH) ** 0.5
        scd = 1.0 / float(D) ** 0.5

        def differ(dve, b, t):
            n = 2 * t
            dve.wait_ge(L["probs"].sem, L["probs"].at(b, n + 2))
            dve.reciprocal(stats[:, 3, n:n + 2], stats[:, 2, n:n + 2]).then_inc(L["inv"].sem, 1)
            dve.wait_ge(L["inv"].sem, L["inv"].at(b, 2 * t + 1))
            dve.tensor_tensor(stats[:, 3, n + 1:n + 2], stats[:, 3, n + 1:n + 2], w("slr_lam"), ALU.mult)\
                .then_inc(L["inv"].sem, 1)
            dve.wait_ge(L["inv"].sem, L["inv"].at(b, 2 * t + 2))
            dve.tensor_scalar(probs[:, n + 1, :], probs[:, n + 1, :], stats[:, 3, n + 1:n + 2], None, ALU.mult)\
                .then_inc(L["second"].sem, 1)
            dve.wait_ge(L["second"].sem, L["second"].at(b, t + 1))
            dve.scalar_tensor_tensor(out=probs[:, n, :], in0=probs[:, n, :], scalar=stats[:, 3, n:n + 1],
                                     in1=probs[:, n + 1, :], op0=ALU.mult, op1=ALU.subtract).then_inc(L["mixp"].sem, 1)

        with nc.Block() as block:
            @block.tensor
            def _(pe):
                with pe.Fori(0, B) as b:
                    ln_tensor(pe, L, b)
                    rms_tensor(pe, b, 0)
                    pe.wait_ge(L["xn"].sem, L["xn"].at(b, 2))
                    for i, n in enumerate(("wq", "wk")):
                        pe.matmul((pb, pc)[i][0:2 * SH, :], w(n), xn[:, :], start=True, stop=True)\
                            .then_inc(L["qk"].sem, 1)
                    for t in range(TT):
                        mm = pe.matmul(pt[:, t * SH:(t + 1) * SH], xn[:, t * P:(t + 1) * P], w("wv"),
                                       start=True, stop=True)
                    mm.then_inc(L["v_ps"].sem, 1)
                    pe.wait_ge(L["route"].sem, L["route"].at(b, 1))
                    pe.matmul(pu[0:64, 0:1], w("r1"), c(C_MEAN), start=True, stop=True).then_inc(L["hid"].sem, 1)
                    pe.wait_ge(L["wide"].sem, L["wide"].at(b, 1))
                    pe.matmul(pu[:, 4:7], wide[0:64, :], w("r2"), start=True, stop=True).then_inc(L["logit"].sem, 1)
                    pe.wait_ge(L["qwide"].sem, L["qwide"].at(b, 1))
                    pe.wait_ge(L["lmax"].sem, L["lmax"].at(b, 1))
                    pe.matmul(pu[:, 64:64 + SLOTS], qwide[:, :], w("landmarks_t"), start=True, stop=True)\
                        .then_inc(L["lscore"].sem, 1)
                    pe.wait_ge(L["qk_sb"].sem, L["qk_sb"].at(b, 2))
                    for n in range(NA):
                        t, i = divmod(n, 2)
                        r = slice(i * SH, (i + 1) * SH)
                        if n >= 2:
                            pe.wait_ge(L["probs"].sem, L["probs"].at(b, n - 1))
                        pe.matmul((pb, pc)[i][:, :], qk[r, 0, t * P:(t + 1) * P], qk[r, 1, :],
                                  start=True, stop=True).then_inc(L["scores"].sem, 1)
                    pe.wait_ge(L["v_sb"].sem, L["v_sb"].at(b, 1))
                    for t in range(TT):
                        pe.wait_ge(L["mixp"].sem, L["mixp"].at(b, t + 1))
                        ps = (pt, out)[t % 2]
                        if t >= 2:
                            pe.wait_ge(L["turn_sb"].sem, L["turn_sb"].at(b, t - 1))
                        if t == 1:
                            pe.wait_ge(L["done"].sem, L["done"].at(b, 0))
                        for o in range(TT):
                            mm = pe.transpose(ps[:, o * P:(o + 1) * P], probs[:, 2 * t, o * P:(o + 1) * P], eye)
                        mm.then_inc(L["turn"].sem, 1)
                    pe.wait_ge(L["turn_sb"].sem, L["turn_sb"].at(b, TT))
                    for o in range(TT):
                        mm = pe.matmul(pb[0:SH, :], v[:, o, :], turned[:, o, :], start=o == 0, stop=o == TT - 1)
                    mm.then_inc(L["averaged"].sem, 1)
                    pe.wait_ge(L["ctx_sb"].sem, L["ctx_sb"].at(b, 1))
                    pe.matmul(pc[:, :], w("wo"), ctx_t[:, :], start=True, stop=True).then_inc(L["slr"].sem, 1)
                    pe.matmul(out[:, :], w("mix2"), xn[:, :], start=True, stop=False)
                    pe.wait_ge(L["arc"].sem, L["arc"].at(b, 2))
                    pe.matmul(out[:, :], w("mix1"), joined[:, :], start=False, stop=True).then_inc(L["mix"].sem, 1)
                    rms_tensor(pe, b, 1)
                    pe.wait_ge(L["mean"].sem, L["mean"].at(b, 1))
                    for i, n in enumerate(("compress", "publish", "expand")):
                        if i:
                            pe.wait_ge(L["bus_sb"].sem, L["bus_sb"].at(b, i))
                        pe.matmul(pu[:, 200 + i:201 + i], w(n), c((C_M2, C_B0, C_B1)[i]), start=True, stop=True)\
                            .then_inc(L["bus"].sem, 1)

            @block.scalar
            def _(act):
                with act.Fori(0, B) as b:
                    ln_scalar(act, L, b)
                    act.wait_ge(L["ln_xn"].sem, L["ln_xn"].at(b, 1))
                    act.activation(sq[:, :], xl[:, :], ACT.Square).then_inc(L["sq"].sem, 1)
                    for i in range(2):
                        act.wait_ge(L["qk"].sem, L["qk"].at(b, i + 1))
                        act.activation(qk[:, i, :], (pb, pc)[i][0:2 * SH, :], ACT.Copy).then_inc(L["qk_sb"].sem, 1)
                    act.wait_ge(L["v_ps"].sem, L["v_ps"].at(b, 1))
                    act.activation(v[:, :, :], pt[:, 0:TT * SH].rearrange("p (t d) -> p t d", t=TT), ACT.Copy)\
                        .then_inc(L["v_sb"].sem, 1)
                    act.wait_ge(L["hid"].sem, L["hid"].at(b, 1))
                    act.activation(col[0:64, C_HID:C_HID + 1], pu[0:64, 0:1], ACT.Silu, scale=1.0 / S)\
                        .then_inc(L["hid_sb"].sem, 1)
                    act.wait_ge(L["lmax"].sem, L["lmax"].at(b, 3))
                    act.activation(probs3[:, 4:7], probs3[:, 0:3], ACT.Exp, bias=c(C_NMX),
                                   accum_out=c(C_SUM)).then_inc(L["lexp"].sem, 1)
                    for n in range(NA):
                        act.wait_ge(L["shift"].sem, L["shift"].at(b, n + 1))
                        act.activation(probs[:, n, :], (pb, pc)[n % 2][:, :], ACT.Exp, bias=stats[:, 1, n:n + 1],
                                       scale=sc, accum_out=stats[:, 2, n:n + 1]).then_inc(L["probs"].sem, 1)
                    act.wait_ge(L["attn"].sem, L["attn"].at(b, 2))
                    act.activation(attn[:, 0, :], attn[:, 2, :], ACT.Exp, bias=c(C_SHIFT), scale=scd,
                                   accum_out=c(C_ASUM)).then_inc(L["aexp"].sem, 1)
                    for t in range(TT):
                        act.wait_ge(L["turn"].sem, L["turn"].at(b, t + 1))
                        act.activation(turned[:, :, t * P:(t + 1) * P],
                                       (pt, out)[t % 2][:, :].rearrange("p (o c) -> p o c", o=TT), ACT.Copy)\
                            .then_inc(L["turn_sb"].sem, 1)
                    act.wait_ge(L["averaged"].sem, L["averaged"].at(b, 1))
                    act.activation(ctx_t[:, :], pb[0:SH, :], ACT.Copy).then_inc(L["ctx_sb"].sem, 1)
                    act.wait_ge(L["mix"].sem, L["mix"].at(b, 1))
                    act.activation(sq[:, :], out[:, :], ACT.Square).then_inc(L["sq"].sem, 1)
                    act.activation(mix[:, :], out[:, :], ACT.Copy).then_inc(L["mix_sb"].sem, 1)
                    for i in range(3):
                        act.wait_ge(L["bus"].sem, L["bus"].at(b, i + 1))
                        act.activation(c((C_B0, C_B1, C_B2)[i]), pu[:, 200 + i:201 + i], ACT.Copy,
                                       scale=(1.0 / S, 1.0, 0.1)[i]).then_inc(L["bus_sb"].sem, 1)

            @block.vector
            def _(dve):
                dve.tensor_copy(lam_row[:, :], w("lam").to_broadcast([P, S])).then_inc(L["lam"].sem, 1)
                dve.tensor_scalar(c(C_LAM1), w("lam"), -1.0, 1.0, ALU.mult, ALU.add).then_inc(L["lam"].sem, 1)
                dve.wait_ge(L["lam"].sem, L["lam"].at(0, 2))
                with dve.Fori(0, B) as b:
                    ln_vector(dve, L, b, xl[:, :])
                    rms_vector(dve, b, 0)
                    dve.wait_ge(L["spread"].sem, L["spread"].at(b, 1))
                    dve.tensor_tensor(mix[:, :], xl[:, :], pa[:, :], ALU.mult).then_inc(L["xn"].sem, 1)
                    dve.wait_ge(L["xn"].sem, L["xn"].at(b, 1))
                    dve.tensor_scalar(xn[:, :], mix[:, :], w("norm_in"), None, ALU.mult).then_inc(L["xn"].sem, 1)
                    dve.wait_ge(L["xn"].sem, L["xn"].at(b, 2))
                    dve.tensor_reduce(c(C_MEAN), xn[:, :], AX.X, ALU.add).then_inc(L["route"].sem, 1)
                    dve.tensor_scalar(drive[:, :], xn[:, :], c(C_LAM1), None, ALU.mult).then_inc(L["decayed"].sem, 1)
                    dve.tensor_scalar(qwide[:, :], ones, xn[:, S - 1:S], None, ALU.mult).then_inc(L["qwide"].sem, 1)
                    dve.wait_ge(L["decayed"].sem, L["decayed"].at(b, 1))
                    dve.tensor_tensor_scan(ema[:, :], lam_row[:, :], drive[:, :], 0.0, ALU.mult, ALU.add)\
                        .then_inc(L["ema"].sem, 1)
                    dve.wait_ge(L["hid_sb"].sem, L["hid_sb"].at(b, 1))
                    dve.tensor_scalar(wide[0:64, :], ones[0:64, :], col[0:64, C_HID:C_HID + 1], None, ALU.mult)\
                        .then_inc(L["wide"].sem, 1)
                    dve.wait_ge(L["logit"].sem, L["logit"].at(b, 1))
                    dve.tensor_tensor(probs3[:, 0:3], pu[:, 4:7], w("r2b"), ALU.add).then_inc(L["lmax"].sem, 1)
                    dve.wait_ge(L["lmax"].sem, L["lmax"].at(b, 1))
                    dve.tensor_reduce(c(C_MX), probs3[:, 0:3], AX.X, ALU.max).then_inc(L["lmax"].sem, 1)
                    dve.wait_ge(L["lmax"].sem, L["lmax"].at(b, 2))
                    dve.tensor_scalar(c(C_NMX), c(C_MX), -1.0, None, ALU.mult).then_inc(L["lmax"].sem, 1)
                    dve.wait_ge(L["lexp"].sem, L["lexp"].at(b, 1))
                    dve.reciprocal(c(C_INV), c(C_SUM)).then_inc(L["lsum"].sem, 1)
                    dve.wait_ge(L["lsum"].sem, L["lsum"].at(b, 1))
                    dve.tensor_scalar(probs3[:, 4:7], probs3[:, 4:7], c(C_INV), None, ALU.mult).then_inc(L["lsum"].sem, 1)
                    dve.wait_ge(L["lsum"].sem, L["lsum"].at(b, 2))
                    dve.tensor_tensor(c(C_PMF), probs3[:, 5:6], probs3[:, 6:7], ALU.add).then_inc(L["lsum"].sem, 1)
                    dve.wait_ge(L["lscore"].sem, L["lscore"].at(b, 1))
                    dve.tensor_copy(attn[:, 2, :], pu[:, 64:64 + SLOTS]).then_inc(L["route"].sem, 1)
                    dve.wait_ge(L["route"].sem, L["route"].at(b, 2))
                    dve.tensor_reduce(c(C_AMX), attn[:, 2, :], AX.X, ALU.max).then_inc(L["attn"].sem, 1)
                    dve.wait_ge(L["attn"].sem, L["attn"].at(b, 1))
                    dve.tensor_scalar(c(C_SHIFT), c(C_AMX), -scd, None, ALU.mult).then_inc(L["attn"].sem, 1)
                    for n in range(NA):
                        dve.wait_ge(L["scores"].sem, L["scores"].at(b, n + 1))
                        dve.tensor_reduce(stats[:, 0, n:n + 1], (pb, pc)[n % 2][:, :], AX.X, ALU.max)\
                            .then_inc(L["top"].sem, 1)
                        dve.wait_ge(L["top"].sem, L["top"].at(b, n + 1))
                        dve.tensor_scalar(stats[:, 1, n:n + 1], stats[:, 0, n:n + 1], -sc, None, ALU.mult)\
                            .then_inc(L["shift"].sem, 1)
                        if n % 2 == 1 and n >= 3:
                            differ(dve, b, n // 2 - 1)
                    differ(dve, b, TT - 1)
                    dve.wait_ge(L["aexp"].sem, L["aexp"].at(b, 1))
                    dve.reciprocal(c(C_AINV), c(C_ASUM)).then_inc(L["attn"].sem, 1)
                    dve.wait_ge(L["attn"].sem, L["attn"].at(b, 3))
                    dve.tensor_tensor(attn[:, 1, :], attn[:, 0, :], w("landmarks_t"), ALU.mult).then_inc(L["attn"].sem, 1)
                    dve.wait_ge(L["attn"].sem, L["attn"].at(b, 4))
                    dve.tensor_reduce(c(C_ARC), attn[:, 1, :], AX.X, ALU.add).then_inc(L["attn"].sem, 1)
                    dve.wait_ge(L["attn"].sem, L["attn"].at(b, 5))
                    dve.tensor_scalar(c(C_ARC), c(C_ARC), c(C_AINV), probs3[:, 6:7], ALU.mult, ALU.mult)\
                        .then_inc(L["route"].sem, 1)
                    dve.wait_ge(L["slr"].sem, L["slr"].at(b, 1))
                    dve.wait_ge(L["lsum"].sem, L["lsum"].at(b, 3))
                    dve.scalar_tensor_tensor(out=joined[:, :], in0=pc[:, :], scalar=c(C_PMF), in1=ema[:, :],
                                             op0=ALU.mult, op1=ALU.add).then_inc(L["arc"].sem, 1)
                    dve.wait_ge(L["arc"].sem, L["arc"].at(b, 1))
                    dve.wait_ge(L["route"].sem, L["route"].at(b, 3))
                    dve.tensor_tensor(joined[:, S - 1:S], joined[:, S - 1:S], c(C_ARC), ALU.add).then_inc(L["arc"].sem, 1)
                    rms_vector(dve, b, 1)
                    dve.wait_ge(L["spread"].sem, L["spread"].at(b, 2))
                    dve.wait_ge(L["mix_sb"].sem, L["mix_sb"].at(b, 1))
                    dve.tensor_tensor(joined[:, :], mix[:, :], pa[:, :], ALU.mult).then_inc(L["scaled"].sem, 1)
                    dve.wait_ge(L["scaled"].sem, L["scaled"].at(b, 1))
                    dve.scalar_tensor_tensor(out=result[:, :], in0=joined[:, :], scalar=w("norm_out"), in1=xl[:, :],
                                             op0=ALU.mult, op1=ALU.add).then_inc(L["result"].sem, 1)
                    dve.wait_ge(L["result"].sem, L["result"].at(b, 1))
                    dve.tensor_reduce(c(C_M2), result[:, :], AX.X, ALU.add).then_inc(L["mean"].sem, 1)
                    dve.wait_ge(L["bus_sb"].sem, L["bus_sb"].at(b, 3))
                    dve.scalar_tensor_tensor(out=core.batch(b), in0=result[:, :], scalar=c(C_B2), in1=core.batch(b),
                                             op0=ALU.add, op1=ALU.add).then_inc(L["done"].sem, 1)

            @block.gpsimd
            def _(pool):
                with pool.Fori(0, B) as b:
                    ln_pool(pool, L, b)
                    rms_pool(pool, b, 0)
                    rms_pool(pool, b, 1)
    L.close()


def pair_attention(nc, core, name):
    L = Layer(nc, name, core, ["pairs"], **LN_SIGNALS, prep=6, bdiff=2, expb=1,
              qkv=3,
              soft=3,
              partner=2,
              kv=2,
              sums=4,
              terms=4, joined=2, inverse=1, mixed=1,
              projected=1, done=1)
    with L.ctx:
        g = "pairs"
        xn, q, k, v, q2, k2 = (L.sb(n, [P, S]) for n in ("xn", "q", "k", "v", "q2", "k2"))
        kv, kv2, sa, sbb, sn, sn2 = (L.sb(n, [P, S]) for n in ("kv", "kv2", "sa", "sbb", "sn", "sn2"))
        mixed = L.sb("mixed", [P, S])
        wq, wk = L.sb("wq", [P, D]), L.sb("wk", [P, D])
        col = L.sb("col", [P, 5])
        ps = [L.ps(n, [P, S]) for n in ("ps_q", "ps_k", "ps_v")]
        out = L.ps("out", [P, S])
        ln_buffers(L, L.ps("ln", [P, S])[:, :], L.ps("var", [P, TT])[:, :])
        ones_row = core.w("const", "ones_s")
        with nc.Block() as block:
            @block.tensor
            def _(pe):
                pe.wait_ge(L["prep"].sem, L["prep"].at(0, 6))
                with pe.Fori(0, B) as b:
                    ln_tensor(pe, L, b)
                    pe.wait_ge(L["ln_xn"].sem, L["ln_xn"].at(b, 1))
                    pe.wait_ge(L["soft"].sem, L["soft"].at(b, 0))
                    for i, w in enumerate((wq[:, :], wk[:, :], core.w(g, "wv"))):
                        pe.matmul(ps[i][:, :], w, xn[:, :], start=True, stop=True).then_inc(L["qkv"].sem, 1)
                    pe.wait_ge(L["mixed"].sem, L["mixed"].at(b, 1))
                    pe.matmul(out[:, :], core.w(g, "wo"), mixed[:, :], start=True, stop=True)\
                        .then_inc(L["projected"].sem, 1)

            @block.scalar
            def _(act):
                act.activation(col[:, 2:3], core.w(g, "beta"), ACT.Exp).then_inc(L["expb"].sem, 1)
                act.wait_ge(L["prep"].sem, L["prep"].at(0, 6))
                with act.Fori(0, B) as b:
                    ln_scalar(act, L, b)
                    for i, to in enumerate((q, k)):
                        act.wait_ge(L["qkv"].sem, L["qkv"].at(b, i + 1))
                        act.wait_ge(L["mixed"].sem, L["mixed"].at(b, 0))
                        act.activation(to[:, :], ps[i][:, :], ACT.Sigmoid, bias=col[:, i:i + 1],
                                       scale=col[:, 2:3]).then_inc(L["soft"].sem, 1)
                    act.wait_ge(L["qkv"].sem, L["qkv"].at(b, 3))
                    act.activation(v[:, :], ps[2][:, :], ACT.Identity, bias=core.w(g, "bv")).then_inc(L["soft"].sem, 1)

            @block.vector
            def _(dve):
                for w, to in ((core.w(g, "wq"), wq), (core.w(g, "wk"), wk)):
                    pair = w.rearrange("p (h d) -> p h d", d=2)
                    diff = to[:, :].rearrange("p (h d) -> p h d", d=2)
                    for d in range(2):
                        dve.tensor_tensor(diff[:, :, d], pair[:, :, d], pair[:, :, 1 - d], ALU.subtract)\
                            .then_inc(L["prep"].sem, 1)
                dve.wait_ge(L["expb"].sem, L["expb"].at(0, 1))
                for i, n in enumerate(("bq", "bk")):
                    dve.tensor_tensor(col[:, 3 + i:4 + i], core.w(g, n, 0, 1), core.w(g, n, 1, 2), ALU.subtract)\
                        .then_inc(L["bdiff"].sem, 1)
                    dve.wait_ge(L["bdiff"].sem, L["bdiff"].at(0, i + 1))
                    dve.tensor_tensor(col[:, i:i + 1], col[:, 3 + i:4 + i], col[:, 2:3], ALU.mult).then_inc(L["prep"].sem, 1)
                with dve.Fori(0, B) as b:
                    ln_vector(dve, L, b, xn[:, :])
                    dve.wait_ge(L["soft"].sem, L["soft"].at(b, 2))
                    dve.tensor_scalar(q2[:, :], q[:, :], -1.0, 1.0, ALU.mult, ALU.add).then_inc(L["partner"].sem, 1)
                    dve.tensor_scalar(k2[:, :], k[:, :], -1.0, 1.0, ALU.mult, ALU.add).then_inc(L["partner"].sem, 1)
                    dve.tensor_tensor_scan(sn[:, :], ones_row, k[:, :], 0.0, ALU.mult, ALU.add)\
                        .then_inc(L["sums"].sem, 1)
                    dve.wait_ge(L["soft"].sem, L["soft"].at(b, 3))
                    dve.tensor_tensor(kv[:, :], k[:, :], v[:, :], ALU.mult).then_inc(L["kv"].sem, 1)
                    dve.wait_ge(L["partner"].sem, L["partner"].at(b, 2))
                    dve.tensor_tensor(kv2[:, :], k2[:, :], v[:, :], ALU.mult).then_inc(L["kv"].sem, 1)
                    dve.wait_ge(L["kv"].sem, L["kv"].at(b, 1))
                    dve.tensor_tensor_scan(sa[:, :], ones_row, kv[:, :], 0.0, ALU.mult, ALU.add)\
                        .then_inc(L["sums"].sem, 1)
                    dve.wait_ge(L["kv"].sem, L["kv"].at(b, 2))
                    dve.tensor_tensor_scan(sbb[:, :], ones_row, kv2[:, :], 0.0, ALU.mult, ALU.add)\
                        .then_inc(L["sums"].sem, 1)
                    dve.wait_ge(L["sums"].sem, L["sums"].at(b, 1))
                    dve.tensor_tensor_scan(sn2[:, :], ones_row, k2[:, :], 0.0, ALU.mult, ALU.add)\
                        .then_inc(L["sums"].sem, 1)
                    dve.wait_ge(L["sums"].sem, L["sums"].at(b, 4))
                    for to, a, c in ((kv, q, sa), (kv2, q2, sbb), (k, q, sn), (k2, q2, sn2)):
                        dve.tensor_tensor(to[:, :], a[:, :], c[:, :], ALU.mult).then_inc(L["terms"].sem, 1)
                    dve.wait_ge(L["terms"].sem, L["terms"].at(b, 4))
                    dve.tensor_tensor(sn[:, :], k[:, :], k2[:, :], ALU.add).then_inc(L["joined"].sem, 1)
                    dve.tensor_tensor(sa[:, :], kv[:, :], kv2[:, :], ALU.add).then_inc(L["joined"].sem, 1)
                    dve.wait_ge(L["joined"].sem, L["joined"].at(b, 1))
                    dve.reciprocal(sn2[:, :], sn[:, :]).then_inc(L["inverse"].sem, 1)
                    dve.wait_ge(L["joined"].sem, L["joined"].at(b, 2))
                    dve.wait_ge(L["inverse"].sem, L["inverse"].at(b, 1))
                    dve.tensor_tensor(mixed[:, :], sa[:, :], sn2[:, :], ALU.mult).then_inc(L["mixed"].sem, 1)
                    dve.wait_ge(L["projected"].sem, L["projected"].at(b, 1))
                    dve.scalar_tensor_tensor(out=core.batch(b), in0=out[:, :], scalar=core.w(g, "bo"),
                                             in1=core.batch(b), op0=ALU.add, op1=ALU.add).then_inc(L["done"].sem, 1)

            @block.gpsimd
            def _(pool):
                with pool.Fori(0, B) as b:
                    ln_pool(pool, L, b)
    L.close()



def cell(nc, core, name):
    L = Layer(nc, name, core, ["cell"], **LN_SIGNALS, start=1,
              gates=3,
              opened=3,
              parts=2,
              state=1,
              answer=1,
              answered=1,
              done=1)
    with L.ctx:
        g = "cell"
        xn = L.sb("xn", [P, B * S])
        c, f, i_, n_, ig, h = (L.sb(k, [P, S]) for k in ("c", "f", "i", "n", "ig", "h"))
        ps = [L.ps(n, [P, S]) for n in ("ps_f", "ps_i", "ps_n")]
        out = L.ps("out", [P, S])
        ln_buffers(L, L.ps("ln", [P, S])[:, :], L.ps("var", [P, TT])[:, :])

        def batch_of(t, b):
            return t[:, bass.ds(b * S, S)]

        with nc.Block() as block:
            @block.tensor
            def _(pe):
                with pe.Fori(0, B) as b:
                    ln_tensor(pe, L, b)
                    pe.wait_ge(L["ln_xn"].sem, L["ln_xn"].at(b, 1))
                    pe.wait_ge(L["opened"].sem, L["opened"].at(b, 0))
                    for j, w in enumerate(("wf", "wi", "wc")):
                        pe.matmul(ps[j][:, :], core.w(g, w), batch_of(xn, b), start=True, stop=False)
                    pe.wait_ge(L["state"].sem, L["state"].at(b, 0))
                    pe.wait_ge(L["start"].sem, L["start"].at(0, 1))
                    for j, w in enumerate(("uf", "ui", "uc")):
                        pe.matmul(ps[j][:, :], core.w(g, w), c[:, :], start=False, stop=True)\
                            .then_inc(L["gates"].sem, 1)
                pe.wait_ge(L["state"].sem, L["state"].at(B - 1, 1))
                with pe.Fori(0, B) as b:
                    pe.wait_ge(L["answered"].sem, L["answered"].at(b, 0))
                    pe.matmul(out[:, :], core.w(g, "wo"), batch_of(xn, b), start=True, stop=False)
                    pe.matmul(out[:, :], core.w(g, "uo"), c[:, :], start=False, stop=True)\
                        .then_inc(L["answer"].sem, 1)

            @block.scalar
            def _(act):
                with act.Fori(0, B) as b:
                    ln_scalar(act, L, b)
                    act.wait_ge(L["state"].sem, L["state"].at(b, 0))
                    for j, (to, fn, bias) in enumerate(((f, ACT.Sigmoid, "bf"), (i_, ACT.Sigmoid, "bi"),
                                                        (n_, ACT.Tanh, "bc"))):
                        act.wait_ge(L["gates"].sem, L["gates"].at(b, j + 1))
                        act.activation(to[:, :], ps[j][:, :], fn, bias=core.w(g, bias)).then_inc(L["opened"].sem, 1)
                with act.Fori(0, B) as b:
                    act.wait_ge(L["answer"].sem, L["answer"].at(b, 1))
                    act.wait_ge(L["done"].sem, L["done"].at(b, 0))
                    act.activation(h[:, :], out[:, :], ACT.Tanh, bias=core.w(g, "bo")).then_inc(L["answered"].sem, 1)

            @block.vector
            def _(dve):
                dve.tensor_copy(c[:, :], core.w(g, "in_c").to_broadcast([P, S])).then_inc(L["start"].sem, 1)
                dve.wait_ge(L["start"].sem, L["start"].at(0, 1))
                with dve.Fori(0, B) as b:
                    ln_vector(dve, L, b, batch_of(xn, b))
                    dve.wait_ge(L["opened"].sem, L["opened"].at(b, 3))
                    dve.tensor_tensor(ig[:, :], i_[:, :], n_[:, :], ALU.mult).then_inc(L["parts"].sem, 1)
                    dve.tensor_tensor(h[:, :], f[:, :], c[:, :], ALU.mult).then_inc(L["parts"].sem, 1)
                    dve.wait_ge(L["parts"].sem, L["parts"].at(b, 2))
                    dve.tensor_tensor(c[:, :], ig[:, :], h[:, :], ALU.add).then_inc(L["state"].sem, 1)
                with dve.Fori(0, B) as b:
                    dve.wait_ge(L["answered"].sem, L["answered"].at(b, 1))
                    dve.tensor_tensor(core.batch(b), h[:, :], core.batch(b), ALU.add).then_inc(L["done"].sem, 1)

            @block.gpsimd
            def _(pool):
                with pool.Fori(0, B) as b:
                    ln_pool(pool, L, b)
    L.close()

DI, NS, CONV, RANK = 256, 16, 4, 64
CT = DI // P


def state_space(nc, core, name, g):
    ST = NS * CT
    L = Layer(nc, name, core, [g], **LN_SIGNALS, consts=1, history=1, a_exp=1, a_neg=1,
              xz=2 * CT,
              padded=CT,
              zs=CT,
              tap=CT * CONV,
              u=CT,
              low=1,
              low_sb=1, split=5,
              pre=CT,
              soft=3 * CT,
              delta=CT,
              soft_pos=CT,
              du=CT,
              rows=2 * NS,
              bsb=NS,
              decay=ST,
              drive=ST,
              state=ST,
              read=ST,
              summed=ST,
              skip=CT, gated=CT, projected=1, done=1)
    with L.ctx:
        xn = L.sb("xn", [P, S])
        padded = L.sb("padded", [P, CT, CONV - 1 + S])
        zs, u, delta, du = (L.sb(n, [P, CT, S]) for n in ("zs", "u", "delta", "du"))
        conv = L.sb("conv", [P, CT, S])
        low = L.sb("low", [RANK, S])
        rest = L.sb("rest", [2 * NS, 2, S])
        mid = L.sb("mid", [2 * NS, S], BF16)
        parts = L.sb("parts", [3 * 2 * NS, S], BF16)
        spread16 = L.sb("spread16", [3 * 2 * NS, 2 * NS, P], BF16)
        a = L.sb("a", [P, CT, NS])
        bsb = L.sb("bsb", [P, 2, S])
        drive, state, read = (L.sb(n, [P, 2, S]) for n in ("drive", "state", "read"))
        y = L.sb("y", [P, CT, S])
        pd = L.ps("pd", [P, 2, S])
        pb = L.ps("pb", [P, S])
        pc = L.ps("pc", [P, S])
        py = L.ps("py", [P, CT, S])
        bank, out = L.ps("bank", [P, S]), L.ps("out", [P, S])
        ln_buffers(L, bank[:, :], out[:, 0:TT])
        eye = core.w("const", "eye")

        def add_up(pe, b, n):
            for t in range(CT):
                s = n * CT + t
                pe.wait_ge(L["read"].sem, L["read"].at(b, s + 1))
                if n == 0:
                    pe.wait_ge(L["zs"].sem, L["zs"].at(b, t + 1))
                pe.matmul(py[:, t, :], eye, read[:, s % 2, :], start=n == 0, stop=n == NS - 1)\
                    .then_inc(L["summed"].sem, 1)

        def read_out(dve, b, s):
            dve.wait_ge(L["state"].sem, L["state"].at(b, s + 1))
            dve.wait_ge(L["rows"].sem, L["rows"].at(b, 2 * (s // CT) + 2))
            dve.wait_ge(L["summed"].sem, L["summed"].at(b, max(s - 1, 0)))
            dve.tensor_tensor(read[:, s % 2, :], state[:, s % 2, :], pc[:, :], ALU.mult).then_inc(L["read"].sem, 1)

        with nc.Block() as block:
            @block.tensor
            def _(pe):
                pe.wait_ge(L["consts"].sem, L["consts"].at(0, 1))
                with pe.Fori(0, B) as b:
                    pe.wait_ge(L["done"].sem, L["done"].at(b, 0))
                    ln_tensor(pe, L, b)
                    pe.wait_ge(L["ln_xn"].sem, L["ln_xn"].at(b, 1))
                    pe.wait_ge(L["state"].sem, L["state"].at(b, 0))
                    for t in range(CT):
                        pe.matmul(pd[:, t, :], core.w(g, "w_in", t * P, (t + 1) * P), xn[:, :],
                                  start=True, stop=True).then_inc(L["xz"].sem, 1)
                    pe.wait_ge(L["gated"].sem, L["gated"].at(b, 0))
                    for t in range(CT):
                        pe.matmul(py[:, t, :], core.w(g, "w_in", DI + t * P, DI + (t + 1) * P), xn[:, :],
                                  start=True, stop=True).then_inc(L["xz"].sem, 1)
                    pe.wait_ge(L["u"].sem, L["u"].at(b, CT))
                    for t in range(CT):
                        pe.matmul(bank[0:RANK, :], core.w(g, "w_low", t * RANK, (t + 1) * RANK), u[:, t, :],
                                  start=t == 0, stop=t == CT - 1)
                    for t in range(CT):
                        mm = pe.matmul(out[0:2 * NS, :], core.w(g, "w_bc", t * 2 * NS, (t + 1) * 2 * NS), u[:, t, :],
                                       start=t == 0, stop=t == CT - 1)
                    mm.then_inc(L["low"].sem, 1)
                    pe.wait_ge(L["low_sb"].sem, L["low_sb"].at(b, 1))
                    for t in range(CT):
                        pe.matmul(pd[:, t, :], core.w(g, "w_dt", t * P, (t + 1) * P), low[:, :],
                                  start=True, stop=True).then_inc(L["pre"].sem, 1)
                    pe.wait_ge(L["split"].sem, L["split"].at(b, 5))
                    for n in range(NS):
                        pe.wait_ge(L["bsb"].sem, L["bsb"].at(b, n))
                        pe.matmul(pb[:, :], spread16[:, n, :], parts[:, :], start=True, stop=True)\
                            .then_inc(L["rows"].sem, 1)
                        pe.wait_ge(L["read"].sem, L["read"].at(b, n * CT))
                        pe.matmul(pc[:, :], spread16[:, NS + n, :], parts[:, :], start=True, stop=True)\
                            .then_inc(L["rows"].sem, 1)
                        if n >= 1:
                            add_up(pe, b, n - 1)
                    add_up(pe, b, NS - 1)
                    pe.wait_ge(L["gated"].sem, L["gated"].at(b, CT))
                    for t in range(CT):
                        mm = pe.matmul(out[:, :], core.w(g, "w_out", t * P, (t + 1) * P), y[:, t, :],
                                       start=t == 0, stop=t == CT - 1)
                    mm.then_inc(L["projected"].sem, 1)

            @block.scalar
            def _(act):
                act.activation(a[:, :, :], core.w(g, "a_log").rearrange("p (t n) -> p t n", t=CT), ACT.Exp)\
                    .then_inc(L["a_exp"].sem, 1)
                act.wait_ge(L["a_neg"].sem, L["a_neg"].at(0, 1))
                with act.Fori(0, B) as b:
                    ln_scalar(act, L, b)
                    for t in range(CT):
                        act.wait_ge(L["xz"].sem, L["xz"].at(b, t + 1))
                        act.wait_ge(L["tap"].sem, L["tap"].at(b, 0))
                        act.activation(padded[:, t, CONV - 1:], pd[:, t, :], ACT.Copy).then_inc(L["padded"].sem, 1)
                    for t in range(CT):
                        act.wait_ge(L["xz"].sem, L["xz"].at(b, CT + t + 1))
                        act.wait_ge(L["gated"].sem, L["gated"].at(b, 0))
                        act.activation(zs[:, t, :], py[:, t, :], ACT.Silu).then_inc(L["zs"].sem, 1)
                    for t in range(CT):
                        act.wait_ge(L["tap"].sem, L["tap"].at(b, CONV * (t + 1)))
                        act.activation(u[:, t, :], conv[:, t, :], ACT.Silu, bias=core.w(g, "conv_b", t, t + 1))\
                            .then_inc(L["u"].sem, 1)
                    act.wait_ge(L["low"].sem, L["low"].at(b, 1))
                    act.activation(low[:, :], bank[0:RANK, :], ACT.Copy).then_inc(L["low_sb"].sem, 1)
                    for t in range(CT):
                        act.wait_ge(L["pre"].sem, L["pre"].at(b, t + 1))
                        act.wait_ge(L["tap"].sem, L["tap"].at(b, CONV * CT))
                        act.activation(delta[:, t, :], pd[:, t, :], ACT.Abs, bias=core.w(g, "dt_b", t, t + 1))\
                            .then_inc(L["soft"].sem, 1)
                    for t in range(CT):
                        act.wait_ge(L["soft"].sem, L["soft"].at(b, t + 1))
                        act.activation(delta[:, t, :], delta[:, t, :], ACT.Exp, scale=-1.0).then_inc(L["soft"].sem, 1)
                    for t in range(CT):
                        act.wait_ge(L["soft"].sem, L["soft"].at(b, CT + t + 1))
                        act.activation(delta[:, t, :], delta[:, t, :], ACT.Ln, bias=1.0).then_inc(L["soft"].sem, 1)
                    act.wait_ge(L["du"].sem, L["du"].at(b, CT))
                    for n in range(NS):
                        act.wait_ge(L["rows"].sem, L["rows"].at(b, 2 * n + 1))
                        act.wait_ge(L["drive"].sem, L["drive"].at(b, CT * max(n - 1, 0)))
                        act.activation(bsb[:, n % 2, :], pb[:, :], ACT.Copy).then_inc(L["bsb"].sem, 1)
                        for t in range(CT):
                            act.wait_ge(L["state"].sem, L["state"].at(b, CT * max(n - 1, 0) + (t if n >= 1 else 0)))
                            if n >= 1:
                                act.wait_ge(L["state"].sem, L["state"].at(b, CT * (n - 1) + t + 1))
                            act.activation(pd[:, t, :], delta[:, t, :], ACT.Exp, scale=a[:, t, n:n + 1])\
                                .then_inc(L["decay"].sem, 1)

            @block.vector
            def _(dve):
                dve.memset(padded[:, :, 0:CONV - 1], 0.0).then_inc(L["history"].sem, 1)
                dve.wait_ge(L["history"].sem, L["history"].at(0, 1))
                dve.wait_ge(L["a_exp"].sem, L["a_exp"].at(0, 1))
                dve.tensor_scalar(a[:, :, :], a[:, :, :], -1.0, None, ALU.mult).then_inc(L["a_neg"].sem, 1)
                with dve.Fori(0, B) as b:
                    ln_vector(dve, L, b, xn[:, :])
                    for t in range(CT):
                        dve.wait_ge(L["padded"].sem, L["padded"].at(b, t + 1))
                        for i in range(CONV):
                            tap = core.w(g, "conv_w", t * CONV + i, t * CONV + i + 1)
                            src = padded[:, t, i:i + S]
                            if i == 0:
                                dve.tensor_scalar(conv[:, t, :], src, tap, None, ALU.mult).then_inc(L["tap"].sem, 1)
                            else:
                                dve.wait_ge(L["tap"].sem, L["tap"].at(b, t * CONV + i))
                                dve.scalar_tensor_tensor(out=conv[:, t, :], in0=src, scalar=tap, in1=conv[:, t, :],
                                                         op0=ALU.mult, op1=ALU.add).then_inc(L["tap"].sem, 1)
                    dve.wait_ge(L["low"].sem, L["low"].at(b, 1))
                    R = 2 * NS
                    dve.tensor_copy(parts[0:R, :], out[0:R, :]).then_inc(L["split"].sem, 1)
                    dve.wait_ge(L["split"].sem, L["split"].at(b, 1))
                    dve.tensor_tensor(rest[:, 0, :], out[0:R, :], parts[0:R, :], ALU.subtract).then_inc(L["split"].sem, 1)
                    dve.wait_ge(L["split"].sem, L["split"].at(b, 2))
                    dve.tensor_copy(parts[R:2 * R, :], rest[:, 0, :]).then_inc(L["split"].sem, 1)
                    dve.tensor_copy(mid[:, :], rest[:, 0, :]).then_inc(L["split"].sem, 1)
                    dve.wait_ge(L["split"].sem, L["split"].at(b, 4))
                    dve.tensor_tensor(parts[2 * R:3 * R, :], rest[:, 0, :], mid[:, :], ALU.subtract)\
                        .then_inc(L["split"].sem, 1)
                    for t in range(CT):
                        dve.wait_ge(L["soft"].sem, L["soft"].at(b, CT))
                        dve.wait_ge(L["u"].sem, L["u"].at(b, CT))
                        dve.tensor_scalar(conv[:, t, :], pd[:, t, :], core.w(g, "dt_b", t, t + 1), 0.0,
                                          ALU.add, ALU.max).then_inc(L["soft_pos"].sem, 1)
                    for t in range(CT):
                        dve.wait_ge(L["soft"].sem, L["soft"].at(b, 2 * CT + t + 1))
                        dve.wait_ge(L["soft_pos"].sem, L["soft_pos"].at(b, t + 1))
                        dve.tensor_tensor(delta[:, t, :], delta[:, t, :], conv[:, t, :], ALU.add)\
                            .then_inc(L["delta"].sem, 1)
                    for t in range(CT):
                        dve.wait_ge(L["delta"].sem, L["delta"].at(b, t + 1))
                        dve.wait_ge(L["drive"].sem, L["drive"].at(b, 0))
                        dve.tensor_tensor(du[:, t, :], delta[:, t, :], u[:, t, :], ALU.mult).then_inc(L["du"].sem, 1)
                    for s in range(ST):
                        n, t = divmod(s, CT)
                        dve.wait_ge(L["decay"].sem, L["decay"].at(b, s + 1))
                        dve.wait_ge(L["drive"].sem, L["drive"].at(b, s + 1))
                        dve.wait_ge(L["read"].sem, L["read"].at(b, max(s - 1, 0)))
                        dve.tensor_tensor_scan(state[:, s % 2, :], pd[:, t, :], drive[:, s % 2, :], 0.0,
                                               ALU.mult, ALU.add).then_inc(L["state"].sem, 1)
                        if s >= 1:
                            read_out(dve, b, s - 1)
                    read_out(dve, b, ST - 1)
                    for t in range(CT):
                        dve.wait_ge(L["summed"].sem, L["summed"].at(b, ST - CT + t + 1))
                        dve.wait_ge(L["projected"].sem, L["projected"].at(b, 0))
                        dve.scalar_tensor_tensor(out=conv[:, t, :], in0=u[:, t, :], scalar=core.w(g, "skip", t, t + 1),
                                                 in1=py[:, t, :], op0=ALU.mult, op1=ALU.add).then_inc(L["skip"].sem, 1)
                    for t in range(CT):
                        dve.wait_ge(L["skip"].sem, L["skip"].at(b, t + 1))
                        dve.tensor_tensor(y[:, t, :], conv[:, t, :], zs[:, t, :], ALU.mult).then_inc(L["gated"].sem, 1)
                    dve.wait_ge(L["projected"].sem, L["projected"].at(b, 1))
                    dve.tensor_tensor(core.batch(b), out[:, :], core.batch(b), ALU.add).then_inc(L["done"].sem, 1)

            @block.gpsimd
            def _(pool):
                pool.tensor_copy(spread16[:, :, :], core.w("const", "spread").unsqueeze(2)
                                 .to_broadcast([3 * 2 * NS, 2 * NS, P])).then_inc(L["consts"].sem, 1)
                with pool.Fori(0, B) as b:
                    ln_pool(pool, L, b)
                    pool.wait_ge(L["du"].sem, L["du"].at(b, CT))
                    for s in range(ST):
                        n, t = divmod(s, CT)
                        pool.wait_ge(L["bsb"].sem, L["bsb"].at(b, n + 1))
                        pool.wait_ge(L["state"].sem, L["state"].at(b, max(s - 1, 0)))
                        pool.tensor_tensor(drive[:, s % 2, :], du[:, t, :], bsb[:, n % 2, :], ALU.mult)\
                            .then_inc(L["drive"].sem, 1)
    L.close()

EH, EHD = 16, 8
EW = EHD + 1
VARIANTS = 4


def elu_attention(nc, core, name):
    NSTEP = EH
    L = Layer(nc, name, core, ["elu"], **LN_SIGNALS, start=1,
              proj=2, below=2, above=2, expo=2, feats=2, variant=VARIANTS,
              vk=TT, vk_sb=TT, kturn=1, ktok=1,
              states=TT - 1, states_sb=TT - 1,
              energy=NSTEP, masked=NSTEP, mixed=1, norm=3, outs=2, turned=1, outs_sb=1, projected=1, done=1)
    with L.ctx:
        g = "elu"
        w = lambda n, *a: core.w(g, n, *a)
        xn = L.sb("xn", [P, S])
        low, high, feats = (L.sb(n, [P, 2, S]) for n in ("low", "high", "feats"))
        kvar = L.sb("kvar", [P, VARIANTS, S])
        vaug = L.sb("vaug", [P, TT, EH, EW])
        ktok = L.sb("ktok", [P, TT, P])
        state = L.sb("state", [P, TT - 1, EH * EW])
        energy = L.sb("energy", [P, NSTEP, S])
        den = L.sb("den", [P, TT, EH])
        outs = L.sb("outs", [P, TT, D])
        outs_t = L.sb("outs_t", [P, S])
        bank, small = L.ps("bank", [P, S]), L.ps("small", [P, S])
        pe4 = L.ps("pe4", [P, 4, S])
        pmix = L.ps("pmix", [P, 2, S])
        ln_buffers(L, bank[:, :], small[:, 0:TT])
        eye = core.w("const", "eye")

        def mix_at(t):
            return pmix[:, t // 2, (t % 2) * EH * EW:(t % 2 + 1) * EH * EW]

        with nc.Block() as block:
            @block.tensor
            def _(pe):
                pe.wait_ge(L["start"].sem, L["start"].at(0, 1))
                with pe.Fori(0, B) as b:
                    pe.wait_ge(L["done"].sem, L["done"].at(b, 0))
                    ln_tensor(pe, L, b)
                    pe.wait_ge(L["ln_xn"].sem, L["ln_xn"].at(b, 1))
                    pe.wait_ge(L["masked"].sem, L["masked"].at(b, 0))
                    for i, n in enumerate(("wq", "wk")):
                        pe.matmul(pe4[:, i, :], w(n), xn[:, :], start=True, stop=True).then_inc(L["proj"].sem, 1)
                    for t in range(TT):
                        pe.matmul(small[:, t * P:(t + 1) * P], xn[:, t * P:(t + 1) * P], w("wv"),
                                  start=True, stop=True).then_inc(L["vk"].sem, 1)
                    pe.wait_ge(L["feats"].sem, L["feats"].at(b, 2))
                    for t in range(TT):
                        mm = pe.transpose(bank[:, t * P:(t + 1) * P], feats[:, 1, t * P:(t + 1) * P], eye)
                    mm.then_inc(L["kturn"].sem, 1)
                    pe.wait_ge(L["vk_sb"].sem, L["vk_sb"].at(b, TT))
                    pe.wait_ge(L["ktok"].sem, L["ktok"].at(b, 1))
                    for t in range(1, TT):
                        at = (t - 1) * EH * EW
                        for o in range(t):
                            mm = pe.matmul(small[:, at:at + EH * EW], ktok[:, o, :],
                                           vaug[:, o, :, :].rearrange("p h e -> p (h e)"),
                                           start=o == 0, stop=o == t - 1)
                        mm.then_inc(L["states"].sem, 1)
                    for s in range(NSTEP):
                        j, r = divmod(s, 4)
                        rows = slice(32 * r, 32 * r + 32)
                        pe.wait_ge(L["variant"].sem, L["variant"].at(b, j + 1))
                        if s >= 4:
                            pe.wait_ge(L["masked"].sem, L["masked"].at(b, s - 3))
                        for t in range(TT):
                            tk = slice(t * P, (t + 1) * P)
                            mm = pe.matmul(pe4[:, r, tk], kvar[rows, j, tk], feats[rows, 0, tk], start=True, stop=True)
                        mm.then_inc(L["energy"].sem, 1)
                    pe.wait_ge(L["outs"].sem, L["outs"].at(b, 0))
                    pe.wait_ge(L["states_sb"].sem, L["states_sb"].at(b, TT - 1))
                    pe.wait_ge(L["masked"].sem, L["masked"].at(b, NSTEP))
                    for t in range(TT):
                        if t:
                            pe.matmul(mix_at(t), feats[:, 0, t * P:(t + 1) * P], state[:, t - 1, :],
                                      start=True, stop=True, skip_group_check=True)
                        for s in range(NSTEP):
                            h = 4 * (s % 4) + s // 4
                            mm = pe.matmul(mix_at(t)[:, h * EW:(h + 1) * EW], energy[:, s, t * P:(t + 1) * P],
                                           vaug[:, t, h, :], start=t == 0, stop=True,
                                           skip_group_check=t > 0)
                    mm.then_inc(L["mixed"].sem, 1)
                    pe.wait_ge(L["outs"].sem, L["outs"].at(b, 2))
                    for t in range(TT):
                        mm = pe.transpose(bank[:, t * P:(t + 1) * P], outs[:, t, :], eye)
                    mm.then_inc(L["turned"].sem, 1)
                    pe.wait_ge(L["outs_sb"].sem, L["outs_sb"].at(b, 1))
                    pe.matmul(small[:, :], w("wo"), outs_t[:, :], start=True, stop=True).then_inc(L["projected"].sem, 1)

            @block.scalar
            def _(act):
                with act.Fori(0, B) as b:
                    ln_scalar(act, L, b)
                    for i in range(2):
                        act.wait_ge(L["below"].sem, L["below"].at(b, i + 1))
                        act.activation(low[:, i, :], low[:, i, :], ACT.Exp).then_inc(L["expo"].sem, 1)
                    act.wait_ge(L["kturn"].sem, L["kturn"].at(b, 1))
                    act.activation(ktok[:, :, :], bank[:, :].rearrange("p (t c) -> p t c", t=TT), ACT.Copy)\
                        .then_inc(L["ktok"].sem, 1)
                    act.wait_ge(L["turned"].sem, L["turned"].at(b, 1))
                    act.activation(outs_t[:, :], bank[:, :], ACT.Copy).then_inc(L["outs_sb"].sem, 1)

            @block.vector
            def _(dve):
                dve.memset(vaug[:, :, :, :], 1.0).then_inc(L["start"].sem, 1)
                dve.wait_ge(L["start"].sem, L["start"].at(0, 1))
                with dve.Fori(0, B) as b:
                    ln_vector(dve, L, b, xn[:, :])
                    dve.wait_ge(L["mixed"].sem, L["mixed"].at(b, 0))
                    for i in range(2):
                        dve.wait_ge(L["proj"].sem, L["proj"].at(b, i + 1))
                        bias = w(("bq", "bk")[i])
                        dve.tensor_scalar(low[:, i, :], pe4[:, i, :], bias, 0.0, ALU.add, ALU.min)\
                            .then_inc(L["below"].sem, 1)
                        dve.tensor_scalar(high[:, i, :], pe4[:, i, :], bias, 0.0, ALU.add, ALU.max)\
                            .then_inc(L["above"].sem, 1)
                    for t in range(TT):
                        dve.wait_ge(L["vk"].sem, L["vk"].at(b, TT))
                        dve.tensor_tensor(vaug[:, t, :, 0:EHD],
                                          small[:, t * P:(t + 1) * P].rearrange("p (h e) -> p h e", h=EH),
                                          w("bv").rearrange("p (h e) -> p h e", h=EH), ALU.add).then_inc(L["vk_sb"].sem, 1)
                    for i in range(2):
                        dve.wait_ge(L["expo"].sem, L["expo"].at(b, i + 1))
                        dve.wait_ge(L["above"].sem, L["above"].at(b, i + 1))
                        dve.tensor_tensor(feats[:, i, :], low[:, i, :], high[:, i, :], ALU.add).then_inc(L["feats"].sem, 1)
                    dve.wait_ge(L["feats"].sem, L["feats"].at(b, 2))
                    for j in range(VARIANTS):
                        dve.tensor_scalar(kvar[:, j, :], feats[:, 1, :], core.w("const", "variant", j, j + 1), None,
                                          ALU.mult).then_inc(L["variant"].sem, 1)
                    for t in range(1, TT):
                        dve.wait_ge(L["states"].sem, L["states"].at(b, TT - 1))
                        at = (t - 1) * EH * EW
                        dve.tensor_tensor(state[:, t - 1, :], small[:, at:at + EH * EW], core.w("const", "block16"),
                                          ALU.mult).then_inc(L["states_sb"].sem, 1)
                    for s in range(NSTEP):
                        dve.wait_ge(L["energy"].sem, L["energy"].at(b, s + 1))
                        dve.tensor_tensor(energy[:, s, :].rearrange("p (t c) -> p t c", t=TT),
                                          pe4[:, s % 4, :].rearrange("p (t c) -> p t c", t=TT),
                                          core.w("const", "upper").unsqueeze(1).to_broadcast([P, TT, P]), ALU.mult)\
                            .then_inc(L["masked"].sem, 1)
                    dve.wait_ge(L["mixed"].sem, L["mixed"].at(b, 1))
                    for i in range(2):
                        mix = pmix[:, i, 0:2 * EH * EW].rearrange("p (t h e) -> p t h e", t=2, h=EH)
                        dve.tensor_scalar(den[:, 2 * i:2 * i + 2, :], mix[:, :, :, EHD], 1e-6, None, ALU.add)\
                            .then_inc(L["norm"].sem, 1)
                    dve.wait_ge(L["norm"].sem, L["norm"].at(b, 2))
                    dve.reciprocal(den[:, :, :], den[:, :, :]).then_inc(L["norm"].sem, 1)
                    dve.wait_ge(L["norm"].sem, L["norm"].at(b, 3))
                    for i in range(2):
                        mix = pmix[:, i, 0:2 * EH * EW].rearrange("p (t h e) -> p t h e", t=2, h=EH)
                        for t in range(2):
                            ins = dve.tensor_tensor(
                                outs[:, 2 * i + t, :].rearrange("p (h e) -> p h e", h=EH), mix[:, t, :, 0:EHD],
                                den[:, 2 * i + t, :].unsqueeze(2).to_broadcast([P, EH, EHD]), ALU.mult)
                        ins.then_inc(L["outs"].sem, 1)
                    dve.wait_ge(L["projected"].sem, L["projected"].at(b, 1))
                    dve.scalar_tensor_tensor(out=core.batch(b), in0=small[:, :], scalar=w("bo"), in1=core.batch(b),
                                             op0=ALU.add, op1=ALU.add).then_inc(L["done"].sem, 1)

            @block.gpsimd
            def _(pool):
                with pool.Fori(0, B) as b:
                    ln_pool(pool, L, b)
    L.close()

GROUPS_OF = {0: ["mha"], 1: ["moe"], 2: ["keep"], 3: ["moe"], 4: ["light"], 5: ["bitffn"], 6: ["slr"], 7: ["bitffn"],
             8: ["pairs"], 9: ["gated"], 10: ["ssm2"], 11: ["gated"], 12: ["elu"], 13: ["cell"], 14: ["ssm3"],
             15: ["cell"]}


def run_layer(nc, core, i):
    if i == 2:
        keep_attention(nc, core, "l2")
    if i == 6:
        landmark_layer(nc, core, "l6")
    if i == 4:
        linear_attention(nc, core, "l4")
    if i == 12:
        elu_attention(nc, core, "l12")
    if i == 0:
        query_softmax_attention(nc, core, "l0")
    if i == 10:
        state_space(nc, core, "l10", "ssm2")
    if i == 14:
        state_space(nc, core, "l14", "ssm3")
    if i in (1, 3):
        routed_ffn(nc, core, f"l{i}", "moe", 16, 8, 1, False)
    if i in (9, 11):
        routed_ffn(nc, core, f"l{i}", "gated", 8, 11, 2, True)
    if i == 8:
        pair_attention(nc, core, f"l{i}")
    if i in (13, 15):
        cell(nc, core, f"l{i}")
    if i in (5, 7):
        bit_ffn(nc, core, f"l{i}")


def build_program(nc, x_in, groups_in, out, columns):
    order = ["const"] + [g for i in PLAN for g in GROUPS_OF[i]]
    order = list(dict.fromkeys(order))
    with ExitStack() as ctx:
        x = ctx.enter_context(nc.sbuf_tensor("x", [P, B * S], F32))
        weights = {g: ctx.enter_context(nc.sbuf_tensor(f"w_{g}", list(groups_in[g].shape), F32)) for g in order}
        landed = {g: ctx.enter_context(nc.semaphore(f"landed_{g}")) for g in order}
        landed["x"] = ctx.enter_context(nc.semaphore("landed_x"))
        stored = ctx.enter_context(nc.semaphore("stored"))
        core = Core(x, weights, landed, columns)
        with nc.Block() as block:
            @block.sync
            def _(sync):
                sync.dma_start(x[:, :], x_in).then_inc(landed["x"], 16)
                for g in order:
                    sync.dma_start(weights[g][:, :], groups_in[g]).then_inc(landed[g], 16)
                sync.wait_ge(landed["x"], 16)
                sync.wait_ge(landed["const"], 16)
        if 5 in PLAN or 7 in PLAN:
            quantise(nc, core)
        for i in PLAN:
            run_layer(nc, core, i)
        with nc.Block() as block:
            @block.sync
            def _(sync):
                sync.dma_start(out, x[:, :]).then_inc(stored, 16)
                sync.wait_ge(stored, 16)



def constants():
    eye = np.eye(P, dtype=np.float32)
    row = np.arange(P)
    spot = lambda at: (row % 32 == at).astype(np.float32)
    mask_rows = np.zeros((P, KJ, P), np.float32)
    for r in row[row % 32 < B * KJ]:
        mask_rows[r, r % KJ, r // 32 * 32] = 1
    return {
        "ones": np.ones((P, P), np.float32),
        "centre": eye - np.float32(1 / D),
        "mean": np.full((P, P), 1 / D, np.float32),
        "eye": eye,
        "falling": rows_of(np.tile(np.arange(16, 0, -1, dtype=np.float32), TT)),
        "falling8": rows_of(np.tile(np.arange(8, 0, -1, dtype=np.float32), TT)),
        "ones_s": np.ones((P, S), np.float32),
        "spread": np.tile(np.eye(2 * NS, dtype=np.float32), (3, 1)),
        "upper": np.triu(np.ones((P, P), np.float32)),
        "token": rows_of(np.arange(S, dtype=np.float32)),
        "block4": np.kron(np.eye(HG), np.ones((32, LHD))).astype(np.float32),
        "block16": np.kron(np.eye(EH), np.ones((EHD, EW))).astype(np.float32),
        "variant": np.stack([(np.arange(P) // EHD % 4 == j) for j in range(VARIANTS)], 1).astype(np.float32),
        "later": np.triu(np.full((P, P), NEG, np.float32), 1),
        "units32": rows_of(np.eye(B * KJ, 32, dtype=np.float32)),
        "batch_rows": np.stack([((row % 32) // KJ == b) for b in range(B)], 1).astype(np.float32),
        "mask_rows": mask_rows.reshape(P, KJ * P),
        "q_ones": columns_of(spot(0)),
        "k_ones": columns_of(spot(SHIFT_ROW)),
        "v_ones": rows_of((np.arange(KH * 32) % 32 == KHD).astype(np.float32)),
        "minus_half": np.full((P, TT), -0.5, np.float32),
    }


def columns_of(v, width=P):
    return np.asarray(v).reshape(-1, width).T


def row_blocks(m, width=P):
    m = np.asarray(m)
    t = m.shape[0] // width
    return m.reshape(t, width, m.shape[1]).transpose(1, 0, 2).reshape(width, -1)


def rows_of(v):
    return np.broadcast_to(np.asarray(v).reshape(1, -1), (P, np.asarray(v).size))


def side_by_side(m):
    return np.asarray(m).transpose(1, 0, 2).reshape(m.shape[1], -1)


def pick(experts, hidden):
    return np.tile(np.repeat(np.eye(experts, dtype=np.float32), hidden, axis=1), (3, 1))


def in_row_groups(m, first):
    out = np.zeros((D, KH, 32), np.float32)
    out[:, :, first:first + KHD] = m.reshape(D, KH, KHD)
    return out.reshape(D, KH * 32)


def lay_out(v):
    g = {"const": constants()}
    g["moe"] = {"wr": v["L0_ffn_Wr"],
                "w1": np.concatenate([side_by_side(v["L0_ffn_Wg"]), v["L0_ffn_Sg"]], 1),
                "w3": np.concatenate([side_by_side(v["L0_ffn_Wu"]), v["L0_ffn_Su"]], 1),
                "w2": row_blocks(np.concatenate([v["L0_ffn_Wd"].reshape(-1, D), v["L0_ffn_Sd"]])),
                "pick": pick(16, 64)}
    hid = 8 * 176 + 176
    pad = np.zeros((-hid % P, D), np.float32)
    g["gated"] = {"wr": v["L2_ffn_gate_w"].T,
                  "w1": np.concatenate([side_by_side(v["L2_ffn_w1"]), v["L2_ffn_sw1"]], 1),
                  "w3": np.concatenate([side_by_side(v["L2_ffn_w3"]), v["L2_ffn_sw3"]], 1),
                  "w2": row_blocks(np.concatenate([v["L2_ffn_w2"].reshape(-1, D), v["L2_ffn_sw2"], pad])),
                  "b1": columns_of(np.concatenate([v["L2_ffn_b1"].ravel(), v["L2_ffn_sb1"], pad[:, 0]])),
                  "b3": columns_of(np.concatenate([v["L2_ffn_b3"].ravel(), v["L2_ffn_sb3"], pad[:, 0]])),
                  "b2": v["L2_ffn_b2"], "sb2": columns_of(v["L2_ffn_sb2"]),
                  "gate_b": rows_of(np.tile(v["L2_ffn_gate_b"], TT)),
                  "pick": pick(8, 176)}
    swap = np.arange(D) ^ 1
    p = "L2_attn_a_"
    g["pairs"] = {"wq": v[p + "Wq"].T, "wk": v[p + "Wk"].T, "wv": v[p + "Wv"].T, "wo": v[p + "Wo"].T,
                  "bq": np.stack([v[p + "bq"], v[p + "bq"][swap]], 1),
                  "bk": np.stack([v[p + "bk"], v[p + "bk"][swap]], 1),
                  "bv": columns_of(v[p + "bv"]), "bo": columns_of(v[p + "bo"]), "beta": rows_of(v[p + "beta"])}
    p = "L0_attn_a_"
    g["mha"] = {"wq": v[p + "q_w"].reshape(-1, D).T, "wk": v[p + "k_w"].reshape(-1, D).T,
                "wv": v[p + "v_w"].reshape(-1, D).T, "wl": row_blocks(v[p + "l_w"].T),
                "bq": columns_of(v[p + "q_b"]), "bk": columns_of(v[p + "k_b"]), "bv": rows_of(v[p + "v_b"]),
                "bl": columns_of(v[p + "l_b"])}
    p = "L2_attn_b_"
    low = v[p + "x_proj_w"].T
    g["ssm2"] = {"w_in": v[p + "in_proj_w"].T, "w_low": row_blocks(low[:, :RANK]), "w_bc": row_blocks(low[:, RANK:]),
                 "w_dt": v[p + "dt_proj_w"].T, "w_out": row_blocks(v[p + "out_proj_w"].T),
                 "conv_w": row_blocks(v[p + "conv_w"]), "conv_b": columns_of(v[p + "conv_b"]),
                 "dt_b": columns_of(v[p + "dt_proj_b"]), "a_log": row_blocks(v[p + "A_log"]),
                 "skip": columns_of(v[p + "D"])}
    p = "L3_attn_b_"
    low = v[p + "x_proj_w"]
    g["ssm3"] = {"w_in": v[p + "in_proj_w"], "w_low": row_blocks(low[:, :RANK]), "w_bc": row_blocks(low[:, RANK:]),
                 "w_dt": v[p + "dt_proj_w"], "w_out": row_blocks(v[p + "out_proj_w"]),
                 "conv_w": row_blocks(v[p + "conv_w"][:, 0, :]), "conv_b": columns_of(v[p + "conv_b"]),
                 "dt_b": columns_of(v[p + "dt_proj_b"]), "a_log": row_blocks(v[p + "A_log"]),
                 "skip": columns_of(v[p + "D_param"])}
    p = "L1_attn_a_"
    wq, wk, wv, wu = np.split(v[p + "qkvu_w"].T, 4, axis=1)
    bq, bk, bv, bu = np.split(v[p + "qkvu_b"], 4)
    twice = np.concatenate([np.concatenate([np.arange(h * LHD, (h + 1) * LHD)] * 2) for h in range(LH)])
    slope = v[p + "slope_rate"].reshape(LH)
    g["light"] = {"wq": wq[:, twice], "wk": wk[:, twice], "wv": wv, "wu": wu, "wo": v[p + "out_w"].T,
                  "bq": columns_of(bq[twice]), "bk": columns_of(bk[twice]), "bv": rows_of(bv), "bu": rows_of(bu),
                  "bo": columns_of(v[p + "out_b"]), "slope": rows_of(slope),
                  "slope_cols": rows_of(np.repeat(slope, LHD)),
                  "theta": columns_of(v[p + "theta"].reshape(-1)[twice]),
                  "shift": columns_of(np.tile(np.repeat(np.float32([np.pi / 2, 0]), LHD), LH))}
    p = "L3_attn_a_"
    wq, wk, wv = np.split(v[p + "qkv_w"], 3, axis=1)
    bq, bk, bv = np.split(v[p + "qkv_b"], 3)
    g["elu"] = {"wq": wq, "wk": wk, "wv": wv, "wo": v[p + "out_w"], "bq": columns_of(bq), "bk": columns_of(bk),
                "bv": rows_of(bv), "bo": columns_of(v[p + "out_b"])}
    p = "L1_attn_b_"
    g["slr"] = {"wq": np.concatenate([v[p + "slr_wq1"], v[p + "slr_wq2"]], 1),
                "wk": np.concatenate([v[p + "slr_wk1"], v[p + "slr_wk2"]], 1), "wv": v[p + "slr_wv"],
                "wo": v[p + "slr_wo"], "r1": v[p + "router_w1"], "r2": v[p + "router_w2"],
                "r2b": rows_of(v[p + "router_b2"]), "landmarks_t": v[p + "landmarks"].T,
                "mix1": v[p + "mix_w"][:D], "mix2": v[p + "mix_w"][D:], "compress": v[p + "bus_compress"],
                "publish": v[p + "bus_publish"], "expand": v[p + "bus_expand"],
                "lam": columns_of(np.repeat(v[p + "lambdas"], D // 8)), "slr_lam": rows_of(v[p + "slr_lam"]),
                "norm_in": columns_of(v[p + "w_norm_in"]), "norm_out": columns_of(v[p + "w_norm_out"])}
    p = "L0_attn_b_"
    wq, wk, wv = (m.T for m in np.split(v[p + "w_attn"], 3))
    g["keep"] = {"wq": in_row_groups(wq, 1), "wk": in_row_groups(wk, 1), "wv": in_row_groups(wv, 0),
                 "wo": v[p + "w_proj"].T}
    p = "L3_ffn_"
    g["cell"] = {k: v[p + k].T for k in ("wf", "uf", "wi", "ui", "wc", "uc", "wo", "uo")}
    g["cell"].update({k: columns_of(v[p + k]) for k in ("bf", "bi", "bc", "bo", "in_c")})
    g["bitffn"] = {"w1": v["L1_ffn_W1"].T, "w2": row_blocks(v["L1_ffn_W2"].T),
                   "b1": columns_of(v["L1_ffn_b1"]), "b2": columns_of(v["L1_ffn_b2"])}
    return g


def pack(matrices):
    at, columns, parts = 0, {}, []
    for name, m in matrices.items():
        m = np.asarray(m)
        columns[name] = (at, m.shape[0], m.shape[1])
        full = np.zeros((P, m.shape[1]), np.float32)
        full[:m.shape[0]] = m
        parts.append(full)
        at += m.shape[1]
    return np.ascontiguousarray(np.concatenate(parts, axis=1)), columns


def kernel(**inputs):
    import concourse.bacc as bacc
    from concourse.bass_utils import run_bass_kernel_spmd

    v = {k: np.asarray(a) for k, a in inputs.items()}
    x = np.ascontiguousarray(v["L0_attn_a_x"].reshape(B * S, D).T)
    nc = bacc.Bacc("TRN2", target_bir_lowering=False, num_devices=1)
    arrays = {"x_in": x}
    x_in = nc.dram_tensor("x_in", x.shape, F32, kind="ExternalInput").ap()
    groups_in, columns = {}, {}
    used = {"const"} | {g for i in PLAN for g in GROUPS_OF[i]}
    for g, matrices in lay_out(v).items():
        if g not in used:
            continue
        packed, columns[g] = pack(matrices)
        arrays[f"in_{g}"] = packed
        groups_in[g] = nc.dram_tensor(f"in_{g}", packed.shape, F32, kind="ExternalInput").ap()
    out = nc.dram_tensor("out", (P, B * S), F32, kind="ExternalOutput").ap()
    build_program(nc, x_in, groups_in, out, columns)
    r = run_bass_kernel_spmd(nc, [arrays], core_ids=[0])
    return np.ascontiguousarray(r.results[0]["out"].T).reshape(B, S, D)
```

```python
from contextlib import ExitStack

import numpy as np

import concourse.bass as bass
from concourse import mybir

F32 = mybir.dt.float32
BF16 = mybir.dt.bfloat16
ALU = mybir.AluOpType
ACT = mybir.ActivationFunctionType
AX = mybir.AxisListType

B, S, D = 4, 512, 128
P = 128
TT = S // P
LN_EPS = 1e-5
NEG = -1e30

PLAN = list(range(16))


class Signal:

    def __init__(self, sem, per):
        self.sem, self.per = sem, per

    def at(self, b, k):
        return b * self.per + (k + 1)


class Layer:

    def __init__(self, nc, name, core, groups, **signals):
        self.nc, self.name, self.core = nc, name, core
        self.ctx = ExitStack()
        self.sems, self.signals = [], {}
        for key, per in signals.items():
            sem = nc.alloc_semaphore(f"{name}_{key}")
            self.sems.append(sem)
            nc.sync.sem_inc(sem, 1)
            self.signals[key] = Signal(sem, per)
        for eng in (nc.tensor, nc.scalar, nc.vector, nc.gpsimd):
            wait_weights(eng, core, "const", *groups)
        nc.all_engine_barrier()

    def __getitem__(self, key):
        return self.signals[key]

    def sb(self, key, shape, dt=F32):
        return self.ctx.enter_context(self.nc.sbuf_tensor(f"{self.name}_{key}", shape, dt))

    def ps(self, key, shape, dt=F32):
        return self.ctx.enter_context(self.nc.psum_tensor(f"{self.name}_{key}", shape, dt))

    def close(self):
        self.ctx.close()
        self.nc.clear_and_free_semaphores(self.sems)
        self.nc.all_engine_barrier()


def wait_weights(eng, core, *groups):
    for g in groups:
        eng.wait_ge(core.landed[g], 16)


class Core:

    def __init__(self, x, xn, weights, landed, columns):
        self.x, self.xn, self.weights, self.landed, self.columns = x, xn, weights, landed, columns

    def w(self, group, name, lo=0, hi=None):
        at, rows, width = self.columns[group][name]
        hi = width if hi is None else hi
        return self.weights[group][0:rows, at + lo:at + hi]

    def normed(self, b):
        return self.xn[:, bass.ds(b * S, S)]

    def batch(self, b):
        return self.x[:, bass.ds(b * S, S)]




def normalise(nc, core, name):
    L = Layer(nc, name, core, [],
              centred=B,
              square=B,
              kept=B,
              var=B,
              eps=1,
              rstd=1,
              diag=B,
              spread=B,
              xn=B)
    with L.ctx:
        centred, square = L.sb("centred", [P, B, S]), L.sb("square", [P, B, S])
        small = L.sb("small", [P, 2, B * TT])
        diag = L.sb("diag", [P, B, TT, P])
        banks = L.ps("banks", [P, B, S])
        ps_var = L.ps("ps_var", [P, B * TT])
        eye = core.w("const", "eye")
        with nc.Block() as block:
            @block.tensor
            def _(pe):
                for b in range(B):
                    pe.matmul(banks[:, b, :], core.w("const", "centre"), core.x[:, b * S:(b + 1) * S],
                              start=True, stop=True).then_inc(L["centred"].sem, 1)
                for b in range(B):
                    pe.wait_ge(L["square"].sem, L["square"].at(0, b + 1))
                    for t in range(TT):
                        n = b * TT + t
                        mm = pe.matmul(ps_var[:, n:n + 1], square[:, b, t * P:(t + 1) * P],
                                       core.w("const", "mean", 0, 1), start=True, stop=True)
                    mm.then_inc(L["var"].sem, 1)
                for b in range(B):
                    pe.wait_ge(L["diag"].sem, L["diag"].at(0, b + 1))
                    pe.wait_ge(L["kept"].sem, L["kept"].at(0, b + 1))
                    pe.matmul(banks[:, b, :], core.w("const", "ones"), diag[:, b, :, :], start=True, stop=True)\
                        .then_inc(L["spread"].sem, 1)

            @block.scalar
            def _(act):
                for b in range(B):
                    act.wait_ge(L["centred"].sem, L["centred"].at(0, b + 1))
                    act.activation(square[:, b, :], banks[:, b, :], ACT.Square).then_inc(L["square"].sem, 1)

            @block.vector
            def _(dve):
                for b in range(B):
                    dve.wait_ge(L["square"].sem, L["square"].at(0, b + 1))
                    dve.tensor_copy(centred[:, b, :], banks[:, b, :]).then_inc(L["kept"].sem, 1)
                dve.wait_ge(L["var"].sem, L["var"].at(0, B))
                dve.tensor_scalar(small[:, 0, :], ps_var[:, :], LN_EPS, None, ALU.add).then_inc(L["eps"].sem, 1)
                dve.wait_ge(L["rstd"].sem, L["rstd"].at(0, 1))
                for b in range(B):
                    dve.tensor_tensor(diag[:, b, :, :], eye.unsqueeze(1).to_broadcast([P, TT, P]),
                                      small[:, 1, b * TT:(b + 1) * TT].unsqueeze(2).to_broadcast([P, TT, P]), ALU.mult)\
                        .then_inc(L["diag"].sem, 1)
                for b in range(B):
                    dve.wait_ge(L["kept"].sem, L["kept"].at(0, b + 1))
                    dve.wait_ge(L["spread"].sem, L["spread"].at(0, b + 1))
                    dve.tensor_tensor(core.xn[:, b * S:(b + 1) * S], centred[:, b, :], banks[:, b, :], ALU.mult)\
                        .then_inc(L["xn"].sem, 1)

            @block.gpsimd
            def _(pool):
                pool.wait_ge(L["eps"].sem, L["eps"].at(0, 1))
                pool.tensor_tensor(small[:, 1, :], small[:, 0, :], core.w("const", "minus_half"), ALU.pow)\
                    .then_inc(L["rstd"].sem, 1)
    L.close()


NEXT = dict(now=1)


def take_normed(dve, L, b, xn):
    dve.tensor_copy(xn, L.core.normed(b)).then_inc(L["now"].sem, 1)

HEADS, HD = 16, 64


def query_softmax_attention(nc, core, name):
    PAIRS = HEADS // 2
    STEPS = PAIRS * TT
    L = Layer(nc, name, core, ["mha"], **NEXT,
              v_ps=2 * TT,
              v_sb=2 * TT,
              qk_ps=2 * PAIRS,
              qk_sb=2 * PAIRS,
              scores=STEPS,
              top=STEPS,
              shift=STEPS,
              probs=2 * STEPS,
              inverse=STEPS,
              vs=STEPS,
              ctx_ps=STEPS,
              ctx_sb=PAIRS,
              joined=PAIRS,
              done=1)
    with L.ctx:
        g = "mha"
        scale = float(HD) ** -0.5
        xn = L.sb("xn", [P, S])
        v = L.sb("v", [P, TT, HEADS * HD])
        q, k = L.sb("q", [P, 2, S]), L.sb("k", [P, 2, S])
        probs = L.sb("probs", [P, 2, 2, S])
        vs = L.sb("vs", [P, 2, 2, HD])
        heads_out = L.sb("heads_out", [P, 2, S])
        stats = L.sb("stats", [P, 2, 4, 2])
        psp = L.ps("psp", [P, 2, 2, S])
        psq = L.ps("psq", [P, S])
        ps_ctx, out, bank = L.ps("ps_ctx", [P, S]), L.ps("out", [P, S]), L.ps("bank", [P, S])

        def project(pe, b, hp):
            for i, (w, ps) in enumerate((("wq", bank), ("wk", psq))):
                if hp == 0:
                    pe.wait_ge(L["v_sb"].sem, L["v_sb"].at(b, 2 * TT))
                else:
                    pe.wait_ge(L["qk_sb"].sem, L["qk_sb"].at(b, 2 * (hp - 1) + i + 1))
                pe.matmul(ps[:, :], core.w(g, w, hp * P, (hp + 1) * P), xn[:, :], start=True, stop=True)\
                    .then_inc(L["qk_ps"].sem, 1)

        def score(pe, b, s):
            hp, kt = divmod(s, TT)
            if kt == 0:
                pe.wait_ge(L["qk_sb"].sem, L["qk_sb"].at(b, 2 * hp + 2))
            pe.wait_ge(L["probs"].sem, L["probs"].at(b, 2 * max(s - 1, 0)))
            for i in range(2):
                r = slice(i * HD, (i + 1) * HD)
                mm = pe.matmul(psp[:, s % 2, i, :], k[r, hp % 2, kt * P:(kt + 1) * P], q[r, hp % 2, :],
                               start=True, stop=True)
            mm.then_inc(L["scores"].sem, 1)

        def context(pe, b, s):
            hp, kt = divmod(s, TT)
            pe.wait_ge(L["vs"].sem, L["vs"].at(b, s + 1))
            if kt == 0:
                pe.wait_ge(L["ctx_sb"].sem, L["ctx_sb"].at(b, hp))
            for i in range(2):
                mm = pe.matmul(ps_ctx[i * HD:(i + 1) * HD, :], vs[:, s % 2, i, :], probs[:, s % 2, i, :],
                               start=kt == 0, stop=kt == TT - 1)
            mm.then_inc(L["ctx_ps"].sem, 1)

        def join(pe, b, hp):
            pe.wait_ge(L["ctx_sb"].sem, L["ctx_sb"].at(b, hp + 1))
            if hp == 0:
                pe.wait_ge(L["done"].sem, L["done"].at(b, 0))
            pe.matmul(out[:, :], core.w(g, "wl", hp * P, (hp + 1) * P), heads_out[:, hp % 2, :],
                      start=hp == 0, stop=hp == PAIRS - 1).then_inc(L["joined"].sem, 1)

        with nc.Block() as block:
            @block.tensor
            def _(pe):
                with pe.Fori(0, B) as b:
                    pe.wait_ge(L["now"].sem, L["now"].at(b, 1))
                    for n in range(2 * TT):
                        t, half = divmod(n, 2)
                        ps = (bank, psq)[half]
                        if n >= 2:
                            pe.wait_ge(L["v_sb"].sem, L["v_sb"].at(b, n - 1))
                        pe.matmul(ps[:, :], xn[:, t * P:(t + 1) * P], core.w(g, "wv", half * S, (half + 1) * S),
                                  start=True, stop=True).then_inc(L["v_ps"].sem, 1)
                    project(pe, b, 0)
                    score(pe, b, 0)
                    for s in range(STEPS):
                        hp, kt = divmod(s, TT)
                        if kt == 1 and hp + 1 < PAIRS:
                            project(pe, b, hp + 1)
                        if s + 1 < STEPS:
                            score(pe, b, s + 1)
                        context(pe, b, s)
                        if kt == 2 and hp >= 1:
                            join(pe, b, hp - 1)
                    join(pe, b, PAIRS - 1)

            def bias_qk(act, b, hp):
                for i, (n, to, ps) in enumerate((("bq", q, bank), ("bk", k, psq))):
                    act.wait_ge(L["qk_ps"].sem, L["qk_ps"].at(b, 2 * hp + i + 1))
                    act.wait_ge(L["scores"].sem, L["scores"].at(b, TT * max(hp - 1, 0)))
                    act.activation(to[:, hp % 2, :], ps[:, :], ACT.Identity, bias=core.w(g, n, hp, hp + 1))\
                        .then_inc(L["qk_sb"].sem, 1)

            @block.scalar
            def _(act):
                with act.Fori(0, B) as b:
                    bias_qk(act, b, 0)
                    for s in range(STEPS):
                        hp, kt = divmod(s, TT)
                        act.wait_ge(L["shift"].sem, L["shift"].at(b, s + 1))
                        act.wait_ge(L["ctx_ps"].sem, L["ctx_ps"].at(b, max(s - 1, 0)))
                        for i in range(2):
                            act.activation(probs[:, s % 2, i, :], psp[:, s % 2, i, :], ACT.Exp,
                                           bias=stats[:, s % 2, 1, i:i + 1], scale=scale,
                                           accum_out=stats[:, s % 2, 2, i:i + 1]).then_inc(L["probs"].sem, 1)
                        if kt == 1 and hp + 1 < PAIRS:
                            bias_qk(act, b, hp + 1)

            def maxima(dve, b, s):
                dve.wait_ge(L["scores"].sem, L["scores"].at(b, s + 1))
                dve.wait_ge(L["inverse"].sem, L["inverse"].at(b, max(s - 1, 0)))
                dve.tensor_reduce(stats[:, s % 2, 0, :], psp[:, s % 2, :, :], AX.X, ALU.max).then_inc(L["top"].sem, 1)
                dve.wait_ge(L["top"].sem, L["top"].at(b, s + 1))
                dve.tensor_scalar(stats[:, s % 2, 1, :], stats[:, s % 2, 0, :], -scale, None, ALU.mult)\
                    .then_inc(L["shift"].sem, 1)

            def scale_v(dve, b, s):
                hp, kt = divmod(s, TT)
                dve.wait_ge(L["probs"].sem, L["probs"].at(b, 2 * s + 2))
                dve.wait_ge(L["vs"].sem, L["vs"].at(b, max(s - 1, 0)))
                dve.reciprocal(stats[:, s % 2, 3, :], stats[:, s % 2, 2, :]).then_inc(L["inverse"].sem, 1)
                dve.wait_ge(L["inverse"].sem, L["inverse"].at(b, s + 1))
                dve.wait_ge(L["ctx_ps"].sem, L["ctx_ps"].at(b, max(s - 1, 0)))
                dve.tensor_tensor(vs[:, s % 2, :, :],
                                  v[:, kt, hp * P:(hp + 1) * P].rearrange("p (i d) -> p i d", i=2),
                                  stats[:, s % 2, 3, :].unsqueeze(2).to_broadcast([P, 2, HD]), ALU.mult)\
                    .then_inc(L["vs"].sem, 1)

            def take_context(dve, b, hp):
                dve.wait_ge(L["ctx_ps"].sem, L["ctx_ps"].at(b, TT * (hp + 1)))
                dve.wait_ge(L["joined"].sem, L["joined"].at(b, max(hp - 1, 0)))
                dve.tensor_copy(heads_out[:, hp % 2, :], ps_ctx[:, :]).then_inc(L["ctx_sb"].sem, 1)

            @block.vector
            def _(dve):
                with dve.Fori(0, B) as b:
                    take_normed(dve, L, b, xn[:, :])
                    dve.wait_ge(L["vs"].sem, L["vs"].at(b, 0))
                    for n in range(2 * TT):
                        t, half = divmod(n, 2)
                        dve.wait_ge(L["v_ps"].sem, L["v_ps"].at(b, n + 1))
                        dve.tensor_tensor(v[:, t, half * S:(half + 1) * S], (bank, psq)[half][:, :],
                                          core.w(g, "bv", half * S, (half + 1) * S), ALU.add).then_inc(L["v_sb"].sem, 1)
                    maxima(dve, b, 0)
                    for s in range(STEPS):
                        hp, kt = divmod(s, TT)
                        if s + 1 < STEPS:
                            maxima(dve, b, s + 1)
                        if s == 0:
                            dve.wait_ge(L["v_sb"].sem, L["v_sb"].at(b, 2 * TT))
                        scale_v(dve, b, s)
                        if kt == 0 and hp >= 1:
                            take_context(dve, b, hp - 1)
                    take_context(dve, b, PAIRS - 1)
                    dve.wait_ge(L["joined"].sem, L["joined"].at(b, PAIRS))
                    dve.scalar_tensor_tensor(out=core.batch(b), in0=out[:, :], scalar=core.w(g, "bl"),
                                             in1=core.batch(b), op0=ALU.add, op1=ALU.add).then_inc(L["done"].sem, 1)

    L.close()


def routed_ffn(nc, core, name, group, E, routed, shared, gated):
    NT = routed + shared
    total = core.columns[group]["w1"][2]
    rows = [min(P, total - m * P) for m in range(NT)]
    PARTS = 3 * E
    L = Layer(nc, name, core, [group], **NEXT,
              logits=1,
              route=23,
              expd=1,
              turned=1,
              rows_in=1 + gated,
              up=NT,
              first=NT,
              product=NT,
              silu=NT,
              spread=routed,
              hidden=routed,
              down=NT + gated,
              cast=3, done=1)
    with L.ctx:
        xn = L.sb("xn", [P, S])
        pick16 = L.sb("pick16", [PARTS, routed * P], BF16)
        eye16 = L.sb("eye16", [P, P], BF16)
        small = L.sb("small", [P, 4, TT])
        e = L.sb("e", [P, TT, E])
        prob = L.sb("prob", [P, TT, E])
        key = L.sb("key", [P, TT, E])
        tie = L.sb("tie", [P, TT, E])
        chosen = L.sb("chosen", [P, 2, TT, E])
        cw = L.sb("cw", [P, TT, E])
        rest = L.sb("rest", [P, 2, TT, E])
        parts_wide = L.sb("parts", [P, TT, P], BF16)
        parts = parts_wide[:, :, 0:PARTS].rearrange("p t (a e) -> p t a e", e=E)
        cw_rows = L.sb("cw_rows", [E, S])
        part_rows = L.sb("part_rows", [PARTS, S], BF16)
        first = L.sb("first", [P, 2, S])
        product = L.sb("product", [P, 2, S])
        act_out = L.sb("act_out", [P, 2, S])
        h = L.sb("h", [P, 2, S])
        psg, psu = L.ps("psg", [P, 2, S]), L.ps("psu", [P, 2, S])
        psc, out, bank, ps_small = (L.ps(k, [P, S]) for k in ("psc", "out", "bank", "ps_small"))
        logits = ps_small[:, TT:TT + TT * E].rearrange("p (t e) -> p t e", e=E)
        ps_parts = ps_small[:, S // 2:S].bitcast(BF16)
        w1, w3, w2 = (core.w(group, k) for k in ("w1", "w3", "w2"))
        eye = core.w("const", "eye")
        falling = core.w("const", "falling" if E == 16 else "falling8").rearrange("p (t e) -> p t e", e=E)

        def over_e(col):
            return col.unsqueeze(2).to_broadcast([P, TT, E])

        def up(pe, b, m):
            M = rows[m]
            pe.wait_ge(L["first"].sem, L["first"].at(b, max(m - 1, 0)))
            pe.wait_ge(L["product"].sem, L["product"].at(b, max(m - 1, 0)))
            pe.matmul(psg[0:M, m % 2, :], w1[:, m * P:m * P + M], xn[:, :], start=True, stop=True)
            pe.matmul(psu[0:M, m % 2, :], w3[:, m * P:m * P + M], xn[:, :], start=True, stop=True)\
                .then_inc(L["up"].sem, 1)

        def spread(pe, b, m):
            pe.wait_ge(L["hidden"].sem, L["hidden"].at(b, m))
            pe.matmul(psc[:, :], pick16[:, m * P:(m + 1) * P], part_rows[:, :], start=True, stop=True)\
                .then_inc(L["spread"].sem, 1)

        def down(pe, b, m):
            M = rows[m]
            if m < routed:
                pe.wait_ge(L["hidden"].sem, L["hidden"].at(b, m + 1))
            elif gated:
                pe.wait_ge(L["silu"].sem, L["silu"].at(b, m + 1))
            else:
                pe.wait_ge(L["product"].sem, L["product"].at(b, m + 1))
            pe.matmul(out[:, :], w2[0:M, m * P:(m + 1) * P], h[0:M, m % 2, :], start=m == 0,
                      stop=m == NT - 1 and not gated).then_inc(L["down"].sem, 1)

        def factor(act, b, m):
            M = rows[m]
            act.wait_ge(L["up"].sem, L["up"].at(b, m + 1))
            act.wait_ge(L["product"].sem, L["product"].at(b, max(m - 1, 0)))
            if gated:
                act.activation(first[0:M, m % 2, :], psg[0:M, m % 2, :], ACT.Identity,
                               bias=core.w(group, "b1", m, m + 1)[0:M, :]).then_inc(L["first"].sem, 1)
            else:
                act.activation(first[0:M, m % 2, :], psg[0:M, m % 2, :], ACT.Silu).then_inc(L["first"].sem, 1)

        def silu(act, b, m):
            M = rows[m]
            act.wait_ge(L["product"].sem, L["product"].at(b, m + 1))
            if m < routed:
                act.wait_ge(L["hidden"].sem, L["hidden"].at(b, max(m - 1, 0)))
                to = act_out
            else:
                act.wait_ge(L["down"].sem, L["down"].at(b, m - 1))
                to = h
            act.activation(to[0:M, m % 2, :], product[0:M, m % 2, :], ACT.Silu).then_inc(L["silu"].sem, 1)

        def multiply(dve, b, m):
            M = rows[m]
            dve.wait_ge(L["first"].sem, L["first"].at(b, m + 1))
            if gated:
                dve.wait_ge(L["silu"].sem, L["silu"].at(b, max(m - 1, 0)))
                dve.scalar_tensor_tensor(out=product[0:M, m % 2, :], in0=psu[0:M, m % 2, :],
                                         scalar=core.w(group, "b3", m, m + 1)[0:M, :], in1=first[0:M, m % 2, :],
                                         op0=ALU.add, op1=ALU.mult).then_inc(L["product"].sem, 1)
                return
            dve.wait_ge(L["hidden"].sem, L["hidden"].at(b, max(m - 1, 0)))
            to = product
            if m >= routed:
                dve.wait_ge(L["down"].sem, L["down"].at(b, m - 1))
                to = h
            dve.tensor_tensor(to[0:M, m % 2, :], psu[0:M, m % 2, :], first[0:M, m % 2, :], ALU.mult)\
                .then_inc(L["product"].sem, 1)

        def finish(dve, b, m):
            if gated:
                dve.wait_ge(L["silu"].sem, L["silu"].at(b, m + 1))
            else:
                dve.wait_ge(L["product"].sem, L["product"].at(b, m + 1))
            dve.wait_ge(L["spread"].sem, L["spread"].at(b, m + 1))
            dve.wait_ge(L["down"].sem, L["down"].at(b, max(m - 1, 0)))
            dve.tensor_tensor(h[:, m % 2, :], (act_out if gated else product)[:, m % 2, :], psc[:, :], ALU.mult)\
                .then_inc(L["hidden"].sem, 1)

        def choose(dve, b):
            dve.wait_ge(L["logits"].sem, L["logits"].at(b, 1))
            dve.tensor_reduce(small[:, 0, :], logits, AX.X, ALU.max).then_inc(L["route"].sem, 1)
            dve.wait_ge(L["route"].sem, L["route"].at(b, 1))
            dve.tensor_tensor(e[:, :, :], logits, over_e(small[:, 0, :]), ALU.subtract).then_inc(L["route"].sem, 1)
            dve.wait_ge(L["expd"].sem, L["expd"].at(b, 1))
            dve.tensor_reduce(small[:, 1, :], e[:, :, :], AX.X, ALU.add).then_inc(L["route"].sem, 1)
            dve.wait_ge(L["route"].sem, L["route"].at(b, 3))
            dve.reciprocal(small[:, 2, :], small[:, 1, :]).then_inc(L["route"].sem, 1)
            dve.wait_ge(L["route"].sem, L["route"].at(b, 4))
            dve.tensor_tensor(prob[:, :, :], e[:, :, :], over_e(small[:, 2, :]), ALU.mult).then_inc(L["route"].sem, 1)
            dve.wait_ge(L["route"].sem, L["route"].at(b, 5))
            if gated:
                bias = core.w(group, "gate_b").rearrange("p (t e) -> p t e", e=E)
                dve.tensor_tensor(key[:, :, :], prob[:, :, :], bias, ALU.add).then_inc(L["route"].sem, 1)
            else:
                dve.tensor_copy(key[:, :, :], prob[:, :, :]).then_inc(L["route"].sem, 1)
            n = 6
            for i in range(2):
                dve.wait_ge(L["route"].sem, L["route"].at(b, n))
                dve.tensor_reduce(small[:, 3, :], key[:, :, :], AX.X, ALU.max).then_inc(L["route"].sem, 1)
                dve.wait_ge(L["route"].sem, L["route"].at(b, n + 1))
                dve.tensor_tensor(tie[:, :, :], key[:, :, :], over_e(small[:, 3, :]), ALU.is_equal)\
                    .then_inc(L["route"].sem, 1)
                dve.wait_ge(L["route"].sem, L["route"].at(b, n + 2))
                dve.tensor_tensor(tie[:, :, :], tie[:, :, :], falling, ALU.mult).then_inc(L["route"].sem, 1)
                dve.wait_ge(L["route"].sem, L["route"].at(b, n + 3))
                dve.tensor_reduce(small[:, 3, :], tie[:, :, :], AX.X, ALU.max).then_inc(L["route"].sem, 1)
                dve.wait_ge(L["route"].sem, L["route"].at(b, n + 4))
                dve.tensor_tensor(chosen[:, i, :, :], tie[:, :, :], over_e(small[:, 3, :]), ALU.is_equal)\
                    .then_inc(L["route"].sem, 1)
                dve.wait_ge(L["route"].sem, L["route"].at(b, n + 5))
                if i == 0:
                    dve.scalar_tensor_tensor(out=key[:, :, :], in0=chosen[:, 0, :, :], scalar=NEG, in1=key[:, :, :],
                                             op0=ALU.mult, op1=ALU.add).then_inc(L["route"].sem, 1)
                    n += 6
            dve.tensor_tensor(chosen[:, 0, :, :], chosen[:, 0, :, :], chosen[:, 1, :, :], ALU.add)\
                .then_inc(L["route"].sem, 1)
            dve.wait_ge(L["route"].sem, L["route"].at(b, 18))
            dve.tensor_tensor(cw[:, :, :], chosen[:, 0, :, :], prob[:, :, :], ALU.mult).then_inc(L["route"].sem, 1)
            dve.wait_ge(L["route"].sem, L["route"].at(b, 19))
            dve.tensor_copy(parts[:, :, 0, :], cw[:, :, :]).then_inc(L["route"].sem, 1)
            dve.wait_ge(L["route"].sem, L["route"].at(b, 20))
            dve.tensor_tensor(rest[:, 0, :, :], cw[:, :, :], parts[:, :, 0, :], ALU.subtract).then_inc(L["route"].sem, 1)
            dve.wait_ge(L["route"].sem, L["route"].at(b, 21))
            dve.tensor_copy(parts[:, :, 1, :], rest[:, 0, :, :]).then_inc(L["route"].sem, 1)
            dve.wait_ge(L["route"].sem, L["route"].at(b, 22))
            dve.tensor_tensor(parts[:, :, 2, :], rest[:, 0, :, :], parts[:, :, 1, :], ALU.subtract)\
                .then_inc(L["route"].sem, 1)

        STEPS = 23
        with nc.Block() as block:
            @block.tensor
            def _(pe):
                pe.wait_ge(L["cast"].sem, L["cast"].at(0, 3))
                with pe.Fori(0, B) as b:
                    pe.wait_ge(L["now"].sem, L["now"].at(b, 1))
                    for t in range(TT):
                        mm = pe.matmul(logits[:, t, :], xn[:, t * P:(t + 1) * P], core.w(group, "wr"),
                                       start=True, stop=True)
                    mm.then_inc(L["logits"].sem, 1)
                    up(pe, b, 0)
                    up(pe, b, 1)
                    pe.wait_ge(L["route"].sem, L["route"].at(b, STEPS))
                    pe.wait_ge(L["hidden"].sem, L["hidden"].at(b, 0))
                    if gated:
                        for t in range(TT):
                            pe.transpose(psc[0:E, t * P:(t + 1) * P], cw[:, t, :], eye)
                    for t in range(TT):
                        mm = pe.transpose(ps_parts[:, t * P:(t + 1) * P], parts_wide[:, t, :], eye16[:, :])
                    mm.then_inc(L["turned"].sem, 1)
                    pe.wait_ge(L["rows_in"].sem, L["rows_in"].at(b, 2 if gated else 1))
                    pe.wait_ge(L["done"].sem, L["done"].at(b, 0))
                    spread(pe, b, 0)
                    for m in range(NT):
                        if m + 2 < NT:
                            up(pe, b, m + 2)
                        down(pe, b, m)
                        if m + 1 < routed:
                            spread(pe, b, m + 1)
                    if gated:
                        pe.matmul(out[:, :], core.w(group, "b2"), cw_rows[:, :], start=False, stop=True)\
                            .then_inc(L["down"].sem, 1)

            @block.scalar
            def _(act):
                with act.Fori(0, B) as b:
                    act.wait_ge(L["route"].sem, L["route"].at(b, 2))
                    act.activation(e[:, :, :], e[:, :, :], ACT.Exp).then_inc(L["expd"].sem, 1)
                    factor(act, b, 0)
                    factor(act, b, 1)
                    act.wait_ge(L["turned"].sem, L["turned"].at(b, 1))
                    act.activation(part_rows[:, :], ps_parts[0:PARTS, :], ACT.Copy).then_inc(L["rows_in"].sem, 1)
                    for m in range(NT):
                        if gated:
                            silu(act, b, m)
                        if m + 2 < NT:
                            factor(act, b, m + 2)

            @block.vector
            def _(dve):
                dve.wait_ge(L["cast"].sem, L["cast"].at(0, 1))
                with dve.Fori(0, B) as b:
                    take_normed(dve, L, b, xn[:, :])
                    choose(dve, b)
                    if gated:
                        dve.wait_ge(L["turned"].sem, L["turned"].at(b, 1))
                        dve.tensor_copy(cw_rows[:, :], psc[0:E, :]).then_inc(L["rows_in"].sem, 1)
                    multiply(dve, b, 0)
                    for m in range(NT):
                        if m + 1 < NT:
                            multiply(dve, b, m + 1)
                        if m < routed:
                            finish(dve, b, m)
                    dve.wait_ge(L["down"].sem, L["down"].at(b, NT + gated))
                    dve.scalar_tensor_tensor(out=core.batch(b), in0=out[:, :],
                                             scalar=core.w(group, "sb2") if gated else 0.0, in1=core.batch(b),
                                             op0=ALU.add, op1=ALU.add).then_inc(L["done"].sem, 1)

            @block.gpsimd
            def _(pool):
                pool.memset(parts_wide[:, :, :], 0.0).then_inc(L["cast"].sem, 1)
                pool.tensor_copy(pick16[:, :], core.w(group, "pick")).then_inc(L["cast"].sem, 1)
                pool.tensor_copy(eye16[:, :], eye).then_inc(L["cast"].sem, 1)
    L.close()

KH, KHD = 16, 8
KJ, KG = 4, 4
KEPT, RECENT = 391, 64
DROPPED = S - KEPT
OLD = S - RECENT
KT = KH // 2
HALF = P // 2
Q_PARTS, K_PARTS = "hhmhlm", "hmhlhm"
MASK_ROW = len(Q_PARTS) * KHD
SHIFT_ROW = MASK_ROW + 1
KSTEPS = KT * TT
LAG = 6


def keep_attention(nc, core, name):
    ROUNDS = DROPPED // 8
    L = Layer(nc, name, core, ["keep"], cast=4, zero=2,
              p1=2 * KT, high1=2 * KT, rest1=2 * KT, mid1=2 * KT, stack1=2 * KT,
              p2=2 * KT, high2=2 * KT, rest2=2 * KT, mid2=2 * KT, stack2=2 * KT,
              s1=KSTEPS, top1=KSTEPS, shift1=KSTEPS, exp1=2 * KSTEPS, inv1=KSTEPS, pick1=KSTEPS,
              sums1=KSTEPS, added=1,
              choice=2 * ROUNDS + 13,
              masked=1,
              current=1,
              pv=TT, v=TT,
              s2=2 * KSTEPS, top2=2 * KSTEPS,
              low2=4 * KT,
              rows=KT, q2=KT,
              st=2 * KSTEPS, exp2=2 * KSTEPS, av=KSTEPS,
              c_sb=KJ, c_turn=KJ, c_inv=KJ, c_out=KJ,
              o_turn=1, o_sb=1, projected=1, done=1)
    with L.ctx:
        w = lambda n, *a: core.w("keep", n, *a)
        scale = float(KHD) ** -0.5
        cur = L.sb("cur", [P, S])
        high, mid = L.sb("high", [P, 2, S], BF16), L.sb("mid", [P, 2, S], BF16)
        rest = L.sb("rest", [P, 2, S])
        stack = L.sb("stack", [P, 3, 2, S], BF16)
        probs = L.sb("probs", [P, 2, 2, S])
        stats = L.sb("stats", [P, 4, 4, 2])
        pick = L.sb("pick", [P, 2, 2, 32])
        sums = L.sb("sums", [P, S])
        work = L.sb("work", [P, OLD])
        best = L.sb("best", [P, 8])
        lt, eq, cum = (L.sb(n, [P, OLD]) for n in ("lt", "eq", "cum"))
        counts = L.sb("counts", [P, 2])
        mask = L.sb("mask", [P, S])
        bmask = L.sb("bmask", [P, S], BF16)
        tops, tops_rest = L.sb("tops", [P, 2, TT, 2]), L.sb("tops_rest", [P, TT, 2])
        low = L.sb("low", [P, 2, TT, P], BF16)
        v = L.sb("v", [P, TT, KH * 32])
        c_sb = L.sb("c_sb", [P, S])
        c_inv = L.sb("c_inv", [P, TT, KG])
        outs, outs_t = L.sb("outs", [P, TT, D]), L.sb("outs_t", [P, S])
        eye16, later16 = L.sb("eye16", [P, P], BF16), L.sb("later16", [P, P], BF16)
        mask_rows16 = L.sb("mask_rows16", [P, KT * P], BF16)
        ring = L.ps("ring", [P, 4, S])
        acc, psq, pst, out = (L.ps(n, [P, S]) for n in ("acc", "psq", "pst", "out"))
        eye = core.w("const", "eye")
        sources = (("wq", psq, "q_ones", "q_rest", "q_last"), ("wk", pst, "k_ones", "k_rest", "k_last"))

        def half(i):
            return slice(i * HALF, (i + 1) * HALF)

        def group_of(T, i):
            g = 2 * (T % 2) + i
            return slice(32 * g, 32 * g + 32)


        def project(pe, b, n, T):
            for i, (matrix, ps, *_) in enumerate(sources):
                pe.wait_ge(L["rest" + n].sem, L["rest" + n].at(b, max(2 * T - 1 + i, 0)))
                mm = pe.matmul(ps[:, :], w(matrix, T * P, (T + 1) * P), core.normed(b), start=True, stop=True,
                               skip_group_check=True)
                if n == "2" and i == 1:
                    pe.wait_ge(L["masked"].sem, L["masked"].at(b, 1))
                    mm = pe.matmul(ps[:, :], mask_rows16[:, T * P:(T + 1) * P], bmask[:, :], start=False, stop=True,
                                   skip_group_check=True)
                mm.then_inc(L["p" + n].sem, 1)

        def high_part(act, b, n, T):
            for i, (_, ps, ones, _, _) in enumerate(sources):
                act.wait_ge(L["p" + n].sem, L["p" + n].at(b, 2 * T + i + 1))
                act.wait_ge(L["rest" + n].sem, L["rest" + n].at(b, max(2 * T - 1 + i, 0)))
                act.activation(high[:, i, :], ps[:, :], ACT.Identity, bias=core.w("const", ones))\
                    .then_inc(L["high" + n].sem, 1)

        def take_rest(dve, b, n, T):
            for i, (_, ps, _, coefficient, _) in enumerate(sources):
                dve.wait_ge(L["high" + n].sem, L["high" + n].at(b, 2 * T + i + 1))
                dve.wait_ge(L["stack" + n].sem, L["stack" + n].at(b, max(2 * T - 1 + i, 0)))
                dve.scalar_tensor_tensor(out=rest[:, i, :], in0=high[:, i, :], scalar=core.w("const", coefficient),
                                         in1=ps[:, :], op0=ALU.mult, op1=ALU.add).then_inc(L["rest" + n].sem, 1)

        def middle_part(pool, b, n, T):
            for i in range(2):
                pool.wait_ge(L["rest" + n].sem, L["rest" + n].at(b, 2 * T + i + 1))
                pool.wait_ge(L["stack" + n].sem, L["stack" + n].at(b, max(2 * T - 1 + i, 0)))
                pool.tensor_tensor(mid[:, i, :], rest[:, i, :], core.w("const", "ones_s"), ALU.mult).then_inc(L["mid" + n].sem, 1)

        def stack_parts(dve, b, n, T):
            for i, (_, _, _, _, coefficient) in enumerate(sources):
                dve.wait_ge(L["mid" + n].sem, L["mid" + n].at(b, 2 * T + i + 1))
                if n == "1":
                    dve.wait_ge(L["s1"].sem, L["s1"].at(b, TT * max(T - 2, 0)))
                else:
                    dve.wait_ge(L["st"].sem, L["st"].at(b, 2 * TT * max(T - 2, 0)))
                dve.scalar_tensor_tensor(out=stack[:, T % 3, i, :], in0=mid[:, i, :],
                                         scalar=core.w("const", coefficient), in1=rest[:, i, :],
                                         op0=ALU.mult, op1=ALU.add).then_inc(L["stack" + n].sem, 1)


        def score1(pe, b, s):
            T, t = divmod(s, TT)
            qt = TT - 1 - t
            N = (qt + 1) * P
            if t == 0:
                pe.wait_ge(L["stack1"].sem, L["stack1"].at(b, 2 * T + 2))
            pe.wait_ge(L["exp1"].sem, L["exp1"].at(b, 2 * max(s - 1, 0)))
            for i in range(2):
                bank = ring[:, 2 * (s % 2) + i, :]
                pe.matmul(bank[:, 0:N], stack[half(i), T % 3, 0, qt * P:(qt + 1) * P], stack[half(i), T % 3, 1, 0:N],
                          start=True, stop=True, skip_group_check=True)
            for i in range(2):
                mm = pe.matmul(ring[:, 2 * (s % 2) + i, qt * P:N], eye16[:, :], later16[:, :], start=False, stop=True,
                               skip_group_check=True)
            mm.then_inc(L["s1"].sem, 1)

        def importance(pe, b, s):
            T, t = divmod(s, TT)
            N = (TT - t) * P
            pe.wait_ge(L["pick1"].sem, L["pick1"].at(b, s + 1))
            if s == 0:
                pe.wait_ge(L["added"].sem, L["added"].at(b, 0))
            for i in range(2):
                mm = pe.matmul(acc[group_of(T, i), 0:N], pick[:, s % 2, i, :], probs[:, s % 2, i, 0:N],
                               start=T < 2 and t == 0, stop=True, skip_group_check=True)
            mm.then_inc(L["sums1"].sem, 1)

        def maxima1(dve, b, s):
            N = (TT - s % TT) * P
            dve.wait_ge(L["s1"].sem, L["s1"].at(b, s + 1))
            dve.wait_ge(L["inv1"].sem, L["inv1"].at(b, max(s - 3, 0)))
            dve.tensor_reduce(stats[:, s % 4, 0, :], ring[:, 2 * (s % 2):2 * (s % 2) + 2, 0:N], AX.X, ALU.max)\
                .then_inc(L["top1"].sem, 1)
            dve.wait_ge(L["top1"].sem, L["top1"].at(b, s + 1))
            dve.tensor_scalar(stats[:, s % 4, 1, :], stats[:, s % 4, 0, :], -scale, None, ALU.mult)\
                .then_inc(L["shift1"].sem, 1)

        def inverse1(dve, b, s):
            j = s // (2 * TT)
            dve.wait_ge(L["exp1"].sem, L["exp1"].at(b, 2 * s + 2))
            dve.wait_ge(L["pick1"].sem, L["pick1"].at(b, max(s - 3, 0)))
            dve.reciprocal(stats[:, s % 4, 3, :], stats[:, s % 4, 2, :]).then_inc(L["inv1"].sem, 1)
            dve.wait_ge(L["inv1"].sem, L["inv1"].at(b, s + 1))
            dve.wait_ge(L["sums1"].sem, L["sums1"].at(b, max(s - 1, 0)))
            at = core.columns["const"]["units32"][0]
            hot = core.weights["const"][:, bass.ds(b * (KJ * 32) + (at + j * 32), 32)]
            dve.tensor_tensor(pick[:, s % 2, :, :], hot.unsqueeze(1).to_broadcast([P, 2, 32]),
                              stats[:, s % 4, 3, :].unsqueeze(2).to_broadcast([P, 2, 32]), ALU.mult)\
                .then_inc(L["pick1"].sem, 1)


        def choose(dve):
            dve.wait_ge(L["added"].sem, L["added"].at(B - 1, 1))
            dve.tensor_scalar(work[:, :], sums[:, 0:OLD], -1.0, None, ALU.mult)\
                .then_inc(L["choice"].sem, 1)
            dve.wait_ge(L["choice"].sem, L["choice"].at(0, 1))
            for r in range(ROUNDS):
                dve.max(best[:, :], work[:, :])\
                    .then_inc(L["choice"].sem, 1)
                dve.wait_ge(L["choice"].sem, L["choice"].at(0, 2 * r + 2))
                dve.match_replace(out=work[:, :], in_to_replace=best[:, :], in_values=work[:, :], imm_value=NEG)\
                    .then_inc(L["choice"].sem, 1)
                dve.wait_ge(L["choice"].sem, L["choice"].at(0, 2 * r + 3))
            n = 2 * ROUNDS + 1
            dve.max(best[:, :], work[:, :])\
                .then_inc(L["choice"].sem, 1)
            dve.wait_ge(L["choice"].sem, L["choice"].at(0, n + 1))
            last = best[:, (DROPPED - 1) % 8:(DROPPED - 1) % 8 + 1]
            dve.tensor_scalar(work[:, :], sums[:, 0:OLD], -1.0, None, ALU.mult)\
                .then_inc(L["choice"].sem, 1)
            dve.wait_ge(L["choice"].sem, L["choice"].at(0, n + 2))
            dve.tensor_scalar(lt[:, :], work[:, :], last, None, ALU.is_gt)\
                .then_inc(L["choice"].sem, 1)
            dve.wait_ge(L["choice"].sem, L["choice"].at(0, n + 3))
            dve.tensor_scalar(eq[:, :], work[:, :], last, None, ALU.is_equal)\
                .then_inc(L["choice"].sem, 1)
            dve.wait_ge(L["choice"].sem, L["choice"].at(0, n + 4))
            dve.tensor_reduce(counts[:, 0:1], lt[:, :], AX.X, ALU.add)\
                .then_inc(L["choice"].sem, 1)
            dve.wait_ge(L["choice"].sem, L["choice"].at(0, n + 5))
            dve.tensor_tensor_scan(cum[:, :], core.w("const", "ones_s", 0, OLD), eq[:, :], 0.0, ALU.mult, ALU.add)\
                .then_inc(L["choice"].sem, 1)
            dve.wait_ge(L["choice"].sem, L["choice"].at(0, n + 6))
            dve.tensor_scalar(counts[:, 1:2], counts[:, 0:1], cum[:, OLD - 1:OLD], -float(DROPPED), ALU.add, ALU.add)\
                .then_inc(L["choice"].sem, 1)
            dve.wait_ge(L["choice"].sem, L["choice"].at(0, n + 7))
            dve.tensor_tensor(work[:, :], eq[:, :], cum[:, :], ALU.subtract)\
                .then_inc(L["choice"].sem, 1)
            dve.wait_ge(L["choice"].sem, L["choice"].at(0, n + 8))
            dve.tensor_scalar(work[:, :], work[:, :], counts[:, 1:2], 0.0, ALU.add, ALU.is_le)\
                .then_inc(L["choice"].sem, 1)
            dve.wait_ge(L["choice"].sem, L["choice"].at(0, n + 9))
            dve.tensor_tensor(work[:, :], work[:, :], eq[:, :], ALU.mult)\
                .then_inc(L["choice"].sem, 1)
            dve.wait_ge(L["choice"].sem, L["choice"].at(0, n + 10))
            dve.tensor_tensor(work[:, :], work[:, :], lt[:, :], ALU.add)\
                .then_inc(L["choice"].sem, 1)
            dve.wait_ge(L["choice"].sem, L["choice"].at(0, n + 11))
            dve.tensor_scalar(mask[:, 0:OLD], work[:, :], NEG, None, ALU.mult)\
                .then_inc(L["choice"].sem, 1)
            dve.wait_ge(L["choice"].sem, L["choice"].at(0, n + 12))


        def score2(pe, b, s, i):
            T, t = divmod(s, TT)
            if t == 0 and i == 0:
                pe.wait_ge(L["stack2"].sem, L["stack2"].at(b, 2 * T + 2))
            pe.wait_ge(L["top2"].sem, L["top2"].at(b, max(2 * s - 1 + i, 0)))
            pe.matmul(ring[:, i, :], stack[half(i), T % 3, 0, t * P:(t + 1) * P], stack[half(i), T % 3, 1, :],
                      start=True, stop=True).then_inc(L["s2"].sem, 1)

        def score_by_keys(pe, b, s, i):
            T, t = divmod(s, TT)
            if t == 0 and i == 0:
                pe.wait_ge(L["q2"].sem, L["q2"].at(b, T + 1))
            pe.wait_ge(L["exp2"].sem, L["exp2"].at(b, max(2 * s - 1 + i, 0)))
            pe.matmul(ring[:, 2 + i, :], stack[half(i), T % 3, 1, t * P:(t + 1) * P], stack[half(i), T % 3, 0, :],
                      start=True, stop=True).then_inc(L["st"].sem, 1)

        def contexts(pe, b, s):
            T, t = divmod(s, TT)
            pe.wait_ge(L["exp2"].sem, L["exp2"].at(b, 2 * s + 2))
            if s % (2 * TT) == 0:
                pe.wait_ge(L["c_sb"].sem, L["c_sb"].at(b, T // 2))
            for i in range(2):
                h = 2 * T + i
                mm = pe.matmul(acc[group_of(T, i), :], v[:, t, 32 * h:32 * h + 32], probs[:, s % 2, i, :],
                               start=t == 0, stop=t == TT - 1, skip_group_check=True)
            mm.then_inc(L["av"].sem, 1)

        def shift_rows(pe, b, T):
            pe.wait_ge(L["low2"].sem, L["low2"].at(b, 4 * (T + 1)))
            if T == 0:
                pe.wait_ge(L["done"].sem, L["done"].at(b, 0))
            pe.wait_ge(L["q2"].sem, L["q2"].at(b, T))
            pe.wait_ge(L["c_out"].sem, L["c_out"].at(b, max((T - 2) // 2, 0)))
            for t in range(TT):
                mm = pe.matmul(out[:, t * P:(t + 1) * P], low[:, T % 2, t, :], eye16[:, :], start=True, stop=True,
                               skip_group_check=True)
            mm.then_inc(L["rows"].sem, 1)

        def lower_parts(dve, b, T):
            to = low[:, T % 2, :, :].rearrange("p t (i c) -> p t i c", i=2)
            dve.wait_ge(L["top2"].sem, L["top2"].at(b, 2 * TT * (T + 1)))
            dve.wait_ge(L["rows"].sem, L["rows"].at(b, max(T - 1, 0)))
            dve.wait_ge(L["low2"].sem, L["low2"].at(b, 4 * T))
            dve.tensor_scalar(to[:, :, :, SHIFT_ROW], tops[:, T % 2, :, :], -1.0, None, ALU.mult)\
                .then_inc(L["low2"].sem, 1)
            dve.wait_ge(L["low2"].sem, L["low2"].at(b, 4 * T + 1))
            dve.scalar_tensor_tensor(out=tops_rest[:, :, :], in0=tops[:, T % 2, :, :], scalar=-1.0,
                                     in1=to[:, :, :, SHIFT_ROW], op0=ALU.mult, op1=ALU.subtract)\
                .then_inc(L["low2"].sem, 1)
            dve.wait_ge(L["low2"].sem, L["low2"].at(b, 4 * T + 2))
            dve.tensor_copy(to[:, :, :, SHIFT_ROW + 1], tops_rest[:, :, :]).then_inc(L["low2"].sem, 1)
            dve.wait_ge(L["low2"].sem, L["low2"].at(b, 4 * T + 3))
            dve.tensor_tensor(to[:, :, :, SHIFT_ROW + 2], tops_rest[:, :, :], to[:, :, :, SHIFT_ROW + 1], ALU.subtract)\
                .then_inc(L["low2"].sem, 1)

        with nc.Block() as block:
            @block.tensor
            def _(pe):
                pe.wait_ge(L["cast"].sem, L["cast"].at(0, 3))
                with pe.Fori(0, B) as b:
                    project(pe, b, "1", 0)
                    score1(pe, b, 0)
                    score1(pe, b, 1)
                    for s in range(KSTEPS):
                        if s % TT == 0 and s // TT + 1 < KT:
                            project(pe, b, "1", s // TT + 1)
                        if s + 2 < KSTEPS:
                            score1(pe, b, s + 2)
                        importance(pe, b, s)
                pe.wait_ge(L["choice"].sem, L["choice"].at(0, L["choice"].per))
                with pe.Fori(0, B) as b:
                    pe.wait_ge(L["o_sb"].sem, L["o_sb"].at(b, 0))
                    pe.wait_ge(L["current"].sem, L["current"].at(b, 1))
                    for t in range(TT):
                        if t >= 2:
                            pe.wait_ge(L["v"].sem, L["v"].at(b, t - 1))
                        pe.matmul((psq, pst)[t % 2][:, :], cur[:, t * P:(t + 1) * P], w("wv"), start=True, stop=True)\
                            .then_inc(L["pv"].sem, 1)
                    pe.wait_ge(L["v"].sem, L["v"].at(b, TT))
                    project(pe, b, "2", 0)
                    for i in range(KSTEPS + LAG + 2):
                        s = i - LAG
                        for h in range(2):
                            if i < KSTEPS:
                                score2(pe, b, i, h)
                            if 0 <= s < KSTEPS:
                                score_by_keys(pe, b, s, h)
                        if i % TT == 1 and TT < i < KSTEPS + TT:
                            shift_rows(pe, b, i // TT - 1)
                        if 1 <= s <= KSTEPS:
                            contexts(pe, b, s - 1)
                        if i % TT == 1 and i // TT + 1 < KT:
                            project(pe, b, "2", i // TT + 1)
                        if s > 1 and (s - 1) % (2 * TT) == 0:
                            j = s // (2 * TT)
                            pe.wait_ge(L["c_sb"].sem, L["c_sb"].at(b, j))
                            pe.wait_ge(L["q2"].sem, L["q2"].at(b, min(2 * j + 1, KT)))
                            for t in range(TT):
                                mm = pe.transpose(out[:, t * P:(t + 1) * P], c_sb[:, t * P:(t + 1) * P], eye)
                            mm.then_inc(L["c_turn"].sem, 1)
                    pe.wait_ge(L["c_out"].sem, L["c_out"].at(b, KJ))
                    pe.wait_ge(L["rest2"].sem, L["rest2"].at(b, 2 * KT))
                    for t in range(TT):
                        mm = pe.transpose(psq[:, t * P:(t + 1) * P], outs[:, t, :], eye)
                    mm.then_inc(L["o_turn"].sem, 1)
                    pe.wait_ge(L["o_sb"].sem, L["o_sb"].at(b, 1))
                    pe.matmul(out[:, :], w("wo"), outs_t[:, :], start=True, stop=True).then_inc(L["projected"].sem, 1)

            @block.scalar
            def _(act):
                with act.Fori(0, B) as b:
                    high_part(act, b, "1", 0)
                    for s in range(KSTEPS):
                        N = (TT - s % TT) * P
                        act.wait_ge(L["shift1"].sem, L["shift1"].at(b, s + 1))
                        act.wait_ge(L["sums1"].sem, L["sums1"].at(b, max(s - 1, 0)))
                        for i in range(2):
                            act.activation(probs[:, s % 2, i, 0:N], ring[:, 2 * (s % 2) + i, 0:N], ACT.Exp,
                                           bias=stats[:, s % 4, 1, i:i + 1], scale=scale,
                                           accum_out=stats[:, s % 4, 2, i:i + 1]).then_inc(L["exp1"].sem, 1)
                        if s % TT == 0 and s // TT + 1 < KT:
                            high_part(act, b, "1", s // TT + 1)
                with act.Fori(0, B) as b:
                    act.wait_ge(L["pv"].sem, L["pv"].at(b, 0))
                    act.activation(cur[:, :], core.normed(b), ACT.Copy).then_inc(L["current"].sem, 1)
                    high_part(act, b, "2", 0)
                    for i in range(KSTEPS + LAG + 2):
                        s = i - LAG
                        if 0 <= s < KSTEPS:
                            act.wait_ge(L["av"].sem, L["av"].at(b, max(s - 1, 0)))
                            for h in range(2):
                                act.wait_ge(L["st"].sem, L["st"].at(b, 2 * s + h + 1))
                                act.activation(probs[:, s % 2, h, :], ring[:, 2 + h, :], ACT.Exp, scale=scale)\
                                    .then_inc(L["exp2"].sem, 1)
                        if s > 0 and s % (2 * TT) == 0:
                            act.wait_ge(L["av"].sem, L["av"].at(b, s))
                            act.wait_ge(L["c_turn"].sem, L["c_turn"].at(b, s // (2 * TT) - 1))
                            act.activation(c_sb[:, :], acc[:, :], ACT.Copy).then_inc(L["c_sb"].sem, 1)
                        if i % TT == 1 and i // TT + 1 < KT:
                            high_part(act, b, "2", i // TT + 1)
                    act.wait_ge(L["o_turn"].sem, L["o_turn"].at(b, 1))
                    act.activation(outs_t[:, :], psq[:, :], ACT.Copy).then_inc(L["o_sb"].sem, 1)

            @block.vector
            def _(dve):
                dve.memset(sums[:, :], 0.0).then_inc(L["zero"].sem, 1)
                dve.memset(mask[:, :], 0.0).then_inc(L["zero"].sem, 1)
                dve.wait_ge(L["zero"].sem, L["zero"].at(0, 2))
                with dve.Fori(0, B) as b:
                    take_rest(dve, b, "1", 0)
                    stack_parts(dve, b, "1", 0)
                    maxima1(dve, b, 0)
                    maxima1(dve, b, 1)
                    for s in range(KSTEPS):
                        inverse1(dve, b, s)
                        if s + 2 < KSTEPS:
                            maxima1(dve, b, s + 2)
                        if s % TT == 0 and s // TT + 1 < KT:
                            take_rest(dve, b, "1", s // TT + 1)
                        if s % TT == 1 and s // TT + 1 < KT:
                            stack_parts(dve, b, "1", s // TT + 1)
                    dve.wait_ge(L["sums1"].sem, L["sums1"].at(b, KSTEPS))
                    dve.tensor_tensor(sums[:, :], acc[:, :], sums[:, :], ALU.add).then_inc(L["added"].sem, 1)
                choose(dve)
                dve.wait_ge(L["cast"].sem, L["cast"].at(0, 4))
                with dve.Fori(0, B) as b:
                    dve.wait_ge(L["p2"].sem, L["p2"].at(b, 0))
                    at = core.columns["const"]["batch_rows"][0]
                    dve.tensor_scalar(bmask[:, :], mask[:, :], core.weights["const"][:, bass.ds(b + at, 1)], None,
                                      ALU.mult).then_inc(L["masked"].sem, 1)
                    for t in range(TT):
                        dve.wait_ge(L["pv"].sem, L["pv"].at(b, t + 1))
                        dve.tensor_tensor(v[:, t, :], (psq, pst)[t % 2][:, :], core.w("const", "v_ones"), ALU.add)\
                            .then_inc(L["v"].sem, 1)
                    take_rest(dve, b, "2", 0)
                    stack_parts(dve, b, "2", 0)
                    for i in range(KSTEPS + LAG + 2):
                        T, t = divmod(i, TT)
                        s = i - LAG
                        if i < KSTEPS:
                            for h in range(2):
                                dve.wait_ge(L["s2"].sem, L["s2"].at(b, 2 * i + h + 1))
                                dve.wait_ge(L["low2"].sem, L["low2"].at(b, 4 * max(T - 1, 0)))
                                dve.tensor_reduce(tops[:, T % 2, t, h:h + 1], ring[:, h, :], AX.X, ALU.max)\
                                    .then_inc(L["top2"].sem, 1)
                        if t == 0 and 1 <= T <= KT:
                            lower_parts(dve, b, T - 1)
                        if t == 1 and 1 <= T <= KT:
                            dve.wait_ge(L["rows"].sem, L["rows"].at(b, T))
                            dve.tensor_tensor(stack[:, (T - 1) % 3, 0, :], stack[:, (T - 1) % 3, 0, :], out[:, :], ALU.add)\
                                .then_inc(L["q2"].sem, 1)
                        if t == 2 and T + 1 < KT:
                            take_rest(dve, b, "2", T + 1)
                        if t == 3 and T + 1 < KT:
                            stack_parts(dve, b, "2", T + 1)
                        if s > 1 and (s - 1) % (2 * TT) == 0:
                            j = s // (2 * TT) - 1
                            dve.wait_ge(L["c_turn"].sem, L["c_turn"].at(b, j + 1))
                            turned = out[:, :].rearrange("p (t g c) -> p t g c", t=TT, g=KG)
                            dve.wait_ge(L["c_out"].sem, L["c_out"].at(b, j))
                            dve.reciprocal(c_inv[:, :, :], turned[:, :, :, KHD]).then_inc(L["c_inv"].sem, 1)
                            dve.wait_ge(L["c_inv"].sem, L["c_inv"].at(b, j + 1))
                            dve.tensor_tensor(
                                outs[:, :, 32 * j:32 * j + 32].rearrange("p t (g c) -> p t g c", g=KG),
                                turned[:, :, :, 0:KHD], c_inv[:, :, :].unsqueeze(3).to_broadcast([P, TT, KG, KHD]),
                                ALU.mult).then_inc(L["c_out"].sem, 1)
                    dve.wait_ge(L["projected"].sem, L["projected"].at(b, 1))
                    dve.tensor_tensor(core.batch(b), out[:, :], core.batch(b), ALU.add).then_inc(L["done"].sem, 1)

            @block.gpsimd
            def _(pool):
                pool.tensor_copy(eye16[:, :], eye).then_inc(L["cast"].sem, 1)
                pool.tensor_copy(later16[:, :], core.w("const", "later")).then_inc(L["cast"].sem, 1)
                pool.tensor_copy(mask_rows16[:, :], core.w("const", "mask_rows")).then_inc(L["cast"].sem, 1)
                pool.memset(low[:, :, :, :], 0.0).then_inc(L["cast"].sem, 1)
                for n in ("1", "2"):
                    with pool.Fori(0, B) as b:
                        for T in range(KT):
                            middle_part(pool, b, n, T)
    L.close()

LH, LHD = 8, 16
FG = 2
HG = LH // FG


def linear_attention(nc, core, name):
    NSTEP = FG * HG
    L = Layer(nc, name, core, ["light"], **NEXT, masks=LH, vscale=1,
              angle=16, table=FG,
              proj=2 * FG,
              feats=2 * FG,
              rot=2 * FG,
              vu=2 * TT,
              vu_sb=2 * TT,
              v_late=1,
              kturn=FG, ktok=FG,
              states=FG,
              states_sb=FG,
              energy=NSTEP,
              masked=NSTEP,
              mixed=1,
              squares=TT, inv=2, outs=TT, turned=1, outs_sb=1, projected=1, done=1)
    with L.ctx:
        g = "light"
        w = lambda n, *a: core.w(g, n, *a)
        xn = L.sb("xn", [P, S])
        table = L.sb("table", [P, FG, S])
        turns = L.sb("turns", [P, 2, S])
        wholes = L.sb("wholes", [P, S], mybir.dt.int32)
        feats = L.sb("feats", [P, 2, FG, S])
        qk = L.sb("qk", [P, 2, FG, S])
        v, u = L.sb("v", [P, TT, D]), L.sb("u", [P, TT, D])
        v_late = L.sb("v_late", [P, TT, D])
        growth = L.sb("growth", [P, D])
        ktok = L.sb("ktok", [P, FG, TT, P])
        state = L.sb("state", [P, FG, TT, D // FG])
        masks = L.sb("masks", [P, LH, P])
        energy = L.sb("energy", [P, NSTEP, S])
        square = L.sb("square", [P, D])
        sums = L.sb("sums", [P, 3, TT])
        outs = L.sb("outs", [P, TT, D])
        outs_t = L.sb("outs_t", [P, S])
        bank = L.ps("bank", [P, S])
        small = L.ps("small", [P, S])
        pe4 = L.ps("pe4", [P, HG, S])
        pmix = L.ps("pmix", [P, TT, D])
        pout = L.ps("pout", [P, S])
        eye = core.w("const", "eye")
        TWO_PI = 2 * np.pi
        c1 = float(np.float32(6.28125))
        c2 = float(np.float32(np.round((TWO_PI - c1) * 2 ** 20) / 2 ** 20))
        c3 = float(np.float32(TWO_PI - c1 - c2))
        magic = 1.5 * 2.0 ** 23

        with nc.Block() as block:
            @block.tensor
            def _(pe):
                with pe.Fori(0, B) as b:
                    pe.wait_ge(L["now"].sem, L["now"].at(b, 1))
                    pe.wait_ge(L["masked"].sem, L["masked"].at(b, 0))
                    for i in range(2):
                        for j in range(FG):
                            pe.matmul(pe4[:, i * FG + j, :], w(("wq", "wk")[i], j * P, (j + 1) * P), xn[:, :],
                                      start=True, stop=True).then_inc(L["proj"].sem, 1)
                    pe.wait_ge(L["states_sb"].sem, L["states_sb"].at(b, 0))
                    pe.wait_ge(L["done"].sem, L["done"].at(b, 0))
                    for i, (n, ps) in enumerate((("wv", small), ("wu", pout))):
                        for t in range(TT):
                            pe.matmul(ps[:, t * P:(t + 1) * P], xn[:, t * P:(t + 1) * P], w(n),
                                      start=True, stop=True).then_inc(L["vu"].sem, 1)
                    for j in range(FG):
                        pe.wait_ge(L["rot"].sem, L["rot"].at(b, FG + j + 1))
                        if j >= 1:
                            pe.wait_ge(L["ktok"].sem, L["ktok"].at(b, j))
                        for t in range(TT):
                            mm = pe.transpose(bank[:, t * P:(t + 1) * P], qk[:, 1, j, t * P:(t + 1) * P], eye)
                        mm.then_inc(L["kturn"].sem, 1)
                    pe.wait_ge(L["vu_sb"].sem, L["vu_sb"].at(b, 2 * TT))
                    pe.wait_ge(L["v_late"].sem, L["v_late"].at(b, 1))
                    for j in range(FG):
                        pe.wait_ge(L["ktok"].sem, L["ktok"].at(b, j + 1))
                        c = slice(j * (D // FG), (j + 1) * (D // FG))
                        for t in range(TT):
                            others = [o for o in range(TT) if o != t]
                            at = (j * TT + t) * (D // FG)
                            for o in others:
                                mm = pe.matmul(small[:, at:at + D // FG], ktok[:, j, o, :],
                                               (v_late if o < t else v)[:, o, c],
                                               start=o == others[0], stop=o == others[-1])
                        mm.then_inc(L["states"].sem, 1)
                    for j in range(FG):
                        pe.wait_ge(L["rot"].sem, L["rot"].at(b, FG + j + 1))
                        for h in range(HG):
                            r = slice(32 * h, 32 * h + 32)
                            if j == 0:
                                pe.wait_ge(L["feats"].sem, L["feats"].at(b, 2 * FG))
                            else:
                                pe.wait_ge(L["masked"].sem, L["masked"].at(b, h + 1))
                            for t in range(TT):
                                tk = slice(t * P, (t + 1) * P)
                                mm = pe.matmul(pe4[:, h, tk], qk[r, 1, j, tk], qk[r, 0, j, tk], start=True, stop=True)
                            mm.then_inc(L["energy"].sem, 1)
                    pe.wait_ge(L["outs"].sem, L["outs"].at(b, 0))
                    pe.wait_ge(L["states_sb"].sem, L["states_sb"].at(b, FG))
                    pe.wait_ge(L["masked"].sem, L["masked"].at(b, NSTEP))
                    for t in range(TT):
                        for j in range(FG):
                            at = j * (D // FG)
                            pe.matmul(pmix[:, t, at:at + D // FG], qk[:, 0, j, t * P:(t + 1) * P], state[:, j, t, :],
                                      start=True, stop=True, skip_group_check=True)
                            for h in range(HG):
                                hh = j * HG + h
                                mm = pe.matmul(pmix[:, t, hh * LHD:(hh + 1) * LHD], energy[:, hh, t * P:(t + 1) * P],
                                               v[:, t, hh * LHD:(hh + 1) * LHD], start=False, stop=True,
                                               skip_group_check=True)
                    mm.then_inc(L["mixed"].sem, 1)
                    pe.wait_ge(L["outs"].sem, L["outs"].at(b, TT))
                    for t in range(TT):
                        mm = pe.transpose(bank[:, t * P:(t + 1) * P], outs[:, t, :], eye)
                    mm.then_inc(L["turned"].sem, 1)
                    pe.wait_ge(L["outs_sb"].sem, L["outs_sb"].at(b, 1))
                    pe.matmul(pout[:, :], w("wo"), outs_t[:, :], start=True, stop=True).then_inc(L["projected"].sem, 1)

            @block.scalar
            def _(act):
                for h in range(LH):
                    act.activation(masks[:, h, :], core.w("const", "upper"), ACT.Exp, scale=w("slope", h, h + 1))\
                        .then_inc(L["masks"].sem, 1)
                act.activation(growth[:, :], w("slope_cols"), ACT.Exp).then_inc(L["vscale"].sem, 1)
                for j in range(FG):
                    act.wait_ge(L["angle"].sem, L["angle"].at(0, 8 * (j + 1)))
                    act.activation(table[:, j, :], turns[:, j, :], ACT.Sin).then_inc(L["table"].sem, 1)
                with act.Fori(0, B) as b:
                    for i in range(2):
                        for j in range(FG):
                            n = i * FG + j
                            act.wait_ge(L["proj"].sem, L["proj"].at(b, n + 1))
                            act.wait_ge(L["rot"].sem, L["rot"].at(b, 0))
                            act.activation(feats[:, i, j, :], pe4[:, n, :], ACT.Silu,
                                           bias=w(("bq", "bk")[i], j, j + 1)).then_inc(L["feats"].sem, 1)
                    for j in range(FG):
                        act.wait_ge(L["kturn"].sem, L["kturn"].at(b, j + 1))
                        act.activation(ktok[:, j, :, :], bank[:, :].rearrange("p (t c) -> p t c", t=TT), ACT.Copy)\
                            .then_inc(L["ktok"].sem, 1)
                    for t in range(TT):
                        act.wait_ge(L["mixed"].sem, L["mixed"].at(b, 1))
                        if t:
                            act.wait_ge(L["squares"].sem, L["squares"].at(b, t))
                        act.activation(square[:, :], pmix[:, t, :], ACT.Square, accum_out=sums[:, 0, t:t + 1])\
                            .then_inc(L["squares"].sem, 1)
                    act.wait_ge(L["turned"].sem, L["turned"].at(b, 1))
                    act.activation(outs_t[:, :], bank[:, :], ACT.Copy).then_inc(L["outs_sb"].sem, 1)

            @block.vector
            def _(dve):
                for j in range(FG):
                    t0, t1 = turns[:, j, :], feats[:, 0, 0, :]
                    dve.tensor_scalar(t0, core.w("const", "token"), w("theta", j, j + 1), None, ALU.mult)\
                        .then_inc(L["angle"].sem, 1)
                    dve.wait_ge(L["angle"].sem, L["angle"].at(0, 8 * j + 1))
                    dve.tensor_scalar(t1, t0, w("shift", j, j + 1), 1.0 / TWO_PI, ALU.add, ALU.mult)\
                        .then_inc(L["angle"].sem, 1)
                    dve.wait_ge(L["angle"].sem, L["angle"].at(0, 8 * j + 2))
                    dve.tensor_scalar(t1, t1, magic, magic, ALU.add, ALU.subtract).then_inc(L["angle"].sem, 1)
                    for n, cc in enumerate((c1, c2, c3)):
                        dve.wait_ge(L["angle"].sem, L["angle"].at(0, 8 * j + 3 + n))
                        dve.scalar_tensor_tensor(out=t0, in0=t1, scalar=-cc, in1=t0, op0=ALU.mult, op1=ALU.add)\
                            .then_inc(L["angle"].sem, 1)
                    dve.wait_ge(L["angle"].sem, L["angle"].at(0, 8 * j + 6))
                    dve.tensor_scalar(t0, t0, w("shift", j, j + 1), float(np.float32(3.1415925)), ALU.add, ALU.min)\
                        .then_inc(L["angle"].sem, 1)
                    dve.wait_ge(L["angle"].sem, L["angle"].at(0, 8 * j + 7))
                    dve.tensor_scalar(t0, t0, -float(np.float32(3.1415925)), None, ALU.max).then_inc(L["angle"].sem, 1)
                dve.wait_ge(L["masks"].sem, L["masks"].at(0, LH))
                dve.wait_ge(L["vscale"].sem, L["vscale"].at(0, 1))
                dve.wait_ge(L["table"].sem, L["table"].at(0, FG))
                with dve.Fori(0, B) as b:
                    take_normed(dve, L, b, xn[:, :])
                    dve.wait_ge(L["outs"].sem, L["outs"].at(b, 0))
                    for i, (to, ps, bias) in enumerate(((v, small, "bv"), (u, pout, "bu"))):
                        for t in range(TT):
                            dve.wait_ge(L["vu"].sem, L["vu"].at(b, TT * (i + 1)))
                            dve.tensor_tensor(to[:, t, :], ps[:, t * P:(t + 1) * P], w(bias), ALU.add)\
                                .then_inc(L["vu_sb"].sem, 1)
                    dve.wait_ge(L["vu_sb"].sem, L["vu_sb"].at(b, TT))
                    dve.tensor_tensor(v_late[:, :, :], v[:, :, :],
                                      growth[:, :].unsqueeze(1).to_broadcast([P, TT, D]), ALU.mult)\
                        .then_inc(L["v_late"].sem, 1)
                    for i in range(2):
                        for j in range(FG):
                            dve.wait_ge(L["feats"].sem, L["feats"].at(b, i * FG + j + 1))
                            dve.tensor_tensor(qk[:, i, j, :], feats[:, i, j, :], table[:, j, :], ALU.mult)\
                                .then_inc(L["rot"].sem, 1)
                    for j in range(FG):
                        dve.wait_ge(L["states"].sem, L["states"].at(b, FG))
                        W = TT * (D // FG)
                        dve.tensor_tensor(state[:, j, :, :],
                                          small[:, j * W:(j + 1) * W].rearrange("p (t c) -> p t c", t=TT),
                                          core.w("const", "block4").unsqueeze(1).to_broadcast([P, TT, D // FG]),
                                          ALU.mult).then_inc(L["states_sb"].sem, 1)
                    for s in range(NSTEP):
                        dve.wait_ge(L["energy"].sem, L["energy"].at(b, s + 1))
                        dve.tensor_tensor(energy[:, s, :].rearrange("p (t c) -> p t c", t=TT),
                                          pe4[:, s % HG, :].rearrange("p (t c) -> p t c", t=TT),
                                          masks[:, s, :].unsqueeze(1).to_broadcast([P, TT, P]), ALU.mult)\
                            .then_inc(L["masked"].sem, 1)
                    dve.wait_ge(L["squares"].sem, L["squares"].at(b, TT))
                    dve.tensor_scalar(sums[:, 1, :], sums[:, 0, :], 1.0 / D, 1e-6, ALU.mult, ALU.add)\
                        .then_inc(L["inv"].sem, 1)
                    dve.wait_ge(L["inv"].sem, L["inv"].at(b, 2))
                    for t in range(TT):
                        dve.wait_ge(L["vu_sb"].sem, L["vu_sb"].at(b, 2 * TT))
                        dve.scalar_tensor_tensor(out=outs[:, t, :], in0=pmix[:, t, :], scalar=sums[:, 2, t:t + 1],
                                                 in1=u[:, t, :], op0=ALU.mult, op1=ALU.mult).then_inc(L["outs"].sem, 1)
                    dve.wait_ge(L["projected"].sem, L["projected"].at(b, 1))
                    dve.scalar_tensor_tensor(out=core.batch(b), in0=pout[:, :], scalar=w("bo"), in1=core.batch(b),
                                             op0=ALU.add, op1=ALU.add).then_inc(L["done"].sem, 1)

            @block.gpsimd
            def _(pool):
                with pool.Fori(0, B) as b:
                    pool.wait_ge(L["inv"].sem, L["inv"].at(b, 1))
                    pool.tensor_tensor(sums[:, 2, :], sums[:, 1, :], core.w("const", "minus_half", 0, TT), ALU.pow)\
                        .then_inc(L["inv"].sem, 1)
    L.close()

DFF = 512
FT = DFF // P


def quantise(nc, core):
    L = Layer(nc, "quant", core, ["bitffn"], rowsum=2, total=1, gamma=2, scaled=2, rounded=2, clipped=2)
    with L.ctx:
        rowsum = L.sb("rowsums", [P, 2])
        gamma = L.sb("gammas", [P, 2])
        total = L.ps("totals", [P, 2])
        mats = [core.w("bitffn", "w1"), core.w("bitffn", "w2")]
        magic = 1.5 * 2.0 ** 23
        with nc.Block() as block:
            @block.vector
            def _(dve):
                for i, w in enumerate(mats):
                    dve.tensor_reduce(rowsum[:, i:i + 1], w, AX.X, ALU.add, apply_absolute_value=True)\
                        .then_inc(L["rowsum"].sem, 1)
                dve.wait_ge(L["total"].sem, L["total"].at(0, 1))
                dve.tensor_scalar(gamma[:, :], total[:, :], 1.0 / (DFF * D), 1e-5, ALU.mult, ALU.add)\
                    .then_inc(L["gamma"].sem, 1)
                dve.wait_ge(L["gamma"].sem, L["gamma"].at(0, 1))
                dve.reciprocal(gamma[:, :], gamma[:, :]).then_inc(L["gamma"].sem, 1)
                dve.wait_ge(L["gamma"].sem, L["gamma"].at(0, 2))
                for i, w in enumerate(mats):
                    dve.tensor_scalar(w, w, gamma[:, i:i + 1], None, ALU.mult).then_inc(L["scaled"].sem, 1)
                    dve.wait_ge(L["scaled"].sem, L["scaled"].at(0, i + 1))
                    dve.tensor_scalar(w, w, magic, magic, ALU.add, ALU.subtract).then_inc(L["rounded"].sem, 1)
                    dve.wait_ge(L["rounded"].sem, L["rounded"].at(0, i + 1))
                    dve.tensor_scalar(w, w, 1.0, -1.0, ALU.min, ALU.max).then_inc(L["clipped"].sem, 1)

            @block.tensor
            def _(pe):
                pe.wait_ge(L["rowsum"].sem, L["rowsum"].at(0, 2))
                pe.matmul(total[:, :], core.w("const", "ones"), rowsum[:, :], start=True, stop=True)\
                    .then_inc(L["total"].sem, 1)
    L.close()


def bit_ffn(nc, core, name):
    L = Layer(nc, name, core, ["bitffn"], **NEXT, up=FT, hidden=FT, down=FT, done=1)
    with L.ctx:
        xn = L.sb("xn", [P, S])
        h = L.sb("h", [P, 2, S])
        out = L.ps("out", [P, S])
        up = L.ps("up", [P, 2, S])
        w1, w2 = core.w("bitffn", "w1"), core.w("bitffn", "w2")
        b1, b2 = core.w("bitffn", "b1"), core.w("bitffn", "b2")
        def down(pe, b, m):
            pe.wait_ge(L["hidden"].sem, L["hidden"].at(b, m + 1))
            if m == 0:
                pe.wait_ge(L["done"].sem, L["done"].at(b, 0))
            pe.matmul(out[:, :], w2[:, m * P:(m + 1) * P], h[:, m % 2, :], start=m == 0, stop=m == FT - 1)\
                .then_inc(L["down"].sem, 1)

        with nc.Block() as block:
            @block.tensor
            def _(pe):
                with pe.Fori(0, B) as b:
                    pe.wait_ge(L["now"].sem, L["now"].at(b, 1))
                    for m in range(FT):
                        pe.wait_ge(L["hidden"].sem, L["hidden"].at(b, max(m - 1, 0)))
                        pe.matmul(up[:, m % 2, :], w1[:, m * P:(m + 1) * P], xn[:, :], start=True, stop=True)\
                            .then_inc(L["up"].sem, 1)
                        if m >= 1:
                            down(pe, b, m - 1)
                    down(pe, b, FT - 1)

            @block.scalar
            def _(act):
                with act.Fori(0, B) as b:
                    for m in range(FT):
                        act.wait_ge(L["up"].sem, L["up"].at(b, m + 1))
                        act.wait_ge(L["down"].sem, L["down"].at(b, max(m - 1, 0)))
                        act.activation(h[:, m % 2, :], up[:, m % 2, :], ACT.Relu, bias=b1[:, m:m + 1])\
                            .then_inc(L["hidden"].sem, 1)

            @block.vector
            def _(dve):
                with dve.Fori(0, B) as b:
                    take_normed(dve, L, b, xn[:, :])
                    dve.wait_ge(L["down"].sem, L["down"].at(b, FT))
                    dve.scalar_tensor_tensor(out=core.batch(b), in0=out[:, :], scalar=b2, in1=core.batch(b),
                                             op0=ALU.add, op1=ALU.add).then_inc(L["done"].sem, 1)

    L.close()

SH = 32
SLOTS = 64
RMS_EPS = 1.1920929e-07


def landmark_layer(nc, core, name):
    NA = 2 * TT
    L = Layer(nc, name, core, ["slr"], **NEXT, lam=2,
              sq=2, var=2, eps=2, rstd=2, diag=2, spread=2,
              xn=2,
              route=3,
              hid=1, hid_sb=1, wide=1, logit=1, lmax=3, lexp=1, lsum=3,
              decayed=1, ema=1,
              qk=2, qk_sb=2, v_ps=1, v_sb=1,
              scores=NA, top=NA, shift=NA, probs=NA, inv=2 * TT, second=TT, mixp=TT,
              turn=TT, turn_sb=TT, averaged=1, ctx_sb=1, slr=1, joined=1,
              qwide=1, lscore=1, attn=5, aexp=1, arc=2,
              mix=1, mix_sb=1, scaled=1, result=1,
              mean=1, bus=3, bus_sb=3, final=1, done=1)
    with L.ctx:
        g = "slr"
        w = lambda n, *a: core.w(g, n, *a)
        xl, xn, sq = (L.sb(n, [P, S]) for n in ("xl", "xn", "sq"))
        small = L.sb("small", [P, 2, 2, TT])
        diag = L.sb("diag", [P, TT, P])
        col = L.sb("col", [P, 32])
        wide = L.sb("wide", [P, P])
        probs3 = L.sb("probs3", [P, 8])
        lam_row = L.sb("lam_row", [P, S])
        drive, ema, joined = (L.sb(n, [P, S]) for n in ("drive", "ema", "joined"))
        qk = L.sb("qk", [2 * SH, 2, S])
        v = L.sb("v", [P, TT, SH])
        stats = L.sb("stats", [P, 4, NA])
        probs = L.sb("probs", [P, NA, S])
        turned = L.sb("turned", [P, TT, S])
        ctx_t = L.sb("ctx_t", [SH, S])
        qwide = L.sb("qwide", [P, P])
        attn = L.sb("attn", [P, 3, SLOTS])
        mix, result = L.sb("mix", [P, S]), L.sb("result", [P, S])
        bank, ps_small, pa, pb, pc, pt, pu, out = (L.ps(n, [P, S]) for n in
                                                  ("bank", "ps_small", "pa", "pb", "pc", "pt", "pu", "out"))
        eye = core.w("const", "eye")
        ones = core.w("const", "ones")
        C_MEAN, C_HID, C_P, C_MX, C_SUM, C_INV, C_PMF, C_LAM1, C_AMX, C_ASUM, C_AINV, C_ARC, C_M2, C_B0, C_B1, C_B2, \
            C_NMX, C_SHIFT = range(18)

        def c(i):
            return col[:, i:i + 1]

        def rms_tensor(pe, b, i):
            pe.wait_ge(L["sq"].sem, L["sq"].at(b, i + 1))
            for t in range(TT):
                mm = pe.matmul(ps_small[:, 8 + TT * i + t:9 + TT * i + t], sq[:, t * P:(t + 1) * P],
                               core.w("const", "mean", 0, 1), start=True, stop=True)
            mm.then_inc(L["var"].sem, 1)
            pe.wait_ge(L["diag"].sem, L["diag"].at(b, i + 1))
            pe.matmul(pa[:, :], ones, diag[:, :, :], start=True, stop=True).then_inc(L["spread"].sem, 1)

        def rms_vector(dve, b, i):
            dve.wait_ge(L["var"].sem, L["var"].at(b, i + 1))
            at = 8 + TT * i
            dve.tensor_scalar(small[:, i, 0, :], ps_small[:, at:at + TT], RMS_EPS, None, ALU.add)\
                .then_inc(L["eps"].sem, 1)
            dve.wait_ge(L["rstd"].sem, L["rstd"].at(b, i + 1))
            dve.wait_ge(L["spread"].sem, L["spread"].at(b, i))
            dve.tensor_tensor(diag[:, :, :], eye.unsqueeze(1).to_broadcast([P, TT, P]),
                              small[:, i, 1, :].unsqueeze(2).to_broadcast([P, TT, P]), ALU.mult)\
                .then_inc(L["diag"].sem, 1)

        def rms_pool(pool, b, i):
            pool.wait_ge(L["eps"].sem, L["eps"].at(b, i + 1))
            pool.tensor_tensor(small[:, i, 1, :], small[:, i, 0, :], core.w("const", "minus_half", 0, TT), ALU.pow)\
                .then_inc(L["rstd"].sem, 1)

        sc = 1.0 / float(SH) ** 0.5
        scd = 1.0 / float(D) ** 0.5

        def differ(dve, b, t):
            n = 2 * t
            dve.wait_ge(L["probs"].sem, L["probs"].at(b, n + 2))
            dve.reciprocal(stats[:, 3, n:n + 2], stats[:, 2, n:n + 2]).then_inc(L["inv"].sem, 1)
            dve.wait_ge(L["inv"].sem, L["inv"].at(b, 2 * t + 1))
            dve.tensor_tensor(stats[:, 3, n + 1:n + 2], stats[:, 3, n + 1:n + 2], w("slr_lam"), ALU.mult)\
                .then_inc(L["inv"].sem, 1)
            dve.wait_ge(L["inv"].sem, L["inv"].at(b, 2 * t + 2))
            dve.tensor_scalar(probs[:, n + 1, :], probs[:, n + 1, :], stats[:, 3, n + 1:n + 2], None, ALU.mult)\
                .then_inc(L["second"].sem, 1)
            dve.wait_ge(L["second"].sem, L["second"].at(b, t + 1))
            dve.scalar_tensor_tensor(out=probs[:, n, :], in0=probs[:, n, :], scalar=stats[:, 3, n:n + 1],
                                     in1=probs[:, n + 1, :], op0=ALU.mult, op1=ALU.subtract).then_inc(L["mixp"].sem, 1)

        with nc.Block() as block:
            @block.tensor
            def _(pe):
                with pe.Fori(0, B) as b:
                    rms_tensor(pe, b, 0)
                    pe.wait_ge(L["xn"].sem, L["xn"].at(b, 2))
                    for i, n in enumerate(("wq", "wk")):
                        pe.matmul((pb, pc)[i][0:2 * SH, :], w(n), xn[:, :], start=True, stop=True)\
                            .then_inc(L["qk"].sem, 1)
                    for t in range(TT):
                        mm = pe.matmul(pt[:, t * SH:(t + 1) * SH], xn[:, t * P:(t + 1) * P], w("wv"),
                                       start=True, stop=True)
                    mm.then_inc(L["v_ps"].sem, 1)
                    pe.wait_ge(L["route"].sem, L["route"].at(b, 1))
                    pe.matmul(pu[0:64, 0:1], w("r1"), c(C_MEAN), start=True, stop=True).then_inc(L["hid"].sem, 1)
                    pe.wait_ge(L["wide"].sem, L["wide"].at(b, 1))
                    pe.matmul(pu[:, 4:7], wide[0:64, :], w("r2"), start=True, stop=True).then_inc(L["logit"].sem, 1)
                    pe.wait_ge(L["qwide"].sem, L["qwide"].at(b, 1))
                    pe.wait_ge(L["lmax"].sem, L["lmax"].at(b, 1))
                    pe.matmul(pu[:, 64:64 + SLOTS], qwide[:, :], w("landmarks_t"), start=True, stop=True)\
                        .then_inc(L["lscore"].sem, 1)
                    pe.wait_ge(L["qk_sb"].sem, L["qk_sb"].at(b, 2))
                    for n in range(NA):
                        t, i = divmod(n, 2)
                        r = slice(i * SH, (i + 1) * SH)
                        if n >= 2:
                            pe.wait_ge(L["probs"].sem, L["probs"].at(b, n - 1))
                        pe.matmul((pb, pc)[i][:, :], qk[r, 0, t * P:(t + 1) * P], qk[r, 1, :],
                                  start=True, stop=True).then_inc(L["scores"].sem, 1)
                    pe.wait_ge(L["v_sb"].sem, L["v_sb"].at(b, 1))
                    for t in range(TT):
                        pe.wait_ge(L["mixp"].sem, L["mixp"].at(b, t + 1))
                        ps = (pt, out)[t % 2]
                        if t >= 2:
                            pe.wait_ge(L["turn_sb"].sem, L["turn_sb"].at(b, t - 1))
                        if t == 1:
                            pe.wait_ge(L["done"].sem, L["done"].at(b, 0))
                        for o in range(TT):
                            mm = pe.transpose(ps[:, o * P:(o + 1) * P], probs[:, 2 * t, o * P:(o + 1) * P], eye)
                        mm.then_inc(L["turn"].sem, 1)
                    pe.wait_ge(L["turn_sb"].sem, L["turn_sb"].at(b, TT))
                    for o in range(TT):
                        mm = pe.matmul(pb[0:SH, :], v[:, o, :], turned[:, o, :], start=o == 0, stop=o == TT - 1)
                    mm.then_inc(L["averaged"].sem, 1)
                    pe.wait_ge(L["ctx_sb"].sem, L["ctx_sb"].at(b, 1))
                    pe.matmul(pc[:, :], w("wo"), ctx_t[:, :], start=True, stop=True).then_inc(L["slr"].sem, 1)
                    pe.matmul(out[:, :], w("mix2"), xn[:, :], start=True, stop=False)
                    pe.wait_ge(L["arc"].sem, L["arc"].at(b, 2))
                    pe.matmul(out[:, :], w("mix1"), joined[:, :], start=False, stop=True).then_inc(L["mix"].sem, 1)
                    rms_tensor(pe, b, 1)
                    pe.wait_ge(L["mean"].sem, L["mean"].at(b, 1))
                    for i, n in enumerate(("compress", "publish", "expand")):
                        if i:
                            pe.wait_ge(L["bus_sb"].sem, L["bus_sb"].at(b, i))
                        pe.matmul(pu[:, 200 + i:201 + i], w(n), c((C_M2, C_B0, C_B1)[i]), start=True, stop=True)\
                            .then_inc(L["bus"].sem, 1)

            @block.scalar
            def _(act):
                with act.Fori(0, B) as b:
                    act.wait_ge(L["now"].sem, L["now"].at(b, 1))
                    act.activation(sq[:, :], xl[:, :], ACT.Square).then_inc(L["sq"].sem, 1)
                    for i in range(2):
                        act.wait_ge(L["qk"].sem, L["qk"].at(b, i + 1))
                        act.activation(qk[:, i, :], (pb, pc)[i][0:2 * SH, :], ACT.Copy).then_inc(L["qk_sb"].sem, 1)
                    act.wait_ge(L["v_ps"].sem, L["v_ps"].at(b, 1))
                    act.activation(v[:, :, :], pt[:, 0:TT * SH].rearrange("p (t d) -> p t d", t=TT), ACT.Copy)\
                        .then_inc(L["v_sb"].sem, 1)
                    act.wait_ge(L["hid"].sem, L["hid"].at(b, 1))
                    act.activation(col[0:64, C_HID:C_HID + 1], pu[0:64, 0:1], ACT.Silu, scale=1.0 / S)\
                        .then_inc(L["hid_sb"].sem, 1)
                    act.wait_ge(L["lmax"].sem, L["lmax"].at(b, 3))
                    act.activation(probs3[:, 4:7], probs3[:, 0:3], ACT.Exp, bias=c(C_NMX),
                                   accum_out=c(C_SUM)).then_inc(L["lexp"].sem, 1)
                    for n in range(NA):
                        act.wait_ge(L["shift"].sem, L["shift"].at(b, n + 1))
                        act.activation(probs[:, n, :], (pb, pc)[n % 2][:, :], ACT.Exp, bias=stats[:, 1, n:n + 1],
                                       scale=sc, accum_out=stats[:, 2, n:n + 1]).then_inc(L["probs"].sem, 1)
                    act.wait_ge(L["attn"].sem, L["attn"].at(b, 2))
                    act.activation(attn[:, 0, :], attn[:, 2, :], ACT.Exp, bias=c(C_SHIFT), scale=scd,
                                   accum_out=c(C_ASUM)).then_inc(L["aexp"].sem, 1)
                    for t in range(TT):
                        act.wait_ge(L["turn"].sem, L["turn"].at(b, t + 1))
                        act.activation(turned[:, :, t * P:(t + 1) * P],
                                       (pt, out)[t % 2][:, :].rearrange("p (o c) -> p o c", o=TT), ACT.Copy)\
                            .then_inc(L["turn_sb"].sem, 1)
                    act.wait_ge(L["averaged"].sem, L["averaged"].at(b, 1))
                    act.activation(ctx_t[:, :], pb[0:SH, :], ACT.Copy).then_inc(L["ctx_sb"].sem, 1)
                    act.wait_ge(L["mix"].sem, L["mix"].at(b, 1))
                    act.activation(sq[:, :], out[:, :], ACT.Square).then_inc(L["sq"].sem, 1)
                    act.activation(mix[:, :], out[:, :], ACT.Copy).then_inc(L["mix_sb"].sem, 1)
                    for i in range(3):
                        act.wait_ge(L["bus"].sem, L["bus"].at(b, i + 1))
                        act.activation(c((C_B0, C_B1, C_B2)[i]), pu[:, 200 + i:201 + i], ACT.Copy,
                                       scale=(1.0 / S, 1.0, 0.1)[i]).then_inc(L["bus_sb"].sem, 1)

            @block.vector
            def _(dve):
                dve.tensor_copy(lam_row[:, :], w("lam").to_broadcast([P, S])).then_inc(L["lam"].sem, 1)
                dve.tensor_scalar(c(C_LAM1), w("lam"), -1.0, 1.0, ALU.mult, ALU.add).then_inc(L["lam"].sem, 1)
                dve.wait_ge(L["lam"].sem, L["lam"].at(0, 2))
                with dve.Fori(0, B) as b:
                    take_normed(dve, L, b, xl[:, :])
                    rms_vector(dve, b, 0)
                    dve.wait_ge(L["spread"].sem, L["spread"].at(b, 1))
                    dve.tensor_tensor(mix[:, :], xl[:, :], pa[:, :], ALU.mult).then_inc(L["xn"].sem, 1)
                    dve.wait_ge(L["xn"].sem, L["xn"].at(b, 1))
                    dve.tensor_scalar(xn[:, :], mix[:, :], w("norm_in"), None, ALU.mult).then_inc(L["xn"].sem, 1)
                    dve.wait_ge(L["xn"].sem, L["xn"].at(b, 2))
                    dve.tensor_reduce(c(C_MEAN), xn[:, :], AX.X, ALU.add).then_inc(L["route"].sem, 1)
                    dve.tensor_scalar(drive[:, :], xn[:, :], c(C_LAM1), None, ALU.mult).then_inc(L["decayed"].sem, 1)
                    dve.tensor_scalar(qwide[:, :], ones, xn[:, S - 1:S], None, ALU.mult).then_inc(L["qwide"].sem, 1)
                    dve.wait_ge(L["decayed"].sem, L["decayed"].at(b, 1))
                    dve.tensor_tensor_scan(ema[:, :], lam_row[:, :], drive[:, :], 0.0, ALU.mult, ALU.add)\
                        .then_inc(L["ema"].sem, 1)
                    dve.wait_ge(L["hid_sb"].sem, L["hid_sb"].at(b, 1))
                    dve.tensor_scalar(wide[0:64, :], ones[0:64, :], col[0:64, C_HID:C_HID + 1], None, ALU.mult)\
                        .then_inc(L["wide"].sem, 1)
                    dve.wait_ge(L["logit"].sem, L["logit"].at(b, 1))
                    dve.tensor_tensor(probs3[:, 0:3], pu[:, 4:7], w("r2b"), ALU.add).then_inc(L["lmax"].sem, 1)
                    dve.wait_ge(L["lmax"].sem, L["lmax"].at(b, 1))
                    dve.tensor_reduce(c(C_MX), probs3[:, 0:3], AX.X, ALU.max).then_inc(L["lmax"].sem, 1)
                    dve.wait_ge(L["lmax"].sem, L["lmax"].at(b, 2))
                    dve.tensor_scalar(c(C_NMX), c(C_MX), -1.0, None, ALU.mult).then_inc(L["lmax"].sem, 1)
                    dve.wait_ge(L["lexp"].sem, L["lexp"].at(b, 1))
                    dve.reciprocal(c(C_INV), c(C_SUM)).then_inc(L["lsum"].sem, 1)
                    dve.wait_ge(L["lsum"].sem, L["lsum"].at(b, 1))
                    dve.tensor_scalar(probs3[:, 4:7], probs3[:, 4:7], c(C_INV), None, ALU.mult).then_inc(L["lsum"].sem, 1)
                    dve.wait_ge(L["lsum"].sem, L["lsum"].at(b, 2))
                    dve.tensor_tensor(c(C_PMF), probs3[:, 5:6], probs3[:, 6:7], ALU.add).then_inc(L["lsum"].sem, 1)
                    dve.wait_ge(L["lscore"].sem, L["lscore"].at(b, 1))
                    dve.tensor_copy(attn[:, 2, :], pu[:, 64:64 + SLOTS]).then_inc(L["route"].sem, 1)
                    dve.wait_ge(L["route"].sem, L["route"].at(b, 2))
                    dve.tensor_reduce(c(C_AMX), attn[:, 2, :], AX.X, ALU.max).then_inc(L["attn"].sem, 1)
                    dve.wait_ge(L["attn"].sem, L["attn"].at(b, 1))
                    dve.tensor_scalar(c(C_SHIFT), c(C_AMX), -scd, None, ALU.mult).then_inc(L["attn"].sem, 1)
                    for n in range(NA):
                        dve.wait_ge(L["scores"].sem, L["scores"].at(b, n + 1))
                        dve.tensor_reduce(stats[:, 0, n:n + 1], (pb, pc)[n % 2][:, :], AX.X, ALU.max)\
                            .then_inc(L["top"].sem, 1)
                        dve.wait_ge(L["top"].sem, L["top"].at(b, n + 1))
                        dve.tensor_scalar(stats[:, 1, n:n + 1], stats[:, 0, n:n + 1], -sc, None, ALU.mult)\
                            .then_inc(L["shift"].sem, 1)
                        if n % 2 == 1 and n >= 3:
                            differ(dve, b, n // 2 - 1)
                    differ(dve, b, TT - 1)
                    dve.wait_ge(L["aexp"].sem, L["aexp"].at(b, 1))
                    dve.reciprocal(c(C_AINV), c(C_ASUM)).then_inc(L["attn"].sem, 1)
                    dve.wait_ge(L["attn"].sem, L["attn"].at(b, 3))
                    dve.tensor_tensor(attn[:, 1, :], attn[:, 0, :], w("landmarks_t"), ALU.mult).then_inc(L["attn"].sem, 1)
                    dve.wait_ge(L["attn"].sem, L["attn"].at(b, 4))
                    dve.tensor_reduce(c(C_ARC), attn[:, 1, :], AX.X, ALU.add).then_inc(L["attn"].sem, 1)
                    dve.wait_ge(L["attn"].sem, L["attn"].at(b, 5))
                    dve.tensor_scalar(c(C_ARC), c(C_ARC), c(C_AINV), probs3[:, 6:7], ALU.mult, ALU.mult)\
                        .then_inc(L["route"].sem, 1)
                    dve.wait_ge(L["slr"].sem, L["slr"].at(b, 1))
                    dve.wait_ge(L["lsum"].sem, L["lsum"].at(b, 3))
                    dve.scalar_tensor_tensor(out=joined[:, :], in0=pc[:, :], scalar=c(C_PMF), in1=ema[:, :],
                                             op0=ALU.mult, op1=ALU.add).then_inc(L["arc"].sem, 1)
                    dve.wait_ge(L["arc"].sem, L["arc"].at(b, 1))
                    dve.wait_ge(L["route"].sem, L["route"].at(b, 3))
                    dve.tensor_tensor(joined[:, S - 1:S], joined[:, S - 1:S], c(C_ARC), ALU.add).then_inc(L["arc"].sem, 1)
                    rms_vector(dve, b, 1)
                    dve.wait_ge(L["spread"].sem, L["spread"].at(b, 2))
                    dve.wait_ge(L["mix_sb"].sem, L["mix_sb"].at(b, 1))
                    dve.tensor_tensor(joined[:, :], mix[:, :], pa[:, :], ALU.mult).then_inc(L["scaled"].sem, 1)
                    dve.wait_ge(L["scaled"].sem, L["scaled"].at(b, 1))
                    dve.scalar_tensor_tensor(out=result[:, :], in0=joined[:, :], scalar=w("norm_out"), in1=xl[:, :],
                                             op0=ALU.mult, op1=ALU.add).then_inc(L["result"].sem, 1)
                    dve.wait_ge(L["result"].sem, L["result"].at(b, 1))
                    dve.tensor_reduce(c(C_M2), result[:, :], AX.X, ALU.add).then_inc(L["mean"].sem, 1)
                    dve.wait_ge(L["bus_sb"].sem, L["bus_sb"].at(b, 3))
                    dve.scalar_tensor_tensor(out=core.batch(b), in0=result[:, :], scalar=c(C_B2), in1=core.batch(b),
                                             op0=ALU.add, op1=ALU.add).then_inc(L["done"].sem, 1)

            @block.gpsimd
            def _(pool):
                with pool.Fori(0, B) as b:
                    rms_pool(pool, b, 0)
                    rms_pool(pool, b, 1)
    L.close()


def pair_attention(nc, core, name):
    L = Layer(nc, name, core, ["pairs"], **NEXT, prep=6, bdiff=2, expb=1,
              qkv=3,
              soft=3,
              partner=2,
              kv=2,
              sums=4,
              terms=4, joined=2, inverse=1, mixed=1,
              projected=1, done=1)
    with L.ctx:
        g = "pairs"
        xn, q, k, v, q2, k2 = (L.sb(n, [P, S]) for n in ("xn", "q", "k", "v", "q2", "k2"))
        kv, kv2, sa, sbb, sn, sn2 = (L.sb(n, [P, S]) for n in ("kv", "kv2", "sa", "sbb", "sn", "sn2"))
        mixed = L.sb("mixed", [P, S])
        wq, wk = L.sb("wq", [P, D]), L.sb("wk", [P, D])
        col = L.sb("col", [P, 5])
        ps = [L.ps(n, [P, S]) for n in ("ps_q", "ps_k", "ps_v")]
        out = L.ps("out", [P, S])
        ones_row = core.w("const", "ones_s")
        with nc.Block() as block:
            @block.tensor
            def _(pe):
                pe.wait_ge(L["prep"].sem, L["prep"].at(0, 6))
                with pe.Fori(0, B) as b:
                    pe.wait_ge(L["now"].sem, L["now"].at(b, 1))
                    pe.wait_ge(L["soft"].sem, L["soft"].at(b, 0))
                    for i, w in enumerate((wq[:, :], wk[:, :], core.w(g, "wv"))):
                        pe.matmul(ps[i][:, :], w, xn[:, :], start=True, stop=True).then_inc(L["qkv"].sem, 1)
                    pe.wait_ge(L["mixed"].sem, L["mixed"].at(b, 1))
                    pe.matmul(out[:, :], core.w(g, "wo"), mixed[:, :], start=True, stop=True)\
                        .then_inc(L["projected"].sem, 1)

            @block.scalar
            def _(act):
                act.activation(col[:, 2:3], core.w(g, "beta"), ACT.Exp).then_inc(L["expb"].sem, 1)
                act.wait_ge(L["prep"].sem, L["prep"].at(0, 6))
                with act.Fori(0, B) as b:
                    for i, to in enumerate((q, k)):
                        act.wait_ge(L["qkv"].sem, L["qkv"].at(b, i + 1))
                        act.wait_ge(L["mixed"].sem, L["mixed"].at(b, 0))
                        act.activation(to[:, :], ps[i][:, :], ACT.Sigmoid, bias=col[:, i:i + 1],
                                       scale=col[:, 2:3]).then_inc(L["soft"].sem, 1)
                    act.wait_ge(L["qkv"].sem, L["qkv"].at(b, 3))
                    act.activation(v[:, :], ps[2][:, :], ACT.Identity, bias=core.w(g, "bv")).then_inc(L["soft"].sem, 1)

            @block.vector
            def _(dve):
                for w, to in ((core.w(g, "wq"), wq), (core.w(g, "wk"), wk)):
                    pair = w.rearrange("p (h d) -> p h d", d=2)
                    diff = to[:, :].rearrange("p (h d) -> p h d", d=2)
                    for d in range(2):
                        dve.tensor_tensor(diff[:, :, d], pair[:, :, d], pair[:, :, 1 - d], ALU.subtract)\
                            .then_inc(L["prep"].sem, 1)
                dve.wait_ge(L["expb"].sem, L["expb"].at(0, 1))
                for i, n in enumerate(("bq", "bk")):
                    dve.tensor_tensor(col[:, 3 + i:4 + i], core.w(g, n, 0, 1), core.w(g, n, 1, 2), ALU.subtract)\
                        .then_inc(L["bdiff"].sem, 1)
                    dve.wait_ge(L["bdiff"].sem, L["bdiff"].at(0, i + 1))
                    dve.tensor_tensor(col[:, i:i + 1], col[:, 3 + i:4 + i], col[:, 2:3], ALU.mult).then_inc(L["prep"].sem, 1)
                with dve.Fori(0, B) as b:
                    take_normed(dve, L, b, xn[:, :])
                    dve.wait_ge(L["soft"].sem, L["soft"].at(b, 2))
                    dve.tensor_scalar(q2[:, :], q[:, :], -1.0, 1.0, ALU.mult, ALU.add).then_inc(L["partner"].sem, 1)
                    dve.tensor_scalar(k2[:, :], k[:, :], -1.0, 1.0, ALU.mult, ALU.add).then_inc(L["partner"].sem, 1)
                    dve.tensor_tensor_scan(sn[:, :], ones_row, k[:, :], 0.0, ALU.mult, ALU.add)\
                        .then_inc(L["sums"].sem, 1)
                    dve.wait_ge(L["soft"].sem, L["soft"].at(b, 3))
                    dve.tensor_tensor(kv[:, :], k[:, :], v[:, :], ALU.mult).then_inc(L["kv"].sem, 1)
                    dve.wait_ge(L["partner"].sem, L["partner"].at(b, 2))
                    dve.tensor_tensor(kv2[:, :], k2[:, :], v[:, :], ALU.mult).then_inc(L["kv"].sem, 1)
                    dve.wait_ge(L["kv"].sem, L["kv"].at(b, 1))
                    dve.tensor_tensor_scan(sa[:, :], ones_row, kv[:, :], 0.0, ALU.mult, ALU.add)\
                        .then_inc(L["sums"].sem, 1)
                    dve.wait_ge(L["kv"].sem, L["kv"].at(b, 2))
                    dve.tensor_tensor_scan(sbb[:, :], ones_row, kv2[:, :], 0.0, ALU.mult, ALU.add)\
                        .then_inc(L["sums"].sem, 1)
                    dve.wait_ge(L["sums"].sem, L["sums"].at(b, 1))
                    dve.tensor_tensor_scan(sn2[:, :], ones_row, k2[:, :], 0.0, ALU.mult, ALU.add)\
                        .then_inc(L["sums"].sem, 1)
                    dve.wait_ge(L["sums"].sem, L["sums"].at(b, 4))
                    for to, a, c in ((kv, q, sa), (kv2, q2, sbb), (k, q, sn), (k2, q2, sn2)):
                        dve.tensor_tensor(to[:, :], a[:, :], c[:, :], ALU.mult).then_inc(L["terms"].sem, 1)
                    dve.wait_ge(L["terms"].sem, L["terms"].at(b, 4))
                    dve.tensor_tensor(sn[:, :], k[:, :], k2[:, :], ALU.add).then_inc(L["joined"].sem, 1)
                    dve.tensor_tensor(sa[:, :], kv[:, :], kv2[:, :], ALU.add).then_inc(L["joined"].sem, 1)
                    dve.wait_ge(L["joined"].sem, L["joined"].at(b, 1))
                    dve.reciprocal(sn2[:, :], sn[:, :]).then_inc(L["inverse"].sem, 1)
                    dve.wait_ge(L["joined"].sem, L["joined"].at(b, 2))
                    dve.wait_ge(L["inverse"].sem, L["inverse"].at(b, 1))
                    dve.tensor_tensor(mixed[:, :], sa[:, :], sn2[:, :], ALU.mult).then_inc(L["mixed"].sem, 1)
                    dve.wait_ge(L["projected"].sem, L["projected"].at(b, 1))
                    dve.scalar_tensor_tensor(out=core.batch(b), in0=out[:, :], scalar=core.w(g, "bo"),
                                             in1=core.batch(b), op0=ALU.add, op1=ALU.add).then_inc(L["done"].sem, 1)

    L.close()



def cell(nc, core, name):
    L = Layer(nc, name, core, ["cell"], start=1,
              gates=3,
              opened=3,
              parts=2,
              state=1,
              answer=1,
              answered=1,
              done=1)
    with L.ctx:
        g = "cell"
        c, f, i_, n_, ig, h = (L.sb(k, [P, S]) for k in ("c", "f", "i", "n", "ig", "h"))
        ps = [L.ps(n, [P, S]) for n in ("ps_f", "ps_i", "ps_n")]
        out = L.ps("out", [P, S])


        with nc.Block() as block:
            @block.tensor
            def _(pe):
                with pe.Fori(0, B) as b:
                    pe.wait_ge(L["opened"].sem, L["opened"].at(b, 0))
                    for j, w in enumerate(("wf", "wi", "wc")):
                        pe.matmul(ps[j][:, :], core.w(g, w), core.normed(b), start=True, stop=False)
                    pe.wait_ge(L["state"].sem, L["state"].at(b, 0))
                    pe.wait_ge(L["start"].sem, L["start"].at(0, 1))
                    for j, w in enumerate(("uf", "ui", "uc")):
                        pe.matmul(ps[j][:, :], core.w(g, w), c[:, :], start=False, stop=True)\
                            .then_inc(L["gates"].sem, 1)
                pe.wait_ge(L["state"].sem, L["state"].at(B - 1, 1))
                with pe.Fori(0, B) as b:
                    pe.wait_ge(L["answered"].sem, L["answered"].at(b, 0))
                    pe.matmul(out[:, :], core.w(g, "wo"), core.normed(b), start=True, stop=False)
                    pe.matmul(out[:, :], core.w(g, "uo"), c[:, :], start=False, stop=True)\
                        .then_inc(L["answer"].sem, 1)

            @block.scalar
            def _(act):
                with act.Fori(0, B) as b:
                    act.wait_ge(L["state"].sem, L["state"].at(b, 0))
                    for j, (to, fn, bias) in enumerate(((f, ACT.Sigmoid, "bf"), (i_, ACT.Sigmoid, "bi"),
                                                        (n_, ACT.Tanh, "bc"))):
                        act.wait_ge(L["gates"].sem, L["gates"].at(b, j + 1))
                        act.activation(to[:, :], ps[j][:, :], fn, bias=core.w(g, bias)).then_inc(L["opened"].sem, 1)
                with act.Fori(0, B) as b:
                    act.wait_ge(L["answer"].sem, L["answer"].at(b, 1))
                    act.wait_ge(L["done"].sem, L["done"].at(b, 0))
                    act.activation(h[:, :], out[:, :], ACT.Tanh, bias=core.w(g, "bo")).then_inc(L["answered"].sem, 1)

            @block.vector
            def _(dve):
                dve.tensor_copy(c[:, :], core.w(g, "in_c").to_broadcast([P, S])).then_inc(L["start"].sem, 1)
                dve.wait_ge(L["start"].sem, L["start"].at(0, 1))
                with dve.Fori(0, B) as b:
                    dve.wait_ge(L["opened"].sem, L["opened"].at(b, 3))
                    dve.tensor_tensor(ig[:, :], i_[:, :], n_[:, :], ALU.mult).then_inc(L["parts"].sem, 1)
                    dve.tensor_tensor(h[:, :], f[:, :], c[:, :], ALU.mult).then_inc(L["parts"].sem, 1)
                    dve.wait_ge(L["parts"].sem, L["parts"].at(b, 2))
                    dve.tensor_tensor(c[:, :], ig[:, :], h[:, :], ALU.add).then_inc(L["state"].sem, 1)
                with dve.Fori(0, B) as b:
                    dve.wait_ge(L["answered"].sem, L["answered"].at(b, 1))
                    dve.tensor_tensor(core.batch(b), h[:, :], core.batch(b), ALU.add).then_inc(L["done"].sem, 1)

    L.close()

DI, NS, CONV, RANK = 256, 16, 4, 64
CT = DI // P


def state_space(nc, core, name, g):
    ST = NS * CT
    L = Layer(nc, name, core, [g], **NEXT, consts=1, history=1, a_exp=1, a_neg=1,
              xz=2 * CT,
              padded=CT,
              zs=CT,
              tap=CT * CONV,
              u=CT,
              low=1,
              low_sb=1, split=5,
              pre=CT,
              soft=3 * CT,
              delta=CT,
              soft_pos=CT,
              du=CT,
              rows=2 * NS,
              bsb=NS,
              decay=ST,
              drive=ST,
              state=ST,
              read=ST,
              summed=ST,
              skip=CT, gated=CT, projected=1, done=1)
    with L.ctx:
        xn = L.sb("xn", [P, S])
        padded = L.sb("padded", [P, CT, CONV - 1 + S])
        zs, u, delta, du = (L.sb(n, [P, CT, S]) for n in ("zs", "u", "delta", "du"))
        conv = L.sb("conv", [P, CT, S])
        low = L.sb("low", [RANK, S])
        rest = L.sb("rest", [2 * NS, 2, S])
        mid = L.sb("mid", [2 * NS, S], BF16)
        parts = L.sb("parts", [3 * 2 * NS, S], BF16)
        spread16 = L.sb("spread16", [3 * 2 * NS, 2 * NS, P], BF16)
        a = L.sb("a", [P, CT, NS])
        bsb = L.sb("bsb", [P, 2, S])
        drive, state, read = (L.sb(n, [P, 2, S]) for n in ("drive", "state", "read"))
        y = L.sb("y", [P, CT, S])
        pd = L.ps("pd", [P, 2, S])
        pb = L.ps("pb", [P, S])
        pc = L.ps("pc", [P, S])
        py = L.ps("py", [P, CT, S])
        bank, out = L.ps("bank", [P, S]), L.ps("out", [P, S])
        eye = core.w("const", "eye")

        def add_up(pe, b, n):
            for t in range(CT):
                s = n * CT + t
                pe.wait_ge(L["read"].sem, L["read"].at(b, s + 1))
                if n == 0:
                    pe.wait_ge(L["zs"].sem, L["zs"].at(b, t + 1))
                pe.matmul(py[:, t, :], eye, read[:, s % 2, :], start=n == 0, stop=n == NS - 1)\
                    .then_inc(L["summed"].sem, 1)

        def read_out(dve, b, s):
            dve.wait_ge(L["state"].sem, L["state"].at(b, s + 1))
            dve.wait_ge(L["rows"].sem, L["rows"].at(b, 2 * (s // CT) + 2))
            dve.wait_ge(L["summed"].sem, L["summed"].at(b, max(s - 1, 0)))
            dve.tensor_tensor(read[:, s % 2, :], state[:, s % 2, :], pc[:, :], ALU.mult).then_inc(L["read"].sem, 1)

        with nc.Block() as block:
            @block.tensor
            def _(pe):
                pe.wait_ge(L["consts"].sem, L["consts"].at(0, 1))
                with pe.Fori(0, B) as b:
                    pe.wait_ge(L["done"].sem, L["done"].at(b, 0))
                    pe.wait_ge(L["now"].sem, L["now"].at(b, 1))
                    pe.wait_ge(L["state"].sem, L["state"].at(b, 0))
                    for t in range(CT):
                        pe.matmul(pd[:, t, :], core.w(g, "w_in", t * P, (t + 1) * P), xn[:, :],
                                  start=True, stop=True).then_inc(L["xz"].sem, 1)
                    pe.wait_ge(L["gated"].sem, L["gated"].at(b, 0))
                    for t in range(CT):
                        pe.matmul(py[:, t, :], core.w(g, "w_in", DI + t * P, DI + (t + 1) * P), xn[:, :],
                                  start=True, stop=True).then_inc(L["xz"].sem, 1)
                    pe.wait_ge(L["u"].sem, L["u"].at(b, CT))
                    for t in range(CT):
                        pe.matmul(bank[0:RANK, :], core.w(g, "w_low", t * RANK, (t + 1) * RANK), u[:, t, :],
                                  start=t == 0, stop=t == CT - 1)
                    for t in range(CT):
                        mm = pe.matmul(out[0:2 * NS, :], core.w(g, "w_bc", t * 2 * NS, (t + 1) * 2 * NS), u[:, t, :],
                                       start=t == 0, stop=t == CT - 1)
                    mm.then_inc(L["low"].sem, 1)
                    pe.wait_ge(L["low_sb"].sem, L["low_sb"].at(b, 1))
                    for t in range(CT):
                        pe.matmul(pd[:, t, :], core.w(g, "w_dt", t * P, (t + 1) * P), low[:, :],
                                  start=True, stop=True).then_inc(L["pre"].sem, 1)
                    pe.wait_ge(L["split"].sem, L["split"].at(b, 5))
                    for n in range(NS):
                        pe.wait_ge(L["bsb"].sem, L["bsb"].at(b, n))
                        pe.matmul(pb[:, :], spread16[:, n, :], parts[:, :], start=True, stop=True)\
                            .then_inc(L["rows"].sem, 1)
                        pe.wait_ge(L["read"].sem, L["read"].at(b, n * CT))
                        pe.matmul(pc[:, :], spread16[:, NS + n, :], parts[:, :], start=True, stop=True)\
                            .then_inc(L["rows"].sem, 1)
                        if n >= 1:
                            add_up(pe, b, n - 1)
                    add_up(pe, b, NS - 1)
                    pe.wait_ge(L["gated"].sem, L["gated"].at(b, CT))
                    for t in range(CT):
                        mm = pe.matmul(out[:, :], core.w(g, "w_out", t * P, (t + 1) * P), y[:, t, :],
                                       start=t == 0, stop=t == CT - 1)
                    mm.then_inc(L["projected"].sem, 1)

            @block.scalar
            def _(act):
                act.activation(a[:, :, :], core.w(g, "a_log").rearrange("p (t n) -> p t n", t=CT), ACT.Exp)\
                    .then_inc(L["a_exp"].sem, 1)
                act.wait_ge(L["a_neg"].sem, L["a_neg"].at(0, 1))
                with act.Fori(0, B) as b:
                    for t in range(CT):
                        act.wait_ge(L["xz"].sem, L["xz"].at(b, t + 1))
                        act.wait_ge(L["tap"].sem, L["tap"].at(b, 0))
                        act.activation(padded[:, t, CONV - 1:], pd[:, t, :], ACT.Copy).then_inc(L["padded"].sem, 1)
                    for t in range(CT):
                        act.wait_ge(L["xz"].sem, L["xz"].at(b, CT + t + 1))
                        act.wait_ge(L["gated"].sem, L["gated"].at(b, 0))
                        act.activation(zs[:, t, :], py[:, t, :], ACT.Silu).then_inc(L["zs"].sem, 1)
                    for t in range(CT):
                        act.wait_ge(L["tap"].sem, L["tap"].at(b, CONV * (t + 1)))
                        act.activation(u[:, t, :], conv[:, t, :], ACT.Silu, bias=core.w(g, "conv_b", t, t + 1))\
                            .then_inc(L["u"].sem, 1)
                    act.wait_ge(L["low"].sem, L["low"].at(b, 1))
                    act.activation(low[:, :], bank[0:RANK, :], ACT.Copy).then_inc(L["low_sb"].sem, 1)
                    for t in range(CT):
                        act.wait_ge(L["pre"].sem, L["pre"].at(b, t + 1))
                        act.wait_ge(L["tap"].sem, L["tap"].at(b, CONV * CT))
                        act.activation(delta[:, t, :], pd[:, t, :], ACT.Abs, bias=core.w(g, "dt_b", t, t + 1))\
                            .then_inc(L["soft"].sem, 1)
                    for t in range(CT):
                        act.wait_ge(L["soft"].sem, L["soft"].at(b, t + 1))
                        act.activation(delta[:, t, :], delta[:, t, :], ACT.Exp, scale=-1.0).then_inc(L["soft"].sem, 1)
                    for t in range(CT):
                        act.wait_ge(L["soft"].sem, L["soft"].at(b, CT + t + 1))
                        act.activation(delta[:, t, :], delta[:, t, :], ACT.Ln, bias=1.0).then_inc(L["soft"].sem, 1)
                    act.wait_ge(L["du"].sem, L["du"].at(b, CT))
                    for n in range(NS):
                        act.wait_ge(L["rows"].sem, L["rows"].at(b, 2 * n + 1))
                        act.wait_ge(L["drive"].sem, L["drive"].at(b, CT * max(n - 1, 0)))
                        act.activation(bsb[:, n % 2, :], pb[:, :], ACT.Copy).then_inc(L["bsb"].sem, 1)
                        for t in range(CT):
                            act.wait_ge(L["state"].sem, L["state"].at(b, CT * max(n - 1, 0) + (t if n >= 1 else 0)))
                            if n >= 1:
                                act.wait_ge(L["state"].sem, L["state"].at(b, CT * (n - 1) + t + 1))
                            act.activation(pd[:, t, :], delta[:, t, :], ACT.Exp, scale=a[:, t, n:n + 1])\
                                .then_inc(L["decay"].sem, 1)

            @block.vector
            def _(dve):
                dve.memset(padded[:, :, 0:CONV - 1], 0.0).then_inc(L["history"].sem, 1)
                dve.wait_ge(L["history"].sem, L["history"].at(0, 1))
                dve.wait_ge(L["a_exp"].sem, L["a_exp"].at(0, 1))
                dve.tensor_scalar(a[:, :, :], a[:, :, :], -1.0, None, ALU.mult).then_inc(L["a_neg"].sem, 1)
                with dve.Fori(0, B) as b:
                    take_normed(dve, L, b, xn[:, :])
                    for t in range(CT):
                        dve.wait_ge(L["padded"].sem, L["padded"].at(b, t + 1))
                        for i in range(CONV):
                            tap = core.w(g, "conv_w", t * CONV + i, t * CONV + i + 1)
                            src = padded[:, t, i:i + S]
                            if i == 0:
                                dve.tensor_scalar(conv[:, t, :], src, tap, None, ALU.mult).then_inc(L["tap"].sem, 1)
                            else:
                                dve.wait_ge(L["tap"].sem, L["tap"].at(b, t * CONV + i))
                                dve.scalar_tensor_tensor(out=conv[:, t, :], in0=src, scalar=tap, in1=conv[:, t, :],
                                                         op0=ALU.mult, op1=ALU.add).then_inc(L["tap"].sem, 1)
                    dve.wait_ge(L["low"].sem, L["low"].at(b, 1))
                    R = 2 * NS
                    dve.tensor_copy(parts[0:R, :], out[0:R, :]).then_inc(L["split"].sem, 1)
                    dve.wait_ge(L["split"].sem, L["split"].at(b, 1))
                    dve.tensor_tensor(rest[:, 0, :], out[0:R, :], parts[0:R, :], ALU.subtract).then_inc(L["split"].sem, 1)
                    dve.wait_ge(L["split"].sem, L["split"].at(b, 2))
                    dve.tensor_copy(parts[R:2 * R, :], rest[:, 0, :]).then_inc(L["split"].sem, 1)
                    dve.tensor_copy(mid[:, :], rest[:, 0, :]).then_inc(L["split"].sem, 1)
                    dve.wait_ge(L["split"].sem, L["split"].at(b, 4))
                    dve.tensor_tensor(parts[2 * R:3 * R, :], rest[:, 0, :], mid[:, :], ALU.subtract)\
                        .then_inc(L["split"].sem, 1)
                    for t in range(CT):
                        dve.wait_ge(L["soft"].sem, L["soft"].at(b, CT))
                        dve.wait_ge(L["u"].sem, L["u"].at(b, CT))
                        dve.tensor_scalar(conv[:, t, :], pd[:, t, :], core.w(g, "dt_b", t, t + 1), 0.0,
                                          ALU.add, ALU.max).then_inc(L["soft_pos"].sem, 1)
                    for t in range(CT):
                        dve.wait_ge(L["soft"].sem, L["soft"].at(b, 2 * CT + t + 1))
                        dve.wait_ge(L["soft_pos"].sem, L["soft_pos"].at(b, t + 1))
                        dve.tensor_tensor(delta[:, t, :], delta[:, t, :], conv[:, t, :], ALU.add)\
                            .then_inc(L["delta"].sem, 1)
                    for t in range(CT):
                        dve.wait_ge(L["delta"].sem, L["delta"].at(b, t + 1))
                        dve.wait_ge(L["drive"].sem, L["drive"].at(b, 0))
                        dve.tensor_tensor(du[:, t, :], delta[:, t, :], u[:, t, :], ALU.mult).then_inc(L["du"].sem, 1)
                    for s in range(ST):
                        n, t = divmod(s, CT)
                        dve.wait_ge(L["decay"].sem, L["decay"].at(b, s + 1))
                        dve.wait_ge(L["drive"].sem, L["drive"].at(b, s + 1))
                        dve.wait_ge(L["read"].sem, L["read"].at(b, max(s - 1, 0)))
                        dve.tensor_tensor_scan(state[:, s % 2, :], pd[:, t, :], drive[:, s % 2, :], 0.0,
                                               ALU.mult, ALU.add).then_inc(L["state"].sem, 1)
                        if s >= 1:
                            read_out(dve, b, s - 1)
                    read_out(dve, b, ST - 1)
                    for t in range(CT):
                        dve.wait_ge(L["summed"].sem, L["summed"].at(b, ST - CT + t + 1))
                        dve.wait_ge(L["projected"].sem, L["projected"].at(b, 0))
                        dve.scalar_tensor_tensor(out=conv[:, t, :], in0=u[:, t, :], scalar=core.w(g, "skip", t, t + 1),
                                                 in1=py[:, t, :], op0=ALU.mult, op1=ALU.add).then_inc(L["skip"].sem, 1)
                    for t in range(CT):
                        dve.wait_ge(L["skip"].sem, L["skip"].at(b, t + 1))
                        dve.tensor_tensor(y[:, t, :], conv[:, t, :], zs[:, t, :], ALU.mult).then_inc(L["gated"].sem, 1)
                    dve.wait_ge(L["projected"].sem, L["projected"].at(b, 1))
                    dve.tensor_tensor(core.batch(b), out[:, :], core.batch(b), ALU.add).then_inc(L["done"].sem, 1)

            @block.gpsimd
            def _(pool):
                pool.tensor_copy(spread16[:, :, :], core.w("const", "spread").unsqueeze(2)
                                 .to_broadcast([3 * 2 * NS, 2 * NS, P])).then_inc(L["consts"].sem, 1)
                with pool.Fori(0, B) as b:
                    pool.wait_ge(L["du"].sem, L["du"].at(b, CT))
                    for s in range(ST):
                        n, t = divmod(s, CT)
                        pool.wait_ge(L["bsb"].sem, L["bsb"].at(b, n + 1))
                        pool.wait_ge(L["state"].sem, L["state"].at(b, max(s - 1, 0)))
                        pool.tensor_tensor(drive[:, s % 2, :], du[:, t, :], bsb[:, n % 2, :], ALU.mult)\
                            .then_inc(L["drive"].sem, 1)
    L.close()

EH, EHD = 16, 8
EW = EHD + 1
VARIANTS = 4


def elu_attention(nc, core, name):
    NSTEP = EH
    L = Layer(nc, name, core, ["elu"], **NEXT, start=1,
              proj=2, below=2, above=2, expo=2, feats=2, variant=VARIANTS,
              vk=TT, vk_sb=TT, kturn=1, ktok=1,
              states=TT - 1, states_sb=TT - 1,
              energy=NSTEP, masked=NSTEP, mixed=1, norm=3, outs=2, turned=1, outs_sb=1, projected=1, done=1)
    with L.ctx:
        g = "elu"
        w = lambda n, *a: core.w(g, n, *a)
        xn = L.sb("xn", [P, S])
        low, high, feats = (L.sb(n, [P, 2, S]) for n in ("low", "high", "feats"))
        kvar = L.sb("kvar", [P, VARIANTS, S])
        vaug = L.sb("vaug", [P, TT, EH, EW])
        ktok = L.sb("ktok", [P, TT, P])
        state = L.sb("state", [P, TT - 1, EH * EW])
        energy = L.sb("energy", [P, NSTEP, S])
        den = L.sb("den", [P, TT, EH])
        outs = L.sb("outs", [P, TT, D])
        outs_t = L.sb("outs_t", [P, S])
        bank, small = L.ps("bank", [P, S]), L.ps("small", [P, S])
        pe4 = L.ps("pe4", [P, 4, S])
        pmix = L.ps("pmix", [P, 2, S])
        eye = core.w("const", "eye")

        def mix_at(t):
            return pmix[:, t // 2, (t % 2) * EH * EW:(t % 2 + 1) * EH * EW]

        with nc.Block() as block:
            @block.tensor
            def _(pe):
                pe.wait_ge(L["start"].sem, L["start"].at(0, 1))
                with pe.Fori(0, B) as b:
                    pe.wait_ge(L["done"].sem, L["done"].at(b, 0))
                    pe.wait_ge(L["now"].sem, L["now"].at(b, 1))
                    pe.wait_ge(L["masked"].sem, L["masked"].at(b, 0))
                    for i, n in enumerate(("wq", "wk")):
                        pe.matmul(pe4[:, i, :], w(n), xn[:, :], start=True, stop=True).then_inc(L["proj"].sem, 1)
                    for t in range(TT):
                        pe.matmul(small[:, t * P:(t + 1) * P], xn[:, t * P:(t + 1) * P], w("wv"),
                                  start=True, stop=True).then_inc(L["vk"].sem, 1)
                    pe.wait_ge(L["feats"].sem, L["feats"].at(b, 2))
                    for t in range(TT):
                        mm = pe.transpose(bank[:, t * P:(t + 1) * P], feats[:, 1, t * P:(t + 1) * P], eye)
                    mm.then_inc(L["kturn"].sem, 1)
                    pe.wait_ge(L["vk_sb"].sem, L["vk_sb"].at(b, TT))
                    pe.wait_ge(L["ktok"].sem, L["ktok"].at(b, 1))
                    for t in range(1, TT):
                        at = (t - 1) * EH * EW
                        for o in range(t):
                            mm = pe.matmul(small[:, at:at + EH * EW], ktok[:, o, :],
                                           vaug[:, o, :, :].rearrange("p h e -> p (h e)"),
                                           start=o == 0, stop=o == t - 1)
                        mm.then_inc(L["states"].sem, 1)
                    for s in range(NSTEP):
                        j, r = divmod(s, 4)
                        rows = slice(32 * r, 32 * r + 32)
                        pe.wait_ge(L["variant"].sem, L["variant"].at(b, j + 1))
                        if s >= 4:
                            pe.wait_ge(L["masked"].sem, L["masked"].at(b, s - 3))
                        for t in range(TT):
                            tk = slice(t * P, (t + 1) * P)
                            mm = pe.matmul(pe4[:, r, tk], kvar[rows, j, tk], feats[rows, 0, tk], start=True, stop=True)
                        mm.then_inc(L["energy"].sem, 1)
                    pe.wait_ge(L["outs"].sem, L["outs"].at(b, 0))
                    pe.wait_ge(L["states_sb"].sem, L["states_sb"].at(b, TT - 1))
                    pe.wait_ge(L["masked"].sem, L["masked"].at(b, NSTEP))
                    for t in range(TT):
                        if t:
                            pe.matmul(mix_at(t), feats[:, 0, t * P:(t + 1) * P], state[:, t - 1, :],
                                      start=True, stop=True, skip_group_check=True)
                        for s in range(NSTEP):
                            h = 4 * (s % 4) + s // 4
                            mm = pe.matmul(mix_at(t)[:, h * EW:(h + 1) * EW], energy[:, s, t * P:(t + 1) * P],
                                           vaug[:, t, h, :], start=t == 0, stop=True,
                                           skip_group_check=t > 0)
                    mm.then_inc(L["mixed"].sem, 1)
                    pe.wait_ge(L["outs"].sem, L["outs"].at(b, 2))
                    for t in range(TT):
                        mm = pe.transpose(bank[:, t * P:(t + 1) * P], outs[:, t, :], eye)
                    mm.then_inc(L["turned"].sem, 1)
                    pe.wait_ge(L["outs_sb"].sem, L["outs_sb"].at(b, 1))
                    pe.matmul(small[:, :], w("wo"), outs_t[:, :], start=True, stop=True).then_inc(L["projected"].sem, 1)

            @block.scalar
            def _(act):
                with act.Fori(0, B) as b:
                    for i in range(2):
                        act.wait_ge(L["below"].sem, L["below"].at(b, i + 1))
                        act.activation(low[:, i, :], low[:, i, :], ACT.Exp).then_inc(L["expo"].sem, 1)
                    act.wait_ge(L["kturn"].sem, L["kturn"].at(b, 1))
                    act.activation(ktok[:, :, :], bank[:, :].rearrange("p (t c) -> p t c", t=TT), ACT.Copy)\
                        .then_inc(L["ktok"].sem, 1)
                    act.wait_ge(L["turned"].sem, L["turned"].at(b, 1))
                    act.activation(outs_t[:, :], bank[:, :], ACT.Copy).then_inc(L["outs_sb"].sem, 1)

            @block.vector
            def _(dve):
                dve.memset(vaug[:, :, :, :], 1.0).then_inc(L["start"].sem, 1)
                dve.wait_ge(L["start"].sem, L["start"].at(0, 1))
                with dve.Fori(0, B) as b:
                    take_normed(dve, L, b, xn[:, :])
                    dve.wait_ge(L["mixed"].sem, L["mixed"].at(b, 0))
                    for i in range(2):
                        dve.wait_ge(L["proj"].sem, L["proj"].at(b, i + 1))
                        bias = w(("bq", "bk")[i])
                        dve.tensor_scalar(low[:, i, :], pe4[:, i, :], bias, 0.0, ALU.add, ALU.min)\
                            .then_inc(L["below"].sem, 1)
                        dve.tensor_scalar(high[:, i, :], pe4[:, i, :], bias, 0.0, ALU.add, ALU.max)\
                            .then_inc(L["above"].sem, 1)
                    for t in range(TT):
                        dve.wait_ge(L["vk"].sem, L["vk"].at(b, TT))
                        dve.tensor_tensor(vaug[:, t, :, 0:EHD],
                                          small[:, t * P:(t + 1) * P].rearrange("p (h e) -> p h e", h=EH),
                                          w("bv").rearrange("p (h e) -> p h e", h=EH), ALU.add).then_inc(L["vk_sb"].sem, 1)
                    for i in range(2):
                        dve.wait_ge(L["expo"].sem, L["expo"].at(b, i + 1))
                        dve.wait_ge(L["above"].sem, L["above"].at(b, i + 1))
                        dve.tensor_tensor(feats[:, i, :], low[:, i, :], high[:, i, :], ALU.add).then_inc(L["feats"].sem, 1)
                    dve.wait_ge(L["feats"].sem, L["feats"].at(b, 2))
                    for j in range(VARIANTS):
                        dve.tensor_scalar(kvar[:, j, :], feats[:, 1, :], core.w("const", "variant", j, j + 1), None,
                                          ALU.mult).then_inc(L["variant"].sem, 1)
                    for t in range(1, TT):
                        dve.wait_ge(L["states"].sem, L["states"].at(b, TT - 1))
                        at = (t - 1) * EH * EW
                        dve.tensor_tensor(state[:, t - 1, :], small[:, at:at + EH * EW], core.w("const", "block16"),
                                          ALU.mult).then_inc(L["states_sb"].sem, 1)
                    for s in range(NSTEP):
                        dve.wait_ge(L["energy"].sem, L["energy"].at(b, s + 1))
                        dve.tensor_tensor(energy[:, s, :].rearrange("p (t c) -> p t c", t=TT),
                                          pe4[:, s % 4, :].rearrange("p (t c) -> p t c", t=TT),
                                          core.w("const", "upper").unsqueeze(1).to_broadcast([P, TT, P]), ALU.mult)\
                            .then_inc(L["masked"].sem, 1)
                    dve.wait_ge(L["mixed"].sem, L["mixed"].at(b, 1))
                    for i in range(2):
                        mix = pmix[:, i, 0:2 * EH * EW].rearrange("p (t h e) -> p t h e", t=2, h=EH)
                        dve.tensor_scalar(den[:, 2 * i:2 * i + 2, :], mix[:, :, :, EHD], 1e-6, None, ALU.add)\
                            .then_inc(L["norm"].sem, 1)
                    dve.wait_ge(L["norm"].sem, L["norm"].at(b, 2))
                    dve.reciprocal(den[:, :, :], den[:, :, :]).then_inc(L["norm"].sem, 1)
                    dve.wait_ge(L["norm"].sem, L["norm"].at(b, 3))
                    for i in range(2):
                        mix = pmix[:, i, 0:2 * EH * EW].rearrange("p (t h e) -> p t h e", t=2, h=EH)
                        for t in range(2):
                            ins = dve.tensor_tensor(
                                outs[:, 2 * i + t, :].rearrange("p (h e) -> p h e", h=EH), mix[:, t, :, 0:EHD],
                                den[:, 2 * i + t, :].unsqueeze(2).to_broadcast([P, EH, EHD]), ALU.mult)
                        ins.then_inc(L["outs"].sem, 1)
                    dve.wait_ge(L["projected"].sem, L["projected"].at(b, 1))
                    dve.scalar_tensor_tensor(out=core.batch(b), in0=small[:, :], scalar=w("bo"), in1=core.batch(b),
                                             op0=ALU.add, op1=ALU.add).then_inc(L["done"].sem, 1)

    L.close()

GROUPS_OF = {0: ["mha"], 1: ["moe"], 2: ["keep"], 3: ["moe"], 4: ["light"], 5: ["bitffn"], 6: ["slr"], 7: ["bitffn"],
             8: ["pairs"], 9: ["gated"], 10: ["ssm2"], 11: ["gated"], 12: ["elu"], 13: ["cell"], 14: ["ssm3"],
             15: ["cell"]}


def run_layer(nc, core, i):
    if i == 2:
        keep_attention(nc, core, "l2")
    if i == 6:
        landmark_layer(nc, core, "l6")
    if i == 4:
        linear_attention(nc, core, "l4")
    if i == 12:
        elu_attention(nc, core, "l12")
    if i == 0:
        query_softmax_attention(nc, core, "l0")
    if i == 10:
        state_space(nc, core, "l10", "ssm2")
    if i == 14:
        state_space(nc, core, "l14", "ssm3")
    if i in (1, 3):
        routed_ffn(nc, core, f"l{i}", "moe", 16, 8, 1, False)
    if i in (9, 11):
        routed_ffn(nc, core, f"l{i}", "gated", 8, 11, 2, True)
    if i == 8:
        pair_attention(nc, core, f"l{i}")
    if i in (13, 15):
        cell(nc, core, f"l{i}")
    if i in (5, 7):
        bit_ffn(nc, core, f"l{i}")


def build_program(nc, x_in, groups_in, out, columns):
    order = ["const"] + [g for i in PLAN for g in GROUPS_OF[i]]
    order = list(dict.fromkeys(order))
    with ExitStack() as ctx:
        x = ctx.enter_context(nc.sbuf_tensor("x", [P, B * S], F32))
        xn = ctx.enter_context(nc.sbuf_tensor("xn", [P, B * S], F32))
        weights = {g: ctx.enter_context(nc.sbuf_tensor(f"w_{g}", list(groups_in[g].shape), F32)) for g in order}
        landed = {g: ctx.enter_context(nc.semaphore(f"landed_{g}")) for g in order}
        landed["x"] = ctx.enter_context(nc.semaphore("landed_x"))
        stored = ctx.enter_context(nc.semaphore("stored"))
        core = Core(x, xn, weights, landed, columns)
        with nc.Block() as block:
            @block.sync
            def _(sync):
                sync.dma_start(x[:, :], x_in).then_inc(landed["x"], 16)
                for g in order:
                    sync.dma_start(weights[g][:, :], groups_in[g]).then_inc(landed[g], 16)
                sync.wait_ge(landed["x"], 16)
                sync.wait_ge(landed["const"], 16)
        if 5 in PLAN or 7 in PLAN:
            quantise(nc, core)
        for i in PLAN:
            normalise(nc, core, f"n{i}")
            run_layer(nc, core, i)
        with nc.Block() as block:
            @block.sync
            def _(sync):
                sync.dma_start(out, x[:, :]).then_inc(stored, 16)
                sync.wait_ge(stored, 16)



def constants():
    eye = np.eye(P, dtype=np.float32)
    row = np.arange(P)
    mask_rows = np.zeros((P, KT, P), np.float32)
    for r in row[row % 32 < B * KJ]:
        T, i = divmod(KG * (r % KJ) + r // 32, 2)
        mask_rows[r, T, i * HALF + MASK_ROW] = 1
    one_rows = {"q": row[:HALF] == MASK_ROW, "k": (row[:HALF] >= SHIFT_ROW) & (row[:HALF] < SHIFT_ROW + 3)}
    splits = {}
    for n, parts in (("q", Q_PARTS), ("k", K_PARTS)):
        part = np.array(list(parts.ljust(HALF // KHD))).repeat(KHD)
        rest = np.where(one_rows[n], 1, -((part == "m") | (part == "l")).astype(np.float32))
        for key, column in (("ones", one_rows[n]), ("rest", rest), ("last", -(part == "l").astype(np.float32))):
            splits[f"{n}_{key}"] = columns_of(np.tile(np.asarray(column, np.float32), 2))
    return {
        "ones": np.ones((P, P), np.float32),
        "centre": eye - np.float32(1 / D),
        "mean": np.full((P, P), 1 / D, np.float32),
        "eye": eye,
        "falling": rows_of(np.tile(np.arange(16, 0, -1, dtype=np.float32), TT)),
        "falling8": rows_of(np.tile(np.arange(8, 0, -1, dtype=np.float32), TT)),
        "ones_s": np.ones((P, S), np.float32),
        "spread": np.tile(np.eye(2 * NS, dtype=np.float32), (3, 1)),
        "upper": np.triu(np.ones((P, P), np.float32)),
        "token": rows_of(np.arange(S, dtype=np.float32)),
        "block4": np.kron(np.eye(HG), np.ones((32, LHD))).astype(np.float32),
        "block16": np.kron(np.eye(EH), np.ones((EHD, EW))).astype(np.float32),
        "variant": np.stack([(np.arange(P) // EHD % 4 == j) for j in range(VARIANTS)], 1).astype(np.float32),
        "later": np.triu(np.full((P, P), NEG, np.float32), 1),
        "units32": rows_of(np.eye(B * KJ, 32, dtype=np.float32)),
        "batch_rows": np.stack([((row % 32) // KJ == b) for b in range(B)], 1).astype(np.float32),
        "mask_rows": mask_rows.reshape(P, KT * P),
        **splits,
        "v_ones": rows_of((np.arange(KH * 32) % 32 == KHD).astype(np.float32)),
        "minus_half": np.full((P, B * TT), -0.5, np.float32),
    }


def columns_of(v, width=P):
    return np.asarray(v).reshape(-1, width).T


def row_blocks(m, width=P):
    m = np.asarray(m)
    t = m.shape[0] // width
    return m.reshape(t, width, m.shape[1]).transpose(1, 0, 2).reshape(width, -1)


def rows_of(v):
    return np.broadcast_to(np.asarray(v).reshape(1, -1), (P, np.asarray(v).size))


def side_by_side(m):
    return np.asarray(m).transpose(1, 0, 2).reshape(m.shape[1], -1)


def pick(experts, hidden):
    return np.tile(np.repeat(np.eye(experts, dtype=np.float32), hidden, axis=1), (3, 1))


def in_row_groups(m, first):
    out = np.zeros((D, KH, 32), np.float32)
    out[:, :, first:first + KHD] = m.reshape(D, KH, KHD)
    return out.reshape(D, KH * 32)


def in_part_rows(m, parts):
    out = np.zeros((D, KH, HALF), np.float32)
    out[:, :, :len(parts) * KHD] = np.tile(m.reshape(D, KH, KHD), (1, 1, len(parts)))
    return out.reshape(D, KH * HALF)


def lay_out(v):
    g = {"const": constants()}
    g["moe"] = {"wr": v["L0_ffn_Wr"],
                "w1": np.concatenate([side_by_side(v["L0_ffn_Wg"]), v["L0_ffn_Sg"]], 1),
                "w3": np.concatenate([side_by_side(v["L0_ffn_Wu"]), v["L0_ffn_Su"]], 1),
                "w2": row_blocks(np.concatenate([v["L0_ffn_Wd"].reshape(-1, D), v["L0_ffn_Sd"]])),
                "pick": pick(16, 64)}
    hid = 8 * 176 + 176
    pad = np.zeros((-hid % P, D), np.float32)
    g["gated"] = {"wr": v["L2_ffn_gate_w"].T,
                  "w1": np.concatenate([side_by_side(v["L2_ffn_w1"]), v["L2_ffn_sw1"]], 1),
                  "w3": np.concatenate([side_by_side(v["L2_ffn_w3"]), v["L2_ffn_sw3"]], 1),
                  "w2": row_blocks(np.concatenate([v["L2_ffn_w2"].reshape(-1, D), v["L2_ffn_sw2"], pad])),
                  "b1": columns_of(np.concatenate([v["L2_ffn_b1"].ravel(), v["L2_ffn_sb1"], pad[:, 0]])),
                  "b3": columns_of(np.concatenate([v["L2_ffn_b3"].ravel(), v["L2_ffn_sb3"], pad[:, 0]])),
                  "b2": v["L2_ffn_b2"], "sb2": columns_of(v["L2_ffn_sb2"]),
                  "gate_b": rows_of(np.tile(v["L2_ffn_gate_b"], TT)),
                  "pick": pick(8, 176)}
    swap = np.arange(D) ^ 1
    p = "L2_attn_a_"
    g["pairs"] = {"wq": v[p + "Wq"].T, "wk": v[p + "Wk"].T, "wv": v[p + "Wv"].T, "wo": v[p + "Wo"].T,
                  "bq": np.stack([v[p + "bq"], v[p + "bq"][swap]], 1),
                  "bk": np.stack([v[p + "bk"], v[p + "bk"][swap]], 1),
                  "bv": columns_of(v[p + "bv"]), "bo": columns_of(v[p + "bo"]), "beta": rows_of(v[p + "beta"])}
    p = "L0_attn_a_"
    g["mha"] = {"wq": v[p + "q_w"].reshape(-1, D).T, "wk": v[p + "k_w"].reshape(-1, D).T,
                "wv": v[p + "v_w"].reshape(-1, D).T, "wl": row_blocks(v[p + "l_w"].T),
                "bq": columns_of(v[p + "q_b"]), "bk": columns_of(v[p + "k_b"]), "bv": rows_of(v[p + "v_b"]),
                "bl": columns_of(v[p + "l_b"])}
    p = "L2_attn_b_"
    low = v[p + "x_proj_w"].T
    g["ssm2"] = {"w_in": v[p + "in_proj_w"].T, "w_low": row_blocks(low[:, :RANK]), "w_bc": row_blocks(low[:, RANK:]),
                 "w_dt": v[p + "dt_proj_w"].T, "w_out": row_blocks(v[p + "out_proj_w"].T),
                 "conv_w": row_blocks(v[p + "conv_w"]), "conv_b": columns_of(v[p + "conv_b"]),
                 "dt_b": columns_of(v[p + "dt_proj_b"]), "a_log": row_blocks(v[p + "A_log"]),
                 "skip": columns_of(v[p + "D"])}
    p = "L3_attn_b_"
    low = v[p + "x_proj_w"]
    g["ssm3"] = {"w_in": v[p + "in_proj_w"], "w_low": row_blocks(low[:, :RANK]), "w_bc": row_blocks(low[:, RANK:]),
                 "w_dt": v[p + "dt_proj_w"], "w_out": row_blocks(v[p + "out_proj_w"]),
                 "conv_w": row_blocks(v[p + "conv_w"][:, 0, :]), "conv_b": columns_of(v[p + "conv_b"]),
                 "dt_b": columns_of(v[p + "dt_proj_b"]), "a_log": row_blocks(v[p + "A_log"]),
                 "skip": columns_of(v[p + "D_param"])}
    p = "L1_attn_a_"
    wq, wk, wv, wu = np.split(v[p + "qkvu_w"].T, 4, axis=1)
    bq, bk, bv, bu = np.split(v[p + "qkvu_b"], 4)
    twice = np.concatenate([np.concatenate([np.arange(h * LHD, (h + 1) * LHD)] * 2) for h in range(LH)])
    slope = v[p + "slope_rate"].reshape(LH)
    g["light"] = {"wq": wq[:, twice], "wk": wk[:, twice], "wv": wv, "wu": wu, "wo": v[p + "out_w"].T,
                  "bq": columns_of(bq[twice]), "bk": columns_of(bk[twice]), "bv": rows_of(bv), "bu": rows_of(bu),
                  "bo": columns_of(v[p + "out_b"]), "slope": rows_of(slope),
                  "slope_cols": rows_of(np.repeat(slope, LHD)),
                  "theta": columns_of(v[p + "theta"].reshape(-1)[twice]),
                  "shift": columns_of(np.tile(np.repeat(np.float32([np.pi / 2, 0]), LHD), LH))}
    p = "L3_attn_a_"
    wq, wk, wv = np.split(v[p + "qkv_w"], 3, axis=1)
    bq, bk, bv = np.split(v[p + "qkv_b"], 3)
    g["elu"] = {"wq": wq, "wk": wk, "wv": wv, "wo": v[p + "out_w"], "bq": columns_of(bq), "bk": columns_of(bk),
                "bv": rows_of(bv), "bo": columns_of(v[p + "out_b"])}
    p = "L1_attn_b_"
    g["slr"] = {"wq": np.concatenate([v[p + "slr_wq1"], v[p + "slr_wq2"]], 1),
                "wk": np.concatenate([v[p + "slr_wk1"], v[p + "slr_wk2"]], 1), "wv": v[p + "slr_wv"],
                "wo": v[p + "slr_wo"], "r1": v[p + "router_w1"], "r2": v[p + "router_w2"],
                "r2b": rows_of(v[p + "router_b2"]), "landmarks_t": v[p + "landmarks"].T,
                "mix1": v[p + "mix_w"][:D], "mix2": v[p + "mix_w"][D:], "compress": v[p + "bus_compress"],
                "publish": v[p + "bus_publish"], "expand": v[p + "bus_expand"],
                "lam": columns_of(np.repeat(v[p + "lambdas"], D // 8)), "slr_lam": rows_of(v[p + "slr_lam"]),
                "norm_in": columns_of(v[p + "w_norm_in"]), "norm_out": columns_of(v[p + "w_norm_out"])}
    p = "L0_attn_b_"
    wq, wk, wv = (m.T for m in np.split(v[p + "w_attn"], 3))
    g["keep"] = {"wq": in_part_rows(wq, Q_PARTS), "wk": in_part_rows(wk, K_PARTS), "wv": in_row_groups(wv, 0),
                 "wo": v[p + "w_proj"].T}
    p = "L3_ffn_"
    g["cell"] = {k: v[p + k].T for k in ("wf", "uf", "wi", "ui", "wc", "uc", "wo", "uo")}
    g["cell"].update({k: columns_of(v[p + k]) for k in ("bf", "bi", "bc", "bo", "in_c")})
    g["bitffn"] = {"w1": v["L1_ffn_W1"].T, "w2": row_blocks(v["L1_ffn_W2"].T),
                   "b1": columns_of(v["L1_ffn_b1"]), "b2": columns_of(v["L1_ffn_b2"])}
    return g


def pack(matrices):
    at, columns, parts = 0, {}, []
    for name, m in matrices.items():
        m = np.asarray(m)
        columns[name] = (at, m.shape[0], m.shape[1])
        full = np.zeros((P, m.shape[1]), np.float32)
        full[:m.shape[0]] = m
        parts.append(full)
        at += m.shape[1]
    return np.ascontiguousarray(np.concatenate(parts, axis=1)), columns


def kernel(**inputs):
    import concourse.bacc as bacc
    from concourse.bass_utils import run_bass_kernel_spmd

    v = {k: np.asarray(a) for k, a in inputs.items()}
    x = np.ascontiguousarray(v["L0_attn_a_x"].reshape(B * S, D).T)
    nc = bacc.Bacc("TRN2", target_bir_lowering=False, num_devices=1)
    arrays = {"x_in": x}
    x_in = nc.dram_tensor("x_in", x.shape, F32, kind="ExternalInput").ap()
    groups_in, columns = {}, {}
    used = {"const"} | {g for i in PLAN for g in GROUPS_OF[i]}
    for g, matrices in lay_out(v).items():
        if g not in used:
            continue
        packed, columns[g] = pack(matrices)
        arrays[f"in_{g}"] = packed
        groups_in[g] = nc.dram_tensor(f"in_{g}", packed.shape, F32, kind="ExternalInput").ap()
    out = nc.dram_tensor("out", (P, B * S), F32, kind="ExternalOutput").ap()
    build_program(nc, x_in, groups_in, out, columns)
    r = run_bass_kernel_spmd(nc, [arrays], core_ids=[0])
    return np.ascontiguousarray(r.results[0]["out"].T).reshape(B, S, D)
```

```python
from contextlib import ExitStack

import numpy as np

import concourse.bass as bass
from concourse import mybir

F32 = mybir.dt.float32
BF16 = mybir.dt.bfloat16
ALU = mybir.AluOpType
ACT = mybir.ActivationFunctionType
AX = mybir.AxisListType

B, S, D = 4, 512, 128
P = 128
TT = S // P
LN_EPS = 1e-5
NEG = -1e30

PLAN = list(range(16))


class Signal:

    def __init__(self, sem, per):
        self.sem, self.per = sem, per

    def at(self, b, k):
        return b * self.per + (k + 1)


class Layer:

    def __init__(self, nc, name, core, groups, **signals):
        self.nc, self.name, self.core = nc, name, core
        self.ctx = ExitStack()
        self.sems, self.signals = [], {}
        for key, per in signals.items():
            sem = nc.alloc_semaphore(f"{name}_{key}")
            self.sems.append(sem)
            nc.sync.sem_inc(sem, 1)
            self.signals[key] = Signal(sem, per)
        for eng in (nc.tensor, nc.scalar, nc.vector, nc.gpsimd):
            wait_weights(eng, core, "const", *groups)
        nc.all_engine_barrier()

    def __getitem__(self, key):
        return self.signals[key]

    def sb(self, key, shape, dt=F32):
        return self.ctx.enter_context(self.nc.sbuf_tensor(f"{self.name}_{key}", shape, dt))

    def ps(self, key, shape, dt=F32):
        return self.ctx.enter_context(self.nc.psum_tensor(f"{self.name}_{key}", shape, dt))

    def close(self):
        self.ctx.close()
        self.nc.clear_and_free_semaphores(self.sems)
        self.nc.all_engine_barrier()


def wait_weights(eng, core, *groups):
    for g in groups:
        eng.wait_ge(core.landed[g], 16)


class Core:

    def __init__(self, x, xn, weights, landed, columns):
        self.x, self.xn, self.weights, self.landed, self.columns = x, xn, weights, landed, columns

    def w(self, group, name, lo=0, hi=None):
        at, rows, width = self.columns[group][name]
        hi = width if hi is None else hi
        return self.weights[group][0:rows, at + lo:at + hi]

    def all_rows(self, group, name):
        at, _, width = self.columns[group][name]
        return self.weights[group][:, at:at + width]

    def normed(self, b):
        return self.xn[:, bass.ds(b * S, S)]

    def batch(self, b):
        return self.x[:, bass.ds(b * S, S)]




def normalise(nc, core, name):
    L = Layer(nc, name, core, [],
              centred=B,
              square=B,
              kept=B,
              var=B,
              eps=B,
              rstd=B,
              diag=B,
              spread=B,
              xn=B)
    with L.ctx:
        centred, square = L.sb("centred", [P, B, S]), L.sb("square", [P, B, S])
        small = L.sb("small", [P, 2, B, TT])
        diag = L.sb("diag", [P, B, TT, P])
        banks = L.ps("banks", [P, B, S])
        ps_var = L.ps("ps_var", [P, B, S])
        eye = core.w("const", "eye")
        with nc.Block() as block:
            @block.tensor
            def _(pe):
                for step in range(B + 3):
                    if step < B:
                        pe.matmul(banks[:, step, :], core.w("const", "centre"), core.x[:, step * S:(step + 1) * S],
                                  start=True, stop=True).then_inc(L["centred"].sem, 1)
                    b = step - 1
                    if 0 <= b < B:
                        pe.wait_ge(L["square"].sem, L["square"].at(0, b + 1))
                        for t in range(TT):
                            mm = pe.matmul(ps_var[:, b, t:t + 1], square[:, b, t * P:(t + 1) * P],
                                           core.w("const", "mean", 0, 1), start=True, stop=True)
                        mm.then_inc(L["var"].sem, 1)
                    b = step - 3
                    if b >= 0:
                        pe.wait_ge(L["diag"].sem, L["diag"].at(0, b + 1))
                        pe.wait_ge(L["kept"].sem, L["kept"].at(0, b + 1))
                        pe.matmul(banks[:, b, :], core.w("const", "ones"), diag[:, b, :, :], start=True, stop=True)\
                            .then_inc(L["spread"].sem, 1)

            @block.scalar
            def _(act):
                for b in range(B):
                    act.wait_ge(L["centred"].sem, L["centred"].at(0, b + 1))
                    act.activation(square[:, b, :], banks[:, b, :], ACT.Square).then_inc(L["square"].sem, 1)

            @block.vector
            def _(dve):
                for step in range(B + 3):
                    if step < B:
                        b = step
                        dve.wait_ge(L["square"].sem, L["square"].at(0, b + 1))
                        dve.tensor_copy(centred[:, b, :], banks[:, b, :]).then_inc(L["kept"].sem, 1)
                    b = step - 1
                    if 0 <= b < B:
                        dve.wait_ge(L["var"].sem, L["var"].at(0, b + 1))
                        dve.tensor_scalar(small[:, 0, b, :], ps_var[:, b, 0:TT], LN_EPS, None, ALU.add)\
                            .then_inc(L["eps"].sem, 1)
                    b = step - 2
                    if 0 <= b < B:
                        dve.wait_ge(L["rstd"].sem, L["rstd"].at(0, b + 1))
                        dve.tensor_tensor(diag[:, b, :, :], eye.unsqueeze(1).to_broadcast([P, TT, P]),
                                          small[:, 1, b, :].unsqueeze(2).to_broadcast([P, TT, P]), ALU.mult)\
                            .then_inc(L["diag"].sem, 1)
                    b = step - 3
                    if b >= 0:
                        dve.wait_ge(L["kept"].sem, L["kept"].at(0, b + 1))
                        dve.wait_ge(L["spread"].sem, L["spread"].at(0, b + 1))
                        dve.tensor_tensor(core.xn[:, b * S:(b + 1) * S], centred[:, b, :], banks[:, b, :], ALU.mult)\
                            .then_inc(L["xn"].sem, 1)

            @block.gpsimd
            def _(pool):
                for b in range(B):
                    pool.wait_ge(L["eps"].sem, L["eps"].at(0, b + 1))
                    pool.tensor_tensor(small[:, 1, b, :], small[:, 0, b, :], core.w("const", "minus_half", 0, TT), ALU.pow)\
                        .then_inc(L["rstd"].sem, 1)
    L.close()


NEXT = dict(now=1)


def take_normed(dve, L, b, xn):
    dve.tensor_copy(xn, L.core.normed(b)).then_inc(L["now"].sem, 1)

HEADS, HD = 16, 64


def query_softmax_attention(nc, core, name):
    PAIRS = HEADS // 2
    STEPS = PAIRS * TT
    L = Layer(nc, name, core, ["mha"], **NEXT,
              v_ps=2 * TT,
              v_sb=2 * TT,
              qk_ps=2 * PAIRS,
              qk_sb=2 * PAIRS,
              scores=STEPS,
              top=STEPS,
              shift=STEPS,
              probs=2 * STEPS,
              inverse=STEPS,
              vs=STEPS,
              ctx_ps=STEPS,
              ctx_sb=PAIRS,
              joined=PAIRS,
              done=1)
    with L.ctx:
        g = "mha"
        scale = float(HD) ** -0.5
        xn = L.sb("xn", [P, S])
        v = L.sb("v", [P, TT, HEADS * HD])
        q, k = L.sb("q", [P, 2, S]), L.sb("k", [P, 2, S])
        probs = L.sb("probs", [P, 2, 2, S])
        vs = L.sb("vs", [P, 2, 2, HD])
        heads_out = L.sb("heads_out", [P, 2, S])
        stats = L.sb("stats", [P, 4, 4, 2])
        psp = L.ps("psp", [P, 2, 2, S])
        psq = L.ps("psq", [P, S])
        ps_ctx, out, bank = L.ps("ps_ctx", [P, S]), L.ps("out", [P, S]), L.ps("bank", [P, S])

        def project(pe, b, hp):
            for i, (w, ps) in enumerate((("wq", bank), ("wk", psq))):
                if hp == 0:
                    pe.wait_ge(L["v_sb"].sem, L["v_sb"].at(b, 2 * TT))
                else:
                    pe.wait_ge(L["qk_sb"].sem, L["qk_sb"].at(b, 2 * (hp - 1) + i + 1))
                pe.matmul(ps[:, :], core.w(g, w, hp * P, (hp + 1) * P), xn[:, :], start=True, stop=True)\
                    .then_inc(L["qk_ps"].sem, 1)

        def score(pe, b, s):
            hp, kt = divmod(s, TT)
            if kt == 0:
                pe.wait_ge(L["qk_sb"].sem, L["qk_sb"].at(b, 2 * hp + 2))
            pe.wait_ge(L["probs"].sem, L["probs"].at(b, 2 * max(s - 1, 0)))
            for i in range(2):
                r = slice(i * HD, (i + 1) * HD)
                mm = pe.matmul(psp[:, s % 2, i, :], k[r, hp % 2, kt * P:(kt + 1) * P], q[r, hp % 2, :],
                               start=True, stop=True)
            mm.then_inc(L["scores"].sem, 1)

        def context(pe, b, s):
            hp, kt = divmod(s, TT)
            pe.wait_ge(L["vs"].sem, L["vs"].at(b, s + 1))
            if kt == 0:
                pe.wait_ge(L["ctx_sb"].sem, L["ctx_sb"].at(b, hp))
            for i in range(2):
                mm = pe.matmul(ps_ctx[i * HD:(i + 1) * HD, :], vs[:, s % 2, i, :], probs[:, s % 2, i, :],
                               start=kt == 0, stop=kt == TT - 1)
            mm.then_inc(L["ctx_ps"].sem, 1)

        def join(pe, b, hp):
            pe.wait_ge(L["ctx_sb"].sem, L["ctx_sb"].at(b, hp + 1))
            if hp == 0:
                pe.wait_ge(L["done"].sem, L["done"].at(b, 0))
            pe.matmul(out[:, :], core.w(g, "wl", hp * P, (hp + 1) * P), heads_out[:, hp % 2, :],
                      start=hp == 0, stop=hp == PAIRS - 1).then_inc(L["joined"].sem, 1)

        with nc.Block() as block:
            @block.tensor
            def _(pe):
                with pe.Fori(0, B) as b:
                    pe.wait_ge(L["now"].sem, L["now"].at(b, 1))
                    for n in range(2 * TT):
                        t, half = divmod(n, 2)
                        ps = (bank, psq)[half]
                        if n >= 2:
                            pe.wait_ge(L["v_sb"].sem, L["v_sb"].at(b, n - 1))
                        pe.matmul(ps[:, :], xn[:, t * P:(t + 1) * P], core.w(g, "wv", half * S, (half + 1) * S),
                                  start=True, stop=True).then_inc(L["v_ps"].sem, 1)
                    project(pe, b, 0)
                    score(pe, b, 0)
                    score(pe, b, 1)
                    for s in range(STEPS):
                        hp, kt = divmod(s, TT)
                        if kt == 0 and hp + 1 < PAIRS:
                            project(pe, b, hp + 1)
                        if s + 2 < STEPS:
                            score(pe, b, s + 2)
                        context(pe, b, s)
                        if kt == 2 and hp >= 1:
                            join(pe, b, hp - 1)
                    join(pe, b, PAIRS - 1)

            def bias_qk(act, b, hp):
                for i, (n, to, ps) in enumerate((("bq", q, bank), ("bk", k, psq))):
                    act.wait_ge(L["qk_ps"].sem, L["qk_ps"].at(b, 2 * hp + i + 1))
                    act.wait_ge(L["scores"].sem, L["scores"].at(b, TT * max(hp - 1, 0)))
                    act.activation(to[:, hp % 2, :], ps[:, :], ACT.Identity, bias=core.w(g, n, hp, hp + 1))\
                        .then_inc(L["qk_sb"].sem, 1)

            @block.scalar
            def _(act):
                with act.Fori(0, B) as b:
                    bias_qk(act, b, 0)
                    for s in range(STEPS):
                        hp, kt = divmod(s, TT)
                        act.wait_ge(L["shift"].sem, L["shift"].at(b, s + 1))
                        act.wait_ge(L["ctx_ps"].sem, L["ctx_ps"].at(b, max(s - 1, 0)))
                        for i in range(2):
                            act.activation(probs[:, s % 2, i, :], psp[:, s % 2, i, :], ACT.Exp,
                                           bias=stats[:, s % 4, 1, i:i + 1], scale=scale,
                                           accum_out=stats[:, s % 4, 2, i:i + 1]).then_inc(L["probs"].sem, 1)
                        if kt == 0 and hp + 1 < PAIRS:
                            bias_qk(act, b, hp + 1)

            def maxima(dve, b, s):
                dve.wait_ge(L["scores"].sem, L["scores"].at(b, s + 1))
                dve.wait_ge(L["inverse"].sem, L["inverse"].at(b, max(s - 3, 0)))
                dve.tensor_reduce(stats[:, s % 4, 0, :], psp[:, s % 2, :, :], AX.X, ALU.max).then_inc(L["top"].sem, 1)
                dve.wait_ge(L["top"].sem, L["top"].at(b, s + 1))
                dve.tensor_scalar(stats[:, s % 4, 1, :], stats[:, s % 4, 0, :], -scale, None, ALU.mult)\
                    .then_inc(L["shift"].sem, 1)

            def scale_v(dve, b, s):
                hp, kt = divmod(s, TT)
                dve.wait_ge(L["probs"].sem, L["probs"].at(b, 2 * s + 2))
                dve.wait_ge(L["vs"].sem, L["vs"].at(b, max(s - 3, 0)))
                dve.reciprocal(stats[:, s % 4, 3, :], stats[:, s % 4, 2, :]).then_inc(L["inverse"].sem, 1)
                dve.wait_ge(L["inverse"].sem, L["inverse"].at(b, s + 1))
                dve.wait_ge(L["ctx_ps"].sem, L["ctx_ps"].at(b, max(s - 1, 0)))
                dve.tensor_tensor(vs[:, s % 2, :, :],
                                  v[:, kt, hp * P:(hp + 1) * P].rearrange("p (i d) -> p i d", i=2),
                                  stats[:, s % 4, 3, :].unsqueeze(2).to_broadcast([P, 2, HD]), ALU.mult)\
                    .then_inc(L["vs"].sem, 1)

            def take_context(dve, b, hp):
                dve.wait_ge(L["ctx_ps"].sem, L["ctx_ps"].at(b, TT * (hp + 1)))
                dve.wait_ge(L["joined"].sem, L["joined"].at(b, max(hp - 1, 0)))
                dve.tensor_copy(heads_out[:, hp % 2, :], ps_ctx[:, :]).then_inc(L["ctx_sb"].sem, 1)

            @block.vector
            def _(dve):
                with dve.Fori(0, B) as b:
                    take_normed(dve, L, b, xn[:, :])
                    dve.wait_ge(L["vs"].sem, L["vs"].at(b, 0))
                    for n in range(2 * TT):
                        t, half = divmod(n, 2)
                        dve.wait_ge(L["v_ps"].sem, L["v_ps"].at(b, n + 1))
                        dve.tensor_tensor(v[:, t, half * S:(half + 1) * S], (bank, psq)[half][:, :],
                                          core.w(g, "bv", half * S, (half + 1) * S), ALU.add).then_inc(L["v_sb"].sem, 1)
                    maxima(dve, b, 0)
                    maxima(dve, b, 1)
                    dve.wait_ge(L["v_sb"].sem, L["v_sb"].at(b, 2 * TT))
                    for s in range(STEPS):
                        hp, kt = divmod(s, TT)
                        if kt == 0 and hp >= 1:
                            take_context(dve, b, hp - 1)
                        scale_v(dve, b, s)
                        if s + 2 < STEPS:
                            maxima(dve, b, s + 2)
                    take_context(dve, b, PAIRS - 1)
                    dve.wait_ge(L["joined"].sem, L["joined"].at(b, PAIRS))
                    dve.scalar_tensor_tensor(out=core.batch(b), in0=out[:, :], scalar=core.w(g, "bl"),
                                             in1=core.batch(b), op0=ALU.add, op1=ALU.add).then_inc(L["done"].sem, 1)

    L.close()


def routed_ffn(nc, core, name, group, E, routed, shared, gated):
    NT = routed + shared
    PARTS = 3 * E
    L = Layer(nc, name, core, [group],
              logits=1,
              route=23,
              expd=1,
              turned=1,
              parts_in=1,
              weights_in=1,
              up=NT,
              first=NT,
              product=NT,
              silu=NT,
              spread=routed,
              hidden=routed,
              down=NT + gated,
              cast=4, done=1)
    with L.ctx:
        pick16 = L.sb("pick16", [P, routed * P], BF16)
        eye16 = L.sb("eye16", [P, P], BF16)
        NTOK = B * TT
        small = L.sb("small", [P, 4, NTOK])
        e = L.sb("e", [P, NTOK, E])
        prob = L.sb("prob", [P, NTOK, E])
        key = L.sb("key", [P, NTOK, E])
        tie = L.sb("tie", [P, NTOK, E])
        chosen = L.sb("chosen", [P, 2, NTOK, E])
        cw = L.sb("cw", [P, NTOK, E])
        rest = L.sb("rest", [P, 2, NTOK, E])
        parts_wide = L.sb("parts", [P, NTOK, P], BF16)
        parts = parts_wide[:, :, 0:PARTS].rearrange("p t (a e) -> p t a e", e=E)
        cw_rows = L.sb("cw_rows", [P, B * S])
        part_rows = L.sb("part_rows", [P, B * S], BF16)
        first = L.sb("first", [P, 2, S])
        product = L.sb("product", [P, 2, S])
        act_out = L.sb("act_out", [P, 2, S])
        h = L.sb("h", [P, 2, S])
        psg, psu = L.ps("psg", [P, 2, S]), L.ps("psu", [P, 2, S])
        psc = L.ps("psc", [P, 2, S])
        out, ps_small = L.ps("out", [P, S]), L.ps("ps_small", [P, S])
        logits = ps_small[:, 0:NTOK * E].rearrange("p (t e) -> p t e", e=E)
        ps_parts = psc[:, :, :].rearrange("p i s -> p (i s)").bitcast(BF16)

        def ps_weights(b):
            return (psg, psu)[b // 2][0:E, b % 2, :]

        w1, w3, w2 = (core.w(group, k) for k in ("w1", "w3", "w2"))
        eye = core.w("const", "eye")
        falling = core.w("const", "falling" if E == 16 else "falling8", 0, E).unsqueeze(1).to_broadcast([P, NTOK, E])

        def over_e(col):
            return col.unsqueeze(2).to_broadcast([P, NTOK, E])

        def up(pe, b, m):
            pe.wait_ge(L["first"].sem, L["first"].at(b, max(m - 1, 0)))
            pe.wait_ge(L["product"].sem, L["product"].at(b, max(m - 1, 0)))
            pe.matmul(psg[:, m % 2, :], w1[:, m * P:(m + 1) * P], core.normed(b), start=True, stop=True)
            pe.matmul(psu[:, m % 2, :], w3[:, m * P:(m + 1) * P], core.normed(b), start=True, stop=True)\
                .then_inc(L["up"].sem, 1)

        def spread(pe, b, m):
            pe.wait_ge(L["hidden"].sem, L["hidden"].at(b, max(m - 1, 0)))
            pe.matmul(psc[:, m % 2, :], pick16[:, m * P:(m + 1) * P], part_rows[:, bass.ds(b * S, S)],
                      start=True, stop=True)\
                .then_inc(L["spread"].sem, 1)

        def down(pe, b, m):
            if m == 0:
                pe.wait_ge(L["done"].sem, L["done"].at(b, 0))
            if m < routed:
                pe.wait_ge(L["hidden"].sem, L["hidden"].at(b, m + 1))
            elif gated:
                pe.wait_ge(L["silu"].sem, L["silu"].at(b, m + 1))
            else:
                pe.wait_ge(L["product"].sem, L["product"].at(b, m + 1))
            pe.matmul(out[:, :], w2[:, m * P:(m + 1) * P], h[:, m % 2, :], start=m == 0,
                      stop=m == NT - 1 and not gated).then_inc(L["down"].sem, 1)

        def factor(act, b, m):
            act.wait_ge(L["up"].sem, L["up"].at(b, m + 1))
            act.wait_ge(L["product"].sem, L["product"].at(b, max(m - 1, 0)))
            if gated:
                act.activation(first[:, m % 2, :], psg[:, m % 2, :], ACT.Identity,
                               bias=core.w(group, "b1", m, m + 1)[:, :]).then_inc(L["first"].sem, 1)
            else:
                act.activation(first[:, m % 2, :], psg[:, m % 2, :], ACT.Silu).then_inc(L["first"].sem, 1)

        def silu(act, b, m):
            act.wait_ge(L["product"].sem, L["product"].at(b, m + 1))
            if m < routed:
                act.wait_ge(L["hidden"].sem, L["hidden"].at(b, max(m - 1, 0)))
                to = act_out
            else:
                act.wait_ge(L["down"].sem, L["down"].at(b, m - 1))
                to = h
            act.activation(to[:, m % 2, :], product[:, m % 2, :], ACT.Silu).then_inc(L["silu"].sem, 1)

        def multiply(dve, b, m):
            dve.wait_ge(L["first"].sem, L["first"].at(b, m + 1))
            if gated:
                dve.wait_ge(L["silu"].sem, L["silu"].at(b, max(m - 1, 0)))
                dve.scalar_tensor_tensor(out=product[:, m % 2, :], in0=psu[:, m % 2, :],
                                         scalar=core.w(group, "b3", m, m + 1)[:, :], in1=first[:, m % 2, :],
                                         op0=ALU.add, op1=ALU.mult).then_inc(L["product"].sem, 1)
                return
            dve.wait_ge(L["hidden"].sem, L["hidden"].at(b, max(m - 1, 0)))
            to = product
            if m >= routed:
                dve.wait_ge(L["down"].sem, L["down"].at(b, m - 1))
                to = h
            dve.tensor_tensor(to[:, m % 2, :], psu[:, m % 2, :], first[:, m % 2, :], ALU.mult)\
                .then_inc(L["product"].sem, 1)

        def finish(dve, b, m):
            if gated:
                dve.wait_ge(L["silu"].sem, L["silu"].at(b, m + 1))
            else:
                dve.wait_ge(L["product"].sem, L["product"].at(b, m + 1))
            dve.wait_ge(L["spread"].sem, L["spread"].at(b, m + 1))
            dve.wait_ge(L["down"].sem, L["down"].at(b, max(m - 1, 0)))
            dve.tensor_tensor(h[:, m % 2, :], (act_out if gated else product)[:, m % 2, :], psc[:, m % 2, :], ALU.mult)\
                .then_inc(L["hidden"].sem, 1)

        def choose(dve):
            dve.wait_ge(L["logits"].sem, L["logits"].at(0, 1))
            dve.tensor_reduce(small[:, 0, :], logits, AX.X, ALU.max).then_inc(L["route"].sem, 1)
            dve.wait_ge(L["route"].sem, L["route"].at(0, 1))
            dve.tensor_tensor(e[:, :, :], logits, over_e(small[:, 0, :]), ALU.subtract).then_inc(L["route"].sem, 1)
            dve.wait_ge(L["expd"].sem, L["expd"].at(0, 1))
            dve.tensor_reduce(small[:, 1, :], e[:, :, :], AX.X, ALU.add).then_inc(L["route"].sem, 1)
            dve.wait_ge(L["route"].sem, L["route"].at(0, 3))
            dve.reciprocal(small[:, 2, :], small[:, 1, :]).then_inc(L["route"].sem, 1)
            dve.wait_ge(L["route"].sem, L["route"].at(0, 4))
            dve.tensor_tensor(prob[:, :, :], e[:, :, :], over_e(small[:, 2, :]), ALU.mult).then_inc(L["route"].sem, 1)
            dve.wait_ge(L["route"].sem, L["route"].at(0, 5))
            if gated:
                bias = core.w(group, "gate_b", 0, E).unsqueeze(1).to_broadcast([P, NTOK, E])
                dve.tensor_tensor(key[:, :, :], prob[:, :, :], bias, ALU.add).then_inc(L["route"].sem, 1)
            else:
                dve.tensor_copy(key[:, :, :], prob[:, :, :]).then_inc(L["route"].sem, 1)
            n = 6
            for i in range(2):
                dve.wait_ge(L["route"].sem, L["route"].at(0, n))
                dve.tensor_reduce(small[:, 3, :], key[:, :, :], AX.X, ALU.max).then_inc(L["route"].sem, 1)
                dve.wait_ge(L["route"].sem, L["route"].at(0, n + 1))
                dve.tensor_tensor(tie[:, :, :], key[:, :, :], over_e(small[:, 3, :]), ALU.is_equal)\
                    .then_inc(L["route"].sem, 1)
                dve.wait_ge(L["route"].sem, L["route"].at(0, n + 2))
                dve.tensor_tensor(tie[:, :, :], tie[:, :, :], falling, ALU.mult).then_inc(L["route"].sem, 1)
                dve.wait_ge(L["route"].sem, L["route"].at(0, n + 3))
                dve.tensor_reduce(small[:, 3, :], tie[:, :, :], AX.X, ALU.max).then_inc(L["route"].sem, 1)
                dve.wait_ge(L["route"].sem, L["route"].at(0, n + 4))
                dve.tensor_tensor(chosen[:, i, :, :], tie[:, :, :], over_e(small[:, 3, :]), ALU.is_equal)\
                    .then_inc(L["route"].sem, 1)
                dve.wait_ge(L["route"].sem, L["route"].at(0, n + 5))
                if i == 0:
                    dve.scalar_tensor_tensor(out=key[:, :, :], in0=chosen[:, 0, :, :], scalar=NEG, in1=key[:, :, :],
                                             op0=ALU.mult, op1=ALU.add).then_inc(L["route"].sem, 1)
                    n += 6
            dve.tensor_tensor(chosen[:, 0, :, :], chosen[:, 0, :, :], chosen[:, 1, :, :], ALU.add)\
                .then_inc(L["route"].sem, 1)
            dve.wait_ge(L["route"].sem, L["route"].at(0, 18))
            dve.tensor_tensor(cw[:, :, :], chosen[:, 0, :, :], prob[:, :, :], ALU.mult).then_inc(L["route"].sem, 1)
            dve.wait_ge(L["route"].sem, L["route"].at(0, 19))
            dve.tensor_copy(parts[:, :, 0, :], cw[:, :, :]).then_inc(L["route"].sem, 1)
            dve.wait_ge(L["route"].sem, L["route"].at(0, 20))
            dve.tensor_tensor(rest[:, 0, :, :], cw[:, :, :], parts[:, :, 0, :], ALU.subtract).then_inc(L["route"].sem, 1)
            dve.wait_ge(L["route"].sem, L["route"].at(0, 21))
            dve.tensor_copy(parts[:, :, 1, :], rest[:, 0, :, :]).then_inc(L["route"].sem, 1)
            dve.wait_ge(L["route"].sem, L["route"].at(0, 22))
            dve.tensor_tensor(parts[:, :, 2, :], rest[:, 0, :, :], parts[:, :, 1, :], ALU.subtract)\
                .then_inc(L["route"].sem, 1)

        STEPS = 23
        with nc.Block() as block:
            @block.tensor
            def _(pe):
                for t in range(NTOK):
                    mm = pe.matmul(logits[:, t, :], core.xn[:, t * P:(t + 1) * P], core.w(group, "wr"),
                                   start=True, stop=True)
                mm.then_inc(L["logits"].sem, 1)
                pe.wait_ge(L["cast"].sem, L["cast"].at(0, 4))
                pe.wait_ge(L["route"].sem, L["route"].at(0, STEPS))
                if gated:
                    for t in range(NTOK):
                        pe.transpose(ps_weights(t // TT)[:, t % TT * P:(t % TT + 1) * P], cw[:, t, :], eye)
                for t in range(NTOK):
                    mm = pe.transpose(ps_parts[:, t * P:(t + 1) * P], parts_wide[:, t, :], eye16[:, :])
                mm.then_inc(L["turned"].sem, 1)
                if gated:
                    pe.wait_ge(L["weights_in"].sem, L["weights_in"].at(0, 1))
                pe.wait_ge(L["parts_in"].sem, L["parts_in"].at(0, 1))
                with pe.Fori(0, B) as b:
                    up(pe, b, 0)
                    up(pe, b, 1)
                    spread(pe, b, 0)
                    for m in range(NT):
                        if m + 2 < NT:
                            up(pe, b, m + 2)
                        if m + 1 < routed:
                            spread(pe, b, m + 1)
                        down(pe, b, m)
                    if gated:
                        pe.matmul(out[:, :], core.all_rows(group, "b2"), cw_rows[:, bass.ds(b * S, S)], start=False, stop=True)\
                            .then_inc(L["down"].sem, 1)

            @block.scalar
            def _(act):
                act.wait_ge(L["route"].sem, L["route"].at(0, 2))
                act.activation(e[:, :, :], e[:, :, :], ACT.Exp).then_inc(L["expd"].sem, 1)
                act.wait_ge(L["turned"].sem, L["turned"].at(0, 1))
                act.activation(part_rows[:, :], ps_parts, ACT.Copy).then_inc(L["parts_in"].sem, 1)
                with act.Fori(0, B) as b:
                    factor(act, b, 0)
                    factor(act, b, 1)
                    for m in range(NT):
                        if gated:
                            silu(act, b, m)
                        if m + 2 < NT:
                            factor(act, b, m + 2)

            @block.vector
            def _(dve):
                dve.wait_ge(L["cast"].sem, L["cast"].at(0, 2))
                choose(dve)
                if gated:
                    dve.wait_ge(L["turned"].sem, L["turned"].at(0, 1))
                    for b in range(B):
                        copied = dve.tensor_copy(cw_rows[0:E, b * S:(b + 1) * S], ps_weights(b))
                    copied.then_inc(L["weights_in"].sem, 1)
                with dve.Fori(0, B) as b:
                    multiply(dve, b, 0)
                    for m in range(NT):
                        if m + 1 < NT:
                            multiply(dve, b, m + 1)
                        if m < routed:
                            finish(dve, b, m)
                    dve.wait_ge(L["down"].sem, L["down"].at(b, NT + gated))
                    dve.scalar_tensor_tensor(out=core.batch(b), in0=out[:, :],
                                             scalar=core.w(group, "sb2") if gated else 0.0, in1=core.batch(b),
                                             op0=ALU.add, op1=ALU.add).then_inc(L["done"].sem, 1)

            @block.gpsimd
            def _(pool):
                pool.memset(parts_wide[:, :, :], 0.0).then_inc(L["cast"].sem, 1)
                pool.memset(cw_rows[:, :], 0.0).then_inc(L["cast"].sem, 1)
                pool.tensor_copy(pick16[:, :], core.all_rows(group, "pick")).then_inc(L["cast"].sem, 1)
                pool.tensor_copy(eye16[:, :], eye).then_inc(L["cast"].sem, 1)
    L.close()

KH, KHD = 16, 8
KJ, KG = 4, 4
KEPT, RECENT = 391, 64
DROPPED = S - KEPT
OLD = S - RECENT
KT = KH // 2
HALF = P // 2
Q_PARTS, K_PARTS = "hhmhlm", "hmhlhm"
MASK_ROW = len(Q_PARTS) * KHD
SHIFT_ROW = MASK_ROW + 1
KSTEPS = KT * TT
LAG = 6


def keep_attention(nc, core, name):
    ROUNDS = DROPPED // 8
    L = Layer(nc, name, core, ["keep"], cast=4, zero=2,
              p1=2 * KT, high1=2 * KT, rest1=2 * KT, mid1=2 * KT, stack1=2 * KT,
              p2=2 * KT, high2=2 * KT, rest2=2 * KT, mid2=2 * KT, stack2=2 * KT,
              s1=KSTEPS, top1=KSTEPS, shift1=KSTEPS, exp1=2 * KSTEPS, inv1=KSTEPS, pick1=KSTEPS,
              sums1=KSTEPS, added=1,
              choice=2 * ROUNDS + 13,
              masked=1,
              current=1,
              pv=TT, v=TT,
              s2=2 * KSTEPS, top2=2 * KSTEPS,
              low2=4 * KT,
              rows=KT, q2=KT,
              st=2 * KSTEPS, exp2=2 * KSTEPS, av=KSTEPS,
              c_sb=KJ, c_turn=KJ, c_inv=KJ, c_out=KJ,
              o_turn=1, o_sb=1, projected=1, done=1)
    with L.ctx:
        w = lambda n, *a: core.w("keep", n, *a)
        scale = float(KHD) ** -0.5
        cur = L.sb("cur", [P, S])
        high, mid = L.sb("high", [P, 2, S], BF16), L.sb("mid", [P, 2, S], BF16)
        rest = L.sb("rest", [P, 2, S])
        stack = L.sb("stack", [P, 4, 2, S], BF16)
        probs = L.sb("probs", [P, 2, 2, S])
        stats = L.sb("stats", [P, 4, 4, 2])
        pick = L.sb("pick", [P, 2, 2, 32])
        sums = L.sb("sums", [P, S])
        work = L.sb("work", [P, OLD])
        best = L.sb("best", [P, 8])
        lt, eq, cum = (L.sb(n, [P, OLD]) for n in ("lt", "eq", "cum"))
        counts = L.sb("counts", [P, 2])
        mask = L.sb("mask", [P, S])
        bmask = L.sb("bmask", [P, S], BF16)
        tops, tops_rest = L.sb("tops", [P, 2, TT, 2]), L.sb("tops_rest", [P, TT, 2])
        low = L.sb("low", [P, 2, TT, P], BF16)
        v = L.sb("v", [P, TT, KH * 32])
        c_sb = L.sb("c_sb", [P, S])
        c_inv = L.sb("c_inv", [P, TT, KG])
        outs, outs_t = L.sb("outs", [P, TT, D]), L.sb("outs_t", [P, S])
        eye16, later16 = L.sb("eye16", [P, P], BF16), L.sb("later16", [P, P], BF16)
        mask_rows16 = L.sb("mask_rows16", [P, KT * P], BF16)
        ring = L.ps("ring", [P, 4, S])
        acc, psq, pst, out = (L.ps(n, [P, S]) for n in ("acc", "psq", "pst", "out"))
        eye = core.w("const", "eye")
        sources = (("wq", psq, "q_ones", "q_rest", "q_last"), ("wk", pst, "k_ones", "k_rest", "k_last"))

        def half(i):
            return slice(i * HALF, (i + 1) * HALF)

        def group_of(T, i):
            g = 2 * (T % 2) + i
            return slice(32 * g, 32 * g + 32)


        def project(pe, b, n, T, which=(0, 1)):
            for i in which:
                matrix, ps, *_ = sources[i]
                pe.wait_ge(L["rest" + n].sem, L["rest" + n].at(b, max(2 * T - 1 + i, 0)))
                mm = pe.matmul(ps[:, :], w(matrix, T * P, (T + 1) * P), core.normed(b), start=True, stop=True,
                               skip_group_check=True)
                if n == "2" and i == 1:
                    pe.wait_ge(L["masked"].sem, L["masked"].at(b, 1))
                    mm = pe.matmul(ps[:, :], mask_rows16[:, T * P:(T + 1) * P], bmask[:, :], start=False, stop=True,
                                   skip_group_check=True)
                mm.then_inc(L["p" + n].sem, 1)

        def high_part(act, b, n, T, which=(0, 1)):
            for i in which:
                _, ps, ones, _, _ = sources[i]
                act.wait_ge(L["p" + n].sem, L["p" + n].at(b, 2 * T + i + 1))
                act.wait_ge(L["rest" + n].sem, L["rest" + n].at(b, max(2 * T - 1 + i, 0)))
                act.activation(high[:, i, :], ps[:, :], ACT.Identity, bias=core.w("const", ones))\
                    .then_inc(L["high" + n].sem, 1)

        def take_rest(dve, b, n, T, which=(0, 1)):
            for i in which:
                _, ps, _, coefficient, _ = sources[i]
                dve.wait_ge(L["high" + n].sem, L["high" + n].at(b, 2 * T + i + 1))
                dve.wait_ge(L["stack" + n].sem, L["stack" + n].at(b, max(2 * T - 1 + i, 0)))
                dve.scalar_tensor_tensor(out=rest[:, i, :], in0=high[:, i, :], scalar=core.w("const", coefficient),
                                         in1=ps[:, :], op0=ALU.mult, op1=ALU.add).then_inc(L["rest" + n].sem, 1)

        def middle_part(pool, b, n, T):
            for i in range(2):
                pool.wait_ge(L["rest" + n].sem, L["rest" + n].at(b, 2 * T + i + 1))
                pool.wait_ge(L["stack" + n].sem, L["stack" + n].at(b, max(2 * T - 1 + i, 0)))
                pool.tensor_tensor(mid[:, i, :], rest[:, i, :], core.w("const", "ones_s"), ALU.mult).then_inc(L["mid" + n].sem, 1)

        def stack_parts(dve, b, n, T, which=(0, 1)):
            for i in which:
                coefficient = sources[i][4]
                dve.wait_ge(L["mid" + n].sem, L["mid" + n].at(b, 2 * T + i + 1))
                if n == "1":
                    dve.wait_ge(L["s1"].sem, L["s1"].at(b, TT * max(T - 3, 0)))
                else:
                    dve.wait_ge(L["st"].sem, L["st"].at(b, 2 * TT * max(T - 3, 0)))
                dve.scalar_tensor_tensor(out=stack[:, T % 4, i, :], in0=mid[:, i, :],
                                         scalar=core.w("const", coefficient), in1=rest[:, i, :],
                                         op0=ALU.mult, op1=ALU.add).then_inc(L["stack" + n].sem, 1)


        def score1(pe, b, s):
            T, t = divmod(s, TT)
            qt = TT - 1 - t
            N = (qt + 1) * P
            if t == 0:
                pe.wait_ge(L["stack1"].sem, L["stack1"].at(b, 2 * T + 2))
            pe.wait_ge(L["exp1"].sem, L["exp1"].at(b, 2 * max(s - 1, 0)))
            for i in range(2):
                bank = ring[:, 2 * (s % 2) + i, :]
                pe.matmul(bank[:, 0:N], stack[half(i), T % 4, 0, qt * P:(qt + 1) * P], stack[half(i), T % 4, 1, 0:N],
                          start=True, stop=True, skip_group_check=True)
            for i in range(2):
                mm = pe.matmul(ring[:, 2 * (s % 2) + i, qt * P:N], eye16[:, :], later16[:, :], start=False, stop=True,
                               skip_group_check=True)
            mm.then_inc(L["s1"].sem, 1)

        def importance(pe, b, s):
            T, t = divmod(s, TT)
            N = (TT - t) * P
            pe.wait_ge(L["pick1"].sem, L["pick1"].at(b, s + 1))
            if s == 0:
                pe.wait_ge(L["added"].sem, L["added"].at(b, 0))
            for i in range(2):
                mm = pe.matmul(acc[group_of(T, i), 0:N], pick[:, s % 2, i, :], probs[:, s % 2, i, 0:N],
                               start=T < 2 and t == 0, stop=True, skip_group_check=True)
            mm.then_inc(L["sums1"].sem, 1)

        def maxima1(dve, b, s):
            N = (TT - s % TT) * P
            dve.wait_ge(L["s1"].sem, L["s1"].at(b, s + 1))
            dve.wait_ge(L["inv1"].sem, L["inv1"].at(b, max(s - 3, 0)))
            dve.tensor_reduce(stats[:, s % 4, 0, :], ring[:, 2 * (s % 2):2 * (s % 2) + 2, 0:N], AX.X, ALU.max)\
                .then_inc(L["top1"].sem, 1)
            dve.wait_ge(L["top1"].sem, L["top1"].at(b, s + 1))
            dve.tensor_scalar(stats[:, s % 4, 1, :], stats[:, s % 4, 0, :], -scale, None, ALU.mult)\
                .then_inc(L["shift1"].sem, 1)

        def inverse1(dve, b, s):
            j = s // (2 * TT)
            dve.wait_ge(L["exp1"].sem, L["exp1"].at(b, 2 * s + 2))
            dve.wait_ge(L["pick1"].sem, L["pick1"].at(b, max(s - 3, 0)))
            dve.reciprocal(stats[:, s % 4, 3, :], stats[:, s % 4, 2, :]).then_inc(L["inv1"].sem, 1)
            dve.wait_ge(L["inv1"].sem, L["inv1"].at(b, s + 1))
            dve.wait_ge(L["sums1"].sem, L["sums1"].at(b, max(s - 1, 0)))
            at = core.columns["const"]["units32"][0]
            hot = core.weights["const"][:, bass.ds(b * (KJ * 32) + (at + j * 32), 32)]
            dve.tensor_tensor(pick[:, s % 2, :, :], hot.unsqueeze(1).to_broadcast([P, 2, 32]),
                              stats[:, s % 4, 3, :].unsqueeze(2).to_broadcast([P, 2, 32]), ALU.mult)\
                .then_inc(L["pick1"].sem, 1)


        def choose(dve):
            dve.wait_ge(L["added"].sem, L["added"].at(B - 1, 1))
            dve.tensor_scalar(work[:, :], sums[:, 0:OLD], -1.0, None, ALU.mult)\
                .then_inc(L["choice"].sem, 1)
            dve.wait_ge(L["choice"].sem, L["choice"].at(0, 1))
            for r in range(ROUNDS):
                dve.max(best[:, :], work[:, :])\
                    .then_inc(L["choice"].sem, 1)
                dve.wait_ge(L["choice"].sem, L["choice"].at(0, 2 * r + 2))
                dve.match_replace(out=work[:, :], in_to_replace=best[:, :], in_values=work[:, :], imm_value=NEG)\
                    .then_inc(L["choice"].sem, 1)
                dve.wait_ge(L["choice"].sem, L["choice"].at(0, 2 * r + 3))
            n = 2 * ROUNDS + 1
            dve.max(best[:, :], work[:, :])\
                .then_inc(L["choice"].sem, 1)
            dve.wait_ge(L["choice"].sem, L["choice"].at(0, n + 1))
            last = best[:, (DROPPED - 1) % 8:(DROPPED - 1) % 8 + 1]
            dve.tensor_scalar(work[:, :], sums[:, 0:OLD], -1.0, None, ALU.mult)\
                .then_inc(L["choice"].sem, 1)
            dve.wait_ge(L["choice"].sem, L["choice"].at(0, n + 2))
            dve.tensor_scalar(lt[:, :], work[:, :], last, None, ALU.is_gt)\
                .then_inc(L["choice"].sem, 1)
            dve.wait_ge(L["choice"].sem, L["choice"].at(0, n + 3))
            dve.tensor_scalar(eq[:, :], work[:, :], last, None, ALU.is_equal)\
                .then_inc(L["choice"].sem, 1)
            dve.wait_ge(L["choice"].sem, L["choice"].at(0, n + 4))
            dve.tensor_reduce(counts[:, 0:1], lt[:, :], AX.X, ALU.add)\
                .then_inc(L["choice"].sem, 1)
            dve.wait_ge(L["choice"].sem, L["choice"].at(0, n + 5))
            dve.tensor_tensor_scan(cum[:, :], core.w("const", "ones_s", 0, OLD), eq[:, :], 0.0, ALU.mult, ALU.add)\
                .then_inc(L["choice"].sem, 1)
            dve.wait_ge(L["choice"].sem, L["choice"].at(0, n + 6))
            dve.tensor_scalar(counts[:, 1:2], counts[:, 0:1], cum[:, OLD - 1:OLD], -float(DROPPED), ALU.add, ALU.add)\
                .then_inc(L["choice"].sem, 1)
            dve.wait_ge(L["choice"].sem, L["choice"].at(0, n + 7))
            dve.tensor_tensor(work[:, :], eq[:, :], cum[:, :], ALU.subtract)\
                .then_inc(L["choice"].sem, 1)
            dve.wait_ge(L["choice"].sem, L["choice"].at(0, n + 8))
            dve.tensor_scalar(work[:, :], work[:, :], counts[:, 1:2], 0.0, ALU.add, ALU.is_le)\
                .then_inc(L["choice"].sem, 1)
            dve.wait_ge(L["choice"].sem, L["choice"].at(0, n + 9))
            dve.tensor_tensor(work[:, :], work[:, :], eq[:, :], ALU.mult)\
                .then_inc(L["choice"].sem, 1)
            dve.wait_ge(L["choice"].sem, L["choice"].at(0, n + 10))
            dve.tensor_tensor(work[:, :], work[:, :], lt[:, :], ALU.add)\
                .then_inc(L["choice"].sem, 1)
            dve.wait_ge(L["choice"].sem, L["choice"].at(0, n + 11))
            dve.tensor_scalar(mask[:, 0:OLD], work[:, :], NEG, None, ALU.mult)\
                .then_inc(L["choice"].sem, 1)
            dve.wait_ge(L["choice"].sem, L["choice"].at(0, n + 12))


        def score2(pe, b, s, i):
            T, t = divmod(s, TT)
            if t == 0 and i == 0:
                pe.wait_ge(L["stack2"].sem, L["stack2"].at(b, 2 * T + 2))
            pe.wait_ge(L["top2"].sem, L["top2"].at(b, max(2 * s - 1 + i, 0)))
            pe.matmul(ring[:, i, :], stack[half(i), T % 4, 0, t * P:(t + 1) * P], stack[half(i), T % 4, 1, :],
                      start=True, stop=True).then_inc(L["s2"].sem, 1)

        def score_by_keys(pe, b, s, i):
            T, t = divmod(s, TT)
            if t == 0 and i == 0:
                pe.wait_ge(L["q2"].sem, L["q2"].at(b, T + 1))
            pe.wait_ge(L["exp2"].sem, L["exp2"].at(b, max(2 * s - 1 + i, 0)))
            pe.matmul(ring[:, 2 + i, :], stack[half(i), T % 4, 1, t * P:(t + 1) * P], stack[half(i), T % 4, 0, :],
                      start=True, stop=True).then_inc(L["st"].sem, 1)

        def contexts(pe, b, s):
            T, t = divmod(s, TT)
            pe.wait_ge(L["exp2"].sem, L["exp2"].at(b, 2 * s + 2))
            if s % (2 * TT) == 0:
                pe.wait_ge(L["c_sb"].sem, L["c_sb"].at(b, T // 2))
            for i in range(2):
                h = 2 * T + i
                mm = pe.matmul(acc[group_of(T, i), :], v[:, t, 32 * h:32 * h + 32], probs[:, s % 2, i, :],
                               start=t == 0, stop=t == TT - 1, skip_group_check=True)
            mm.then_inc(L["av"].sem, 1)

        def shift_rows(pe, b, T):
            pe.wait_ge(L["low2"].sem, L["low2"].at(b, 4 * (T + 1)))
            pe.wait_ge(L["v"].sem, L["v"].at(b, TT))
            pe.wait_ge(L["q2"].sem, L["q2"].at(b, T))
            pe.wait_ge(L["c_out"].sem, L["c_out"].at(b, max((T - 2) // 2, 0)))
            for t in range(TT):
                mm = pe.matmul(out[:, t * P:(t + 1) * P], low[:, T % 2, t, :], eye16[:, :], start=True, stop=True,
                               skip_group_check=True)
            mm.then_inc(L["rows"].sem, 1)

        def lower_parts(dve, b, T):
            to = low[:, T % 2, :, :].rearrange("p t (i c) -> p t i c", i=2)
            dve.wait_ge(L["top2"].sem, L["top2"].at(b, 2 * TT * (T + 1)))
            dve.wait_ge(L["rows"].sem, L["rows"].at(b, max(T - 1, 0)))
            dve.wait_ge(L["low2"].sem, L["low2"].at(b, 4 * T))
            dve.tensor_scalar(to[:, :, :, SHIFT_ROW], tops[:, T % 2, :, :], -1.0, None, ALU.mult)\
                .then_inc(L["low2"].sem, 1)
            dve.wait_ge(L["low2"].sem, L["low2"].at(b, 4 * T + 1))
            dve.scalar_tensor_tensor(out=tops_rest[:, :, :], in0=tops[:, T % 2, :, :], scalar=-1.0,
                                     in1=to[:, :, :, SHIFT_ROW], op0=ALU.mult, op1=ALU.subtract)\
                .then_inc(L["low2"].sem, 1)
            dve.wait_ge(L["low2"].sem, L["low2"].at(b, 4 * T + 2))
            dve.tensor_copy(to[:, :, :, SHIFT_ROW + 1], tops_rest[:, :, :]).then_inc(L["low2"].sem, 1)
            dve.wait_ge(L["low2"].sem, L["low2"].at(b, 4 * T + 3))
            dve.tensor_tensor(to[:, :, :, SHIFT_ROW + 2], tops_rest[:, :, :], to[:, :, :, SHIFT_ROW + 1], ALU.subtract)\
                .then_inc(L["low2"].sem, 1)

        with nc.Block() as block:
            @block.tensor
            def _(pe):
                pe.wait_ge(L["cast"].sem, L["cast"].at(0, 3))
                with pe.Fori(0, B) as b:
                    project(pe, b, "1", 0)
                    project(pe, b, "1", 1)
                    score1(pe, b, 0)
                    score1(pe, b, 1)
                    for s in range(KSTEPS):
                        if s + 2 < KSTEPS:
                            score1(pe, b, s + 2)
                        if s % TT == 1 and s // TT + 2 < KT:
                            project(pe, b, "1", s // TT + 2, (0,))
                        if s % TT == 2 and s // TT + 2 < KT:
                            project(pe, b, "1", s // TT + 2, (1,))
                        importance(pe, b, s)
                pe.wait_ge(L["choice"].sem, L["choice"].at(0, L["choice"].per))
                with pe.Fori(0, B) as b:
                    pe.wait_ge(L["o_sb"].sem, L["o_sb"].at(b, 0))
                    pe.wait_ge(L["current"].sem, L["current"].at(b, 1))
                    project(pe, b, "2", 0)
                    project(pe, b, "2", 1)
                    for i in range(KSTEPS + LAG + 2):
                        s = i - LAG
                        for h in range(2):
                            if i < KSTEPS:
                                score2(pe, b, i, h)
                            if 0 <= s < KSTEPS:
                                score_by_keys(pe, b, s, h)
                        if i < TT:
                            pe.wait_ge(L["v"].sem, L["v"].at(b, i))
                            if i == 0:
                                pe.wait_ge(L["done"].sem, L["done"].at(b, 0))
                            pe.matmul(out[:, :], cur[:, i * P:(i + 1) * P], w("wv"), start=True, stop=True)\
                                .then_inc(L["pv"].sem, 1)
                        if i % TT == 1 and TT < i < KSTEPS + TT:
                            shift_rows(pe, b, i // TT - 1)
                        if 1 <= s <= KSTEPS:
                            contexts(pe, b, s - 1)
                        if i % TT == 1 and i // TT + 2 < KT:
                            project(pe, b, "2", i // TT + 2, (0,))
                        if i % TT == 2 and i // TT + 2 < KT:
                            project(pe, b, "2", i // TT + 2, (1,))
                        if s > 1 and (s - 1) % (2 * TT) == 0:
                            j = s // (2 * TT)
                            pe.wait_ge(L["c_sb"].sem, L["c_sb"].at(b, j))
                            pe.wait_ge(L["q2"].sem, L["q2"].at(b, min(2 * j + 1, KT)))
                            for t in range(TT):
                                mm = pe.transpose(out[:, t * P:(t + 1) * P], c_sb[:, t * P:(t + 1) * P], eye)
                            mm.then_inc(L["c_turn"].sem, 1)
                    pe.wait_ge(L["c_out"].sem, L["c_out"].at(b, KJ))
                    pe.wait_ge(L["rest2"].sem, L["rest2"].at(b, 2 * KT))
                    for t in range(TT):
                        mm = pe.transpose(psq[:, t * P:(t + 1) * P], outs[:, t, :], eye)
                    mm.then_inc(L["o_turn"].sem, 1)
                    pe.wait_ge(L["o_sb"].sem, L["o_sb"].at(b, 1))
                    pe.matmul(out[:, :], w("wo"), outs_t[:, :], start=True, stop=True).then_inc(L["projected"].sem, 1)

            @block.scalar
            def _(act):
                with act.Fori(0, B) as b:
                    high_part(act, b, "1", 0)
                    high_part(act, b, "1", 1)
                    for s in range(KSTEPS):
                        N = (TT - s % TT) * P
                        act.wait_ge(L["shift1"].sem, L["shift1"].at(b, s + 1))
                        act.wait_ge(L["sums1"].sem, L["sums1"].at(b, max(s - 1, 0)))
                        for i in range(2):
                            act.activation(probs[:, s % 2, i, 0:N], ring[:, 2 * (s % 2) + i, 0:N], ACT.Exp,
                                           bias=stats[:, s % 4, 1, i:i + 1], scale=scale,
                                           accum_out=stats[:, s % 4, 2, i:i + 1]).then_inc(L["exp1"].sem, 1)
                        if s % TT == 2 and s // TT + 2 < KT:
                            high_part(act, b, "1", s // TT + 2, (0,))
                        if s % TT == 3 and s // TT + 2 < KT:
                            high_part(act, b, "1", s // TT + 2, (1,))
                with act.Fori(0, B) as b:
                    act.wait_ge(L["pv"].sem, L["pv"].at(b, 0))
                    act.activation(cur[:, :], core.normed(b), ACT.Copy).then_inc(L["current"].sem, 1)
                    high_part(act, b, "2", 0)
                    high_part(act, b, "2", 1)
                    for i in range(KSTEPS + LAG + 2):
                        s = i - LAG
                        if 0 <= s < KSTEPS:
                            act.wait_ge(L["av"].sem, L["av"].at(b, max(s - 1, 0)))
                            for h in range(2):
                                act.wait_ge(L["st"].sem, L["st"].at(b, 2 * s + h + 1))
                                act.activation(probs[:, s % 2, h, :], ring[:, 2 + h, :], ACT.Exp, scale=scale)\
                                    .then_inc(L["exp2"].sem, 1)
                        if s > 0 and s % (2 * TT) == 0:
                            act.wait_ge(L["av"].sem, L["av"].at(b, s))
                            act.wait_ge(L["c_turn"].sem, L["c_turn"].at(b, s // (2 * TT) - 1))
                            act.activation(c_sb[:, :], acc[:, :], ACT.Copy).then_inc(L["c_sb"].sem, 1)
                        if i % TT == 1 and i // TT + 2 < KT:
                            high_part(act, b, "2", i // TT + 2, (0,))
                        if i % TT == 2 and i // TT + 2 < KT:
                            high_part(act, b, "2", i // TT + 2, (1,))
                    act.wait_ge(L["o_turn"].sem, L["o_turn"].at(b, 1))
                    act.activation(outs_t[:, :], psq[:, :], ACT.Copy).then_inc(L["o_sb"].sem, 1)

            @block.vector
            def _(dve):
                dve.memset(sums[:, :], 0.0).then_inc(L["zero"].sem, 1)
                dve.memset(mask[:, :], 0.0).then_inc(L["zero"].sem, 1)
                dve.wait_ge(L["zero"].sem, L["zero"].at(0, 2))
                with dve.Fori(0, B) as b:
                    take_rest(dve, b, "1", 0)
                    stack_parts(dve, b, "1", 0)
                    take_rest(dve, b, "1", 1)
                    maxima1(dve, b, 0)
                    maxima1(dve, b, 1)
                    for s in range(KSTEPS):
                        inverse1(dve, b, s)
                        if s + 2 < KSTEPS:
                            maxima1(dve, b, s + 2)
                        if s % TT == 2 and s // TT + 2 < KT:
                            take_rest(dve, b, "1", s // TT + 2, (0,))
                        if s % TT == 3 and s // TT + 2 < KT:
                            take_rest(dve, b, "1", s // TT + 2, (1,))
                        if s % TT == 0 and s // TT + 1 < KT:
                            stack_parts(dve, b, "1", s // TT + 1, (0,))
                        if s % TT == 1 and s // TT + 1 < KT:
                            stack_parts(dve, b, "1", s // TT + 1, (1,))
                    dve.wait_ge(L["sums1"].sem, L["sums1"].at(b, KSTEPS))
                    dve.tensor_tensor(sums[:, :], acc[:, :], sums[:, :], ALU.add).then_inc(L["added"].sem, 1)
                choose(dve)
                dve.wait_ge(L["cast"].sem, L["cast"].at(0, 4))
                with dve.Fori(0, B) as b:
                    dve.wait_ge(L["p2"].sem, L["p2"].at(b, 0))
                    at = core.columns["const"]["batch_rows"][0]
                    dve.tensor_scalar(bmask[:, :], mask[:, :], core.weights["const"][:, bass.ds(b + at, 1)], None,
                                      ALU.mult).then_inc(L["masked"].sem, 1)
                    take_rest(dve, b, "2", 0)
                    stack_parts(dve, b, "2", 0)
                    take_rest(dve, b, "2", 1)
                    for i in range(KSTEPS + LAG + 2):
                        T, t = divmod(i, TT)
                        s = i - LAG
                        if i < KSTEPS:
                            for h in range(2):
                                dve.wait_ge(L["s2"].sem, L["s2"].at(b, 2 * i + h + 1))
                                dve.wait_ge(L["low2"].sem, L["low2"].at(b, 4 * max(T - 1, 0)))
                                dve.tensor_reduce(tops[:, T % 2, t, h:h + 1], ring[:, h, :], AX.X, ALU.max)\
                                    .then_inc(L["top2"].sem, 1)
                        if i < TT:
                            dve.wait_ge(L["pv"].sem, L["pv"].at(b, i + 1))
                            dve.tensor_tensor(v[:, i, :], out[:, :], core.w("const", "v_ones"), ALU.add)\
                                .then_inc(L["v"].sem, 1)
                        if t == 0 and 1 <= T <= KT:
                            lower_parts(dve, b, T - 1)
                        if t == 1 and 1 <= T <= KT:
                            dve.wait_ge(L["rows"].sem, L["rows"].at(b, T))
                            dve.tensor_tensor(stack[:, (T - 1) % 4, 0, :], stack[:, (T - 1) % 4, 0, :], out[:, :], ALU.add)\
                                .then_inc(L["q2"].sem, 1)
                        if t >= 2 and T + 2 < KT:
                            take_rest(dve, b, "2", T + 2, (t - 2,))
                        if t < 2 and T + 1 < KT:
                            stack_parts(dve, b, "2", T + 1, (t,))
                        if s > 1 and (s - 1) % (2 * TT) == 0:
                            j = s // (2 * TT) - 1
                            dve.wait_ge(L["c_turn"].sem, L["c_turn"].at(b, j + 1))
                            turned = out[:, :].rearrange("p (t g c) -> p t g c", t=TT, g=KG)
                            dve.wait_ge(L["c_out"].sem, L["c_out"].at(b, j))
                            dve.reciprocal(c_inv[:, :, :], turned[:, :, :, KHD]).then_inc(L["c_inv"].sem, 1)
                            dve.wait_ge(L["c_inv"].sem, L["c_inv"].at(b, j + 1))
                            dve.tensor_tensor(
                                outs[:, :, 32 * j:32 * j + 32].rearrange("p t (g c) -> p t g c", g=KG),
                                turned[:, :, :, 0:KHD], c_inv[:, :, :].unsqueeze(3).to_broadcast([P, TT, KG, KHD]),
                                ALU.mult).then_inc(L["c_out"].sem, 1)
                    dve.wait_ge(L["projected"].sem, L["projected"].at(b, 1))
                    dve.tensor_tensor(core.batch(b), out[:, :], core.batch(b), ALU.add).then_inc(L["done"].sem, 1)

            @block.gpsimd
            def _(pool):
                pool.tensor_copy(eye16[:, :], eye).then_inc(L["cast"].sem, 1)
                pool.tensor_copy(later16[:, :], core.w("const", "later")).then_inc(L["cast"].sem, 1)
                pool.tensor_copy(mask_rows16[:, :], core.w("const", "mask_rows")).then_inc(L["cast"].sem, 1)
                pool.memset(low[:, :, :, :], 0.0).then_inc(L["cast"].sem, 1)
                for n in ("1", "2"):
                    with pool.Fori(0, B) as b:
                        for T in range(KT):
                            middle_part(pool, b, n, T)
    L.close()

LH, LHD = 8, 16
FG = 2
HG = LH // FG
LROWS = 32


def linear_attention(nc, core, name):
    NSTEP = FG * HG
    L = Layer(nc, name, core, ["light"], **NEXT, masks=LH, vscale=1, start=2,
              angle=16, table=FG,
              proj=2 * FG,
              feats=2 * FG,
              rot=2 * FG,
              vu=2 * TT,
              vu_sb=2 * TT,
              v_late=1,
              kturn=FG, ktok=FG,
              states=FG,
              states_sb=FG,
              energy=NSTEP,
              masked=NSTEP,
              mixed=FG, c_sb=FG,
              c_turn=FG, tok=FG,
              squares=TT, inv=2, outs=TT, turned=1, outs_sb=1, projected=1, done=1)
    with L.ctx:
        g = "light"
        w = lambda n, *a: core.w(g, n, *a)
        xn = L.sb("xn", [P, S])
        table = L.sb("table", [P, FG, S])
        turns = L.sb("turns", [P, 2, S])
        wholes = L.sb("wholes", [P, S], mybir.dt.int32)
        feats = L.sb("feats", [P, 2, FG, S])
        qk = L.sb("qk", [P, 2, FG, S])
        v = L.sb("v", [P, TT, LH, LROWS])
        u = L.sb("u", [P, TT, D])
        v_late = L.sb("v_late", [P, TT, D])
        growth = L.sb("growth", [P, D])
        ktok = L.sb("ktok", [P, FG, TT, P])
        state = L.sb("state", [P, FG, TT, P])
        masks = L.sb("masks", [P, LH, P])
        energy = L.sb("energy", [P, NSTEP, S])
        square = L.sb("square", [P, D])
        sums = L.sb("sums", [P, 3, TT])
        outs = L.sb("outs", [P, TT, D])
        outs_t = L.sb("outs_t", [P, S])
        c_sb = L.sb("c_sb", [P, S])
        tok = L.sb("tok", [P, TT, D])
        bank = L.ps("bank", [P, S])
        small = L.ps("small", [P, S])
        pe4 = L.ps("pe4", [P, HG, S])
        pmix = L.ps("pmix", [P, S])
        pout = L.ps("pout", [P, S])
        eye = core.w("const", "eye")
        TWO_PI = 2 * np.pi
        c1 = float(np.float32(6.28125))
        c2 = float(np.float32(np.round((TWO_PI - c1) * 2 ** 20) / 2 ** 20))
        c3 = float(np.float32(TWO_PI - c1 - c2))
        magic = 1.5 * 2.0 ** 23

        with nc.Block() as block:
            @block.tensor
            def _(pe):
                pe.wait_ge(L["start"].sem, L["start"].at(0, 2))
                with pe.Fori(0, B) as b:
                    pe.wait_ge(L["now"].sem, L["now"].at(b, 1))
                    pe.wait_ge(L["masked"].sem, L["masked"].at(b, 0))
                    for i in range(2):
                        for j in range(FG):
                            pe.matmul(pe4[:, i * FG + j, :], w(("wq", "wk")[i], j * P, (j + 1) * P), xn[:, :],
                                      start=True, stop=True).then_inc(L["proj"].sem, 1)
                    pe.wait_ge(L["states_sb"].sem, L["states_sb"].at(b, 0))
                    pe.wait_ge(L["done"].sem, L["done"].at(b, 0))
                    for i, (n, ps) in enumerate((("wv", small), ("wu", pout))):
                        for t in range(TT):
                            pe.matmul(ps[:, t * P:(t + 1) * P], xn[:, t * P:(t + 1) * P], w(n),
                                      start=True, stop=True).then_inc(L["vu"].sem, 1)
                    for j in range(FG):
                        pe.wait_ge(L["rot"].sem, L["rot"].at(b, FG + j + 1))
                        if j >= 1:
                            pe.wait_ge(L["ktok"].sem, L["ktok"].at(b, j))
                        for t in range(TT):
                            mm = pe.transpose(bank[:, t * P:(t + 1) * P], qk[:, 1, j, t * P:(t + 1) * P], eye)
                        mm.then_inc(L["kturn"].sem, 1)
                    pe.wait_ge(L["vu_sb"].sem, L["vu_sb"].at(b, 2 * TT))
                    pe.wait_ge(L["v_late"].sem, L["v_late"].at(b, 1))
                    for j in range(FG):
                        pe.wait_ge(L["ktok"].sem, L["ktok"].at(b, j + 1))
                        c = slice(j * (D // FG), (j + 1) * (D // FG))
                        for t in range(TT):
                            others = [o for o in range(TT) if o != t]
                            at = (j * TT + t) * (D // FG)
                            for o in others:
                                values = v_late[:, o, c] if o < t else v[:, o, j * HG:(j + 1) * HG, 0:LHD]
                                mm = pe.matmul(small[:, at:at + D // FG], ktok[:, j, o, :], values,
                                               start=o == others[0], stop=o == others[-1])
                        mm.then_inc(L["states"].sem, 1)
                    for j in range(FG):
                        pe.wait_ge(L["rot"].sem, L["rot"].at(b, FG + j + 1))
                        for h in range(HG):
                            r = slice(32 * h, 32 * h + 32)
                            if j == 0:
                                pe.wait_ge(L["feats"].sem, L["feats"].at(b, 2 * FG))
                            else:
                                pe.wait_ge(L["masked"].sem, L["masked"].at(b, h + 1))
                            for t in range(TT):
                                tk = slice(t * P, (t + 1) * P)
                                mm = pe.matmul(pe4[:, h, tk], qk[r, 1, j, tk], qk[r, 0, j, tk], start=True, stop=True)
                            mm.then_inc(L["energy"].sem, 1)
                    pe.wait_ge(L["states_sb"].sem, L["states_sb"].at(b, FG))
                    for j in range(FG):
                        pe.wait_ge(L["masked"].sem, L["masked"].at(b, HG * (j + 1)))
                        pe.wait_ge(L["c_sb"].sem, L["c_sb"].at(b, j))
                        for t in range(TT):
                            tk = slice(t * P, (t + 1) * P)
                            pe.matmul(pmix[:, tk], state[:, j, t, :], qk[:, 0, j, tk], start=True, stop=True,
                                      skip_group_check=True)
                            for h in range(HG):
                                mm = pe.matmul(pmix[h * LROWS:(h + 1) * LROWS, tk], v[:, t, j * HG + h, :],
                                               energy[:, j * HG + h, tk], start=False, stop=True,
                                               skip_group_check=True)
                        mm.then_inc(L["mixed"].sem, 1)
                        pe.wait_ge(L["c_sb"].sem, L["c_sb"].at(b, j + 1))
                        pe.wait_ge(L["tok"].sem, L["tok"].at(b, j))
                        for t in range(TT):
                            mm = pe.transpose(bank[:, t * P:(t + 1) * P], c_sb[:, t * P:(t + 1) * P], eye)
                        mm.then_inc(L["c_turn"].sem, 1)
                    pe.wait_ge(L["outs"].sem, L["outs"].at(b, TT))
                    for t in range(TT):
                        mm = pe.transpose(bank[:, t * P:(t + 1) * P], outs[:, t, :], eye)
                    mm.then_inc(L["turned"].sem, 1)
                    pe.wait_ge(L["outs_sb"].sem, L["outs_sb"].at(b, 1))
                    pe.matmul(pout[:, :], w("wo"), outs_t[:, :], start=True, stop=True).then_inc(L["projected"].sem, 1)

            @block.scalar
            def _(act):
                for h in range(LH):
                    act.activation(masks[:, h, :], core.w("const", "upper"), ACT.Exp, scale=w("slope", h, h + 1))\
                        .then_inc(L["masks"].sem, 1)
                act.activation(growth[:, :], w("slope_cols"), ACT.Exp).then_inc(L["vscale"].sem, 1)
                for j in range(FG):
                    act.wait_ge(L["angle"].sem, L["angle"].at(0, 8 * (j + 1)))
                    act.activation(table[:, j, :], turns[:, j, :], ACT.Sin).then_inc(L["table"].sem, 1)
                with act.Fori(0, B) as b:
                    for i in range(2):
                        for j in range(FG):
                            n = i * FG + j
                            act.wait_ge(L["proj"].sem, L["proj"].at(b, n + 1))
                            act.wait_ge(L["rot"].sem, L["rot"].at(b, 0))
                            act.activation(feats[:, i, j, :], pe4[:, n, :], ACT.Silu,
                                           bias=w(("bq", "bk")[i], j, j + 1)).then_inc(L["feats"].sem, 1)
                    for j in range(FG):
                        act.wait_ge(L["kturn"].sem, L["kturn"].at(b, j + 1))
                        act.activation(ktok[:, j, :, :], bank[:, :].rearrange("p (t c) -> p t c", t=TT), ACT.Copy)\
                            .then_inc(L["ktok"].sem, 1)
                    for j in range(FG):
                        act.wait_ge(L["mixed"].sem, L["mixed"].at(b, j + 1))
                        act.wait_ge(L["c_turn"].sem, L["c_turn"].at(b, j))
                        act.activation(c_sb[:, :], pmix[:, :], ACT.Copy).then_inc(L["c_sb"].sem, 1)
                        act.wait_ge(L["c_turn"].sem, L["c_turn"].at(b, j + 1))
                        act.wait_ge(L["outs"].sem, L["outs"].at(b, 0))
                        act.activation(tok[:, :, j * (D // FG):(j + 1) * (D // FG)].rearrange("p t (h e) -> p t h e", h=HG),
                                       bank[:, :].rearrange("p (t h w) -> p t h w", t=TT, h=HG)[:, :, :, 0:LHD], ACT.Copy)\
                            .then_inc(L["tok"].sem, 1)
                    for t in range(TT):
                        act.wait_ge(L["tok"].sem, L["tok"].at(b, FG))
                        if t:
                            act.wait_ge(L["squares"].sem, L["squares"].at(b, t))
                        act.activation(square[:, :], tok[:, t, :], ACT.Square, accum_out=sums[:, 0, t:t + 1])\
                            .then_inc(L["squares"].sem, 1)
                    act.wait_ge(L["turned"].sem, L["turned"].at(b, 1))
                    act.activation(outs_t[:, :], bank[:, :], ACT.Copy).then_inc(L["outs_sb"].sem, 1)

            @block.vector
            def _(dve):
                dve.memset(v[:, :, :, :], 0.0).then_inc(L["start"].sem, 1)
                dve.memset(state[:, :, :, :], 0.0).then_inc(L["start"].sem, 1)
                dve.wait_ge(L["start"].sem, L["start"].at(0, 2))
                for j in range(FG):
                    t0, t1 = turns[:, j, :], feats[:, 0, 0, :]
                    dve.tensor_scalar(t0, core.w("const", "token"), w("theta", j, j + 1), None, ALU.mult)\
                        .then_inc(L["angle"].sem, 1)
                    dve.wait_ge(L["angle"].sem, L["angle"].at(0, 8 * j + 1))
                    dve.tensor_scalar(t1, t0, w("shift", j, j + 1), 1.0 / TWO_PI, ALU.add, ALU.mult)\
                        .then_inc(L["angle"].sem, 1)
                    dve.wait_ge(L["angle"].sem, L["angle"].at(0, 8 * j + 2))
                    dve.tensor_scalar(t1, t1, magic, magic, ALU.add, ALU.subtract).then_inc(L["angle"].sem, 1)
                    for n, cc in enumerate((c1, c2, c3)):
                        dve.wait_ge(L["angle"].sem, L["angle"].at(0, 8 * j + 3 + n))
                        dve.scalar_tensor_tensor(out=t0, in0=t1, scalar=-cc, in1=t0, op0=ALU.mult, op1=ALU.add)\
                            .then_inc(L["angle"].sem, 1)
                    dve.wait_ge(L["angle"].sem, L["angle"].at(0, 8 * j + 6))
                    dve.tensor_scalar(t0, t0, w("shift", j, j + 1), float(np.float32(3.1415925)), ALU.add, ALU.min)\
                        .then_inc(L["angle"].sem, 1)
                    dve.wait_ge(L["angle"].sem, L["angle"].at(0, 8 * j + 7))
                    dve.tensor_scalar(t0, t0, -float(np.float32(3.1415925)), None, ALU.max).then_inc(L["angle"].sem, 1)
                dve.wait_ge(L["masks"].sem, L["masks"].at(0, LH))
                dve.wait_ge(L["vscale"].sem, L["vscale"].at(0, 1))
                dve.wait_ge(L["table"].sem, L["table"].at(0, FG))
                with dve.Fori(0, B) as b:
                    take_normed(dve, L, b, xn[:, :])
                    dve.wait_ge(L["outs"].sem, L["outs"].at(b, 0))
                    for i, (ps, bias) in enumerate(((small, "bv"), (pout, "bu"))):
                        for t in range(TT):
                            dve.wait_ge(L["vu"].sem, L["vu"].at(b, TT * (i + 1)))
                            by_head = lambda m: m.rearrange("p (h e) -> p h e", h=LH)
                            dst = v[:, t, :, 0:LHD] if i == 0 else by_head(u[:, t, :])
                            dve.tensor_tensor(dst, by_head(ps[:, t * P:(t + 1) * P]), by_head(w(bias)), ALU.add)\
                                .then_inc(L["vu_sb"].sem, 1)
                    dve.wait_ge(L["vu_sb"].sem, L["vu_sb"].at(b, TT))
                    dve.tensor_tensor(v_late[:, :, :].rearrange("p t (h e) -> p t h e", h=LH), v[:, :, :, 0:LHD],
                                      growth[:, :].rearrange("p (h e) -> p h e", h=LH).unsqueeze(1)
                                      .to_broadcast([P, TT, LH, LHD]), ALU.mult)\
                        .then_inc(L["v_late"].sem, 1)
                    for i in range(2):
                        for j in range(FG):
                            dve.wait_ge(L["feats"].sem, L["feats"].at(b, i * FG + j + 1))
                            dve.tensor_tensor(qk[:, i, j, :], feats[:, i, j, :], table[:, j, :], ALU.mult)\
                                .then_inc(L["rot"].sem, 1)
                    for j in range(FG):
                        dve.wait_ge(L["states"].sem, L["states"].at(b, FG))
                        W = TT * (D // FG)
                        dve.tensor_tensor(state[:, j, :, :].rearrange("p t (h w) -> p t h w", h=HG)[:, :, :, 0:LHD],
                                          small[:, j * W:(j + 1) * W].rearrange("p (t h e) -> p t h e", t=TT, h=HG),
                                          core.w("const", "block4").rearrange("p (h e) -> p h e", h=HG).unsqueeze(1)
                                          .to_broadcast([P, TT, HG, LHD]),
                                          ALU.mult).then_inc(L["states_sb"].sem, 1)
                    for s in range(NSTEP):
                        dve.wait_ge(L["energy"].sem, L["energy"].at(b, s + 1))
                        dve.tensor_tensor(energy[:, s, :].rearrange("p (t c) -> p t c", t=TT),
                                          pe4[:, s % HG, :].rearrange("p (t c) -> p t c", t=TT),
                                          masks[:, s, :].unsqueeze(1).to_broadcast([P, TT, P]), ALU.mult)\
                            .then_inc(L["masked"].sem, 1)
                    dve.wait_ge(L["squares"].sem, L["squares"].at(b, TT))
                    dve.tensor_scalar(sums[:, 1, :], sums[:, 0, :], 1.0 / D, 1e-6, ALU.mult, ALU.add)\
                        .then_inc(L["inv"].sem, 1)
                    dve.wait_ge(L["inv"].sem, L["inv"].at(b, 2))
                    for t in range(TT):
                        dve.wait_ge(L["vu_sb"].sem, L["vu_sb"].at(b, 2 * TT))
                        dve.scalar_tensor_tensor(out=outs[:, t, :], in0=tok[:, t, :], scalar=sums[:, 2, t:t + 1],
                                                 in1=u[:, t, :], op0=ALU.mult, op1=ALU.mult).then_inc(L["outs"].sem, 1)
                    dve.wait_ge(L["projected"].sem, L["projected"].at(b, 1))
                    dve.scalar_tensor_tensor(out=core.batch(b), in0=pout[:, :], scalar=w("bo"), in1=core.batch(b),
                                             op0=ALU.add, op1=ALU.add).then_inc(L["done"].sem, 1)

            @block.gpsimd
            def _(pool):
                with pool.Fori(0, B) as b:
                    pool.wait_ge(L["inv"].sem, L["inv"].at(b, 1))
                    pool.tensor_tensor(sums[:, 2, :], sums[:, 1, :], core.w("const", "minus_half", 0, TT), ALU.pow)\
                        .then_inc(L["inv"].sem, 1)
    L.close()

DFF = 512
FT = DFF // P


def quantise(nc, core):
    L = Layer(nc, "quant", core, ["bitffn"], rowsum=2, total=1, gamma=2, scaled=2, rounded=2, clipped=2)
    with L.ctx:
        rowsum = L.sb("rowsums", [P, 2])
        gamma = L.sb("gammas", [P, 2])
        total = L.ps("totals", [P, 2])
        mats = [core.w("bitffn", "w1"), core.w("bitffn", "w2")]
        magic = 1.5 * 2.0 ** 23
        with nc.Block() as block:
            @block.vector
            def _(dve):
                for i, w in enumerate(mats):
                    dve.tensor_reduce(rowsum[:, i:i + 1], w, AX.X, ALU.add, apply_absolute_value=True)\
                        .then_inc(L["rowsum"].sem, 1)
                dve.wait_ge(L["total"].sem, L["total"].at(0, 1))
                dve.tensor_scalar(gamma[:, :], total[:, :], 1.0 / (DFF * D), 1e-5, ALU.mult, ALU.add)\
                    .then_inc(L["gamma"].sem, 1)
                dve.wait_ge(L["gamma"].sem, L["gamma"].at(0, 1))
                dve.reciprocal(gamma[:, :], gamma[:, :]).then_inc(L["gamma"].sem, 1)
                dve.wait_ge(L["gamma"].sem, L["gamma"].at(0, 2))
                for i, w in enumerate(mats):
                    dve.tensor_scalar(w, w, gamma[:, i:i + 1], None, ALU.mult).then_inc(L["scaled"].sem, 1)
                    dve.wait_ge(L["scaled"].sem, L["scaled"].at(0, i + 1))
                    dve.tensor_scalar(w, w, magic, magic, ALU.add, ALU.subtract).then_inc(L["rounded"].sem, 1)
                    dve.wait_ge(L["rounded"].sem, L["rounded"].at(0, i + 1))
                    dve.tensor_scalar(w, w, 1.0, -1.0, ALU.min, ALU.max).then_inc(L["clipped"].sem, 1)

            @block.tensor
            def _(pe):
                pe.wait_ge(L["rowsum"].sem, L["rowsum"].at(0, 2))
                pe.matmul(total[:, :], core.w("const", "ones"), rowsum[:, :], start=True, stop=True)\
                    .then_inc(L["total"].sem, 1)
    L.close()


def bit_ffn(nc, core, name):
    L = Layer(nc, name, core, ["bitffn"], **NEXT, up=FT, hidden=FT, down=FT, done=1)
    with L.ctx:
        xn = L.sb("xn", [P, S])
        h = L.sb("h", [P, 2, S])
        out = L.ps("out", [P, S])
        up = L.ps("up", [P, 2, S])
        w1, w2 = core.w("bitffn", "w1"), core.w("bitffn", "w2")
        b1, b2 = core.w("bitffn", "b1"), core.w("bitffn", "b2")
        def down(pe, b, m):
            pe.wait_ge(L["hidden"].sem, L["hidden"].at(b, m + 1))
            if m == 0:
                pe.wait_ge(L["done"].sem, L["done"].at(b, 0))
            pe.matmul(out[:, :], w2[:, m * P:(m + 1) * P], h[:, m % 2, :], start=m == 0, stop=m == FT - 1)\
                .then_inc(L["down"].sem, 1)

        with nc.Block() as block:
            @block.tensor
            def _(pe):
                with pe.Fori(0, B) as b:
                    pe.wait_ge(L["now"].sem, L["now"].at(b, 1))
                    for m in range(FT):
                        pe.wait_ge(L["hidden"].sem, L["hidden"].at(b, max(m - 1, 0)))
                        pe.matmul(up[:, m % 2, :], w1[:, m * P:(m + 1) * P], xn[:, :], start=True, stop=True)\
                            .then_inc(L["up"].sem, 1)
                        if m >= 1:
                            down(pe, b, m - 1)
                    down(pe, b, FT - 1)

            @block.scalar
            def _(act):
                with act.Fori(0, B) as b:
                    for m in range(FT):
                        act.wait_ge(L["up"].sem, L["up"].at(b, m + 1))
                        act.wait_ge(L["down"].sem, L["down"].at(b, max(m - 1, 0)))
                        act.activation(h[:, m % 2, :], up[:, m % 2, :], ACT.Relu, bias=b1[:, m:m + 1])\
                            .then_inc(L["hidden"].sem, 1)

            @block.vector
            def _(dve):
                with dve.Fori(0, B) as b:
                    take_normed(dve, L, b, xn[:, :])
                    dve.wait_ge(L["down"].sem, L["down"].at(b, FT))
                    dve.scalar_tensor_tensor(out=core.batch(b), in0=out[:, :], scalar=b2, in1=core.batch(b),
                                             op0=ALU.add, op1=ALU.add).then_inc(L["done"].sem, 1)

    L.close()

SH = 32
SLOTS = 64
RMS_EPS = 1.1920929e-07


def landmark_layer(nc, core, name):
    NA = 2 * TT
    L = Layer(nc, name, core, ["slr"], **NEXT, lam=2,
              sq=2, var=2, eps=2, rstd=2, diag=2, spread=2,
              xn=2,
              route=3,
              hid=1, hid_sb=1, wide=1, logit=1, lmax=3, lexp=1, lsum=3,
              decayed=1, ema=1,
              qk=2, qk_sb=2, v_ps=1, v_sb=1,
              scores=NA, top=NA, shift=NA, probs=NA, inv=2 * TT, second=TT, mixp=TT,
              turn=TT, turn_sb=TT, averaged=1, ctx_sb=1, slr=1, joined=1,
              qwide=1, lscore=1, attn=5, aexp=1, arc=2,
              mix=1, mix_sb=1, scaled=1, result=1,
              mean=1, bus=3, bus_sb=3, final=1, done=1)
    with L.ctx:
        g = "slr"
        w = lambda n, *a: core.w(g, n, *a)
        xl, xn, sq = (L.sb(n, [P, S]) for n in ("xl", "xn", "sq"))
        small = L.sb("small", [P, 2, 2, TT])
        diag = L.sb("diag", [P, TT, P])
        col = L.sb("col", [P, 32])
        wide = L.sb("wide", [P, P])
        probs3 = L.sb("probs3", [P, 8])
        lam_row = L.sb("lam_row", [P, S])
        drive, ema, joined = (L.sb(n, [P, S]) for n in ("drive", "ema", "joined"))
        qk = L.sb("qk", [2 * SH, 2, S])
        v = L.sb("v", [P, TT, SH])
        stats = L.sb("stats", [P, 4, NA])
        probs = L.sb("probs", [P, NA, S])
        turned = L.sb("turned", [P, TT, S])
        ctx_t = L.sb("ctx_t", [SH, S])
        qwide = L.sb("qwide", [P, P])
        attn = L.sb("attn", [P, 3, SLOTS])
        mix, result = L.sb("mix", [P, S]), L.sb("result", [P, S])
        bank, ps_small, pa, pb, pc, pt, pu, out = (L.ps(n, [P, S]) for n in
                                                  ("bank", "ps_small", "pa", "pb", "pc", "pt", "pu", "out"))
        eye = core.w("const", "eye")
        ones = core.w("const", "ones")
        C_MEAN, C_HID, C_P, C_MX, C_SUM, C_INV, C_PMF, C_LAM1, C_AMX, C_ASUM, C_AINV, C_ARC, C_M2, C_B0, C_B1, C_B2, \
            C_NMX, C_SHIFT = range(18)

        def c(i):
            return col[:, i:i + 1]

        def rms_tensor(pe, b, i):
            pe.wait_ge(L["sq"].sem, L["sq"].at(b, i + 1))
            for t in range(TT):
                mm = pe.matmul(ps_small[:, 8 + TT * i + t:9 + TT * i + t], sq[:, t * P:(t + 1) * P],
                               core.w("const", "mean", 0, 1), start=True, stop=True)
            mm.then_inc(L["var"].sem, 1)
            pe.wait_ge(L["diag"].sem, L["diag"].at(b, i + 1))
            pe.matmul(pa[:, :], ones, diag[:, :, :], start=True, stop=True).then_inc(L["spread"].sem, 1)

        def rms_vector(dve, b, i):
            dve.wait_ge(L["var"].sem, L["var"].at(b, i + 1))
            at = 8 + TT * i
            dve.tensor_scalar(small[:, i, 0, :], ps_small[:, at:at + TT], RMS_EPS, None, ALU.add)\
                .then_inc(L["eps"].sem, 1)
            dve.wait_ge(L["rstd"].sem, L["rstd"].at(b, i + 1))
            dve.wait_ge(L["spread"].sem, L["spread"].at(b, i))
            dve.tensor_tensor(diag[:, :, :], eye.unsqueeze(1).to_broadcast([P, TT, P]),
                              small[:, i, 1, :].unsqueeze(2).to_broadcast([P, TT, P]), ALU.mult)\
                .then_inc(L["diag"].sem, 1)

        def rms_pool(pool, b, i):
            pool.wait_ge(L["eps"].sem, L["eps"].at(b, i + 1))
            pool.tensor_tensor(small[:, i, 1, :], small[:, i, 0, :], core.w("const", "minus_half", 0, TT), ALU.pow)\
                .then_inc(L["rstd"].sem, 1)

        sc = 1.0 / float(SH) ** 0.5
        scd = 1.0 / float(D) ** 0.5

        def differ(dve, b, t):
            n = 2 * t
            dve.wait_ge(L["probs"].sem, L["probs"].at(b, n + 2))
            dve.reciprocal(stats[:, 3, n:n + 2], stats[:, 2, n:n + 2]).then_inc(L["inv"].sem, 1)
            dve.wait_ge(L["inv"].sem, L["inv"].at(b, 2 * t + 1))
            dve.tensor_tensor(stats[:, 3, n + 1:n + 2], stats[:, 3, n + 1:n + 2], w("slr_lam"), ALU.mult)\
                .then_inc(L["inv"].sem, 1)
            dve.wait_ge(L["inv"].sem, L["inv"].at(b, 2 * t + 2))
            dve.tensor_scalar(probs[:, n + 1, :], probs[:, n + 1, :], stats[:, 3, n + 1:n + 2], None, ALU.mult)\
                .then_inc(L["second"].sem, 1)
            dve.wait_ge(L["second"].sem, L["second"].at(b, t + 1))
            dve.scalar_tensor_tensor(out=probs[:, n, :], in0=probs[:, n, :], scalar=stats[:, 3, n:n + 1],
                                     in1=probs[:, n + 1, :], op0=ALU.mult, op1=ALU.subtract).then_inc(L["mixp"].sem, 1)

        with nc.Block() as block:
            @block.tensor
            def _(pe):
                with pe.Fori(0, B) as b:
                    rms_tensor(pe, b, 0)
                    pe.wait_ge(L["xn"].sem, L["xn"].at(b, 2))
                    for i, n in enumerate(("wq", "wk")):
                        pe.matmul((pb, pc)[i][0:2 * SH, :], w(n), xn[:, :], start=True, stop=True)\
                            .then_inc(L["qk"].sem, 1)
                    for t in range(TT):
                        mm = pe.matmul(pt[:, t * SH:(t + 1) * SH], xn[:, t * P:(t + 1) * P], w("wv"),
                                       start=True, stop=True)
                    mm.then_inc(L["v_ps"].sem, 1)
                    pe.wait_ge(L["route"].sem, L["route"].at(b, 1))
                    pe.matmul(pu[0:64, 0:1], w("r1"), c(C_MEAN), start=True, stop=True).then_inc(L["hid"].sem, 1)
                    pe.wait_ge(L["wide"].sem, L["wide"].at(b, 1))
                    pe.matmul(pu[:, 4:7], wide[0:64, :], w("r2"), start=True, stop=True).then_inc(L["logit"].sem, 1)
                    pe.wait_ge(L["qwide"].sem, L["qwide"].at(b, 1))
                    pe.wait_ge(L["lmax"].sem, L["lmax"].at(b, 1))
                    pe.matmul(pu[:, 64:64 + SLOTS], qwide[:, :], w("landmarks_t"), start=True, stop=True)\
                        .then_inc(L["lscore"].sem, 1)
                    pe.wait_ge(L["qk_sb"].sem, L["qk_sb"].at(b, 2))
                    for n in range(NA):
                        t, i = divmod(n, 2)
                        r = slice(i * SH, (i + 1) * SH)
                        if n >= 2:
                            pe.wait_ge(L["probs"].sem, L["probs"].at(b, n - 1))
                        pe.matmul((pb, pc)[i][:, :], qk[r, 0, t * P:(t + 1) * P], qk[r, 1, :],
                                  start=True, stop=True).then_inc(L["scores"].sem, 1)
                    pe.wait_ge(L["v_sb"].sem, L["v_sb"].at(b, 1))
                    for t in range(TT):
                        pe.wait_ge(L["mixp"].sem, L["mixp"].at(b, t + 1))
                        ps = (pt, out)[t % 2]
                        if t >= 2:
                            pe.wait_ge(L["turn_sb"].sem, L["turn_sb"].at(b, t - 1))
                        if t == 1:
                            pe.wait_ge(L["done"].sem, L["done"].at(b, 0))
                        for o in range(TT):
                            mm = pe.transpose(ps[:, o * P:(o + 1) * P], probs[:, 2 * t, o * P:(o + 1) * P], eye)
                        mm.then_inc(L["turn"].sem, 1)
                    pe.wait_ge(L["turn_sb"].sem, L["turn_sb"].at(b, TT))
                    for o in range(TT):
                        mm = pe.matmul(pb[0:SH, :], v[:, o, :], turned[:, o, :], start=o == 0, stop=o == TT - 1)
                    mm.then_inc(L["averaged"].sem, 1)
                    pe.wait_ge(L["ctx_sb"].sem, L["ctx_sb"].at(b, 1))
                    pe.matmul(pc[:, :], w("wo"), ctx_t[:, :], start=True, stop=True).then_inc(L["slr"].sem, 1)
                    pe.matmul(out[:, :], w("mix2"), xn[:, :], start=True, stop=False)
                    pe.wait_ge(L["arc"].sem, L["arc"].at(b, 2))
                    pe.matmul(out[:, :], w("mix1"), joined[:, :], start=False, stop=True).then_inc(L["mix"].sem, 1)
                    rms_tensor(pe, b, 1)
                    pe.wait_ge(L["mean"].sem, L["mean"].at(b, 1))
                    for i, n in enumerate(("compress", "publish", "expand")):
                        if i:
                            pe.wait_ge(L["bus_sb"].sem, L["bus_sb"].at(b, i))
                        pe.matmul(pu[:, 200 + i:201 + i], w(n), c((C_M2, C_B0, C_B1)[i]), start=True, stop=True)\
                            .then_inc(L["bus"].sem, 1)

            @block.scalar
            def _(act):
                with act.Fori(0, B) as b:
                    act.wait_ge(L["now"].sem, L["now"].at(b, 1))
                    act.activation(sq[:, :], xl[:, :], ACT.Square).then_inc(L["sq"].sem, 1)
                    for i in range(2):
                        act.wait_ge(L["qk"].sem, L["qk"].at(b, i + 1))
                        act.activation(qk[:, i, :], (pb, pc)[i][0:2 * SH, :], ACT.Copy).then_inc(L["qk_sb"].sem, 1)
                    act.wait_ge(L["v_ps"].sem, L["v_ps"].at(b, 1))
                    act.activation(v[:, :, :], pt[:, 0:TT * SH].rearrange("p (t d) -> p t d", t=TT), ACT.Copy)\
                        .then_inc(L["v_sb"].sem, 1)
                    act.wait_ge(L["hid"].sem, L["hid"].at(b, 1))
                    act.activation(col[0:64, C_HID:C_HID + 1], pu[0:64, 0:1], ACT.Silu, scale=1.0 / S)\
                        .then_inc(L["hid_sb"].sem, 1)
                    act.wait_ge(L["lmax"].sem, L["lmax"].at(b, 3))
                    act.activation(probs3[:, 4:7], probs3[:, 0:3], ACT.Exp, bias=c(C_NMX),
                                   accum_out=c(C_SUM)).then_inc(L["lexp"].sem, 1)
                    for n in range(NA):
                        act.wait_ge(L["shift"].sem, L["shift"].at(b, n + 1))
                        act.activation(probs[:, n, :], (pb, pc)[n % 2][:, :], ACT.Exp, bias=stats[:, 1, n:n + 1],
                                       scale=sc, accum_out=stats[:, 2, n:n + 1]).then_inc(L["probs"].sem, 1)
                    act.wait_ge(L["attn"].sem, L["attn"].at(b, 2))
                    act.activation(attn[:, 0, :], attn[:, 2, :], ACT.Exp, bias=c(C_SHIFT), scale=scd,
                                   accum_out=c(C_ASUM)).then_inc(L["aexp"].sem, 1)
                    for t in range(TT):
                        act.wait_ge(L["turn"].sem, L["turn"].at(b, t + 1))
                        act.activation(turned[:, :, t * P:(t + 1) * P],
                                       (pt, out)[t % 2][:, :].rearrange("p (o c) -> p o c", o=TT), ACT.Copy)\
                            .then_inc(L["turn_sb"].sem, 1)
                    act.wait_ge(L["averaged"].sem, L["averaged"].at(b, 1))
                    act.activation(ctx_t[:, :], pb[0:SH, :], ACT.Copy).then_inc(L["ctx_sb"].sem, 1)
                    act.wait_ge(L["mix"].sem, L["mix"].at(b, 1))
                    act.activation(sq[:, :], out[:, :], ACT.Square).then_inc(L["sq"].sem, 1)
                    act.activation(mix[:, :], out[:, :], ACT.Copy).then_inc(L["mix_sb"].sem, 1)
                    for i in range(3):
                        act.wait_ge(L["bus"].sem, L["bus"].at(b, i + 1))
                        act.activation(c((C_B0, C_B1, C_B2)[i]), pu[:, 200 + i:201 + i], ACT.Copy,
                                       scale=(1.0 / S, 1.0, 0.1)[i]).then_inc(L["bus_sb"].sem, 1)

            @block.vector
            def _(dve):
                dve.tensor_copy(lam_row[:, :], w("lam").to_broadcast([P, S])).then_inc(L["lam"].sem, 1)
                dve.tensor_scalar(c(C_LAM1), w("lam"), -1.0, 1.0, ALU.mult, ALU.add).then_inc(L["lam"].sem, 1)
                dve.wait_ge(L["lam"].sem, L["lam"].at(0, 2))
                with dve.Fori(0, B) as b:
                    take_normed(dve, L, b, xl[:, :])
                    rms_vector(dve, b, 0)
                    dve.wait_ge(L["spread"].sem, L["spread"].at(b, 1))
                    dve.tensor_tensor(mix[:, :], xl[:, :], pa[:, :], ALU.mult).then_inc(L["xn"].sem, 1)
                    dve.wait_ge(L["xn"].sem, L["xn"].at(b, 1))
                    dve.tensor_scalar(xn[:, :], mix[:, :], w("norm_in"), None, ALU.mult).then_inc(L["xn"].sem, 1)
                    dve.wait_ge(L["xn"].sem, L["xn"].at(b, 2))
                    dve.tensor_reduce(c(C_MEAN), xn[:, :], AX.X, ALU.add).then_inc(L["route"].sem, 1)
                    dve.tensor_scalar(drive[:, :], xn[:, :], c(C_LAM1), None, ALU.mult).then_inc(L["decayed"].sem, 1)
                    dve.tensor_scalar(qwide[:, :], ones, xn[:, S - 1:S], None, ALU.mult).then_inc(L["qwide"].sem, 1)
                    dve.wait_ge(L["decayed"].sem, L["decayed"].at(b, 1))
                    dve.tensor_tensor_scan(ema[:, :], lam_row[:, :], drive[:, :], 0.0, ALU.mult, ALU.add)\
                        .then_inc(L["ema"].sem, 1)
                    dve.wait_ge(L["hid_sb"].sem, L["hid_sb"].at(b, 1))
                    dve.tensor_scalar(wide[0:64, :], ones[0:64, :], col[0:64, C_HID:C_HID + 1], None, ALU.mult)\
                        .then_inc(L["wide"].sem, 1)
                    dve.wait_ge(L["logit"].sem, L["logit"].at(b, 1))
                    dve.tensor_tensor(probs3[:, 0:3], pu[:, 4:7], w("r2b"), ALU.add).then_inc(L["lmax"].sem, 1)
                    dve.wait_ge(L["lmax"].sem, L["lmax"].at(b, 1))
                    dve.tensor_reduce(c(C_MX), probs3[:, 0:3], AX.X, ALU.max).then_inc(L["lmax"].sem, 1)
                    dve.wait_ge(L["lmax"].sem, L["lmax"].at(b, 2))
                    dve.tensor_scalar(c(C_NMX), c(C_MX), -1.0, None, ALU.mult).then_inc(L["lmax"].sem, 1)
                    dve.wait_ge(L["lexp"].sem, L["lexp"].at(b, 1))
                    dve.reciprocal(c(C_INV), c(C_SUM)).then_inc(L["lsum"].sem, 1)
                    dve.wait_ge(L["lsum"].sem, L["lsum"].at(b, 1))
                    dve.tensor_scalar(probs3[:, 4:7], probs3[:, 4:7], c(C_INV), None, ALU.mult).then_inc(L["lsum"].sem, 1)
                    dve.wait_ge(L["lsum"].sem, L["lsum"].at(b, 2))
                    dve.tensor_tensor(c(C_PMF), probs3[:, 5:6], probs3[:, 6:7], ALU.add).then_inc(L["lsum"].sem, 1)
                    dve.wait_ge(L["lscore"].sem, L["lscore"].at(b, 1))
                    dve.tensor_copy(attn[:, 2, :], pu[:, 64:64 + SLOTS]).then_inc(L["route"].sem, 1)
                    dve.wait_ge(L["route"].sem, L["route"].at(b, 2))
                    dve.tensor_reduce(c(C_AMX), attn[:, 2, :], AX.X, ALU.max).then_inc(L["attn"].sem, 1)
                    dve.wait_ge(L["attn"].sem, L["attn"].at(b, 1))
                    dve.tensor_scalar(c(C_SHIFT), c(C_AMX), -scd, None, ALU.mult).then_inc(L["attn"].sem, 1)
                    for n in range(NA):
                        dve.wait_ge(L["scores"].sem, L["scores"].at(b, n + 1))
                        dve.tensor_reduce(stats[:, 0, n:n + 1], (pb, pc)[n % 2][:, :], AX.X, ALU.max)\
                            .then_inc(L["top"].sem, 1)
                        dve.wait_ge(L["top"].sem, L["top"].at(b, n + 1))
                        dve.tensor_scalar(stats[:, 1, n:n + 1], stats[:, 0, n:n + 1], -sc, None, ALU.mult)\
                            .then_inc(L["shift"].sem, 1)
                        if n % 2 == 1 and n >= 3:
                            differ(dve, b, n // 2 - 1)
                    differ(dve, b, TT - 1)
                    dve.wait_ge(L["aexp"].sem, L["aexp"].at(b, 1))
                    dve.reciprocal(c(C_AINV), c(C_ASUM)).then_inc(L["attn"].sem, 1)
                    dve.wait_ge(L["attn"].sem, L["attn"].at(b, 3))
                    dve.tensor_tensor(attn[:, 1, :], attn[:, 0, :], w("landmarks_t"), ALU.mult).then_inc(L["attn"].sem, 1)
                    dve.wait_ge(L["attn"].sem, L["attn"].at(b, 4))
                    dve.tensor_reduce(c(C_ARC), attn[:, 1, :], AX.X, ALU.add).then_inc(L["attn"].sem, 1)
                    dve.wait_ge(L["attn"].sem, L["attn"].at(b, 5))
                    dve.tensor_scalar(c(C_ARC), c(C_ARC), c(C_AINV), probs3[:, 6:7], ALU.mult, ALU.mult)\
                        .then_inc(L["route"].sem, 1)
                    dve.wait_ge(L["slr"].sem, L["slr"].at(b, 1))
                    dve.wait_ge(L["lsum"].sem, L["lsum"].at(b, 3))
                    dve.scalar_tensor_tensor(out=joined[:, :], in0=pc[:, :], scalar=c(C_PMF), in1=ema[:, :],
                                             op0=ALU.mult, op1=ALU.add).then_inc(L["arc"].sem, 1)
                    dve.wait_ge(L["arc"].sem, L["arc"].at(b, 1))
                    dve.wait_ge(L["route"].sem, L["route"].at(b, 3))
                    dve.tensor_tensor(joined[:, S - 1:S], joined[:, S - 1:S], c(C_ARC), ALU.add).then_inc(L["arc"].sem, 1)
                    rms_vector(dve, b, 1)
                    dve.wait_ge(L["spread"].sem, L["spread"].at(b, 2))
                    dve.wait_ge(L["mix_sb"].sem, L["mix_sb"].at(b, 1))
                    dve.tensor_tensor(joined[:, :], mix[:, :], pa[:, :], ALU.mult).then_inc(L["scaled"].sem, 1)
                    dve.wait_ge(L["scaled"].sem, L["scaled"].at(b, 1))
                    dve.scalar_tensor_tensor(out=result[:, :], in0=joined[:, :], scalar=w("norm_out"), in1=xl[:, :],
                                             op0=ALU.mult, op1=ALU.add).then_inc(L["result"].sem, 1)
                    dve.wait_ge(L["result"].sem, L["result"].at(b, 1))
                    dve.tensor_reduce(c(C_M2), result[:, :], AX.X, ALU.add).then_inc(L["mean"].sem, 1)
                    dve.wait_ge(L["bus_sb"].sem, L["bus_sb"].at(b, 3))
                    dve.scalar_tensor_tensor(out=core.batch(b), in0=result[:, :], scalar=c(C_B2), in1=core.batch(b),
                                             op0=ALU.add, op1=ALU.add).then_inc(L["done"].sem, 1)

            @block.gpsimd
            def _(pool):
                with pool.Fori(0, B) as b:
                    rms_pool(pool, b, 0)
                    rms_pool(pool, b, 1)
    L.close()


def pair_attention(nc, core, name):
    L = Layer(nc, name, core, ["pairs"], **NEXT, prep=6, bdiff=2, expb=1,
              qkv=3,
              soft=3,
              partner=2,
              kv=2,
              sums=4,
              terms=4, joined=2, inverse=1, mixed=1,
              projected=1, done=1)
    with L.ctx:
        g = "pairs"
        xn, q, k, v, q2, k2 = (L.sb(n, [P, S]) for n in ("xn", "q", "k", "v", "q2", "k2"))
        kv, kv2, sa, sbb, sn, sn2 = (L.sb(n, [P, S]) for n in ("kv", "kv2", "sa", "sbb", "sn", "sn2"))
        mixed = L.sb("mixed", [P, S])
        wq, wk = L.sb("wq", [P, D]), L.sb("wk", [P, D])
        col = L.sb("col", [P, 5])
        ps = [L.ps(n, [P, S]) for n in ("ps_q", "ps_k", "ps_v")]
        out = L.ps("out", [P, S])
        ones_row = core.w("const", "ones_s")
        with nc.Block() as block:
            @block.tensor
            def _(pe):
                pe.wait_ge(L["prep"].sem, L["prep"].at(0, 6))
                with pe.Fori(0, B) as b:
                    pe.wait_ge(L["now"].sem, L["now"].at(b, 1))
                    pe.wait_ge(L["soft"].sem, L["soft"].at(b, 0))
                    for i, w in enumerate((wq[:, :], wk[:, :], core.w(g, "wv"))):
                        pe.matmul(ps[i][:, :], w, xn[:, :], start=True, stop=True).then_inc(L["qkv"].sem, 1)
                    pe.wait_ge(L["mixed"].sem, L["mixed"].at(b, 1))
                    pe.matmul(out[:, :], core.w(g, "wo"), mixed[:, :], start=True, stop=True)\
                        .then_inc(L["projected"].sem, 1)

            @block.scalar
            def _(act):
                act.activation(col[:, 2:3], core.w(g, "beta"), ACT.Exp).then_inc(L["expb"].sem, 1)
                act.wait_ge(L["prep"].sem, L["prep"].at(0, 6))
                with act.Fori(0, B) as b:
                    for i, to in enumerate((q, k)):
                        act.wait_ge(L["qkv"].sem, L["qkv"].at(b, i + 1))
                        act.wait_ge(L["mixed"].sem, L["mixed"].at(b, 0))
                        act.activation(to[:, :], ps[i][:, :], ACT.Sigmoid, bias=col[:, i:i + 1],
                                       scale=col[:, 2:3]).then_inc(L["soft"].sem, 1)
                    act.wait_ge(L["qkv"].sem, L["qkv"].at(b, 3))
                    act.activation(v[:, :], ps[2][:, :], ACT.Identity, bias=core.w(g, "bv")).then_inc(L["soft"].sem, 1)

            @block.vector
            def _(dve):
                for w, to in ((core.w(g, "wq"), wq), (core.w(g, "wk"), wk)):
                    pair = w.rearrange("p (h d) -> p h d", d=2)
                    diff = to[:, :].rearrange("p (h d) -> p h d", d=2)
                    for d in range(2):
                        dve.tensor_tensor(diff[:, :, d], pair[:, :, d], pair[:, :, 1 - d], ALU.subtract)\
                            .then_inc(L["prep"].sem, 1)
                dve.wait_ge(L["expb"].sem, L["expb"].at(0, 1))
                for i, n in enumerate(("bq", "bk")):
                    dve.tensor_tensor(col[:, 3 + i:4 + i], core.w(g, n, 0, 1), core.w(g, n, 1, 2), ALU.subtract)\
                        .then_inc(L["bdiff"].sem, 1)
                    dve.wait_ge(L["bdiff"].sem, L["bdiff"].at(0, i + 1))
                    dve.tensor_tensor(col[:, i:i + 1], col[:, 3 + i:4 + i], col[:, 2:3], ALU.mult).then_inc(L["prep"].sem, 1)
                with dve.Fori(0, B) as b:
                    take_normed(dve, L, b, xn[:, :])
                    dve.wait_ge(L["soft"].sem, L["soft"].at(b, 2))
                    dve.tensor_scalar(q2[:, :], q[:, :], -1.0, 1.0, ALU.mult, ALU.add).then_inc(L["partner"].sem, 1)
                    dve.tensor_scalar(k2[:, :], k[:, :], -1.0, 1.0, ALU.mult, ALU.add).then_inc(L["partner"].sem, 1)
                    dve.tensor_tensor_scan(sn[:, :], ones_row, k[:, :], 0.0, ALU.mult, ALU.add)\
                        .then_inc(L["sums"].sem, 1)
                    dve.wait_ge(L["soft"].sem, L["soft"].at(b, 3))
                    dve.tensor_tensor(kv[:, :], k[:, :], v[:, :], ALU.mult).then_inc(L["kv"].sem, 1)
                    dve.wait_ge(L["partner"].sem, L["partner"].at(b, 2))
                    dve.tensor_tensor(kv2[:, :], k2[:, :], v[:, :], ALU.mult).then_inc(L["kv"].sem, 1)
                    dve.wait_ge(L["kv"].sem, L["kv"].at(b, 1))
                    dve.tensor_tensor_scan(sa[:, :], ones_row, kv[:, :], 0.0, ALU.mult, ALU.add)\
                        .then_inc(L["sums"].sem, 1)
                    dve.wait_ge(L["kv"].sem, L["kv"].at(b, 2))
                    dve.tensor_tensor_scan(sbb[:, :], ones_row, kv2[:, :], 0.0, ALU.mult, ALU.add)\
                        .then_inc(L["sums"].sem, 1)
                    dve.wait_ge(L["sums"].sem, L["sums"].at(b, 1))
                    dve.tensor_tensor_scan(sn2[:, :], ones_row, k2[:, :], 0.0, ALU.mult, ALU.add)\
                        .then_inc(L["sums"].sem, 1)
                    dve.wait_ge(L["sums"].sem, L["sums"].at(b, 4))
                    for to, a, c in ((kv, q, sa), (kv2, q2, sbb), (k, q, sn), (k2, q2, sn2)):
                        dve.tensor_tensor(to[:, :], a[:, :], c[:, :], ALU.mult).then_inc(L["terms"].sem, 1)
                    dve.wait_ge(L["terms"].sem, L["terms"].at(b, 4))
                    dve.tensor_tensor(sn[:, :], k[:, :], k2[:, :], ALU.add).then_inc(L["joined"].sem, 1)
                    dve.tensor_tensor(sa[:, :], kv[:, :], kv2[:, :], ALU.add).then_inc(L["joined"].sem, 1)
                    dve.wait_ge(L["joined"].sem, L["joined"].at(b, 1))
                    dve.reciprocal(sn2[:, :], sn[:, :]).then_inc(L["inverse"].sem, 1)
                    dve.wait_ge(L["joined"].sem, L["joined"].at(b, 2))
                    dve.wait_ge(L["inverse"].sem, L["inverse"].at(b, 1))
                    dve.tensor_tensor(mixed[:, :], sa[:, :], sn2[:, :], ALU.mult).then_inc(L["mixed"].sem, 1)
                    dve.wait_ge(L["projected"].sem, L["projected"].at(b, 1))
                    dve.scalar_tensor_tensor(out=core.batch(b), in0=out[:, :], scalar=core.w(g, "bo"),
                                             in1=core.batch(b), op0=ALU.add, op1=ALU.add).then_inc(L["done"].sem, 1)

    L.close()



def cell(nc, core, name):
    L = Layer(nc, name, core, ["cell"], start=1,
              gates=3,
              opened=3,
              parts=2,
              state=1,
              answer=1,
              answered=1,
              done=1)
    with L.ctx:
        g = "cell"
        c, f, i_, n_, ig, h = (L.sb(k, [P, S]) for k in ("c", "f", "i", "n", "ig", "h"))
        ps = [L.ps(n, [P, S]) for n in ("ps_f", "ps_i", "ps_n")]
        out = L.ps("out", [P, S])


        with nc.Block() as block:
            @block.tensor
            def _(pe):
                with pe.Fori(0, B) as b:
                    pe.wait_ge(L["opened"].sem, L["opened"].at(b, 0))
                    for j, w in enumerate(("wf", "wi", "wc")):
                        pe.matmul(ps[j][:, :], core.w(g, w), core.normed(b), start=True, stop=False)
                    pe.wait_ge(L["state"].sem, L["state"].at(b, 0))
                    pe.wait_ge(L["start"].sem, L["start"].at(0, 1))
                    for j, w in enumerate(("uf", "ui", "uc")):
                        pe.matmul(ps[j][:, :], core.w(g, w), c[:, :], start=False, stop=True)\
                            .then_inc(L["gates"].sem, 1)
                pe.wait_ge(L["state"].sem, L["state"].at(B - 1, 1))
                with pe.Fori(0, B) as b:
                    pe.wait_ge(L["answered"].sem, L["answered"].at(b, 0))
                    pe.matmul(out[:, :], core.w(g, "wo"), core.normed(b), start=True, stop=False)
                    pe.matmul(out[:, :], core.w(g, "uo"), c[:, :], start=False, stop=True)\
                        .then_inc(L["answer"].sem, 1)

            @block.scalar
            def _(act):
                with act.Fori(0, B) as b:
                    act.wait_ge(L["state"].sem, L["state"].at(b, 0))
                    for j, (to, fn, bias) in enumerate(((f, ACT.Sigmoid, "bf"), (i_, ACT.Sigmoid, "bi"),
                                                        (n_, ACT.Tanh, "bc"))):
                        act.wait_ge(L["gates"].sem, L["gates"].at(b, j + 1))
                        act.activation(to[:, :], ps[j][:, :], fn, bias=core.w(g, bias)).then_inc(L["opened"].sem, 1)
                with act.Fori(0, B) as b:
                    act.wait_ge(L["answer"].sem, L["answer"].at(b, 1))
                    act.wait_ge(L["done"].sem, L["done"].at(b, 0))
                    act.activation(h[:, :], out[:, :], ACT.Tanh, bias=core.w(g, "bo")).then_inc(L["answered"].sem, 1)

            @block.vector
            def _(dve):
                dve.tensor_copy(c[:, :], core.w(g, "in_c").to_broadcast([P, S])).then_inc(L["start"].sem, 1)
                dve.wait_ge(L["start"].sem, L["start"].at(0, 1))
                with dve.Fori(0, B) as b:
                    dve.wait_ge(L["opened"].sem, L["opened"].at(b, 3))
                    dve.tensor_tensor(ig[:, :], i_[:, :], n_[:, :], ALU.mult).then_inc(L["parts"].sem, 1)
                    dve.tensor_tensor(h[:, :], f[:, :], c[:, :], ALU.mult).then_inc(L["parts"].sem, 1)
                    dve.wait_ge(L["parts"].sem, L["parts"].at(b, 2))
                    dve.tensor_tensor(c[:, :], ig[:, :], h[:, :], ALU.add).then_inc(L["state"].sem, 1)
                with dve.Fori(0, B) as b:
                    dve.wait_ge(L["answered"].sem, L["answered"].at(b, 1))
                    dve.tensor_tensor(core.batch(b), h[:, :], core.batch(b), ALU.add).then_inc(L["done"].sem, 1)

    L.close()

DI, NS, CONV, RANK = 256, 16, 4, 64
CT = DI // P


def state_space(nc, core, name, g):
    ST = NS * CT
    BT = B * CT
    L = Layer(nc, name, core, [g], consts=1, history=1, a_exp=1, a_neg=1,
              xz=2 * BT,
              padded=BT,
              zs=BT,
              tap=BT * CONV,
              u=BT,
              low=B,
              low_sb=B,
              bc=B,
              split=5 * B,
              pre=BT,
              soft=3 * BT,
              soft_pos=BT,
              delta=BT,
              now=CT,
              du=CT,
              rows_b=NS,
              rows_c=NS,
              bsb=NS,
              decay=ST,
              drive=ST,
              state=ST,
              read=ST,
              summed=NS,
              added=NS - 1,
              skip=CT, gated=CT, projected=1, done=1)
    with L.ctx:
        R = 2 * NS
        padded = L.sb("padded", [P, BT, CONV - 1 + S])
        zs, u, delta = (L.sb(n, [P, BT * S]) for n in ("zs", "u", "delta"))
        conv = L.sb("conv", [P, BT * S])
        low = L.sb("low", [RANK, B, S])
        rest = L.sb("rest", [R, 2, S])
        mid = L.sb("mid", [R, S], BF16)
        parts = L.sb("parts", [3 * R, B * S], BF16)
        spread16 = L.sb("spread16", [3 * R, R, P], BF16)
        a = L.sb("a", [P, CT, NS])
        bsb = L.sb("bsb", [P, 2, S])
        decay, drive = L.sb("decay", [P, 4, S]), L.sb("drive", [P, 4, S])
        tiles = conv[:, :].rearrange("p (k s) -> p k s", k=BT)
        read = tiles[:, 0:2 * CT, :].rearrange("p (t i) s -> p t i s", t=CT)
        y, du_now = tiles[:, 2 * CT:3 * CT, :], tiles[:, 3 * CT:4 * CT, :]
        delta_now = padded[:, 0:CT, 0:S]
        state = padded[:, 4:8, 0:S]
        total = padded[:, CT, 0:S]
        banks = L.ps("banks", [P, 8, S])
        pb, pc, py, out = banks[:, 0:2, :], banks[:, 2:4, :], banks[:, 4, :], banks[:, 5, :]
        eye = core.w("const", "eye")

        def tile_of(buffer, b, t):
            return buffer[:, bass.ds(b * (CT * S) + t * S, S)]

        def flat(buffer, k):
            return buffer[:, k * S:(k + 1) * S]


        def spread_b(pe, b, n):
            pe.wait_ge(L["bsb"].sem, L["bsb"].at(b, max(n - 1, 0)))
            pe.matmul(pb[:, n % 2, :], spread16[:, n, :], parts[:, bass.ds(b * S, S)], start=True, stop=True)\
                .then_inc(L["rows_b"].sem, 1)

        def spread_c(pe, b, n):
            pe.wait_ge(L["read"].sem, L["read"].at(b, CT * max(n - 1, 0)))
            pe.matmul(pc[:, n % 2, :], spread16[:, NS + n, :], parts[:, bass.ds(b * S, S)], start=True, stop=True)\
                .then_inc(L["rows_c"].sem, 1)

        def read_out(dve, b, s):
            n, t = divmod(s, CT)
            dve.wait_ge(L["state"].sem, L["state"].at(b, s + 1))
            dve.wait_ge(L["rows_c"].sem, L["rows_c"].at(b, n + 1))
            if t == 0:
                dve.wait_ge(L["summed"].sem, L["summed"].at(b, max(n - 1, 0)))
            elif n:
                dve.wait_ge(L["added"].sem, L["added"].at(b, max(n - 2, 0)))
            else:
                dve.wait_ge(L["skip"].sem, L["skip"].at(b, 0))
            to = total if t and n == 0 else read[:, t, n % 2, :]
            dve.tensor_tensor(to, state[:, s % 4, :], pc[:, n % 2, :], ALU.mult).then_inc(L["read"].sem, 1)

        def add(dve, b, n):
            dve.wait_ge(L["read"].sem, L["read"].at(b, CT * (n + 1)))
            dve.wait_ge(L["added"].sem, L["added"].at(b, n - 1))
            dve.tensor_tensor(total, total, read[:, 1, n % 2, :], ALU.add).then_inc(L["added"].sem, 1)

        def take_batch(dve, b):
            for t in range(CT):
                dve.wait_ge(L["decay"].sem, L["decay"].at(b, 0))
                dve.tensor_copy(delta_now[:, t, :], tile_of(delta, b, t)).then_inc(L["now"].sem, 1)
                dve.wait_ge(L["drive"].sem, L["drive"].at(b, 0))
                dve.tensor_tensor(du_now[:, t, :], tile_of(delta, b, t), tile_of(u, b, t), ALU.mult)\
                    .then_inc(L["du"].sem, 1)

        def project(pe, b):
            pe.wait_ge(L["gated"].sem, L["gated"].at(b, CT))
            pe.wait_ge(L["done"].sem, L["done"].at(b, 0))
            for t in range(CT):
                mm = pe.matmul(out, core.w(g, "w_out", t * P, (t + 1) * P), y[:, t, :],
                               start=t == 0, stop=t == CT - 1)
            mm.then_inc(L["projected"].sem, 1)

        def sums(pe, b, first):
            spread_b(pe, b, 0)
            spread_b(pe, b, 1)
            spread_c(pe, b, 0)
            for n in range(NS):
                if n + 2 < NS:
                    spread_b(pe, b, n + 2)
                if n + 1 < NS:
                    spread_c(pe, b, n + 1)
                pe.wait_ge(L["read"].sem, L["read"].at(b, CT * n + 1))
                if n == 0:
                    pe.wait_ge(L["skip"].sem, L["skip"].at(b, 0))
                pe.matmul(py, eye, read[:, 0, n % 2, :], start=n == 0, stop=n == NS - 1)\
                    .then_inc(L["summed"].sem, 1)
                if n == 1 and not first:
                    project(pe, b - 1)

        def finish(dve, b):
            dve.wait_ge(L["projected"].sem, L["projected"].at(b, 1))
            dve.tensor_tensor(core.batch(b), out, core.batch(b), ALU.add).then_inc(L["done"].sem, 1)

        def scans(dve, b, first):
            take_batch(dve, b)
            for s in range(ST):
                dve.wait_ge(L["decay"].sem, L["decay"].at(b, s + 1))
                dve.wait_ge(L["drive"].sem, L["drive"].at(b, s + 1))
                dve.wait_ge(L["read"].sem, L["read"].at(b, max(s - 3, 0)))
                dve.tensor_tensor_scan(state[:, s % 4, :], decay[:, s % 4, :], drive[:, s % 4, :], 0.0,
                                       ALU.mult, ALU.add).then_inc(L["state"].sem, 1)
                if s >= 1:
                    read_out(dve, b, s - 1)
                if s >= 2 * CT and s % CT == 1:
                    add(dve, b, s // CT - 1)
                if s == 4 * CT and not first:
                    finish(dve, b - 1)
            read_out(dve, b, ST - 1)
            add(dve, b, NS - 1)
            dve.wait_ge(L["summed"].sem, L["summed"].at(b, NS))
            dve.wait_ge(L["added"].sem, L["added"].at(b, NS - 1))
            dve.wait_ge(L["projected"].sem, L["projected"].at(b, 0))
            for t in range(CT):
                dve.scalar_tensor_tensor(out=y[:, t, :], in0=tile_of(u, b, t), scalar=core.w(g, "skip", t, t + 1),
                                         in1=(py, total)[t], op0=ALU.mult, op1=ALU.add)\
                    .then_inc(L["skip"].sem, 1)
            for t in range(CT):
                dve.wait_ge(L["skip"].sem, L["skip"].at(b, t + 1))
                dve.tensor_tensor(y[:, t, :], y[:, t, :], tile_of(zs, b, t), ALU.mult).then_inc(L["gated"].sem, 1)

        with nc.Block() as block:
            @block.tensor
            def _(pe):
                for k in range(2 * BT):
                    z, (b, t) = k // BT, divmod(k % BT, CT)
                    if z:
                        pe.wait_ge(L["padded"].sem, L["padded"].at(0, k - BT + 1))
                    pe.matmul(banks[:, k % 8, :], core.w(g, "w_in", z * DI + t * P, z * DI + (t + 1) * P),
                              core.xn[:, b * S:(b + 1) * S], start=True, stop=True).then_inc(L["xz"].sem, 1)
                for b in range(B):
                    pe.wait_ge(L["u"].sem, L["u"].at(0, CT * (b + 1)))
                    pe.wait_ge(L["zs"].sem, L["zs"].at(0, b + 1))
                    for t in range(CT):
                        mm = pe.matmul(banks[0:RANK, b, :], core.w(g, "w_low", t * RANK, (t + 1) * RANK),
                                       flat(u, CT * b + t), start=t == 0, stop=t == CT - 1)
                    mm.then_inc(L["low"].sem, 1)
                    pe.wait_ge(L["zs"].sem, L["zs"].at(0, B + b + 1))
                    for t in range(CT):
                        mm = pe.matmul(banks[0:R, B + b, :], core.w(g, "w_bc", t * R, (t + 1) * R),
                                       flat(u, CT * b + t), start=t == 0, stop=t == CT - 1)
                    mm.then_inc(L["bc"].sem, 1)
                for k in range(BT):
                    b, t = divmod(k, CT)
                    pe.wait_ge(L["low_sb"].sem, L["low_sb"].at(0, max(b, min(k, B - 1)) + 1))
                    if k >= B:
                        pe.wait_ge(L["split"].sem, L["split"].at(0, 5 * (k - B + 1)))
                    pe.matmul(banks[:, k, :], core.w(g, "w_dt", t * P, (t + 1) * P), low[:, b, :],
                              start=True, stop=True).then_inc(L["pre"].sem, 1)
                pe.wait_ge(L["consts"].sem, L["consts"].at(0, 1))
                pe.wait_ge(L["soft_pos"].sem, L["soft_pos"].at(0, BT))
                sums(pe, 0, True)
                with pe.Fori(1, B) as b:
                    sums(pe, b, False)
                project(pe, B - 1)

            @block.scalar
            def _(act):
                act.activation(a[:, :, :], core.w(g, "a_log").rearrange("p (t n) -> p t n", t=CT), ACT.Exp)\
                    .then_inc(L["a_exp"].sem, 1)
                act.wait_ge(L["a_neg"].sem, L["a_neg"].at(0, 1))
                for k in range(BT):
                    act.wait_ge(L["xz"].sem, L["xz"].at(0, k + 1))
                    act.activation(padded[:, k, CONV - 1:], banks[:, k % 8, :], ACT.Copy).then_inc(L["padded"].sem, 1)
                for k in range(BT):
                    act.wait_ge(L["xz"].sem, L["xz"].at(0, BT + k + 1))
                    act.activation(flat(zs, k), banks[:, k % 8, :], ACT.Silu).then_inc(L["zs"].sem, 1)
                for k in range(BT):
                    t = k % CT
                    act.wait_ge(L["tap"].sem, L["tap"].at(0, CONV * (k + 1)))
                    act.activation(flat(u, k), flat(conv, k), ACT.Silu, bias=core.w(g, "conv_b", t, t + 1))\
                        .then_inc(L["u"].sem, 1)
                for b in range(B):
                    act.wait_ge(L["low"].sem, L["low"].at(0, b + 1))
                    act.activation(low[:, b, :], banks[0:RANK, b, :], ACT.Copy).then_inc(L["low_sb"].sem, 1)
                for k in range(BT):
                    t = k % CT
                    act.wait_ge(L["pre"].sem, L["pre"].at(0, k + 1))
                    act.activation(flat(delta, k), banks[:, k, :], ACT.Abs, bias=core.w(g, "dt_b", t, t + 1))\
                        .then_inc(L["soft"].sem, 1)
                for k in range(BT):
                    act.wait_ge(L["soft"].sem, L["soft"].at(0, k + 1))
                    act.activation(flat(delta, k), flat(delta, k), ACT.Exp, scale=-1.0).then_inc(L["soft"].sem, 1)
                for k in range(BT):
                    act.wait_ge(L["soft"].sem, L["soft"].at(0, BT + k + 1))
                    act.activation(flat(delta, k), flat(delta, k), ACT.Ln, bias=1.0).then_inc(L["soft"].sem, 1)
                with act.Fori(0, B) as b:
                    for n in range(NS):
                        act.wait_ge(L["rows_b"].sem, L["rows_b"].at(b, n + 1))
                        act.wait_ge(L["drive"].sem, L["drive"].at(b, CT * max(n - 1, 0)))
                        act.activation(bsb[:, n % 2, :], pb[:, n % 2, :], ACT.Copy).then_inc(L["bsb"].sem, 1)
                        for t in range(CT):
                            s = CT * n + t
                            if n == 0:
                                act.wait_ge(L["now"].sem, L["now"].at(b, t + 1))
                            act.wait_ge(L["state"].sem, L["state"].at(b, max(s - 3, 0)))
                            act.activation(decay[:, s % 4, :], delta_now[:, t, :], ACT.Exp, scale=a[:, t, n:n + 1])\
                                .then_inc(L["decay"].sem, 1)

            @block.vector
            def _(dve):
                dve.memset(padded[:, :, 0:CONV - 1], 0.0).then_inc(L["history"].sem, 1)
                dve.wait_ge(L["history"].sem, L["history"].at(0, 1))
                dve.wait_ge(L["a_exp"].sem, L["a_exp"].at(0, 1))
                dve.tensor_scalar(a[:, :, :], a[:, :, :], -1.0, None, ALU.mult).then_inc(L["a_neg"].sem, 1)
                for k in range(BT):
                    dve.wait_ge(L["padded"].sem, L["padded"].at(0, k + 1))
                    for i in range(CONV):
                        tap = core.w(g, "conv_w", k % CT * CONV + i, k % CT * CONV + i + 1)
                        src = padded[:, k, i:i + S]
                        if i == 0:
                            dve.tensor_scalar(flat(conv, k), src, tap, None, ALU.mult).then_inc(L["tap"].sem, 1)
                        else:
                            dve.wait_ge(L["tap"].sem, L["tap"].at(0, k * CONV + i))
                            dve.scalar_tensor_tensor(out=flat(conv, k), in0=src, scalar=tap, in1=flat(conv, k),
                                                     op0=ALU.mult, op1=ALU.add).then_inc(L["tap"].sem, 1)
                for b in range(B):
                    at = slice(b * S, (b + 1) * S)
                    ps = banks[0:R, B + b, :]
                    dve.wait_ge(L["bc"].sem, L["bc"].at(0, b + 1))
                    dve.tensor_copy(parts[0:R, at], ps).then_inc(L["split"].sem, 1)
                    dve.wait_ge(L["split"].sem, L["split"].at(0, 5 * b + 1))
                    dve.tensor_tensor(rest[:, 0, :], ps, parts[0:R, at], ALU.subtract).then_inc(L["split"].sem, 1)
                    dve.wait_ge(L["split"].sem, L["split"].at(0, 5 * b + 2))
                    dve.tensor_copy(parts[R:2 * R, at], rest[:, 0, :]).then_inc(L["split"].sem, 1)
                    dve.tensor_copy(mid[:, :], rest[:, 0, :]).then_inc(L["split"].sem, 1)
                    dve.wait_ge(L["split"].sem, L["split"].at(0, 5 * b + 4))
                    dve.tensor_tensor(parts[2 * R:3 * R, at], rest[:, 0, :], mid[:, :], ALU.subtract)\
                        .then_inc(L["split"].sem, 1)
                for k in range(BT):
                    t = k % CT
                    dve.wait_ge(L["soft"].sem, L["soft"].at(0, k + 1))
                    dve.wait_ge(L["u"].sem, L["u"].at(0, k + 1))
                    dve.tensor_scalar(flat(conv, k), banks[:, k, :], core.w(g, "dt_b", t, t + 1), 0.0,
                                      ALU.add, ALU.max).then_inc(L["soft_pos"].sem, 1)
                for k in range(BT):
                    dve.wait_ge(L["soft"].sem, L["soft"].at(0, 2 * BT + k + 1))
                    dve.wait_ge(L["soft_pos"].sem, L["soft_pos"].at(0, k + 1))
                    dve.tensor_tensor(flat(delta, k), flat(delta, k), flat(conv, k), ALU.add).then_inc(L["delta"].sem, 1)
                dve.wait_ge(L["delta"].sem, L["delta"].at(0, BT))
                scans(dve, 0, True)
                with dve.Fori(1, B) as b:
                    scans(dve, b, False)
                finish(dve, B - 1)

            @block.gpsimd
            def _(pool):
                pool.tensor_copy(spread16[:, :, :], core.w("const", "spread").unsqueeze(2)
                                 .to_broadcast([3 * R, R, P])).then_inc(L["consts"].sem, 1)
                with pool.Fori(0, B) as b:
                    pool.wait_ge(L["du"].sem, L["du"].at(b, CT))
                    for s in range(ST):
                        n, t = divmod(s, CT)
                        pool.wait_ge(L["bsb"].sem, L["bsb"].at(b, n + 1))
                        pool.wait_ge(L["state"].sem, L["state"].at(b, max(s - 3, 0)))
                        pool.tensor_tensor(drive[:, s % 4, :], du_now[:, t, :], bsb[:, n % 2, :], ALU.mult)\
                            .then_inc(L["drive"].sem, 1)
    L.close()

EH, EHD = 16, 8
EW = EHD + 1
EROWS = 32
VARIANTS = 4


def elu_attention(nc, core, name):
    NSTEP = EH
    L = Layer(nc, name, core, ["elu"], **NEXT, start=3,
              proj=2, below=2, above=2, expo=2, feats=2, variant=VARIANTS,
              vk=TT, vk_sb=TT, kturn=1, ktok=1,
              states=TT - 1, states_sb=TT - 1,
              energy=NSTEP, masked=NSTEP, 
              mixed=VARIANTS, c_sb=VARIANTS, c_turn=VARIANTS,
              norm=2 * VARIANTS, outs=VARIANTS, turned=1, outs_sb=1, projected=1, done=1)
    with L.ctx:
        g = "elu"
        w = lambda n, *a: core.w(g, n, *a)
        xn = L.sb("xn", [P, S])
        low, high, feats = (L.sb(n, [P, 2, S]) for n in ("low", "high", "feats"))
        kvar = L.sb("kvar", [P, VARIANTS, S])
        vaug = L.sb("vaug", [P, TT, EH, EROWS])
        ktok = L.sb("ktok", [P, TT, P])
        state = L.sb("state", [P, TT - 1, VARIANTS, P])
        energy = L.sb("energy", [P, NSTEP, S])
        den = L.sb("den", [P, TT, VARIANTS])
        c_sb = L.sb("c_sb", [P, S])
        outs = L.sb("outs", [P, TT, D])
        outs_t = L.sb("outs_t", [P, S])
        bank, small = L.ps("bank", [P, S]), L.ps("small", [P, S])
        pe4 = L.ps("pe4", [P, 4, S])
        pmix = L.ps("pmix", [P, 2, S])
        eye = core.w("const", "eye")

        def energies(pe, b, j):
            pe.wait_ge(L["variant"].sem, L["variant"].at(b, j + 1))
            for r in range(4):
                s = 4 * j + r
                rows = slice(32 * r, 32 * r + 32)
                if j:
                    pe.wait_ge(L["masked"].sem, L["masked"].at(b, s - 3))
                for t in range(TT):
                    tk = slice(t * P, (t + 1) * P)
                    mm = pe.matmul(pe4[:, r, tk], kvar[rows, j, tk], feats[rows, 0, tk], start=True, stop=True)
                mm.then_inc(L["energy"].sem, 1)

        def mix(pe, b, j):
            pe.wait_ge(L["states_sb"].sem, L["states_sb"].at(b, TT - 1))
            pe.wait_ge(L["masked"].sem, L["masked"].at(b, 4 * (j + 1)))
            pe.wait_ge(L["c_sb"].sem, L["c_sb"].at(b, max(j - 1, 0)))
            for t in range(TT):
                tk = slice(t * P, (t + 1) * P)
                if t:
                    pe.matmul(pmix[:, j % 2, tk], state[:, t - 1, j, :], feats[:, 0, tk], start=True, stop=True,
                              skip_group_check=True)
                for r in range(4):
                    mm = pe.matmul(pmix[r * EROWS:(r + 1) * EROWS, j % 2, tk], vaug[:, t, 4 * r + j, :],
                                   energy[:, 4 * j + r, tk], start=t == 0, stop=True, skip_group_check=True)
            mm.then_inc(L["mixed"].sem, 1)

        def turn(pe, b, j):
            pe.wait_ge(L["c_sb"].sem, L["c_sb"].at(b, j + 1))
            pe.wait_ge(L["outs"].sem, L["outs"].at(b, j))
            for t in range(TT):
                mm = pe.transpose(bank[:, t * P:(t + 1) * P], c_sb[:, t * P:(t + 1) * P], eye)
            mm.then_inc(L["c_turn"].sem, 1)

        def mask(dve, b, j):
            for s in range(4 * j, 4 * j + 4):
                dve.wait_ge(L["energy"].sem, L["energy"].at(b, s + 1))
                dve.tensor_tensor(energy[:, s, :].rearrange("p (t c) -> p t c", t=TT),
                                  pe4[:, s % 4, :].rearrange("p (t c) -> p t c", t=TT),
                                  core.w("const", "upper").unsqueeze(1).to_broadcast([P, TT, P]), ALU.mult)\
                    .then_inc(L["masked"].sem, 1)

        def divide(dve, b, j):
            sums = bank[:, :].rearrange("p (t r w) -> p t r w", t=TT, r=4)
            dve.wait_ge(L["c_turn"].sem, L["c_turn"].at(b, j + 1))
            dve.wait_ge(L["outs"].sem, L["outs"].at(b, j))
            dve.tensor_scalar(den[:, :, :], sums[:, :, :, EHD], 1e-6, None, ALU.add).then_inc(L["norm"].sem, 1)
            dve.wait_ge(L["norm"].sem, L["norm"].at(b, 2 * j + 1))
            dve.reciprocal(den[:, :, :], den[:, :, :]).then_inc(L["norm"].sem, 1)
            dve.wait_ge(L["norm"].sem, L["norm"].at(b, 2 * j + 2))
            dve.tensor_tensor(outs[:, :, :].rearrange("p t (r j e) -> p t r j e", r=4, j=VARIANTS)[:, :, :, j, :],
                              sums[:, :, :, 0:EHD], den[:, :, :].unsqueeze(3).to_broadcast([P, TT, 4, EHD]), ALU.mult)\
                .then_inc(L["outs"].sem, 1)

        with nc.Block() as block:
            @block.tensor
            def _(pe):
                pe.wait_ge(L["start"].sem, L["start"].at(0, 3))
                with pe.Fori(0, B) as b:
                    pe.wait_ge(L["done"].sem, L["done"].at(b, 0))
                    pe.wait_ge(L["now"].sem, L["now"].at(b, 1))
                    pe.wait_ge(L["masked"].sem, L["masked"].at(b, 0))
                    for i, n in enumerate(("wq", "wk")):
                        pe.matmul(pe4[:, i, :], w(n), xn[:, :], start=True, stop=True).then_inc(L["proj"].sem, 1)
                    for t in range(TT):
                        pe.matmul(small[:, t * P:(t + 1) * P], xn[:, t * P:(t + 1) * P], w("wv"),
                                  start=True, stop=True).then_inc(L["vk"].sem, 1)
                    pe.wait_ge(L["feats"].sem, L["feats"].at(b, 2))
                    for t in range(TT):
                        mm = pe.transpose(bank[:, t * P:(t + 1) * P], feats[:, 1, t * P:(t + 1) * P], eye)
                    mm.then_inc(L["kturn"].sem, 1)
                    pe.wait_ge(L["vk_sb"].sem, L["vk_sb"].at(b, TT))
                    pe.wait_ge(L["ktok"].sem, L["ktok"].at(b, 1))
                    for t in range(1, TT):
                        at = (t - 1) * EH * EW
                        for o in range(t):
                            mm = pe.matmul(small[:, at:at + EH * EW], ktok[:, o, :],
                                           vaug[:, o, :, 0:EW],
                                           start=o == 0, stop=o == t - 1)
                        mm.then_inc(L["states"].sem, 1)
                    for j in range(VARIANTS):
                        energies(pe, b, j)
                        if j >= 1:
                            mix(pe, b, j - 1)
                        if j >= 2:
                            turn(pe, b, j - 2)
                    mix(pe, b, VARIANTS - 1)
                    turn(pe, b, VARIANTS - 2)
                    turn(pe, b, VARIANTS - 1)
                    pe.wait_ge(L["outs"].sem, L["outs"].at(b, VARIANTS))
                    for t in range(TT):
                        mm = pe.transpose(bank[:, t * P:(t + 1) * P], outs[:, t, :], eye)
                    mm.then_inc(L["turned"].sem, 1)
                    pe.wait_ge(L["outs_sb"].sem, L["outs_sb"].at(b, 1))
                    pe.matmul(small[:, :], w("wo"), outs_t[:, :], start=True, stop=True).then_inc(L["projected"].sem, 1)

            @block.scalar
            def _(act):
                with act.Fori(0, B) as b:
                    for i in range(2):
                        act.wait_ge(L["below"].sem, L["below"].at(b, i + 1))
                        act.activation(low[:, i, :], low[:, i, :], ACT.Exp).then_inc(L["expo"].sem, 1)
                    act.wait_ge(L["kturn"].sem, L["kturn"].at(b, 1))
                    act.activation(ktok[:, :, :], bank[:, :].rearrange("p (t c) -> p t c", t=TT), ACT.Copy)\
                        .then_inc(L["ktok"].sem, 1)
                    for j in range(VARIANTS):
                        act.wait_ge(L["mixed"].sem, L["mixed"].at(b, j + 1))
                        act.wait_ge(L["c_turn"].sem, L["c_turn"].at(b, j))
                        act.activation(c_sb[:, :], pmix[:, j % 2, :], ACT.Copy).then_inc(L["c_sb"].sem, 1)
                    act.wait_ge(L["turned"].sem, L["turned"].at(b, 1))
                    act.activation(outs_t[:, :], bank[:, :], ACT.Copy).then_inc(L["outs_sb"].sem, 1)

            @block.vector
            def _(dve):
                dve.memset(vaug[:, :, :, 0:EW], 1.0).then_inc(L["start"].sem, 1)
                dve.memset(vaug[:, :, :, EW:EROWS], 0.0).then_inc(L["start"].sem, 1)
                dve.memset(state[:, :, :, :], 0.0).then_inc(L["start"].sem, 1)
                dve.wait_ge(L["start"].sem, L["start"].at(0, 3))
                with dve.Fori(0, B) as b:
                    take_normed(dve, L, b, xn[:, :])
                    dve.wait_ge(L["mixed"].sem, L["mixed"].at(b, 0))
                    for i in range(2):
                        dve.wait_ge(L["proj"].sem, L["proj"].at(b, i + 1))
                        bias = w(("bq", "bk")[i])
                        dve.tensor_scalar(low[:, i, :], pe4[:, i, :], bias, 0.0, ALU.add, ALU.min)\
                            .then_inc(L["below"].sem, 1)
                        dve.tensor_scalar(high[:, i, :], pe4[:, i, :], bias, 0.0, ALU.add, ALU.max)\
                            .then_inc(L["above"].sem, 1)
                    for t in range(TT):
                        dve.wait_ge(L["vk"].sem, L["vk"].at(b, TT))
                        dve.tensor_tensor(vaug[:, t, :, 0:EHD],
                                          small[:, t * P:(t + 1) * P].rearrange("p (h e) -> p h e", h=EH),
                                          w("bv").rearrange("p (h e) -> p h e", h=EH), ALU.add).then_inc(L["vk_sb"].sem, 1)
                    for i in range(2):
                        dve.wait_ge(L["expo"].sem, L["expo"].at(b, i + 1))
                        dve.wait_ge(L["above"].sem, L["above"].at(b, i + 1))
                        dve.tensor_tensor(feats[:, i, :], low[:, i, :], high[:, i, :], ALU.add).then_inc(L["feats"].sem, 1)
                    dve.wait_ge(L["feats"].sem, L["feats"].at(b, 2))
                    for j in range(VARIANTS):
                        dve.tensor_scalar(kvar[:, j, :], feats[:, 1, :], core.w("const", "variant", j, j + 1), None,
                                          ALU.mult).then_inc(L["variant"].sem, 1)
                    for t in range(1, TT):
                        dve.wait_ge(L["states"].sem, L["states"].at(b, TT - 1))
                        at = (t - 1) * EH * EW
                        by_head = lambda m: m.rearrange("p (r j e) -> p r j e", r=4, j=VARIANTS)
                        dve.tensor_tensor(state[:, t - 1, :, :].rearrange("p j (r w) -> p r j w", r=4)[:, :, :, 0:EW],
                                          by_head(small[:, at:at + EH * EW]), by_head(core.w("const", "block16")),
                                          ALU.mult).then_inc(L["states_sb"].sem, 1)
                    for j in range(VARIANTS):
                        mask(dve, b, j)
                        if j >= 2:
                            divide(dve, b, j - 2)
                    divide(dve, b, VARIANTS - 2)
                    divide(dve, b, VARIANTS - 1)
                    dve.wait_ge(L["projected"].sem, L["projected"].at(b, 1))
                    dve.scalar_tensor_tensor(out=core.batch(b), in0=small[:, :], scalar=w("bo"), in1=core.batch(b),
                                             op0=ALU.add, op1=ALU.add).then_inc(L["done"].sem, 1)

    L.close()

GROUPS_OF = {0: ["mha"], 1: ["moe"], 2: ["keep"], 3: ["moe"], 4: ["light"], 5: ["bitffn"], 6: ["slr"], 7: ["bitffn"],
             8: ["pairs"], 9: ["gated"], 10: ["ssm2"], 11: ["gated"], 12: ["elu"], 13: ["cell"], 14: ["ssm3"],
             15: ["cell"]}


def run_layer(nc, core, i):
    if i == 2:
        keep_attention(nc, core, "l2")
    if i == 6:
        landmark_layer(nc, core, "l6")
    if i == 4:
        linear_attention(nc, core, "l4")
    if i == 12:
        elu_attention(nc, core, "l12")
    if i == 0:
        query_softmax_attention(nc, core, "l0")
    if i == 10:
        state_space(nc, core, "l10", "ssm2")
    if i == 14:
        state_space(nc, core, "l14", "ssm3")
    if i in (1, 3):
        routed_ffn(nc, core, f"l{i}", "moe", 16, 8, 1, False)
    if i in (9, 11):
        routed_ffn(nc, core, f"l{i}", "gated", 8, 11, 2, True)
    if i == 8:
        pair_attention(nc, core, f"l{i}")
    if i in (13, 15):
        cell(nc, core, f"l{i}")
    if i in (5, 7):
        bit_ffn(nc, core, f"l{i}")


def last_use(g):
    return max([i for i in PLAN if g in GROUPS_OF[i]], default=PLAN[-1] + 1)


def build_program(nc, x_in, groups_in, out, columns):
    order = ["const"] + [g for i in PLAN for g in GROUPS_OF[i]]
    order = list(dict.fromkeys(order))
    with ExitStack() as ctx:
        x = ctx.enter_context(nc.sbuf_tensor("x", [P, B * S], F32))
        xn = ctx.enter_context(nc.sbuf_tensor("xn", [P, B * S], F32))
        weights, held = {}, []
        for g in sorted(order, key=last_use, reverse=True):
            held.append((g, ctx.enter_context(ExitStack())))
            weights[g] = held[-1][1].enter_context(nc.sbuf_tensor(f"w_{g}", list(groups_in[g].shape), F32))
        landed = {g: ctx.enter_context(nc.semaphore(f"landed_{g}")) for g in order}
        landed["x"] = ctx.enter_context(nc.semaphore("landed_x"))
        stored = ctx.enter_context(nc.semaphore("stored"))
        core = Core(x, xn, weights, landed, columns)
        with nc.Block() as block:
            @block.sync
            def _(sync):
                sync.dma_start(x[:, :], x_in).then_inc(landed["x"], 16)
                for g in order:
                    sync.dma_start(weights[g][:, :], groups_in[g]).then_inc(landed[g], 16)
                sync.wait_ge(landed["x"], 16)
                sync.wait_ge(landed["const"], 16)
        if 5 in PLAN or 7 in PLAN:
            quantise(nc, core)
        for i in PLAN:
            normalise(nc, core, f"n{i}")
            run_layer(nc, core, i)
            while held and last_use(held[-1][0]) <= i:
                held.pop()[1].close()
        with nc.Block() as block:
            @block.sync
            def _(sync):
                sync.dma_start(out, x[:, :]).then_inc(stored, 16)
                sync.wait_ge(stored, 16)



def constants():
    eye = np.eye(P, dtype=np.float32)
    row = np.arange(P)
    mask_rows = np.zeros((P, KT, P), np.float32)
    for r in row[row % 32 < B * KJ]:
        T, i = divmod(KG * (r % KJ) + r // 32, 2)
        mask_rows[r, T, i * HALF + MASK_ROW] = 1
    one_rows = {"q": row[:HALF] == MASK_ROW, "k": (row[:HALF] >= SHIFT_ROW) & (row[:HALF] < SHIFT_ROW + 3)}
    splits = {}
    for n, parts in (("q", Q_PARTS), ("k", K_PARTS)):
        part = np.array(list(parts.ljust(HALF // KHD))).repeat(KHD)
        rest = np.where(one_rows[n], 1, -((part == "m") | (part == "l")).astype(np.float32))
        for key, column in (("ones", one_rows[n]), ("rest", rest), ("last", -(part == "l").astype(np.float32))):
            splits[f"{n}_{key}"] = columns_of(np.tile(np.asarray(column, np.float32), 2))
    return {
        "ones": np.ones((P, P), np.float32),
        "centre": eye - np.float32(1 / D),
        "mean": np.full((P, P), 1 / D, np.float32),
        "eye": eye,
        "falling": rows_of(np.tile(np.arange(16, 0, -1, dtype=np.float32), TT)),
        "falling8": rows_of(np.tile(np.arange(8, 0, -1, dtype=np.float32), TT)),
        "ones_s": np.ones((P, S), np.float32),
        "spread": np.tile(np.eye(2 * NS, dtype=np.float32), (3, 1)),
        "upper": np.triu(np.ones((P, P), np.float32)),
        "token": rows_of(np.arange(S, dtype=np.float32)),
        "block4": np.kron(np.eye(HG), np.ones((32, LHD))).astype(np.float32),
        "block16": np.kron(np.eye(EH), np.ones((EHD, EW))).astype(np.float32),
        "variant": np.stack([(np.arange(P) // EHD % 4 == j) for j in range(VARIANTS)], 1).astype(np.float32),
        "later": np.triu(np.full((P, P), NEG, np.float32), 1),
        "units32": rows_of(np.eye(B * KJ, 32, dtype=np.float32)),
        "batch_rows": np.stack([((row % 32) // KJ == b) for b in range(B)], 1).astype(np.float32),
        "mask_rows": mask_rows.reshape(P, KT * P),
        **splits,
        "v_ones": rows_of((np.arange(KH * 32) % 32 == KHD).astype(np.float32)),
        "minus_half": np.full((P, TT), -0.5, np.float32),
    }


def columns_of(v, width=P):
    return np.asarray(v).reshape(-1, width).T


def row_blocks(m, width=P):
    m = np.asarray(m)
    t = m.shape[0] // width
    return m.reshape(t, width, m.shape[1]).transpose(1, 0, 2).reshape(width, -1)


def rows_of(v):
    return np.broadcast_to(np.asarray(v).reshape(1, -1), (P, np.asarray(v).size))


def side_by_side(m):
    return np.asarray(m).transpose(1, 0, 2).reshape(m.shape[1], -1)


def pick(experts, hidden):
    return np.tile(np.repeat(np.eye(experts, dtype=np.float32), hidden, axis=1), (3, 1))


def in_row_groups(m, first):
    out = np.zeros((D, KH, 32), np.float32)
    out[:, :, first:first + KHD] = m.reshape(D, KH, KHD)
    return out.reshape(D, KH * 32)


def in_part_rows(m, parts):
    out = np.zeros((D, KH, HALF), np.float32)
    out[:, :, :len(parts) * KHD] = np.tile(m.reshape(D, KH, KHD), (1, 1, len(parts)))
    return out.reshape(D, KH * HALF)


def lay_out(v):
    g = {"const": constants()}
    g["moe"] = {"wr": v["L0_ffn_Wr"],
                "w1": np.concatenate([side_by_side(v["L0_ffn_Wg"]), v["L0_ffn_Sg"]], 1),
                "w3": np.concatenate([side_by_side(v["L0_ffn_Wu"]), v["L0_ffn_Su"]], 1),
                "w2": row_blocks(np.concatenate([v["L0_ffn_Wd"].reshape(-1, D), v["L0_ffn_Sd"]])),
                "pick": pick(16, 64)}
    hid = 8 * 176 + 176
    pad = np.zeros((-hid % P, D), np.float32)
    g["gated"] = {"wr": v["L2_ffn_gate_w"].T,
                  "w1": np.concatenate([side_by_side(v["L2_ffn_w1"]), v["L2_ffn_sw1"], pad.T], 1),
                  "w3": np.concatenate([side_by_side(v["L2_ffn_w3"]), v["L2_ffn_sw3"], pad.T], 1),
                  "w2": row_blocks(np.concatenate([v["L2_ffn_w2"].reshape(-1, D), v["L2_ffn_sw2"], pad])),
                  "b1": columns_of(np.concatenate([v["L2_ffn_b1"].ravel(), v["L2_ffn_sb1"], pad[:, 0]])),
                  "b3": columns_of(np.concatenate([v["L2_ffn_b3"].ravel(), v["L2_ffn_sb3"], pad[:, 0]])),
                  "b2": v["L2_ffn_b2"], "sb2": columns_of(v["L2_ffn_sb2"]),
                  "gate_b": rows_of(np.tile(v["L2_ffn_gate_b"], TT)),
                  "pick": pick(8, 176)}
    swap = np.arange(D) ^ 1
    p = "L2_attn_a_"
    g["pairs"] = {"wq": v[p + "Wq"].T, "wk": v[p + "Wk"].T, "wv": v[p + "Wv"].T, "wo": v[p + "Wo"].T,
                  "bq": np.stack([v[p + "bq"], v[p + "bq"][swap]], 1),
                  "bk": np.stack([v[p + "bk"], v[p + "bk"][swap]], 1),
                  "bv": columns_of(v[p + "bv"]), "bo": columns_of(v[p + "bo"]), "beta": rows_of(v[p + "beta"])}
    p = "L0_attn_a_"
    g["mha"] = {"wq": v[p + "q_w"].reshape(-1, D).T, "wk": v[p + "k_w"].reshape(-1, D).T,
                "wv": v[p + "v_w"].reshape(-1, D).T, "wl": row_blocks(v[p + "l_w"].T),
                "bq": columns_of(v[p + "q_b"]), "bk": columns_of(v[p + "k_b"]), "bv": rows_of(v[p + "v_b"]),
                "bl": columns_of(v[p + "l_b"])}
    p = "L2_attn_b_"
    low = v[p + "x_proj_w"].T
    g["ssm2"] = {"w_in": v[p + "in_proj_w"].T, "w_low": row_blocks(low[:, :RANK]), "w_bc": row_blocks(low[:, RANK:]),
                 "w_dt": v[p + "dt_proj_w"].T, "w_out": row_blocks(v[p + "out_proj_w"].T),
                 "conv_w": row_blocks(v[p + "conv_w"]), "conv_b": columns_of(v[p + "conv_b"]),
                 "dt_b": columns_of(v[p + "dt_proj_b"]), "a_log": row_blocks(v[p + "A_log"]),
                 "skip": columns_of(v[p + "D"])}
    p = "L3_attn_b_"
    low = v[p + "x_proj_w"]
    g["ssm3"] = {"w_in": v[p + "in_proj_w"], "w_low": row_blocks(low[:, :RANK]), "w_bc": row_blocks(low[:, RANK:]),
                 "w_dt": v[p + "dt_proj_w"], "w_out": row_blocks(v[p + "out_proj_w"]),
                 "conv_w": row_blocks(v[p + "conv_w"][:, 0, :]), "conv_b": columns_of(v[p + "conv_b"]),
                 "dt_b": columns_of(v[p + "dt_proj_b"]), "a_log": row_blocks(v[p + "A_log"]),
                 "skip": columns_of(v[p + "D_param"])}
    p = "L1_attn_a_"
    wq, wk, wv, wu = np.split(v[p + "qkvu_w"].T, 4, axis=1)
    bq, bk, bv, bu = np.split(v[p + "qkvu_b"], 4)
    twice = np.concatenate([np.concatenate([np.arange(h * LHD, (h + 1) * LHD)] * 2) for h in range(LH)])
    slope = v[p + "slope_rate"].reshape(LH)
    g["light"] = {"wq": wq[:, twice], "wk": wk[:, twice], "wv": wv, "wu": wu, "wo": v[p + "out_w"].T,
                  "bq": columns_of(bq[twice]), "bk": columns_of(bk[twice]), "bv": rows_of(bv), "bu": rows_of(bu),
                  "bo": columns_of(v[p + "out_b"]), "slope": rows_of(slope),
                  "slope_cols": rows_of(np.repeat(slope, LHD)),
                  "theta": columns_of(v[p + "theta"].reshape(-1)[twice]),
                  "shift": columns_of(np.tile(np.repeat(np.float32([np.pi / 2, 0]), LHD), LH))}
    p = "L3_attn_a_"
    wq, wk, wv = np.split(v[p + "qkv_w"], 3, axis=1)
    bq, bk, bv = np.split(v[p + "qkv_b"], 3)
    g["elu"] = {"wq": wq, "wk": wk, "wv": wv, "wo": v[p + "out_w"], "bq": columns_of(bq), "bk": columns_of(bk),
                "bv": rows_of(bv), "bo": columns_of(v[p + "out_b"])}
    p = "L1_attn_b_"
    g["slr"] = {"wq": np.concatenate([v[p + "slr_wq1"], v[p + "slr_wq2"]], 1),
                "wk": np.concatenate([v[p + "slr_wk1"], v[p + "slr_wk2"]], 1), "wv": v[p + "slr_wv"],
                "wo": v[p + "slr_wo"], "r1": v[p + "router_w1"], "r2": v[p + "router_w2"],
                "r2b": rows_of(v[p + "router_b2"]), "landmarks_t": v[p + "landmarks"].T,
                "mix1": v[p + "mix_w"][:D], "mix2": v[p + "mix_w"][D:], "compress": v[p + "bus_compress"],
                "publish": v[p + "bus_publish"], "expand": v[p + "bus_expand"],
                "lam": columns_of(np.repeat(v[p + "lambdas"], D // 8)), "slr_lam": rows_of(v[p + "slr_lam"]),
                "norm_in": columns_of(v[p + "w_norm_in"]), "norm_out": columns_of(v[p + "w_norm_out"])}
    p = "L0_attn_b_"
    wq, wk, wv = (m.T for m in np.split(v[p + "w_attn"], 3))
    g["keep"] = {"wq": in_part_rows(wq, Q_PARTS), "wk": in_part_rows(wk, K_PARTS), "wv": in_row_groups(wv, 0),
                 "wo": v[p + "w_proj"].T}
    p = "L3_ffn_"
    g["cell"] = {k: v[p + k].T for k in ("wf", "uf", "wi", "ui", "wc", "uc", "wo", "uo")}
    g["cell"].update({k: columns_of(v[p + k]) for k in ("bf", "bi", "bc", "bo", "in_c")})
    g["bitffn"] = {"w1": v["L1_ffn_W1"].T, "w2": row_blocks(v["L1_ffn_W2"].T),
                   "b1": columns_of(v["L1_ffn_b1"]), "b2": columns_of(v["L1_ffn_b2"])}
    return g


def pack(matrices):
    at, columns, parts = 0, {}, []
    for name, m in matrices.items():
        m = np.asarray(m)
        columns[name] = (at, m.shape[0], m.shape[1])
        full = np.zeros((P, m.shape[1]), np.float32)
        full[:m.shape[0]] = m
        parts.append(full)
        at += m.shape[1]
    return np.ascontiguousarray(np.concatenate(parts, axis=1)), columns


def kernel(**inputs):
    import concourse.bacc as bacc
    from concourse.bass_utils import run_bass_kernel_spmd

    v = {k: np.asarray(a) for k, a in inputs.items()}
    x = np.ascontiguousarray(v["L0_attn_a_x"].reshape(B * S, D).T)
    nc = bacc.Bacc("TRN2", target_bir_lowering=False, num_devices=1)
    arrays = {"x_in": x}
    x_in = nc.dram_tensor("x_in", x.shape, F32, kind="ExternalInput").ap()
    groups_in, columns = {}, {}
    used = {"const"} | {g for i in PLAN for g in GROUPS_OF[i]}
    for g, matrices in lay_out(v).items():
        if g not in used:
            continue
        packed, columns[g] = pack(matrices)
        arrays[f"in_{g}"] = packed
        groups_in[g] = nc.dram_tensor(f"in_{g}", packed.shape, F32, kind="ExternalInput").ap()
    out = nc.dram_tensor("out", (P, B * S), F32, kind="ExternalOutput").ap()
    build_program(nc, x_in, groups_in, out, columns)
    r = run_bass_kernel_spmd(nc, [arrays], core_ids=[0])
    return np.ascontiguousarray(r.results[0]["out"].T).reshape(B, S, D)
```
